# Optimizing a Trainium2 kernel written in Bass

```python
import numpy as np
import jax
import jax.numpy as jnp

def _softmax(x, axis=-1):
    return jax.nn.softmax(x, axis=axis)

def _gelu(x):
    return jax.nn.gelu(x, approximate=True)

def _silu(x):
    return jax.nn.silu(x)

def _sigmoid(x):
    return jax.nn.sigmoid(x)

def _layernorm(x, axis=-1, eps=1e-05):
    m = jnp.mean(x, axis=axis, keepdims=True)
    v = jnp.var(x, axis=axis, keepdims=True)
    return (x - m) / jnp.sqrt(v + eps)

def _scatter_add(tgt, idx, src, axis=0):
    return tgt.at[idx].add(src)

def _segment_sum(src, seg, n):
    return jax.ops.segment_sum(src, seg, n)
kernel_name = 'mk_decoder_postln_d4_seqx_r4_c4b520'

def setup_inputs(seed: int=0):
    np.random.seed(seed)
    _w = jnp.asarray

    def _rec_inputs():
        import jax
        import jax.numpy as jnp
        _rk = jax.random.key(seed)
        x = 0.002226 + 0.9996 * jax.random.normal(jax.random.fold_in(_rk, 1), (8, 256, 256), jnp.float32)
        _lenS = 256 - jax.random.randint(jax.random.fold_in(_rk, 7), (8,), 0, max(1, 256 // 4) + 1, jnp.int32)
        _lenS2 = 77 - jax.random.randint(jax.random.fold_in(_rk, 8), (8,), 0, max(1, 77 // 4) + 1, jnp.int32)
        _ctx_1024P = jax.random.normal(jax.random.fold_in(_rk, 11), (8, 16, 256), jnp.float32)
        _ctx_1024c = jax.random.dirichlet(jax.random.fold_in(_rk, 511), 0.3 * jnp.ones((16,), jnp.float32), (8, 77))
        _ctx_1024t = jnp.einsum('bsk,bkd->bsd', _ctx_1024c, _ctx_1024P)
        _ctx_1024t = _ctx_1024t * jax.lax.rsqrt(jnp.mean(jnp.square(_ctx_1024t)) + 1e-12) * 0.953939
        ctx_1024 = -0.000125008 + 0.999885 * (_ctx_1024t + 0.3 * jax.random.normal(jax.random.fold_in(_rk, 611), (8, 77, 256), jnp.float32))
        return (x, ctx_1024)
    x, ctx_1024 = _rec_inputs()

    def _L0_attn_setup():
        import jax, jax.numpy as jnp
        import numpy as np
        B, T, D, H, PD = (1, 512, 256, 16, 4)
        DH = D // H
        SCALE = DH ** (-0.5)
        _PI = jnp.array([0, 0, 0, 1, 1, 2])
        _PJ = jnp.array([1, 2, 3, 2, 3, 3])
        J6 = jnp.array([[0, 0, 0, 0, 0, 1], [0, 0, 0, 0, -1, 0], [0, 0, 0, 1, 0, 0], [0, 0, 1, 0, 0, 0], [0, -1, 0, 0, 0, 0], [1, 0, 0, 0, 0, 0]], dtype=jnp.float32)

        def exterior(p1, p2):
            L = p1[..., _PI] * p2[..., _PJ] - p1[..., _PJ] * p2[..., _PI]
            n = jnp.clip(jnp.linalg.norm(L, axis=-1, keepdims=True), 1e-12)
            return L / n
        key = jax.random.key(seed)
        ks = jax.random.split(key, 10)
        s = 0.02
        return {'x': jax.random.normal(ks[0], (B, T, D), dtype=jnp.float32), 'qkv_w': jax.random.normal(ks[1], (D, 3 * D), dtype=jnp.float32) * s, 'qkv_b': jnp.zeros((3 * D,), dtype=jnp.float32), 'w1_write': jax.random.normal(ks[2], (D, PD * H), dtype=jnp.float32) * s, 'w2_write': jax.random.normal(ks[3], (D, PD * H), dtype=jnp.float32) * s, 'w1_read': jax.random.normal(ks[4], (D, PD * H), dtype=jnp.float32) * s, 'w2_read': jax.random.normal(ks[5], (D, PD * H), dtype=jnp.float32) * s, 'kv_geo_w': jax.random.normal(ks[6], (D, 2 * D), dtype=jnp.float32) * s, 'out_w': jax.random.normal(ks[7], (D, D), dtype=jnp.float32) * s, 'out_b': jnp.zeros((D,), dtype=jnp.float32), 'kv_gate': jnp.asarray(0.01, dtype=jnp.float32), 'mem_scale': jnp.full((H,), 0.1, dtype=jnp.float32), 'decay_logits': jnp.full((H,), 4.6, dtype=jnp.float32)}
    _L0_attn_all = _L0_attn_setup()
    _L0_attn_in = {k: v for k, v in _L0_attn_all.items() if k in ('qkv_w', 'qkv_b', 'w1_write', 'w2_write', 'w1_read', 'w2_read', 'kv_geo_w', 'out_w', 'out_b', 'kv_gate', 'mem_scale', 'decay_logits')}
    del _L0_attn_all

    def _L0_xattn_setup():
        import jax, jax.numpy as jnp
        import numpy as np
        DIM = 256
        HEADS = 16
        DIM_HEAD = 64
        INNER = HEADS * DIM_HEAD
        EPS = 1e-05

        def _layernorm(t, w, b):
            mu = jnp.mean(t, axis=-1, keepdims=True)
            var = jnp.mean(jnp.square(t - mu), axis=-1, keepdims=True)
            return (t - mu) * jax.lax.rsqrt(var + EPS) * w + b
        key = jax.random.key(seed)
        ks = jax.random.split(key, 8)
        b, n, l = (8, 1024, 64)
        x = jax.random.normal(ks[0], (b, n, DIM), dtype=jnp.float32)
        latents = jax.random.normal(ks[1], (b, l, DIM), dtype=jnp.float32)
        ln1_w = jnp.ones((DIM,), jnp.float32)
        ln1_b = jnp.zeros((DIM,), jnp.float32)
        ln2_w = jnp.ones((DIM,), jnp.float32)
        ln2_b = jnp.zeros((DIM,), jnp.float32)
        Wq = jax.random.normal(ks[2], (DIM, INNER), dtype=jnp.float32) / np.sqrt(DIM)
        Wkv = jax.random.normal(ks[3], (DIM, 2 * INNER), dtype=jnp.float32) / np.sqrt(DIM)
        Wo = jax.random.normal(ks[4], (INNER, DIM), dtype=jnp.float32) / np.sqrt(INNER)
        return {'x': x, 'latents': latents, 'ln1_w': ln1_w, 'ln1_b': ln1_b, 'ln2_w': ln2_w, 'ln2_b': ln2_b, 'Wq': Wq, 'Wkv': Wkv, 'Wo': Wo}
    _L0_xattn_all = _L0_xattn_setup()
    _L0_xattn_in = {k: v for k, v in _L0_xattn_all.items() if k in ('ln1_w', 'ln1_b', 'ln2_w', 'ln2_b', 'Wq', 'Wkv', 'Wo')}
    del _L0_xattn_all

    def _L0_ffn_setup():
        import jax, jax.numpy as jnp
        import numpy as np
        D = 256
        F = 256
        E = 8
        K = 2
        B, T = (2, 512)

        def _moe_forward(x, router_w, w1, w2, shared_gate_up, shared_down, shared_gate_w):
            b, t, d = x.shape
            xf = x.reshape(-1, d)
            n = xf.shape[0]
            logits = xf @ router_w
            probs = jax.nn.softmax(logits, axis=-1)
            topw, topi = jax.lax.top_k(probs, K)
            combine = jnp.zeros((n, E), dtype=probs.dtype).at[jnp.arange(n)[:, None], topi].add(topw)
            h = jax.nn.silu(jnp.einsum('nd,edf->nef', xf, w1))
            ye = jnp.einsum('nef,efd->ned', h, w2)
            routed = jnp.einsum('ne,ned->nd', combine, ye)
            gu = xf @ shared_gate_up
            gate, up = (gu[:, :F], gu[:, F:])
            shared = jax.nn.silu(gate) * up @ shared_down
            shared = jax.nn.sigmoid(xf @ shared_gate_w) * shared
            return (routed + shared).reshape(b, t, d)
        key = jax.random.key(seed)
        ks = jax.random.split(key, 7)
        std = 0.02
        x = jax.random.normal(ks[0], (B, T, D), dtype=jnp.float32)
        router_w = jax.random.normal(ks[1], (D, E), dtype=jnp.float32) * std
        w1 = jax.random.normal(ks[2], (E, D, F), dtype=jnp.float32) * std
        w2 = jax.random.normal(ks[3], (E, F, D), dtype=jnp.float32) * std
        shared_gate_up = jax.random.normal(ks[4], (D, 2 * F), dtype=jnp.float32) * std
        shared_down = jax.random.normal(ks[5], (F, D), dtype=jnp.float32) * std
        shared_gate_w = jax.random.normal(ks[6], (D, 1), dtype=jnp.float32) * std
        return {'x': x, 'router_w': router_w, 'w1': w1, 'w2': w2, 'shared_gate_up': shared_gate_up, 'shared_down': shared_down, 'shared_gate_w': shared_gate_w}
    _L0_ffn_all = _L0_ffn_setup()
    _L0_ffn_in = {k: v for k, v in _L0_ffn_all.items() if k in ('router_w', 'w1', 'w2', 'shared_gate_up', 'shared_down', 'shared_gate_w')}
    del _L0_ffn_all

    def _L1_attn_setup():
        import jax, jax.numpy as jnp
        import numpy as np
        NUM_HEADS = 16
        BLOCK_SIZE = 64
        key = jax.random.key(seed)
        ks = jax.random.split(key, 4)
        B, S, D = (4, 2048, 256)
        x = jax.random.normal(ks[0], (B, S, D), dtype=jnp.float32)
        Wq = jax.random.normal(ks[1], (D, D), dtype=jnp.float32) * 0.02
        Wk = jax.random.normal(ks[2], (D, D), dtype=jnp.float32) * 0.02
        Wv = jax.random.normal(ks[3], (D, D), dtype=jnp.float32) * 0.02
        bq = jnp.zeros((D,), dtype=jnp.float32)
        bk = jnp.zeros((D,), dtype=jnp.float32)
        bv = jnp.zeros((D,), dtype=jnp.float32)
        return {'x': x, 'Wq': Wq, 'bq': bq, 'Wk': Wk, 'bk': bk, 'Wv': Wv, 'bv': bv}
    _L1_attn_all = _L1_attn_setup()
    _L1_attn_in = {k: v for k, v in _L1_attn_all.items() if k in ('Wq', 'bq', 'Wk', 'bk', 'Wv', 'bv')}
    del _L1_attn_all

    def _L1_xattn_setup():
        import jax, jax.numpy as jnp
        import numpy as np
        DIM = 256
        DIM_HEAD = 64
        HEADS = 16
        INNER = DIM_HEAD * HEADS
        EPS = 1e-05

        def layer_norm(x, g, b):
            m = jnp.mean(x, axis=-1, keepdims=True)
            v = jnp.mean(jnp.square(x - m), axis=-1, keepdims=True)
            return (x - m) * jax.lax.rsqrt(v + EPS) * g + b
        key = jax.random.key(seed)
        ks = jax.random.split(key, 8)
        B, N_IMG, N_LAT = (4, 1024, 128)
        std = 1.0 / np.sqrt(DIM)
        return {'image_embeds': jax.random.normal(ks[0], (B, N_IMG, DIM), dtype=jnp.float32), 'latents': jax.random.normal(ks[1], (B, N_LAT, DIM), dtype=jnp.float32), 'ln1_g': jnp.ones((DIM,), jnp.float32), 'ln1_b': jnp.zeros((DIM,), jnp.float32), 'ln2_g': jnp.ones((DIM,), jnp.float32), 'ln2_b': jnp.zeros((DIM,), jnp.float32), 'Wq': jax.random.normal(ks[2], (DIM, INNER), dtype=jnp.float32) * std, 'Wkv': jax.random.normal(ks[3], (DIM, 2 * INNER), dtype=jnp.float32) * std, 'Wo': jax.random.normal(ks[4], (INNER, DIM), dtype=jnp.float32) * std}
    _L1_xattn_all = _L1_xattn_setup()
    _L1_xattn_in = {k: v for k, v in _L1_xattn_all.items() if k in ('ln1_g', 'ln1_b', 'ln2_g', 'ln2_b', 'Wq', 'Wkv', 'Wo')}
    del _L1_xattn_all

    def _L1_ffn_setup():
        import jax, jax.numpy as jnp
        import numpy as np
        DMODEL = 256
        N_EXPERTS = 16
        EXPERT_SIZE = 64
        K = 4
        key = jax.random.key(seed)
        k1, k2, k3, k4 = jax.random.split(key, 4)
        std_sel = 1.0 / np.sqrt(DMODEL)
        std_val = 1.0 / np.sqrt(N_EXPERTS * EXPERT_SIZE)
        return {'x': jax.random.normal(k1, (4, 512, DMODEL), dtype=jnp.float32), 'expert_sel': jax.random.normal(k2, (N_EXPERTS, DMODEL), dtype=jnp.float32) * std_sel, 'keys': jax.random.normal(k3, (N_EXPERTS, DMODEL, EXPERT_SIZE), dtype=jnp.float32) * std_sel, 'values': jax.random.normal(k4, (N_EXPERTS, EXPERT_SIZE, DMODEL), dtype=jnp.float32) * std_val, 'route_scale': jnp.ones((1,), dtype=jnp.float32)}
    _L1_ffn_all = _L1_ffn_setup()
    _L1_ffn_in = {k: v for k, v in _L1_ffn_all.items() if k in ('expert_sel', 'keys', 'values', 'route_scale')}
    del _L1_ffn_all

    def _L2_attn_setup():
        import jax, jax.numpy as jnp
        import numpy as np
        B, T, K, H = (2, 512, 256, 16)
        key = jax.random.key(seed)
        ks = jax.random.split(key, 9)
        sc = 0.02
        return {'x': jax.random.normal(ks[0], (B, T, K), dtype=jnp.float32), 'Wq_w': jax.random.normal(ks[1], (K, K), dtype=jnp.float32) * sc, 'Wq_b': jax.random.normal(ks[2], (K,), dtype=jnp.float32) * sc, 'Wk_w': jax.random.normal(ks[3], (K, K), dtype=jnp.float32) * sc, 'Wk_b': jax.random.normal(ks[4], (K,), dtype=jnp.float32) * sc, 'Wv_w': jax.random.normal(ks[5], (K, K), dtype=jnp.float32) * sc, 'Wv_b': jax.random.normal(ks[6], (K,), dtype=jnp.float32) * sc, 'Wo_w': jax.random.normal(ks[7], (K, K), dtype=jnp.float32) * sc, 'Wo_b': jax.random.normal(ks[8], (K,), dtype=jnp.float32) * sc}
    _L2_attn_all = _L2_attn_setup()
    _L2_attn_in = {k: v for k, v in _L2_attn_all.items() if k in ('Wq_w', 'Wq_b', 'Wk_w', 'Wk_b', 'Wv_w', 'Wv_b', 'Wo_w', 'Wo_b')}
    del _L2_attn_all

    def _L2_xattn_setup():
        import jax, jax.numpy as jnp
        import numpy as np
        E = 256
        H = 16
        D = E // H
        B, L, S = (2, 512, 512)
        key = jax.random.key(seed)
        ks = jax.random.split(key, 10)
        scale = 1.0 / np.sqrt(E)
        return {'x': jax.random.normal(ks[0], (B, L, E), jnp.float32), 'context': jax.random.normal(ks[1], (B, S, E), jnp.float32), 'Wq': jax.random.normal(ks[2], (E, E), jnp.float32) * scale, 'bq': jnp.zeros((E,), jnp.float32), 'Wk': jax.random.normal(ks[3], (E, E), jnp.float32) * scale, 'bk': jnp.zeros((E,), jnp.float32), 'Wv': jax.random.normal(ks[4], (E, E), jnp.float32) * scale, 'bv': jnp.zeros((E,), jnp.float32), 'Wp': jax.random.normal(ks[5], (E, E), jnp.float32) * scale, 'bp': jnp.zeros((E,), jnp.float32)}
    _L2_xattn_all = _L2_xattn_setup()
    _L2_xattn_in = {k: v for k, v in _L2_xattn_all.items() if k in ('Wq', 'bq', 'Wk', 'bk', 'Wv', 'bv', 'Wp', 'bp')}
    del _L2_xattn_all

    def _L2_ffn_setup():
        import jax, jax.numpy as jnp
        import numpy as np
        INT8_MAX = 127.0

        def _absmax_scale(x, axes):
            amax = jnp.max(jnp.abs(x), axis=axes, keepdims=True)
            return jnp.maximum(amax, 1e-12) / INT8_MAX
        key = jax.random.key(seed)
        k1, k2 = jax.random.split(key)
        lhs = jax.random.normal(k1, (4, 2048, 256), dtype=jnp.float32)
        rhs = jax.random.normal(k2, (256, 256), dtype=jnp.float32)
        return {'lhs': lhs, 'rhs': rhs}
    _L2_ffn_all = _L2_ffn_setup()
    _L2_ffn_in = {k: v for k, v in _L2_ffn_all.items() if k in ('rhs',)}
    del _L2_ffn_all

    def _L3_attn_setup():
        import jax, jax.numpy as jnp
        import numpy as np
        B_SZ, SEQ, D_MODEL, D_STATE, EXPAND = (2, 256, 256, 16, 2)
        D_INNER = D_MODEL * EXPAND

        def _selective_scan(x, delta, A_log, B_mat, C_mat, D_vec):
            A = -jnp.exp(A_log)
            c0 = C_mat[0]

            def step(h, inp):
                x_t, d_t = inp
                h = h * jnp.exp(A * d_t[..., None]) + (x_t * d_t)[..., None] * B_mat
                y_t = h @ c0
                return (h, y_t)
            h0 = jnp.zeros((x.shape[0], A.shape[0], A.shape[1]), x.dtype)
            xs = (jnp.moveaxis(x, 1, 0), jnp.moveaxis(delta, 1, 0))
            _, ys = jax.lax.scan(step, h0, xs)
            y = jnp.moveaxis(ys, 0, 1)
            return y + x * D_vec
        key = jax.random.key(seed)
        ks = jax.random.split(key, 11)
        f32 = jnp.float32
        x = jax.random.normal(ks[0], (B_SZ, SEQ, D_MODEL), f32)
        s_in = 1.0 / np.sqrt(D_MODEL)
        W_in = jax.random.uniform(ks[1], (2 * D_INNER, D_MODEL), f32, -s_in, s_in)
        b_in = jax.random.uniform(ks[2], (2 * D_INNER,), f32, -s_in, s_in)
        W_gate = jax.random.uniform(ks[3], (D_INNER, D_MODEL), f32, -s_in, s_in)
        b_gate = jax.random.uniform(ks[4], (D_INNER,), f32, -s_in, s_in)
        s_out = 1.0 / np.sqrt(D_INNER)
        W_out = jax.random.uniform(ks[5], (D_MODEL, D_INNER), f32, -s_out, s_out)
        b_out = jax.random.uniform(ks[6], (D_MODEL,), f32, -s_out, s_out)
        A_log = jax.random.uniform(ks[7], (D_INNER, D_STATE), f32, -3.0, -1.0)
        B_mat = 0.02 * jax.random.normal(ks[8], (D_INNER, D_STATE), f32)
        C_mat = 0.02 * jax.random.normal(ks[9], (D_INNER, D_STATE), f32)
        D_vec = 0.02 * jax.random.normal(ks[10], (D_INNER,), f32)
        return {'x': x, 'W_in': W_in, 'b_in': b_in, 'W_gate': W_gate, 'b_gate': b_gate, 'W_out': W_out, 'b_out': b_out, 'A_log': A_log, 'B_mat': B_mat, 'C_mat': C_mat, 'D_vec': D_vec}
    _L3_attn_all = _L3_attn_setup()
    _L3_attn_in = {k: v for k, v in _L3_attn_all.items() if k in ('W_in', 'b_in', 'W_gate', 'b_gate', 'W_out', 'b_out', 'A_log', 'B_mat', 'C_mat', 'D_vec')}
    del _L3_attn_all

    def _L3_xattn_setup():
        import jax, jax.numpy as jnp
        import numpy as np
        D_MODEL = 256
        NUM_HEADS = 16
        DEPTH = D_MODEL // NUM_HEADS
        key = jax.random.key(seed)
        ks = jax.random.split(key, 10)
        B, T, C = (2, 512, 768)
        s = 1.0 / np.sqrt(D_MODEL)
        inp = {'x': jax.random.normal(ks[0], (B, T, D_MODEL), dtype=jnp.float32), 'context': jax.random.normal(ks[1], (B, C, D_MODEL), dtype=jnp.float32), 'Wq': jax.random.normal(ks[2], (D_MODEL, D_MODEL), dtype=jnp.float32) * s, 'bq': jnp.zeros((D_MODEL,), dtype=jnp.float32), 'Wk': jax.random.normal(ks[3], (D_MODEL, D_MODEL), dtype=jnp.float32) * s, 'bk': jnp.zeros((D_MODEL,), dtype=jnp.float32), 'Wv': jax.random.normal(ks[4], (D_MODEL, D_MODEL), dtype=jnp.float32) * s, 'bv': jnp.zeros((D_MODEL,), dtype=jnp.float32), 'Wo': jax.random.normal(ks[5], (D_MODEL, D_MODEL), dtype=jnp.float32) * s, 'bo': jnp.zeros((D_MODEL,), dtype=jnp.float32)}
        return inp
    _L3_xattn_all = _L3_xattn_setup()
    _L3_xattn_in = {k: v for k, v in _L3_xattn_all.items() if k in ('Wq', 'bq', 'Wk', 'bk', 'Wv', 'bv', 'Wo', 'bo')}
    del _L3_xattn_all

    def _L3_ffn_setup():
        import jax, jax.numpy as jnp
        import numpy as np
        B, S, D = (4, 512, 256)
        E = 8
        F = 1024
        T = B * S
        CAP = 320
        key = jax.random.key(seed)
        k1, k2, k3, k4 = jax.random.split(key, 4)
        inputs = jax.random.normal(k1, (B, S, D), dtype=jnp.float32)
        gate_w = jax.random.normal(k2, (D, E), dtype=jnp.float32) / np.sqrt(D)
        w1 = jax.random.normal(k3, (E, D, F), dtype=jnp.float32) / np.sqrt(D)
        w2 = jax.random.normal(k4, (E, F, D), dtype=jnp.float32) / np.sqrt(F)
        return {'inputs': inputs, 'gate_w': gate_w, 'w1': w1, 'w2': w2}
    _L3_ffn_all = _L3_ffn_setup()
    _L3_ffn_in = {k: v for k, v in _L3_ffn_all.items() if k in ('gate_w', 'w1', 'w2')}
    del _L3_ffn_all
    return {'x': x, 'ctx_1024': ctx_1024, 'L0_attn_qkv_w': _L0_attn_in['qkv_w'], 'L0_attn_qkv_b': _L0_attn_in['qkv_b'], 'L0_attn_w1_write': _L0_attn_in['w1_write'], 'L0_attn_w2_write': _L0_attn_in['w2_write'], 'L0_attn_w1_read': _L0_attn_in['w1_read'], 'L0_attn_w2_read': _L0_attn_in['w2_read'], 'L0_attn_kv_geo_w': _L0_attn_in['kv_geo_w'], 'L0_attn_out_w': _L0_attn_in['out_w'], 'L0_attn_out_b': _L0_attn_in['out_b'], 'L0_attn_kv_gate': _L0_attn_in['kv_gate'], 'L0_attn_mem_scale': _L0_attn_in['mem_scale'], 'L0_attn_decay_logits': _L0_attn_in['decay_logits'], 'L0_xattn_ln1_w': _L0_xattn_in['ln1_w'], 'L0_xattn_ln1_b': _L0_xattn_in['ln1_b'], 'L0_xattn_ln2_w': _L0_xattn_in['ln2_w'], 'L0_xattn_ln2_b': _L0_xattn_in['ln2_b'], 'L0_xattn_Wq': _L0_xattn_in['Wq'], 'L0_xattn_Wkv': _L0_xattn_in['Wkv'], 'L0_xattn_Wo': _L0_xattn_in['Wo'], 'L0_ffn_router_w': _L0_ffn_in['router_w'], 'L0_ffn_w1': _L0_ffn_in['w1'], 'L0_ffn_w2': _L0_ffn_in['w2'], 'L0_ffn_shared_gate_up': _L0_ffn_in['shared_gate_up'], 'L0_ffn_shared_down': _L0_ffn_in['shared_down'], 'L0_ffn_shared_gate_w': _L0_ffn_in['shared_gate_w'], 'L1_attn_Wq': _L1_attn_in['Wq'], 'L1_attn_bq': _L1_attn_in['bq'], 'L1_attn_Wk': _L1_attn_in['Wk'], 'L1_attn_bk': _L1_attn_in['bk'], 'L1_attn_Wv': _L1_attn_in['Wv'], 'L1_attn_bv': _L1_attn_in['bv'], 'L1_xattn_ln1_g': _L1_xattn_in['ln1_g'], 'L1_xattn_ln1_b': _L1_xattn_in['ln1_b'], 'L1_xattn_ln2_g': _L1_xattn_in['ln2_g'], 'L1_xattn_ln2_b': _L1_xattn_in['ln2_b'], 'L1_xattn_Wq': _L1_xattn_in['Wq'], 'L1_xattn_Wkv': _L1_xattn_in['Wkv'], 'L1_xattn_Wo': _L1_xattn_in['Wo'], 'L1_ffn_expert_sel': _L1_ffn_in['expert_sel'], 'L1_ffn_keys': _L1_ffn_in['keys'], 'L1_ffn_values': _L1_ffn_in['values'], 'L1_ffn_route_scale': _L1_ffn_in['route_scale'], 'L2_attn_Wq_w': _L2_attn_in['Wq_w'], 'L2_attn_Wq_b': _L2_attn_in['Wq_b'], 'L2_attn_Wk_w': _L2_attn_in['Wk_w'], 'L2_attn_Wk_b': _L2_attn_in['Wk_b'], 'L2_attn_Wv_w': _L2_attn_in['Wv_w'], 'L2_attn_Wv_b': _L2_attn_in['Wv_b'], 'L2_attn_Wo_w': _L2_attn_in['Wo_w'], 'L2_attn_Wo_b': _L2_attn_in['Wo_b'], 'L2_xattn_Wq': _L2_xattn_in['Wq'], 'L2_xattn_bq': _L2_xattn_in['bq'], 'L2_xattn_Wk': _L2_xattn_in['Wk'], 'L2_xattn_bk': _L2_xattn_in['bk'], 'L2_xattn_Wv': _L2_xattn_in['Wv'], 'L2_xattn_bv': _L2_xattn_in['bv'], 'L2_xattn_Wp': _L2_xattn_in['Wp'], 'L2_xattn_bp': _L2_xattn_in['bp'], 'L2_ffn_rhs': _L2_ffn_in['rhs'], 'L3_attn_W_in': _L3_attn_in['W_in'], 'L3_attn_b_in': _L3_attn_in['b_in'], 'L3_attn_W_gate': _L3_attn_in['W_gate'], 'L3_attn_b_gate': _L3_attn_in['b_gate'], 'L3_attn_W_out': _L3_attn_in['W_out'], 'L3_attn_b_out': _L3_attn_in['b_out'], 'L3_attn_A_log': _L3_attn_in['A_log'], 'L3_attn_B_mat': _L3_attn_in['B_mat'], 'L3_attn_C_mat': _L3_attn_in['C_mat'], 'L3_attn_D_vec': _L3_attn_in['D_vec'], 'L3_xattn_Wq': _L3_xattn_in['Wq'], 'L3_xattn_bq': _L3_xattn_in['bq'], 'L3_xattn_Wk': _L3_xattn_in['Wk'], 'L3_xattn_bk': _L3_xattn_in['bk'], 'L3_xattn_Wv': _L3_xattn_in['Wv'], 'L3_xattn_bv': _L3_xattn_in['bv'], 'L3_xattn_Wo': _L3_xattn_in['Wo'], 'L3_xattn_bo': _L3_xattn_in['bo'], 'L3_ffn_gate_w': _L3_ffn_in['gate_w'], 'L3_ffn_w1': _L3_ffn_in['w1'], 'L3_ffn_w2': _L3_ffn_in['w2']}

def reference(x, ctx_1024, L0_attn_qkv_w, L0_attn_qkv_b, L0_attn_w1_write, L0_attn_w2_write, L0_attn_w1_read, L0_attn_w2_read, L0_attn_kv_geo_w, L0_attn_out_w, L0_attn_out_b, L0_attn_kv_gate, L0_attn_mem_scale, L0_attn_decay_logits, L0_xattn_ln1_w, L0_xattn_ln1_b, L0_xattn_ln2_w, L0_xattn_ln2_b, L0_xattn_Wq, L0_xattn_Wkv, L0_xattn_Wo, L0_ffn_router_w, L0_ffn_w1, L0_ffn_w2, L0_ffn_shared_gate_up, L0_ffn_shared_down, L0_ffn_shared_gate_w, L1_attn_Wq, L1_attn_bq, L1_attn_Wk, L1_attn_bk, L1_attn_Wv, L1_attn_bv, L1_xattn_ln1_g, L1_xattn_ln1_b, L1_xattn_ln2_g, L1_xattn_ln2_b, L1_xattn_Wq, L1_xattn_Wkv, L1_xattn_Wo, L1_ffn_expert_sel, L1_ffn_keys, L1_ffn_values, L1_ffn_route_scale, L2_attn_Wq_w, L2_attn_Wq_b, L2_attn_Wk_w, L2_attn_Wk_b, L2_attn_Wv_w, L2_attn_Wv_b, L2_attn_Wo_w, L2_attn_Wo_b, L2_xattn_Wq, L2_xattn_bq, L2_xattn_Wk, L2_xattn_bk, L2_xattn_Wv, L2_xattn_bv, L2_xattn_Wp, L2_xattn_bp, L2_ffn_rhs, L3_attn_W_in, L3_attn_b_in, L3_attn_W_gate, L3_attn_b_gate, L3_attn_W_out, L3_attn_b_out, L3_attn_A_log, L3_attn_B_mat, L3_attn_C_mat, L3_attn_D_vec, L3_xattn_Wq, L3_xattn_bq, L3_xattn_Wk, L3_xattn_bk, L3_xattn_Wv, L3_xattn_bv, L3_xattn_Wo, L3_xattn_bo, L3_ffn_gate_w, L3_ffn_w1, L3_ffn_w2):
    import jax
    import jax.numpy as jnp

    def _L0_attn_ref(x, qkv_w, qkv_b, w1_write, w2_write, w1_read, w2_read, kv_geo_w, out_w, out_b, kv_gate, mem_scale, decay_logits):
        import jax, jax.numpy as jnp
        import numpy as np
        B, T, D, H, PD = (1, 512, 256, 16, 4)
        DH = D // H
        SCALE = DH ** (-0.5)
        _PI = jnp.array([0, 0, 0, 1, 1, 2])
        _PJ = jnp.array([1, 2, 3, 2, 3, 3])
        J6 = jnp.array([[0, 0, 0, 0, 0, 1], [0, 0, 0, 0, -1, 0], [0, 0, 0, 1, 0, 0], [0, 0, 1, 0, 0, 0], [0, -1, 0, 0, 0, 0], [1, 0, 0, 0, 0, 0]], dtype=jnp.float32)

        def exterior(p1, p2):
            L = p1[..., _PI] * p2[..., _PJ] - p1[..., _PJ] * p2[..., _PI]
            n = jnp.clip(jnp.linalg.norm(L, axis=-1, keepdims=True), 1e-12)
            return L / n
        b, t, d = x.shape
        qkv = (x @ qkv_w + qkv_b).reshape(b, t, 3, H, DH)
        q = qkv[:, :, 0].transpose(0, 2, 1, 3)
        k = qkv[:, :, 1].transpose(0, 2, 1, 3)
        v = qkv[:, :, 2].transpose(0, 2, 1, 3)
        x_prev = jnp.concatenate([jnp.zeros((b, 1, d), x.dtype), x[:, :-1]], axis=1)
        w1 = (x_prev @ w1_write).reshape(b, t, H, PD)
        w2 = (x @ w2_write).reshape(b, t, H, PD)
        write_lines = exterior(w1, w2)
        r1 = (x @ w1_read).reshape(b, t, H, PD)
        r2 = (x @ w2_read).reshape(b, t, H, PD)
        read_lines = exterior(r1, r2)
        j_write = jnp.einsum('bthi,ij->bthj', write_lines, J6)
        incidence = jnp.einsum('bthp,bshp->bhts', read_lines, j_write)
        pos = jnp.arange(t)
        diffs = pos[:, None] - pos[None, :]
        causal = diffs > 0
        decays = jax.nn.sigmoid(decay_logits)
        expn = jnp.maximum(diffs, 0).astype(x.dtype)
        weights = jnp.where(causal[None], decays[:, None, None] ** expn[None], 0.0)
        mem_score = jnp.einsum('bhts,hts->bht', incidence ** 2, weights)
        gram_gate = jax.nn.sigmoid(mem_score * mem_scale[None, :, None])[..., None]
        kv_geo = (x @ kv_geo_w).reshape(b, t, 2, H, DH)
        k_geo = kv_geo[:, :, 0].transpose(0, 2, 1, 3)
        v_geo = kv_geo[:, :, 1].transpose(0, 2, 1, 3)
        k_enh = k + kv_gate * gram_gate * k_geo
        v_enh = v + kv_gate * gram_gate * v_geo
        scores = jnp.einsum('bhtd,bhsd->bhts', q, k_enh) * SCALE
        scores = jnp.where((diffs >= 0)[None, None], scores, -jnp.inf)
        attn = jax.nn.softmax(scores, axis=-1)
        out = jnp.einsum('bhts,bhsd->bhtd', attn, v_enh)
        out = out.transpose(0, 2, 1, 3).reshape(b, t, d)
        return out @ out_w + out_b

    def _L0_xattn_ref(x, latents, ln1_w, ln1_b, ln2_w, ln2_b, Wq, Wkv, Wo):
        import jax, jax.numpy as jnp
        import numpy as np
        DIM = 256
        HEADS = 16
        DIM_HEAD = 64
        INNER = HEADS * DIM_HEAD
        EPS = 1e-05

        def _layernorm(t, w, b):
            mu = jnp.mean(t, axis=-1, keepdims=True)
            var = jnp.mean(jnp.square(t - mu), axis=-1, keepdims=True)
            return (t - mu) * jax.lax.rsqrt(var + EPS) * w + b
        xn = _layernorm(x, ln1_w, ln1_b)
        latn = _layernorm(latents, ln2_w, ln2_b)
        b, l, _ = latn.shape
        q = latn @ Wq
        kv_input = jnp.concatenate([xn, latn], axis=1)
        kv = kv_input @ Wkv
        k, v = jnp.split(kv, 2, axis=-1)

        def heads(t):
            return t.reshape(t.shape[0], t.shape[1], HEADS, DIM_HEAD).transpose(0, 2, 1, 3)
        q, k, v = (heads(q), heads(k), heads(v))
        scale = 1.0 / np.sqrt(np.sqrt(DIM_HEAD))
        weight = jnp.einsum('bhld,bhnd->bhln', q * scale, k * scale)
        weight = jax.nn.softmax(weight.astype(jnp.float32), axis=-1).astype(weight.dtype)
        out = jnp.einsum('bhln,bhnd->bhld', weight, v)
        out = out.transpose(0, 2, 1, 3).reshape(b, l, INNER)
        return out @ Wo

    def _L0_ffn_ref(x, router_w, w1, w2, shared_gate_up, shared_down, shared_gate_w):
        import jax, jax.numpy as jnp
        import numpy as np
        D = 256
        F = 256
        E = 8
        K = 2
        B, T = (2, 512)

        def _moe_forward(x, router_w, w1, w2, shared_gate_up, shared_down, shared_gate_w):
            b, t, d = x.shape
            xf = x.reshape(-1, d)
            n = xf.shape[0]
            logits = xf @ router_w
            probs = jax.nn.softmax(logits, axis=-1)
            topw, topi = jax.lax.top_k(probs, K)
            combine = jnp.zeros((n, E), dtype=probs.dtype).at[jnp.arange(n)[:, None], topi].add(topw)
            h = jax.nn.silu(jnp.einsum('nd,edf->nef', xf, w1))
            ye = jnp.einsum('nef,efd->ned', h, w2)
            routed = jnp.einsum('ne,ned->nd', combine, ye)
            gu = xf @ shared_gate_up
            gate, up = (gu[:, :F], gu[:, F:])
            shared = jax.nn.silu(gate) * up @ shared_down
            shared = jax.nn.sigmoid(xf @ shared_gate_w) * shared
            return (routed + shared).reshape(b, t, d)
        return _moe_forward(x, router_w, w1, w2, shared_gate_up, shared_down, shared_gate_w)

    def _L1_attn_ref(x, Wq, bq, Wk, bk, Wv, bv):
        import jax, jax.numpy as jnp
        import numpy as np
        NUM_HEADS = 16
        BLOCK_SIZE = 64
        B, S, D = x.shape
        H, bs = (NUM_HEADS, BLOCK_SIZE)
        d = D // H
        nb = S // bs
        q = (x @ Wq + bq).reshape(B, nb, bs, H, d)
        k = (x @ Wk + bk).reshape(B, nb, bs, H, d)
        v = (x @ Wv + bv).reshape(B, nb, bs, H, d)
        scale = 1.0 / jnp.sqrt(jnp.asarray(d, dtype=x.dtype))
        scores = jnp.einsum('bnihd,bnjhd->bnhij', q, k) * scale
        attn = jax.nn.softmax(scores, axis=-1)
        out = jnp.einsum('bnhij,bnjhd->bnihd', attn, v)
        return out.reshape(B, S, D)

    def _L1_xattn_ref(image_embeds, latents, ln1_g, ln1_b, ln2_g, ln2_b, Wq, Wkv, Wo):
        import jax, jax.numpy as jnp
        import numpy as np
        DIM = 256
        DIM_HEAD = 64
        HEADS = 16
        INNER = DIM_HEAD * HEADS
        EPS = 1e-05

        def layer_norm(x, g, b):
            m = jnp.mean(x, axis=-1, keepdims=True)
            v = jnp.mean(jnp.square(x - m), axis=-1, keepdims=True)
            return (x - m) * jax.lax.rsqrt(v + EPS) * g + b
        B, S_lat, _ = latents.shape
        x = layer_norm(image_embeds, ln1_g, ln1_b)
        l = layer_norm(latents, ln2_g, ln2_b)
        q = l @ Wq
        kv_in = jnp.concatenate([x, l], axis=1)
        kv = kv_in @ Wkv
        k, v = jnp.split(kv, 2, axis=-1)

        def to_heads(t):
            return t.reshape(t.shape[0], t.shape[1], HEADS, DIM_HEAD).transpose(0, 2, 1, 3)
        q, k, v = (to_heads(q), to_heads(k), to_heads(v))
        scale = 1.0 / np.sqrt(np.sqrt(DIM_HEAD))
        w = jnp.einsum('bhqd,bhkd->bhqk', q * scale, k * scale)
        w = jax.nn.softmax(w.astype(jnp.float32), axis=-1).astype(q.dtype)
        out = jnp.einsum('bhqk,bhkd->bhqd', w, v)
        out = out.transpose(0, 2, 1, 3).reshape(B, S_lat, INNER)
        return out @ Wo

    def _L1_ffn_ref(x, expert_sel, keys, values, route_scale):
        import jax, jax.numpy as jnp
        import numpy as np
        DMODEL = 256
        N_EXPERTS = 16
        EXPERT_SIZE = 64
        K = 4
        sel_logits = jnp.einsum('btd,ed->bte', x, expert_sel)
        sel_probs = jax.nn.sigmoid(sel_logits)
        _, sel_index = jax.lax.top_k(sel_probs, K)
        sel_val = jnp.take_along_axis(sel_probs, sel_index, axis=-1)
        sel_val = sel_val / jnp.clip(sel_val.sum(-1, keepdims=True), 1e-09)
        sel_val = sel_val * route_scale
        scores_all = jax.nn.relu(jnp.einsum('btd,edh->bteh', x, keys))
        values_all = jnp.einsum('bteh,ehv->btev', scores_all, values)
        sel_idx_exp = sel_index[..., None]
        selected = jnp.take_along_axis(values_all, sel_idx_exp, axis=2)
        out = (selected * sel_val[..., None]).sum(axis=2)
        return out

    def _L2_attn_ref(x, Wq_w, Wq_b, Wk_w, Wk_b, Wv_w, Wv_b, Wo_w, Wo_b):
        import jax, jax.numpy as jnp
        import numpy as np
        B, T, K, H = (2, 512, 256, 16)
        b, t, k = x.shape
        h = H
        s = k // h
        q = x @ Wq_w.T + Wq_b
        kk = x @ Wk_w.T + Wk_b
        v = x @ Wv_w.T + Wv_b
        q = q.reshape(b, t, h, s).transpose(0, 2, 1, 3)
        kk = kk.reshape(b, t, h, s).transpose(0, 2, 1, 3)
        v = v.reshape(b, t, h, s).transpose(0, 2, 1, 3)
        dot = jnp.einsum('bhqd,bhkd->bhqk', q, kk)
        causal = jnp.tril(jnp.ones((t, t), dtype=bool))
        dot = jnp.where(causal, dot, -jnp.inf)
        dot = dot / jnp.sqrt(jnp.asarray(k, dot.dtype))
        attn = jax.nn.softmax(dot, axis=-1)
        out = jnp.einsum('bhqk,bhkd->bhqd', attn, v)
        out = out.transpose(0, 2, 1, 3).reshape(b, t, k)
        return out @ Wo_w.T + Wo_b

    def _L2_xattn_ref(x, context, Wq, bq, Wk, bk, Wv, bv, Wp, bp):
        import jax, jax.numpy as jnp
        import numpy as np
        E = 256
        H = 16
        D = E // H
        B, L, S = (2, 512, 512)
        b, l, _ = x.shape
        s = context.shape[1]
        q = (x @ Wq + bq).reshape(b, l, H, D).transpose(0, 2, 1, 3)
        k = (context @ Wk + bk).reshape(b, s, H, D).transpose(0, 2, 1, 3)
        v = (context @ Wv + bv).reshape(b, s, H, D).transpose(0, 2, 1, 3)
        attn = jnp.einsum('bhld,bhsd->bhls', q, k) / jnp.sqrt(jnp.float32(D))
        attn = jax.nn.softmax(attn, axis=-1)
        out = jnp.einsum('bhls,bhsd->bhld', attn, v)
        out = out.transpose(0, 2, 1, 3).reshape(b, l, E)
        return out @ Wp + bp

    def _L2_ffn_ref(lhs, rhs):
        import jax, jax.numpy as jnp
        import numpy as np
        INT8_MAX = 127.0

        def _absmax_scale(x, axes):
            amax = jnp.max(jnp.abs(x), axis=axes, keepdims=True)
            return jnp.maximum(amax, 1e-12) / INT8_MAX
        lhs_scale = _absmax_scale(lhs, (2,))
        rhs_scale = _absmax_scale(rhs, (0,))
        q_lhs = jnp.clip(jnp.round(lhs / lhs_scale), -INT8_MAX, INT8_MAX).astype(jnp.int8)
        q_rhs = jnp.clip(jnp.round(rhs / rhs_scale), -INT8_MAX, INT8_MAX).astype(jnp.int8)
        acc = jax.lax.dot_general(q_lhs, q_rhs, (((2,), (0,)), ((), ())), preferred_element_type=jnp.int32)
        return acc.astype(jnp.float32) * lhs_scale * rhs_scale

    def _L3_attn_ref(x, W_in, b_in, W_gate, b_gate, W_out, b_out, A_log, B_mat, C_mat, D_vec):
        import jax, jax.numpy as jnp
        import numpy as np
        B_SZ, SEQ, D_MODEL, D_STATE, EXPAND = (2, 256, 256, 16, 2)
        D_INNER = D_MODEL * EXPAND

        def _selective_scan(x, delta, A_log, B_mat, C_mat, D_vec):
            A = -jnp.exp(A_log)
            c0 = C_mat[0]

            def step(h, inp):
                x_t, d_t = inp
                h = h * jnp.exp(A * d_t[..., None]) + (x_t * d_t)[..., None] * B_mat
                y_t = h @ c0
                return (h, y_t)
            h0 = jnp.zeros((x.shape[0], A.shape[0], A.shape[1]), x.dtype)
            xs = (jnp.moveaxis(x, 1, 0), jnp.moveaxis(delta, 1, 0))
            _, ys = jax.lax.scan(step, h0, xs)
            y = jnp.moveaxis(ys, 0, 1)
            return y + x * D_vec
        gate = jax.nn.sigmoid(x @ W_gate.T + b_gate)
        proj = x @ W_in.T + b_in
        x_proj, delta_proj = jnp.split(proj, 2, axis=-1)
        delta = jax.nn.relu(delta_proj)
        ss = _selective_scan(x_proj, delta, A_log, B_mat, C_mat, D_vec)
        return gate * ss @ W_out.T + b_out

    def _L3_xattn_ref(x, context, Wq, bq, Wk, bk, Wv, bv, Wo, bo):
        import jax, jax.numpy as jnp
        import numpy as np
        D_MODEL = 256
        NUM_HEADS = 16
        DEPTH = D_MODEL // NUM_HEADS
        B, T, D = x.shape
        C = context.shape[1]
        H, d = (NUM_HEADS, DEPTH)
        q = x @ Wq.T + bq
        k = context @ Wk.T + bk
        v = context @ Wv.T + bv
        q = q.reshape(B, T, H, d).transpose(0, 2, 1, 3)
        k = k.reshape(B, C, H, d).transpose(0, 2, 1, 3)
        v = v.reshape(B, C, H, d).transpose(0, 2, 1, 3)
        scores = jnp.einsum('bhtd,bhcd->bhtc', q, k) / jnp.sqrt(jnp.asarray(d, x.dtype))
        attn = jax.nn.softmax(scores, axis=-1)
        out = jnp.einsum('bhtc,bhcd->bhtd', attn, v)
        out = out.transpose(0, 2, 1, 3).reshape(B, T, D)
        return out @ Wo.T + bo

    def _L3_ffn_ref(inputs, gate_w, w1, w2):
        import jax, jax.numpy as jnp
        import numpy as np
        B, S, D = (4, 512, 256)
        E = 8
        F = 1024
        T = B * S
        CAP = 320
        tokens = inputs.reshape(-1, D)
        logits = tokens @ gate_w
        probs = jax.nn.softmax(logits, axis=-1)
        expert_idx = jnp.argmax(probs, axis=-1)
        mask1 = jax.nn.one_hot(expert_idx, E, dtype=tokens.dtype)
        pos = (jnp.cumsum(mask1, axis=0) - 1.0).astype(jnp.int32)
        sec_mask = mask1[:, :, None] * jax.nn.one_hot(pos, CAP, dtype=tokens.dtype)
        combine_weights = probs[:, :, None] * sec_mask
        expert_input = jnp.einsum('tec,td->ecd', sec_mask, tokens)
        h = jax.nn.relu(jnp.einsum('ecd,edf->ecf', expert_input, w1))
        expert_output = jnp.einsum('ecf,efd->ecd', h, w2)
        out = jnp.einsum('tec,ecd->td', combine_weights, expert_output)
        return out.reshape(inputs.shape)
    x = _layernorm(x + _L0_attn_ref(x, L0_attn_qkv_w, L0_attn_qkv_b, L0_attn_w1_write, L0_attn_w2_write, L0_attn_w1_read, L0_attn_w2_read, L0_attn_kv_geo_w, L0_attn_out_w, L0_attn_out_b, L0_attn_kv_gate, L0_attn_mem_scale, L0_attn_decay_logits), axis=-1)
    x = _layernorm(x + _L0_xattn_ref(ctx_1024, x, L0_xattn_ln1_w, L0_xattn_ln1_b, L0_xattn_ln2_w, L0_xattn_ln2_b, L0_xattn_Wq, L0_xattn_Wkv, L0_xattn_Wo), axis=-1)
    x = _layernorm(x + _L0_ffn_ref(x, L0_ffn_router_w, L0_ffn_w1, L0_ffn_w2, L0_ffn_shared_gate_up, L0_ffn_shared_down, L0_ffn_shared_gate_w), axis=-1)
    x = _layernorm(x + _L1_attn_ref(x, L1_attn_Wq, L1_attn_bq, L1_attn_Wk, L1_attn_bk, L1_attn_Wv, L1_attn_bv), axis=-1)
    x = _layernorm(x + _L1_xattn_ref(ctx_1024, x, L1_xattn_ln1_g, L1_xattn_ln1_b, L1_xattn_ln2_g, L1_xattn_ln2_b, L1_xattn_Wq, L1_xattn_Wkv, L1_xattn_Wo), axis=-1)
    x = _layernorm(x + _L1_ffn_ref(x, L1_ffn_expert_sel, L1_ffn_keys, L1_ffn_values, L1_ffn_route_scale), axis=-1)
    x = _layernorm(x + _L2_attn_ref(x, L2_attn_Wq_w, L2_attn_Wq_b, L2_attn_Wk_w, L2_attn_Wk_b, L2_attn_Wv_w, L2_attn_Wv_b, L2_attn_Wo_w, L2_attn_Wo_b), axis=-1)
    x = _layernorm(x + _L2_xattn_ref(x, ctx_1024, L2_xattn_Wq, L2_xattn_bq, L2_xattn_Wk, L2_xattn_bk, L2_xattn_Wv, L2_xattn_bv, L2_xattn_Wp, L2_xattn_bp), axis=-1)
    x = _layernorm(x + _L2_ffn_ref(x, L2_ffn_rhs), axis=-1)
    x = _layernorm(x + _L3_attn_ref(x, L3_attn_W_in, L3_attn_b_in, L3_attn_W_gate, L3_attn_b_gate, L3_attn_W_out, L3_attn_b_out, L3_attn_A_log, L3_attn_B_mat, L3_attn_C_mat, L3_attn_D_vec), axis=-1)
    x = _layernorm(x + _L3_xattn_ref(x, ctx_1024, L3_xattn_Wq, L3_xattn_bq, L3_xattn_Wk, L3_xattn_bk, L3_xattn_Wv, L3_xattn_bv, L3_xattn_Wo, L3_xattn_bo), axis=-1)
    x = _layernorm(x + _L3_ffn_ref(x, L3_ffn_gate_w, L3_ffn_w1, L3_ffn_w2), axis=-1)
    return x

_drawn_inputs = setup_inputs


def setup_inputs(seed=0):
    import zlib

    import numpy as np

    out = dict(_drawn_inputs(seed))
    spreads = {'L0_attn_qkv_b': (0.0, 0.1),
     'L0_attn_out_b': (0.0, 0.1),
     'L0_attn_mem_scale': (0.10000000149011612, 0.6),
     'L0_attn_decay_logits': (4.599999904632568, 0.6),
     'L0_xattn_ln1_w': (1.0, 0.2),
     'L0_xattn_ln1_b': (0.0, 0.1),
     'L0_xattn_ln2_w': (1.0, 0.2),
     'L0_xattn_ln2_b': (0.0, 0.1),
     'L1_attn_bq': (0.0, 0.445),
     'L1_attn_bk': (0.0, 2.0),
     'L1_attn_bv': (0.0, 0.1),
     'L1_xattn_ln1_g': (1.0, 0.2),
     'L1_xattn_ln1_b': (0.0, 0.1),
     'L1_xattn_ln2_g': (1.0, 0.2),
     'L1_xattn_ln2_b': (0.0, 0.1),
     'L2_xattn_bq': (0.0, 0.1),
     'L2_xattn_bk': (0.0, 2.0),
     'L2_xattn_bv': (0.0, 0.1),
     'L2_xattn_bp': (0.0, 0.1),
     'L3_xattn_bq': (0.0, 0.1),
     'L3_xattn_bk': (0.0, 2.0),
     'L3_xattn_bv': (0.0, 0.1),
     'L3_xattn_bo': (0.0, 0.1)}
    factors = {'L0_attn_w1_write': 64.0,
     'L0_attn_w2_write': 64.0,
     'L0_attn_w1_read': 64.0,
     'L0_attn_w2_read': 64.0,
     'L0_attn_kv_geo_w': 43.576,
     'L0_ffn_shared_gate_up': 2.765,
     'L0_ffn_shared_gate_w': 3.643,
     'L1_attn_Wq': 3.005,
     'L1_attn_Wk': 2.685,
     'L2_attn_Wq_w': 8.0,
     'L2_attn_Wq_b': 56.382,
     'L2_attn_Wk_w': 7.535,
     'L2_attn_Wk_b': 64.0,
     'L2_attn_Wv_b': 3.358,
     'L3_attn_W_in': 3.528,
     'L3_attn_b_in': 8.0,
     'L3_attn_W_gate': 7.186,
     'L3_attn_b_gate': 8.0,
     'L3_attn_W_out': 3.784,
     'L3_attn_A_log': 26.897,
     'L3_attn_B_mat': 5.673,
     'L3_attn_C_mat': 5.362,
     'L3_attn_D_vec': 5.77,
     'L0_ffn_router_w': 2.907,
     'L0_ffn_w1': 2.727,
     'L3_attn_b_out': 4.674}
    for name, (base, spread) in spreads.items():
        noise = np.random.default_rng([zlib.crc32(name.encode()), seed]).standard_normal(out[name].shape)
        drawn = base * np.exp(spread * noise) if base else spread * noise
        out[name] = jnp.asarray(drawn.astype(out[name].dtype))
    for name, factor in factors.items():
        out[name] = (out[name] * factor).astype(out[name].dtype)
    return out
```

```python
from contextlib import ExitStack

import numpy as np

import concourse.bass as bass
from concourse import mybir

F32 = mybir.dt.float32
BF16 = mybir.dt.bfloat16
I32 = mybir.dt.int32
U32 = mybir.dt.uint32
ALU = mybir.AluOpType
ACT = mybir.ActivationFunctionType
AX = mybir.AxisListType

P = 128
B = 8
T = 256
D = 256
C = D // P
TT = T // P
N = B * T
H = 16
HG = 4
CTX = 77
EPS = 1e-5
MASKED = -1e30
BANK = 512
W_COLS = 9984
DH16 = D // H
VA16 = DH16 + 1
XD = 64
XI = H * XD
XK = CTX + T
VA64 = XD + 1
INT8_MAX = 127.0
ROUND = 1.5 * 2.0 ** 23
CAP = 320
E3 = 8
F3 = 1024
ZERO_ROW = E3 * CAP

_PI = [0, 0, 0, 1, 1, 2]
_PJ = [1, 2, 3, 2, 3, 3]
_WI = [2, 3, 1, 0, 2, 0]
_WJ = [3, 1, 2, 3, 0, 1]


def columns(parts):
    at, out = 0, {}
    for name, n in parts:
        out[name] = (at, n)
        at += n
    return out


CONST = columns([("ident", 128), ("causal", 128), ("causal_t", 128), ("block", 128), ("tri", 128), ("ones", 128),
                 ("steps", 256), ("past", 256), ("iota", 16), ("neg_half", 16), ("half", 64), ("row", 1)])
_XATT = [("wq", C * XI), ("wkv", C * 2 * XI), ("wo", (XI // P) * D),
         ("ctx_w", D), ("ctx_b", D), ("lat_w", D), ("lat_b", D)]
_MHA = [("wq", C * 512), ("wk", C * 512), ("wv", C * D), ("wo", C * D), ("bq", 4), ("bk", 4), ("bv", D), ("bo", D)]
PACK = [
    columns([("wq", C * 512), ("bq", 4), ("nat", C * 1024), ("nat_b", 512), ("write1", C * 192), ("write2", C * 192),
             ("read", C * 384), ("wo", C * D), ("bo", D), ("mem_scale", H), ("decay", H), ("kv_gate", 1)]),
    columns(_XATT),
    columns([("w1", 8 * C * 256), ("w2", 8 * C * 256), ("gate_up", C * 512), ("down", C * 256), ("router", C * 9)]),
    columns(_MHA),
    columns(_XATT),
    columns([("keys", C * 1024), ("values", 8 * 256), ("sel", C * 16), ("route_scale", 1)]),
    columns(_MHA),
    columns(_MHA),
    columns([("rhs_t", C * 256)]),
    columns([("wout", 4 * D), ("bo", D)]),
    columns(_MHA),
    columns([("gate", C * E3)]),
]
SCAN = columns([("wx", C * P), ("wd", C * P), ("wg", C * P), ("bx", 1), ("bd", 1), ("bg", 1), ("a_log", 16),
                ("b", 16), ("c0", 16), ("d", 1)])
SCAN_COLS = sum(n for _, n in SCAN.values())


def part(image, table, name, chunks=None):
    at, n = table[name]
    v = image[:, at:at + n]
    return v.rearrange("p (c n) -> p c n", c=chunks) if chunks else v



def tail_dve(nc, S, dve):
    for tt in range(TT):
        nc.vector.bn_stats(S.bst[:, tt, :], S.ysb[:, tt, :])
    dve.drain()
    for tt in range(TT):
        last = nc.vector.bn_aggr(S.mv[:, tt, :], S.bst[:, tt, :])
    last.then_inc(S.ln_stat, 1)
    dve.wait_ge(S.ln_rstd, 1)
    dve.sem_inc(S.ln_rstd, -1)
    dve.wait_ge(S.yn_free, 2)
    dve.sem_inc(S.yn_free, -2)
    for tt in range(TT):
        last = nc.vector.tensor_scalar(S.yn[:, tt, :], S.ysb[:, tt, :], S.mv[:, tt, 0:1], S.rstd[:, tt:tt + 1],
                                       ALU.subtract, ALU.mult)
    last.then_inc(S.yn_ready_pe, 1)
    dve.drain().then_inc(S.yn_ready_pool, 1)


def pool_rstd(nc, S, pool):
    pool.wait_ge(S.ln_stat, 1)
    pool.sem_inc(S.ln_stat, -1)
    nc.gpsimd.tensor_scalar(S.rstd[:], S.mv[:, :, 1], EPS, None, ALU.add)
    pool.drain()
    nc.gpsimd.tensor_tensor(S.rstd[:], S.rstd[:], part(S.const, CONST, "neg_half")[:, 0:TT], ALU.pow)\
        .then_inc(S.ln_rstd, 1)


def tail_pool(nc, S, pool, b):
    pool_rstd(nc, S, pool)
    pool.wait_ge(S.yn_ready_pool, 1)
    pool.sem_inc(S.yn_ready_pool, -1)
    nc.gpsimd.tensor_copy(S.x_nat[:, bass.ds(b * TT, TT), :], S.yn[:]).then_inc(S.yn_free, 1)


def tail_pe(nc, S, pe, slot):
    pe.wait_ge(S.yn_ready_pe, 1)
    pe.sem_inc(S.yn_ready_pe, -1)
    for c in range(C):
        for tt in range(TT):
            last = nc.tensor.transpose(S.O[:, slot, (c * TT + tt) * P:(c * TT + tt + 1) * P],
                                       S.yn[:, tt, c * P:(c + 1) * P], S.ident)
    last.then_inc(S.yt_full, 1)


def tail_act(nc, S, act, slot, b):
    act.wait_ge(S.yt_full, 1)
    act.sem_inc(S.yt_full, -1)
    act.sem_inc(S.yn_free, 1)
    nc.scalar.activation(S.x_t[:, :, bass.ds(b * T, T)],
                         S.O[:, slot, :].rearrange("p (c t) -> p c t", c=C), ACT.Copy).then_inc(S.o_free[slot], 1)


def pool_residual(nc, S, pool, b, bias=None):
    pool.wait_ge(S.xres_free, 1)
    pool.sem_inc(S.xres_free, -1)
    x = S.x_nat[:, bass.ds(b * TT, TT), :]
    if bias is None:
        nc.gpsimd.tensor_copy(S.xres[:], x).then_inc(S.xres_ready, 1)
    else:
        for tt in range(TT):
            last = nc.gpsimd.tensor_tensor(S.xres[:, tt, :], S.x_nat[:, bass.ds(b * TT + tt, 1), :].rearrange("p a d -> p (a d)"), bias, ALU.add)
        last.then_inc(S.xres_ready, 1)


def dve_output(nc, S, dve, slot):
    dve.wait_ge(S.y_full, 1)
    dve.sem_inc(S.y_full, -1)
    dve.wait_ge(S.xres_ready, 1)
    dve.sem_inc(S.xres_ready, -1)
    nc.vector.tensor_tensor(S.ysb[:], S.O[:, slot, :].rearrange("p (t d) -> p t d", t=TT), S.xres[:], ALU.add)\
        .then_inc(S.o_free[slot], 1)
    dve.drain().then_inc(S.xres_free, 1)
    tail_dve(nc, S, dve)


def sync_x(nc, S, sp, b):
    sp.wait_ge(S.xc_free, 1)
    sp.sem_inc(S.xc_free, -1)
    sp.dma_start(S.xc[:, :, 1:1 + T], S.x_t[:, :, bass.ds(b * T, T)]).then_inc(S.xc_ready, 16)


def prefetch(nc, S, sp, k):
    if k < len(PACK):
        n = sum(w for _, w in PACK[k].values())
        sp.dma_start(S.arena[k % 2][:, 0:n], S.packs[k]).then_inc(S.weights_ready[k], 16)



def pe_units(nc, S, pe, n_units, scores, transposes, product, o_slot):
    scores(0).then_inc(S.s_full, 1)
    for u in range(n_units + 1):
        if u + 1 < n_units:
            scores(u + 1).then_inc(S.s_full, 1)
        if u >= 1:
            pe.wait_ge(S.pt_ready, 1)
            pe.sem_inc(S.pt_ready, -1)
            pe.wait_ge(S.o_free[o_slot(u - 1)], 1)
            pe.sem_inc(S.o_free[o_slot(u - 1)], -1)
            product(u - 1).then_inc(S.o_full, 1)
        if u < n_units:
            pe.wait_ge(S.p_ready, 1)
            pe.sem_inc(S.p_ready, -1)
            transposes(u).then_inc(S.t_full, 1)


def dve_units(nc, S, dve, n_units, row_max, evacuate, normalise):
    def maxima(u):
        dve.wait_ge(S.s_full, 1)
        dve.sem_inc(S.s_full, -1)
        row_max(u).then_inc(S.max_ready, 1)

    def norm(u):
        dve.wait_ge(S.o_full, 1)
        dve.sem_inc(S.o_full, -1)
        normalise(u)

    maxima(0)
    for u in range(n_units):
        if u + 1 < n_units:
            maxima(u + 1)
        if u >= 1:
            norm(u - 1)
        dve.wait_ge(S.t_full, 1)
        dve.sem_inc(S.t_full, -1)
        evacuate(u).then_inc(S.pt_ready, 1)
    norm(n_units - 1)


def act_units(nc, S, act, n_units, exps):
    for u in range(n_units):
        act.wait_ge(S.max_ready, 1)
        act.sem_inc(S.max_ready, -1)
        exps(u).then_inc(S.p_ready, 1)



def attention16(nc, S, k, scale, mask=None, cross=False, out=True, geometry=False):
    W, TB = S.arena[k % 2], PACK[k]
    units = [(qt, g) for qt in range(TT) for g in range(HG)]
    NU = len(units)
    key_tiles = 1 if cross else TT
    kn = CTX if cross else P

    def key_range(qt):
        if cross:
            return [0]
        if mask == "block":
            return [qt]
        return list(range(qt + 1)) if mask == "causal" else list(range(TT))

    def o_slot(u):
        return (1 + u) % 2

    with ExitStack() as ctx:
        def sb(name, shape, dt=F32):
            return ctx.enter_context(nc.sbuf_tensor(f"{name}_{k}", shape, dt))

        q_t = sb("q_t", [P, 4, T])
        k_t = sb("k_t", [P, 4, key_tiles * kn])
        v = sb("v", [P, key_tiles, H, VA16])
        prob = sb("prob", [P, 2, 4, T])
        prob_t = sb("prob_t", [P, 2, TT, 4, P])
        neg_max = sb("neg_max", [P, 2, 4])
        rec = sb("rec", [P, 2, 4])
        attn = sb("attn", [P, TT, D])
        attn_t = sb("attn_t", [P, TT, C, P])
        cc = sb("cc", [P, C, CTX]) if cross else None
        if geometry:
            lines = sb("lines", [P, TT, 2, 2, 192])
            prods = sb("prods", [P, TT, 2, 2, 96])
            line = sb("line", [P, TT, 2, H, 6])
            norm2 = sb("norm2", [P, TT, 2, H])
            line_pad = sb("line_pad", [P, TT, 2, H, 32])
            k_pad = sb("k_pad", [P, TT, H, 32])
            kv = sb("kv", [P, TT, 2, H, DH16])
            geo = sb("geo", [P, TT, 2, H, DH16])
            inc2 = prob
            lines_t = prob_t[:].rearrange("p s i t q -> p (s i t q)").rearrange("p (r t q) -> p r t q", r=2, t=4)
            decay_w = sb("decay_w", [P, H, T])
            mem = sb("mem", [P, TT, H])
            log_decay = sb("log_decay", [P, H])
        src = cc if cross else S.xc[:, :, 1:1 + T]
        block = ctx.enter_context(nc.Block())

        @block.sync
        def _(sp):
            prefetch(nc, S, sp, k + 1)
            with sp.Fori(0, B) as b:
                sync_x(nc, S, sp, b)
                if cross:
                    sp.dma_start(cc[:], S.ctx_t[:, :, bass.ds(b * CTX, CTX)]).then_inc(S.xc_ready, 16)
            sp.wait_ge(S.xc_free, 1)

        @block.tensor
        def _(pe):
            wq = part(W, TB, "wq", C)
            wo = part(W, TB, "wo", C) if out else None
            causal = S.masks[:, 0, :]
            blocked = S.masks[:, 1, :]
            pe.wait_ge(S.weights_ready[k], 16)

            def transposed(dst, w, x):
                for t in range(4):
                    for c in range(C):
                        last = nc.tensor.matmul(dst[:, t * T:t * T + x.shape[2]], w[:, c, t * P:(t + 1) * P], x[:, c, :],
                                                start=(c == 0), stop=(c == C - 1))
                return last

            def scores(u):
                qt, g = units[u]
                keys = key_range(qt)
                n = len(keys) * kn
                for t in range(4):
                    S_t = S.R[:, u % 2, t * T:t * T + n]
                    last = nc.tensor.matmul(S_t, q_t[32 * g:32 * g + DH16, t, qt * P:(qt + 1) * P],
                                            k_t[32 * g:32 * g + DH16, t, keys[0] * kn:keys[0] * kn + n],
                                            start=(t % 2 == 0), stop=(mask is None), skip_group_check=True)
                if mask is not None:
                    for t in range(4):
                        last = nc.tensor.matmul(S.R[:, u % 2, t * T + n - P:t * T + n], S.ident_b,
                                                causal if mask == "causal" else blocked,
                                                start=False, stop=True, skip_group_check=True)
                return last

            def transposes(u):
                qt, g = units[u]
                if u == 0:
                    pe.wait_ge(S.t_free[0], 1)
                    pe.sem_inc(S.t_free[0], -1)
                    pe.wait_ge(S.t_free[1], 1)
                    pe.sem_inc(S.t_free[1], -1)
                if u >= NU - 2:
                    pe.sem_inc(S.r_free[u % 2], 1)
                for i in range(len(key_range(qt))):
                    for t in range(4):
                        last = nc.tensor.transpose(S.T[0:kn, i, t * P:(t + 1) * P],
                                                   prob[:, u % 2, t, i * kn:(i + 1) * kn], S.ident)
                return last

            def product(u):
                qt, g = units[u]
                keys = key_range(qt)
                if u == NU - 1:
                    pe.sem_inc(S.t_free[0], 1)
                    pe.sem_inc(S.t_free[1], 1)
                for t in range(4):
                    for i, key in enumerate(keys):
                        last = nc.tensor.matmul(S.O[:, o_slot(u), t * VA16:(t + 1) * VA16],
                                                prob_t[0:kn, u % 2, i, t, :], v[0:kn, key, 4 * t + g, :],
                                                start=(i == 0), stop=(i == len(keys) - 1))
                return last

            with pe.Fori(0, B) as b:
                pe.wait_ge(S.xc_ready, 32 if cross else 16)
                pe.sem_inc(S.xc_ready, -(32 if cross else 16))
                pe.wait_ge(S.r_free[0], 1)
                pe.sem_inc(S.r_free[0], -1)
                transposed(S.R[:, 0, :], wq, S.xc[:, :, 1:1 + T]).then_inc(S.q_full, 1)
                if not geometry:
                    wk, wv = part(W, TB, "wk", C), part(W, TB, "wv", C)
                    pe.wait_ge(S.r_free[1], 1)
                    pe.sem_inc(S.r_free[1], -1)
                    transposed(S.R[:, 1, :], wk, src).then_inc(S.k_full, 1)
                    pe.wait_ge(S.o_free[0], 1)
                    pe.sem_inc(S.o_free[0], -1)
                    for i in range(key_tiles):
                        for c in range(C):
                            last = nc.tensor.matmul(S.O[0:kn, 0, i * D:(i + 1) * D], src[:, c, i * kn:(i + 1) * kn],
                                                    wv[:, c, :], start=(c == 0), stop=(c == C - 1))
                    last.then_inc(S.v_full, 1)
                else:
                    nat, rd = part(W, TB, "nat", C), part(W, TB, "read", C)
                    wr1, wr2 = part(W, TB, "write1", C), part(W, TB, "write2", C)
                    for tt in range(TT):
                        slot = (1 + tt) % 2
                        pe.wait_ge(S.r_free[slot], 1)
                        pe.sem_inc(S.r_free[slot], -1)
                        now = S.xc[:, :, 1 + tt * P:1 + (tt + 1) * P]
                        before = S.xc[:, :, tt * P:(tt + 1) * P]
                        for x, w, at, n in ((before, wr1, 0, 192), (now, wr2, 192, 192), (now, rd, BANK, 384)):
                            for c in range(C):
                                last = nc.tensor.matmul(S.R[:, slot, at:at + n], x[:, c, :], w[:, c, :],
                                                        start=(c == 0), stop=(c == C - 1))
                        last.then_inc(S.lines_full, 1)
                    for tt in range(TT):
                        slot = (1 + tt) % 2
                        pe.wait_ge(S.r_free[slot], 1)
                        pe.sem_inc(S.r_free[slot], -1)
                        for at in (0, BANK):
                            for c in range(C):
                                last = nc.tensor.matmul(S.R[:, slot, at:at + BANK], S.xc[:, c, 1 + tt * P:1 + (tt + 1) * P],
                                                        nat[:, c, at:at + BANK], start=(c == 0), stop=(c == C - 1))
                        last.then_inc(S.nat_full, 1)
                    pe.wait_ge(S.line_ready, 1)
                    pe.sem_inc(S.line_ready, -1)
                    for tt in range(TT):
                        for rw in range(2):
                            pe.wait_ge(S.t_free[rw], 1)
                            pe.sem_inc(S.t_free[rw], -1)
                            for t in range(4):
                                last = nc.tensor.transpose(S.T[:, rw, t * P:(t + 1) * P],
                                                           line_pad[:, tt, rw, 4 * t:4 * t + 4, :].rearrange("p h i -> p (h i)"), S.ident)
                            last.then_inc(S.lt_full, 1)
                    pe.wait_ge(S.t_free[0], 1)
                    pe.sem_inc(S.t_free[0], -1)
                    pe.wait_ge(S.t_free[1], 1)
                    pe.sem_inc(S.t_free[1], -1)
                    pe.sem_inc(S.t_free[0], 1)
                    pe.sem_inc(S.t_free[1], 1)
                    for u, (qt, g) in enumerate(units):
                        n = (qt + 1) * P
                        pe.wait_ge(S.r_free[(1 + u) % 2], 1)
                        pe.sem_inc(S.r_free[(1 + u) % 2], -1)
                        for t in range(4):
                            last = nc.tensor.matmul(S.R[:, (1 + u) % 2, t * T:t * T + n],
                                                    lines_t[32 * g:32 * g + 6, 1, t, qt * P:(qt + 1) * P],
                                                    lines_t[32 * g:32 * g + 6, 0, t, 0:n],
                                                    start=True, stop=True)
                        last.then_inc(S.inc_full, 1)
                    pe.wait_ge(S.kpad_ready, 1)
                    pe.sem_inc(S.kpad_ready, -1)
                    for tt in range(TT):
                        pe.wait_ge(S.t_free[tt], 1)
                        pe.sem_inc(S.t_free[tt], -1)
                        for t in range(4):
                            last = nc.tensor.transpose(S.T[:, tt, t * P:(t + 1) * P],
                                                       k_pad[:, tt, 4 * t:4 * t + 4, :].rearrange("p h i -> p (h i)"), S.ident)
                        last.then_inc(S.lt_full, 1)
                    pe.wait_ge(S.t_free[0], 1)
                    pe.sem_inc(S.t_free[0], -1)
                    pe.wait_ge(S.t_free[1], 1)
                    pe.sem_inc(S.t_free[1], -1)
                    pe.sem_inc(S.t_free[0], 1)
                    pe.sem_inc(S.t_free[1], 1)
                pe.wait_ge(S.r_free[0], 1)
                pe.sem_inc(S.r_free[0], -1)
                pe.wait_ge(S.r_free[1], 1)
                pe.sem_inc(S.r_free[1], -1)
                pe_units(nc, S, pe, NU, scores, transposes, product, o_slot)
                pe.wait_ge(S.o_free[0], 1)
                pe.sem_inc(S.o_free[0], -1)
                pe.wait_ge(S.o_free[1], 1)
                pe.sem_inc(S.o_free[1], -1)
                if out:
                    for qt in range(TT):
                        for c in range(C):
                            last = nc.tensor.transpose(S.O[:, 1, (qt * C + c) * P:(qt * C + c + 1) * P],
                                                       attn[:, qt, c * P:(c + 1) * P], S.ident)
                    last.then_inc(S.at_full, 1)
                    pe.wait_ge(S.o_free[1], 1)
                    pe.sem_inc(S.o_free[1], -1)
                    for qt in range(TT):
                        for c in range(C):
                            last = nc.tensor.matmul(S.O[:, 0, qt * D:(qt + 1) * D], attn_t[:, qt, c, :], wo[:, c, :],
                                                    start=(c == 0), stop=(c == C - 1))
                    last.then_inc(S.y_full, 1)
                else:
                    pe.sem_inc(S.o_free[0], 1)
                tail_pe(nc, S, pe, 1)

        @block.scalar
        def _(act):
            act.wait_ge(S.weights_ready[k], 16)

            def exps(u):
                n = len(key_range(units[u][0])) * kn
                for t in range(4):
                    last = nc.scalar.activation(prob[:, u % 2, t, 0:n], S.R[:, u % 2, t * T:t * T + n], ACT.Exp,
                                                bias=neg_max[:, u % 2, t:t + 1])
                return last

            if geometry:
                nc.scalar.activation(log_decay[:], part(W, TB, "decay"), ACT.Exp, scale=-1.0).then_inc(S.setup_act, 1)
                act.wait_ge(S.setup_dve, 1)
                act.sem_inc(S.setup_dve, -1)
                nc.scalar.activation(log_decay[:], log_decay[:], ACT.Ln)
                act.drain()
                for h in range(H):
                    last = nc.scalar.activation(decay_w[:, h, :], part(S.const, CONST, "steps"), ACT.Exp,
                                                scale=log_decay[:, h:h + 1])
                last.then_inc(S.setup_act, 1)
            with act.Fori(0, B) as b:
                if not geometry:
                    act.wait_ge(S.k_full, 1)
                    act.sem_inc(S.k_full, -1)
                    bk = part(W, TB, "bk")
                    for t in range(4):
                        last = nc.scalar.activation(k_t[:, t, :], S.R[:, 1, t * T:t * T + key_tiles * kn], ACT.Identity,
                                                    bias=bk[:, t:t + 1])
                    last.then_inc(S.r_free[1], 1)
                else:
                    for tt in range(TT):
                        slot = (1 + tt) % 2
                        act.wait_ge(S.lines_full, 1)
                        act.sem_inc(S.lines_full, -1)
                        nc.scalar.activation(lines[:, tt, :, :, :].rearrange("p w a n -> p w (a n)"),
                                             S.R[:, slot, :].rearrange("p (w n) -> p w n", w=2)[:, :, 0:384], ACT.Copy)\
                            .then_inc(S.r_free[slot], 1)
                        act.drain().then_inc(S.lines_sb, 1)
                    for tt in range(TT):
                        slot = (1 + tt) % 2
                        act.wait_ge(S.nat_geo, 1)
                        act.sem_inc(S.nat_geo, -1)
                        nc.scalar.activation(geo[:, tt, :, :, :].rearrange("p a h d -> p (a h d)"),
                                             S.R[:, slot, BANK:2 * BANK], ACT.Copy).then_inc(S.r_free[slot], 1)
                    for tt in range(TT):
                        for rw in range(2):
                            act.wait_ge(S.lt_full, 1)
                            act.sem_inc(S.lt_full, -1)
                            nc.scalar.activation(lines_t[:, rw, :, tt * P:(tt + 1) * P],
                                                 S.T[:, rw, :].rearrange("p (t q) -> p t q", t=4), ACT.Copy)\
                                .then_inc(S.t_free[rw], 1)
                    for u, (qt, g) in enumerate(units):
                        n = (qt + 1) * P
                        act.wait_ge(S.inc_full, 1)
                        act.sem_inc(S.inc_full, -1)
                        act.wait_ge(S.inc_free, 1)
                        act.sem_inc(S.inc_free, -1)
                        nc.scalar.activation(inc2[:, u % 2, :, 0:n],
                                             S.R[:, (1 + u) % 2, :].rearrange("p (t n) -> p t n", t=4)[:, :, 0:n], ACT.Square)\
                            .then_inc(S.r_free[(1 + u) % 2], 1)
                        act.drain().then_inc(S.inc_ready, 1)
                    act.wait_ge(S.mem_ready, 1)
                    act.sem_inc(S.mem_ready, -1)
                    nc.scalar.activation(mem[:], mem[:], ACT.Exp, scale=-1.0).then_inc(S.gate_exp, 1)
                    for tt in range(TT):
                        act.wait_ge(S.lt_full, 1)
                        act.sem_inc(S.lt_full, -1)
                        nc.scalar.activation(k_t[:, :, tt * P:(tt + 1) * P],
                                             S.T[:, tt, :].rearrange("p (t q) -> p t q", t=4), ACT.Copy)\
                            .then_inc(S.t_free[tt], 1)
                act_units(nc, S, act, NU, exps)
                if out:
                    act.wait_ge(S.at_full, 1)
                    act.sem_inc(S.at_full, -1)
                    nc.scalar.activation(attn_t[:].rearrange("p q c t -> p (q c t)"), S.O[:, 1, :], ACT.Copy)\
                        .then_inc(S.o_free[1], 1)
                tail_act(nc, S, act, 1, b)
            if geometry:
                act.wait_ge(S.inc_free, 2)
                act.sem_inc(S.inc_free, -2)

        @block.vector
        def _(dve):
            dve.wait_ge(S.weights_ready[k], 16)
            bq = part(W, TB, "bq")
            nc.vector.memset(v[:, :, :, DH16:VA16], 1.0)

            def row_max(u):
                n = len(key_range(units[u][0])) * kn
                return nc.vector.tensor_reduce(neg_max[:, u % 2, :],
                                               S.R[:, u % 2, :].rearrange("p (t n) -> p t n", t=4)[:, :, 0:n],
                                               AX.X, ALU.max, negate=True)

            def evacuate(u):
                n = len(key_range(units[u][0]))
                return nc.vector.tensor_copy(prob_t[0:kn, u % 2, 0:n, :, :].rearrange("p i t q -> p i (t q)"), S.T[0:kn, 0:n, :])

            def normalise(u):
                qt, g = units[u]
                o = S.O[:, o_slot(u), 0:4 * VA16].rearrange("p (t d) -> p t d", t=4)
                nc.vector.reciprocal(rec[:, u % 2, :], o[:, :, DH16])
                dve.drain()
                nc.vector.tensor_tensor(attn[:, qt, :].rearrange("p (t g d) -> p t g d", t=4, g=HG)[:, :, g, :],
                                        o[:, :, 0:DH16], rec[:, u % 2, :].unsqueeze(2).to_broadcast([P, 4, DH16]), ALU.mult)\
                    .then_inc(S.o_free[o_slot(u)], 1)

            if geometry:
                nc.vector.memset(line_pad[:], 0.0)
                nc.vector.memset(k_pad[:], 0.0)
                dve.wait_ge(S.setup_act, 1)
                dve.sem_inc(S.setup_act, -1)
                nc.vector.tensor_scalar(log_decay[:], log_decay[:], 1.0, None, ALU.add)
                dve.drain()
                nc.vector.reciprocal(log_decay[:], log_decay[:])
                dve.drain()
                nc.vector.tensor_scalar(log_decay[:], log_decay[:], 2.0 ** -63, None, ALU.max).then_inc(S.setup_dve, 1)
                dve.wait_ge(S.setup_act, 1)
                dve.sem_inc(S.setup_act, -1)
                nc.vector.tensor_tensor(decay_w[:], decay_w[:],
                                        part(S.const, CONST, "past").unsqueeze(1).to_broadcast([P, H, T]), ALU.mult)
            dve.drain()
            with dve.Fori(0, B) as b:
                dve.wait_ge(S.q_full, 1)
                dve.sem_inc(S.q_full, -1)
                for t in range(4):
                    last = nc.vector.tensor_scalar(q_t[:, t, :], S.R[:, 0, t * T:(t + 1) * T], bq[:, t:t + 1], scale,
                                                   ALU.add, ALU.mult)
                last.then_inc(S.r_free[0], 1)
                if not geometry:
                    dve.wait_ge(S.v_full, 1)
                    dve.sem_inc(S.v_full, -1)
                    dve.sem_inc(S.xc_free, 1)
                    bv = part(W, TB, "bv").rearrange("p (h d) -> p h d", h=H)
                    for i in range(key_tiles):
                        last = nc.vector.tensor_tensor(v[0:kn, i, :, 0:DH16],
                                                       S.O[0:kn, 0, i * D:(i + 1) * D].rearrange("p (h d) -> p h d", h=H),
                                                       bv[0:kn], ALU.add)
                    last.then_inc(S.o_free[0], 1)
                else:
                    for tt in range(TT):
                        slot = (1 + tt) % 2
                        dve.wait_ge(S.nat_full, 1)
                        dve.sem_inc(S.nat_full, -1)
                        nc.vector.tensor_tensor(kv[:, tt, :, :, :].rearrange("p a h d -> p (a h d)"), S.R[:, slot, 0:BANK],
                                                part(W, TB, "nat_b"), ALU.add).then_inc(S.nat_geo, 1)
                    dve.sem_inc(S.xc_free, 1)
                    dve.wait_ge(S.lines_sb, 2)
                    dve.sem_inc(S.lines_sb, -2)
                    for tt in range(TT):
                        nc.vector.tensor_tensor(prods[:, tt, :, :, :].rearrange("p w a n -> p w (a n)"),
                                                lines[:, tt, :, 0, :], lines[:, tt, :, 1, :], ALU.mult)
                    dve.drain()
                    flat = line[:].rearrange("p t w h i -> p (t w) (h i)")
                    both = prods[:].rearrange("p t w a n -> p (t w) a n")
                    nc.vector.tensor_tensor(flat, both[:, :, 0, :], both[:, :, 1, :], ALU.subtract)
                    dve.drain()
                    nc.vector.tensor_tensor(both[:, :, 0, :], flat, flat, ALU.mult)
                    dve.drain()
                    nc.vector.tensor_reduce(norm2[:].rearrange("p t w h -> p (t w) h"),
                                            both[:, :, 0, :].rearrange("p a (h i) -> p a h i", i=6), AX.X, ALU.add)\
                        .then_inc(S.norm_sum, 1)
                    dve.wait_ge(S.norm_root, 1)
                    dve.sem_inc(S.norm_root, -1)
                    nc.vector.tensor_scalar(norm2[:], norm2[:], 1e-12, None, ALU.max)
                    dve.drain()
                    nc.vector.reciprocal(norm2[:], norm2[:])
                    dve.drain()
                    for tt in range(TT):
                        for rw in range(2):
                            last = nc.vector.tensor_tensor(line_pad[:, tt, rw, :, 0:6], line[:, tt, rw, :, :],
                                                           norm2[:, tt, rw, :].unsqueeze(2).to_broadcast([P, H, 6]), ALU.mult)
                    last.then_inc(S.line_ready, 1)
                    for u, (qt, g) in enumerate(units):
                        n = (qt + 1) * P
                        dve.wait_ge(S.inc_ready, 1)
                        dve.sem_inc(S.inc_ready, -1)
                        for t in range(4):
                            last = nc.vector.tensor_tensor_reduce(
                                inc2[:, u % 2, t, 0:n], inc2[:, u % 2, t, 0:n], decay_w[:, 4 * t + g, T - n:T], 1.0, 0.0,
                                ALU.mult, ALU.add, mem[:, qt, 4 * t + g:4 * t + g + 1])
                        last.then_inc(S.inc_free, 1)
                    dve.drain()
                    nc.vector.tensor_tensor(mem[:], mem[:],
                                            part(W, TB, "mem_scale").unsqueeze(1).to_broadcast([P, TT, H]), ALU.mult)\
                        .then_inc(S.mem_ready, 1)
                    dve.wait_ge(S.gate_exp, 1)
                    dve.sem_inc(S.gate_exp, -1)
                    nc.vector.tensor_scalar(mem[:], mem[:], 1.0, None, ALU.add)
                    dve.drain()
                    nc.vector.reciprocal(mem[:], mem[:])
                    dve.drain()
                    nc.vector.tensor_scalar(mem[:], mem[:], part(W, TB, "kv_gate"), None, ALU.mult)
                    dve.drain()
                    for tt in range(TT):
                        gate = mem[:, tt, :].unsqueeze(2).to_broadcast([P, H, DH16])
                        for a in range(2):
                            nc.vector.tensor_tensor(geo[:, tt, a, :, :], geo[:, tt, a, :, :], gate, ALU.mult)
                    dve.drain()
                    for tt in range(TT):
                        nc.vector.tensor_tensor(v[:, tt, :, 0:DH16], kv[:, tt, 1, :, :], geo[:, tt, 1, :, :], ALU.add)
                    for tt in range(TT):
                        last = nc.vector.tensor_tensor(k_pad[:, tt, :, 0:DH16], kv[:, tt, 0, :, :], geo[:, tt, 0, :, :], ALU.add)
                    last.then_inc(S.kpad_ready, 1)
                dve_units(nc, S, dve, NU, row_max, evacuate, normalise)
                if out:
                    dve_output(nc, S, dve, 0)
                else:
                    dve.drain()
                    dve.wait_ge(S.xres_ready, 1)
                    dve.sem_inc(S.xres_ready, -1)
                    nc.vector.tensor_tensor(S.ysb[:], attn[:], S.xres[:], ALU.add)
                    dve.drain().then_inc(S.xres_free, 1)
                    tail_dve(nc, S, dve)

        @block.gpsimd
        def _(pool):
            pool.wait_ge(S.weights_ready[k], 16)
            if geometry:
                pool.sem_inc(S.inc_free, 2)
            with pool.Fori(0, B) as b:
                pool_residual(nc, S, pool, b, part(W, TB, "bo") if out else None)
                if geometry:
                    pool.wait_ge(S.norm_sum, 1)
                    pool.sem_inc(S.norm_sum, -1)
                    flat = norm2[:].rearrange("p t w h -> p (t w h)")
                    nc.gpsimd.tensor_tensor(flat, flat, part(S.const, CONST, "half"), ALU.pow).then_inc(S.norm_root, 1)
                tail_pool(nc, S, pool, b)



def perceiver(nc, S, k):
    W, TB = S.arena[k % 2], PACK[k]
    HP = H // 2
    units = [(qt, hp) for qt in range(TT) for hp in range(HP)]
    NU = len(units)
    KC = [(0, P, CTX), (1, P, CTX + P), (2, CTX, 0)]
    LC = [(t, min(P, B * CTX - t * P)) for t in range(-(-B * CTX // P))]

    def o_slot(u):
        return u % 2

    with ExitStack() as ctx:
        def sb(name, shape, dt=F32):
            return ctx.enter_context(nc.sbuf_tensor(f"{name}_{k}", shape, dt))

        ctx_n = sb("ctx_n", [P, len(LC), D])
        ctx_nt = sb("ctx_nt", [P, C, B * CTX])
        cst = sb("cst", [P, len(LC), 6])
        cmv = sb("cmv", [P, len(LC), 2])
        crs = sb("crs", [P, len(LC)])
        lat = sb("lat", [P, TT, D])
        keys_in = sb("keys_in", [P, C, XK])
        q_t = sb("q_t", [P, HP, T])
        k_t = sb("k_t", [P, HP, XK])
        v = sb("v", [P, 3, H, VA64])
        prob = sb("prob", [P, 2, 2, XK])
        prob_t = sb("prob_t", [P, 2, 2, 3, P])
        neg_max = sb("neg_max", [P, 2, 2])
        rec = sb("rec", [P, 2, 2])
        attn = sb("attn", [P, TT, XI])
        attn_t = sb("attn_t", [P, XI // P, T])
        block = ctx.enter_context(nc.Block())

        @block.sync
        def _(sp):
            prefetch(nc, S, sp, k + 1)
            for t, n in LC:
                sp.dma_start(ctx_n[0:n, t, :], S.ctx_dram[t * P:t * P + n, :]).then_inc(S.ctx_ready, 16)
            with sp.Fori(0, B) as b:
                sp.wait_ge(S.ctx_nt_ready, 1)
                sp.sem_inc(S.ctx_nt_ready, -1)
                sp.dma_start(keys_in[:, :, 0:CTX], ctx_nt[:, :, bass.ds(b * CTX, CTX)]).then_inc(S.xc_ready, 16)
            sp.wait_ge(S.ctx_nt_ready, 1)
            sp.sem_inc(S.ctx_nt_ready, -1)

        @block.tensor
        def _(pe):
            wq, wkv, wo = part(W, TB, "wq", C), part(W, TB, "wkv", C), part(W, TB, "wo", XI // P)
            pe.wait_ge(S.weights_ready[k], 16)
            pe.wait_ge(S.ctx_norm_ready, 1)
            pe.sem_inc(S.ctx_norm_ready, -1)
            for t, n in LC:
                pe.wait_ge(S.o_free[t % 2], 1)
                pe.sem_inc(S.o_free[t % 2], -1)
                for c in range(C):
                    last = nc.tensor.transpose(S.O[:, t % 2, c * P:c * P + n], ctx_n[0:n, t, c * P:(c + 1) * P], S.ident[0:n, 0:n])
                last.then_inc(S.yt_full, 1)

            def scores(u):
                qt, hp = units[u]
                for i in range(2):
                    last = nc.tensor.matmul(S.R[:, u % 2, i * BANK:i * BANK + XK],
                                            q_t[XD * i:XD * (i + 1), hp, qt * P:(qt + 1) * P],
                                            k_t[XD * i:XD * (i + 1), hp, :], start=True, stop=True)
                return last

            def transposes(u):
                if u == 0:
                    pe.wait_ge(S.t_free[0], 1)
                    pe.sem_inc(S.t_free[0], -1)
                    pe.wait_ge(S.t_free[1], 1)
                    pe.sem_inc(S.t_free[1], -1)
                if u >= NU - 2:
                    pe.sem_inc(S.r_free[u % 2], 1)
                for i in range(2):
                    for c, n, first in KC:
                        last = nc.tensor.transpose(S.T[0:n, i, c * P:(c + 1) * P], prob[:, u % 2, i, first:first + n], S.ident)
                return last

            def product(u):
                qt, hp = units[u]
                if u == NU - 1:
                    pe.sem_inc(S.t_free[0], 1)
                    pe.sem_inc(S.t_free[1], 1)
                for i in range(2):
                    for c, n, first in KC:
                        last = nc.tensor.matmul(S.O[:, o_slot(u), i * VA64:(i + 1) * VA64], prob_t[0:n, u % 2, i, c, :],
                                                v[0:n, c, 2 * hp + i, :], start=(c == 0), stop=(c == len(KC) - 1))
                return last

            with pe.Fori(0, B) as b:
                pe.wait_ge(S.lat_ready, 1)
                pe.sem_inc(S.lat_ready, -1)
                for tt in range(TT):
                    pe.wait_ge(S.o_free[tt], 1)
                    pe.sem_inc(S.o_free[tt], -1)
                    for c in range(C):
                        last = nc.tensor.transpose(S.O[:, tt, c * P:(c + 1) * P], lat[:, tt, c * P:(c + 1) * P], S.ident)
                    last.then_inc(S.yt_full, 1)
                pe.wait_ge(S.lat_t_ready, 1)
                pe.sem_inc(S.lat_t_ready, -1)
                pe.wait_ge(S.xc_ready, 16)
                pe.sem_inc(S.xc_ready, -16)
                for j in range(2):
                    pe.wait_ge(S.r_free[j], 1)
                    pe.sem_inc(S.r_free[j], -1)
                    for i in range(4):
                        for c in range(C):
                            last = nc.tensor.matmul(S.R[:, j, i * T:(i + 1) * T], wq[:, c, (4 * j + i) * P:(4 * j + i + 1) * P],
                                                    keys_in[:, c, CTX:XK], start=(c == 0), stop=(c == C - 1))
                    last.then_inc(S.q_full, 1)
                for j in range(4):
                    pe.wait_ge(S.r_free[j % 2], 1)
                    pe.sem_inc(S.r_free[j % 2], -1)
                    for i in range(2):
                        for c in range(C):
                            last = nc.tensor.matmul(S.R[:, j % 2, i * BANK:i * BANK + XK], wkv[:, c, (2 * j + i) * P:(2 * j + i + 1) * P],
                                                    keys_in[:, c, :], start=(c == 0), stop=(c == C - 1))
                    last.then_inc(S.k_full, 1)
                for kc, n, first in KC:
                    for hv in range(2):
                        slot = (2 * kc + hv) % 2
                        pe.wait_ge(S.r_free[slot], 1)
                        pe.sem_inc(S.r_free[slot], -1)
                        for c in range(C):
                            last = nc.tensor.matmul(S.R[0:n, slot, 0:BANK], keys_in[:, c, first:first + n],
                                                    wkv[:, c, XI + hv * BANK:XI + (hv + 1) * BANK], start=(c == 0), stop=(c == C - 1))
                        last.then_inc(S.v_full, 1)
                pe.wait_ge(S.r_free[0], 1)
                pe.sem_inc(S.r_free[0], -1)
                pe.wait_ge(S.r_free[1], 1)
                pe.sem_inc(S.r_free[1], -1)
                pe.wait_ge(S.k_sb, 1)
                pe.sem_inc(S.k_sb, -1)
                pe_units(nc, S, pe, NU, scores, transposes, product, o_slot)
                pe.wait_ge(S.o_free[0], 1)
                pe.sem_inc(S.o_free[0], -1)
                pe.wait_ge(S.o_free[1], 1)
                pe.sem_inc(S.o_free[1], -1)
                for j in range(4):
                    pe.wait_ge(S.t_free[j % 2], 1)
                    pe.sem_inc(S.t_free[j % 2], -1)
                    for c in range(2):
                        for qt in range(TT):
                            last = nc.tensor.transpose(S.T[:, j % 2, (c * TT + qt) * P:(c * TT + qt + 1) * P],
                                                       attn[:, qt, (2 * j + c) * P:(2 * j + c + 1) * P], S.ident)
                    last.then_inc(S.at_full, 1)
                pe.wait_ge(S.t_free[0], 1)
                pe.sem_inc(S.t_free[0], -1)
                pe.wait_ge(S.t_free[1], 1)
                pe.sem_inc(S.t_free[1], -1)
                pe.sem_inc(S.t_free[0], 1)
                pe.sem_inc(S.t_free[1], 1)
                for qt in range(TT):
                    for c in range(XI // P):
                        last = nc.tensor.matmul(S.O[:, 0, qt * D:(qt + 1) * D], attn_t[:, c, qt * P:(qt + 1) * P], wo[:, c, :],
                                                start=(c == 0), stop=(c == XI // P - 1))
                last.then_inc(S.y_full, 1)
                tail_pe(nc, S, pe, 1)

        @block.scalar
        def _(act):
            act.wait_ge(S.weights_ready[k], 16)
            for t, n in LC:
                act.wait_ge(S.yt_full, 1)
                act.sem_inc(S.yt_full, -1)
                last = nc.scalar.activation(ctx_nt[:, :, t * P:t * P + n],
                                            S.O[:, t % 2, 0:2 * P].rearrange("p (c t) -> p c t", c=C)[:, :, 0:n], ACT.Copy)
                last.then_inc(S.o_free[t % 2], 1)
            act.drain().then_inc(S.ctx_nt_ready, 1)

            def exps(u):
                for i in range(2):
                    last = nc.scalar.activation(prob[:, u % 2, i, :], S.R[:, u % 2, i * BANK:i * BANK + XK], ACT.Exp,
                                                bias=neg_max[:, u % 2, i:i + 1])
                return last

            with act.Fori(0, B) as b:
                for tt in range(TT):
                    act.wait_ge(S.yt_full, 1)
                    act.sem_inc(S.yt_full, -1)
                    nc.scalar.activation(keys_in[:, :, CTX + tt * P:CTX + (tt + 1) * P],
                                         S.O[:, tt, 0:2 * P].rearrange("p (c t) -> p c t", c=C), ACT.Copy)\
                        .then_inc(S.o_free[tt], 1)
                act.drain().then_inc(S.lat_t_ready, 1)
                for j in range(4):
                    act.wait_ge(S.k_full, 1)
                    act.sem_inc(S.k_full, -1)
                    nc.scalar.activation(k_t[:, 2 * j:2 * j + 2, :],
                                         S.R[:, j % 2, :].rearrange("p (i n) -> p i n", i=2)[:, :, 0:XK], ACT.Copy)\
                        .then_inc(S.r_free[j % 2], 1)
                act.drain().then_inc(S.k_sb, 1)
                act_units(nc, S, act, NU, exps)
                for j in range(4):
                    act.wait_ge(S.at_full, 1)
                    act.sem_inc(S.at_full, -1)
                    nc.scalar.activation(attn_t[:, 2 * j:2 * j + 2, :], S.T[:, j % 2, :].rearrange("p (c t) -> p c t", c=2),
                                         ACT.Copy).then_inc(S.t_free[j % 2], 1)
                tail_act(nc, S, act, 1, b)

        @block.vector
        def _(dve):
            dve.wait_ge(S.weights_ready[k], 16)
            nc.vector.memset(v[:, :, :, XD:VA64], 1.0)
            dve.wait_ge(S.ctx_ready, 16 * len(LC))
            dve.sem_inc(S.ctx_ready, -(16 * len(LC)))
            for t, n in LC:
                nc.vector.bn_stats(cst[0:n, t, :], ctx_n[0:n, t, :])
            nc.vector.memset(cmv[:], 1.0)
            dve.drain()
            for t, n in LC:
                last = nc.vector.bn_aggr(cmv[0:n, t, :], cst[0:n, t, :])
            last.then_inc(S.ctx_stat, 1)
            dve.wait_ge(S.ctx_rstd, 1)
            dve.sem_inc(S.ctx_rstd, -1)
            for t, n in LC:
                nc.vector.tensor_scalar(ctx_n[0:n, t, :], ctx_n[0:n, t, :], cmv[0:n, t, 0:1], crs[0:n, t:t + 1],
                                        ALU.subtract, ALU.mult)
            for op, name in ((ALU.mult, "ctx_w"), (ALU.add, "ctx_b")):
                dve.drain()
                for t, n in LC:
                    last = nc.vector.tensor_tensor(ctx_n[0:n, t, :], ctx_n[0:n, t, :], part(W, TB, name)[0:n, :], op)
            last.then_inc(S.ctx_norm_ready, 1)

            def row_max(u):
                return nc.vector.tensor_reduce(neg_max[:, u % 2, :],
                                               S.R[:, u % 2, :].rearrange("p (i n) -> p i n", i=2)[:, :, 0:XK],
                                               AX.X, ALU.max, negate=True)

            def evacuate(u):
                nc.vector.tensor_copy(prob_t[:, u % 2, :, 0:2, :].rearrange("p i c q -> p i (c q)"), S.T[:, :, 0:2 * P])
                return nc.vector.tensor_copy(prob_t[0:CTX, u % 2, :, 2, :], S.T[0:CTX, :, 2 * P:3 * P])

            def normalise(u):
                qt, hp = units[u]
                o = S.O[:, o_slot(u), 0:2 * VA64].rearrange("p (i d) -> p i d", i=2)
                nc.vector.reciprocal(rec[:, u % 2, :], o[:, :, XD])
                dve.drain()
                nc.vector.tensor_tensor(attn[:, qt, hp * P:(hp + 1) * P].rearrange("p (i d) -> p i d", i=2),
                                        o[:, :, 0:XD], rec[:, u % 2, :].unsqueeze(2).to_broadcast([P, 2, XD]), ALU.mult)\
                    .then_inc(S.o_free[o_slot(u)], 1)

            with dve.Fori(0, B) as b:
                dve.wait_ge(S.xres_ready, 1)
                dve.sem_inc(S.xres_ready, -1)
                for tt in range(TT):
                    nc.vector.bn_stats(S.bst[:, tt, :], S.xres[:, tt, :])
                dve.drain()
                for tt in range(TT):
                    last = nc.vector.bn_aggr(S.mv[:, tt, :], S.bst[:, tt, :])
                last.then_inc(S.ln_stat, 1)
                dve.wait_ge(S.ln_rstd, 1)
                dve.sem_inc(S.ln_rstd, -1)
                for tt in range(TT):
                    last = nc.vector.tensor_scalar(lat[:, tt, :], S.xres[:, tt, :], S.mv[:, tt, 0:1], S.rstd[:, tt:tt + 1],
                                                   ALU.subtract, ALU.mult)
                for op, name in ((ALU.mult, "lat_w"), (ALU.add, "lat_b")):
                    dve.drain()
                    last = nc.vector.tensor_tensor(lat[:], lat[:], part(W, TB, name).unsqueeze(1).to_broadcast([P, TT, D]), op)
                last.then_inc(S.lat_ready, 1)
                for j in range(2):
                    dve.wait_ge(S.q_full, 1)
                    dve.sem_inc(S.q_full, -1)
                    nc.vector.tensor_scalar(q_t[:, 4 * j:4 * j + 4, :].rearrange("p i t -> p (i t)"), S.R[:, j, :],
                                            XD ** -0.5, None, ALU.mult).then_inc(S.r_free[j], 1)
                for kc, n, first in KC:
                    for hv in range(2):
                        slot = (2 * kc + hv) % 2
                        dve.wait_ge(S.v_full, 1)
                        dve.sem_inc(S.v_full, -1)
                        last = nc.vector.tensor_copy(v[0:n, kc, hv * 8:hv * 8 + 8, 0:XD],
                                                     S.R[0:n, slot, 0:BANK].rearrange("p (h d) -> p h d", h=8))
                        last.then_inc(S.r_free[slot], 1)
                dve.sem_inc(S.ctx_nt_ready, 1)
                dve_units(nc, S, dve, NU, row_max, evacuate, normalise)
                dve.wait_ge(S.y_full, 1)
                dve.sem_inc(S.y_full, -1)
                nc.vector.tensor_tensor(S.ysb[:], S.O[:, 0, :].rearrange("p (t d) -> p t d", t=TT), S.xres[:], ALU.add)\
                    .then_inc(S.o_free[0], 1)
                dve.drain().then_inc(S.xres_free, 1)
                tail_dve(nc, S, dve)

        @block.gpsimd
        def _(pool):
            pool.wait_ge(S.weights_ready[k], 16)
            pool.wait_ge(S.ctx_stat, 1)
            pool.sem_inc(S.ctx_stat, -1)
            nc.gpsimd.tensor_scalar(crs[:], cmv[:, :, 1], EPS, None, ALU.add)
            pool.drain()
            nc.gpsimd.tensor_tensor(crs[:], crs[:], part(S.const, CONST, "neg_half")[:, 0:len(LC)], ALU.pow).then_inc(S.ctx_rstd, 1)
            with pool.Fori(0, B) as b:
                pool_residual(nc, S, pool, b)
                pool_rstd(nc, S, pool)
                tail_pool(nc, S, pool, b)



def dve_top(nc, S, dve, gate, prob, top, index, index_f, pick, n, experts):
    for tt in range(TT):
        nc.vector.max(top[:, tt, :], prob[:, tt, :])
    dve.drain()
    for tt in range(TT):
        nc.vector.max_index(index[:, tt, :], top[:, tt, :], prob[:, tt, :])
    dve.drain()
    nc.vector.tensor_copy(index_f[:], index[:])
    dve.drain()
    iota = part(S.const, CONST, "iota")[:, 0:experts]
    for tt in range(TT):
        for j in range(n):
            nc.vector.scalar_tensor_tensor(pick[:, tt, j, :], iota, index_f[:, tt, j:j + 1], prob[:, tt, :], ALU.is_equal, ALU.mult)
    dve.drain()
    nc.vector.tensor_reduce(gate[:], pick[:].rearrange("p t j e -> p t e j"), AX.X, ALU.add)
    dve.drain()


def moe_silu(nc, S, k):
    W, TB = S.arena[k % 2], PACK[k]
    E, FC = 8, 2
    with ExitStack() as ctx:
        def sb(name, shape, dt=F32):
            return ctx.enter_context(nc.sbuf_tensor(f"{name}_{k}", shape, dt))

        prob = sb("prob", [P, TT, E])
        logit = sb("logit", [P, TT, E + 1])
        nmax = sb("nmax", [P, TT])
        total = sb("total", [P, TT])
        shared_gate = sb("shared_gate", [P, TT])
        top = sb("top", [P, TT, 8])
        index = sb("index", [P, TT, 8], U32)
        index_f = sb("index_f", [P, TT, 8])
        pick = sb("pick", [P, TT, 2, E])
        gate = sb("gate", [P, TT, E])
        hid = sb("hid", [P, 2, FC * T])
        sg = sb("sg", [P, FC * T])
        block = ctx.enter_context(nc.Block())

        @block.sync
        def _(sp):
            prefetch(nc, S, sp, k + 1)
            with sp.Fori(0, B) as b:
                sync_x(nc, S, sp, b)
            sp.wait_ge(S.xc_free, 1)

        @block.tensor
        def _(pe):
            w1 = part(W, TB, "w1", E * C)
            w2 = part(W, TB, "w2", E * FC)
            gu, down, router = part(W, TB, "gate_up", C), part(W, TB, "down", FC), part(W, TB, "router", C)
            x = S.xc[:, :, 1:1 + T]
            pe.wait_ge(S.weights_ready[k], 16)

            def hidden(w, slot, full):
                for f in range(FC):
                    for c in range(C):
                        last = nc.tensor.matmul(S.R[:, slot, f * T:(f + 1) * T], w(c)[:, f * P:(f + 1) * P], x[:, c, :],
                                                start=(c == 0), stop=(c == C - 1))
                last.then_inc(full, 1)

            def outputs(src, w, slot):
                for tt in range(TT):
                    for f in range(FC):
                        last = nc.tensor.matmul(S.O[:, slot, tt * D:(tt + 1) * D], src[:, f * T + tt * P:f * T + (tt + 1) * P],
                                                w(f), start=(f == 0), stop=(f == FC - 1))
                last.then_inc(S.o_full, 1)

            with pe.Fori(0, B) as b:
                pe.wait_ge(S.xc_ready, 16)
                pe.sem_inc(S.xc_ready, -16)
                pe.wait_ge(S.o_free[0], 1)
                pe.sem_inc(S.o_free[0], -1)
                for tt in range(TT):
                    for c in range(C):
                        last = nc.tensor.matmul(S.O[:, 0, tt * 16:tt * 16 + E + 1], x[:, c, tt * P:(tt + 1) * P], router[:, c, :],
                                                start=(c == 0), stop=(c == C - 1))
                last.then_inc(S.q_full, 1)
                for e in range(E + 3):
                    if e < E + 2:
                        pe.wait_ge(S.r_free[e % 2], 1)
                        pe.sem_inc(S.r_free[e % 2], -1)
                        if e < E:
                            hidden(lambda c: w1[:, e * C + c, :], e % 2, S.h_full)
                        else:
                            hidden(lambda c: gu[:, c, (e - E) * D:(e - E + 1) * D], e % 2, S.h_full if e == E else S.h_full_up)
                    if 1 <= e <= E:
                        pe.wait_ge(S.h_ready, 1)
                        pe.sem_inc(S.h_ready, -1)
                        pe.wait_ge(S.o_free[e % 2], 1)
                        pe.sem_inc(S.o_free[e % 2], -1)
                        outputs(hid[:, (e - 1) % 2, :], lambda f: w2[:, (e - 1) * FC + f, :], e % 2)
                pe.wait_ge(S.sh_ready, 1)
                pe.sem_inc(S.sh_ready, -1)
                pe.wait_ge(S.o_free[1], 1)
                pe.sem_inc(S.o_free[1], -1)
                outputs(sg, lambda f: down[:, f, :], 1)
                pe.wait_ge(S.o_free[0], 1)
                pe.sem_inc(S.o_free[0], -1)
                pe.sem_inc(S.o_free[0], 1)
                pe.wait_ge(S.o_free[1], 1)
                pe.sem_inc(S.o_free[1], -1)
                tail_pe(nc, S, pe, 1)

        @block.scalar
        def _(act):
            act.wait_ge(S.weights_ready[k], 16)
            with act.Fori(0, B) as b:
                act.wait_ge(S.max_ready, 1)
                act.sem_inc(S.max_ready, -1)
                for tt in range(TT):
                    nc.scalar.activation(prob[:, tt, :], logit[:, tt, 0:E], ACT.Exp, bias=nmax[:, tt:tt + 1],
                                         accum_out=total[:, tt:tt + 1])
                nc.scalar.activation(shared_gate[:], logit[:, :, E], ACT.Exp, scale=-1.0)
                act.drain().then_inc(S.p_ready, 1)
                for e in range(E + 1):
                    act.wait_ge(S.h_full, 1)
                    act.sem_inc(S.h_full, -1)
                    if e < E:
                        if e >= 2:
                            act.wait_ge(S.hid_free, 1)
                            act.sem_inc(S.hid_free, -1)
                        nc.scalar.activation(hid[:, e % 2, :], S.R[:, e % 2, 0:FC * T], ACT.Silu).then_inc(S.r_free[e % 2], 1)
                        act.drain().then_inc(S.h_ready, 1)
                    else:
                        nc.scalar.activation(sg[:], S.R[:, e % 2, 0:FC * T], ACT.Silu).then_inc(S.r_free[e % 2], 1)
                        act.drain().then_inc(S.sg_ready, 1)
                act.wait_ge(S.hid_free, 2)
                act.sem_inc(S.hid_free, -2)
                tail_act(nc, S, act, 1, b)

        @block.vector
        def _(dve):
            with dve.Fori(0, B) as b:
                dve.wait_ge(S.q_full, 1)
                dve.sem_inc(S.q_full, -1)
                nc.vector.tensor_copy(logit[:], S.O[:, 0, 0:TT * 16].rearrange("p (t e) -> p t e", t=TT)[:, :, 0:E + 1])\
                    .then_inc(S.o_free[0], 1)
                dve.drain()
                nc.vector.tensor_reduce(nmax[:], logit[:, :, 0:E], AX.X, ALU.max, negate=True).then_inc(S.max_ready, 1)
                dve.wait_ge(S.p_ready, 1)
                dve.sem_inc(S.p_ready, -1)
                nc.vector.tensor_scalar(shared_gate[:], shared_gate[:], 1.0, None, ALU.add)
                nc.vector.reciprocal(total[:], total[:])
                dve.drain()
                nc.vector.reciprocal(shared_gate[:], shared_gate[:])
                for tt in range(TT):
                    nc.vector.tensor_scalar(prob[:, tt, :], prob[:, tt, :], total[:, tt:tt + 1], None, ALU.mult)
                dve.drain()
                dve_top(nc, S, dve, gate, prob, top, index, index_f, pick, 2, E)
                dve.wait_ge(S.xres_ready, 1)
                dve.sem_inc(S.xres_ready, -1)

                def add(slot, scale):
                    for tt in range(TT):
                        last = nc.vector.scalar_tensor_tensor(S.xres[:, tt, :], S.O[:, slot, tt * D:(tt + 1) * D], scale(tt),
                                                              S.xres[:, tt, :], ALU.mult, ALU.add)
                    last.then_inc(S.o_free[slot], 1)
                    dve.drain()

                for e in range(E):
                    dve.wait_ge(S.o_full, 1)
                    dve.sem_inc(S.o_full, -1)
                    dve.sem_inc(S.hid_free, 1)
                    add((e + 1) % 2, lambda tt: gate[:, tt, e:e + 1])
                dve.wait_ge(S.sg_ready, 1)
                dve.sem_inc(S.sg_ready, -1)
                dve.wait_ge(S.h_full_up, 1)
                dve.sem_inc(S.h_full_up, -1)
                nc.vector.tensor_tensor(sg[:], sg[:], S.R[:, (E + 1) % 2, 0:FC * T], ALU.mult).then_inc(S.r_free[(E + 1) % 2], 1)
                dve.drain().then_inc(S.sh_ready, 1)
                dve.wait_ge(S.o_full, 1)
                dve.sem_inc(S.o_full, -1)
                dve.sem_inc(S.xc_free, 1)
                add(1, lambda tt: shared_gate[:, tt:tt + 1])
                nc.vector.tensor_copy(S.ysb[:], S.xres[:])
                dve.drain().then_inc(S.xres_free, 1)
                tail_dve(nc, S, dve)

        @block.gpsimd
        def _(pool):
            with pool.Fori(0, B) as b:
                pool_residual(nc, S, pool, b)
                tail_pool(nc, S, pool, b)


def moe_relu(nc, S, k):
    W, TB = S.arena[k % 2], PACK[k]
    E, EH, CHOSEN = 16, 64, 4
    HC = E * EH // P
    with ExitStack() as ctx:
        def sb(name, shape, dt=F32):
            return ctx.enter_context(nc.sbuf_tensor(f"{name}_{k}", shape, dt))

        prob = sb("prob", [P, TT, E])
        top = sb("top", [P, TT, 8])
        index = sb("index", [P, TT, 8], U32)
        index_f = sb("index_f", [P, TT, 8])
        pick = sb("pick", [P, TT, CHOSEN, E])
        gate = sb("gate", [P, TT, E])
        total = sb("total", [P, TT])
        hid = sb("hid", [P, TT, E * EH])
        hid_t = sb("hid_t", [P, HC, T])
        block = ctx.enter_context(nc.Block())

        @block.sync
        def _(sp):
            prefetch(nc, S, sp, k + 1)
            with sp.Fori(0, B) as b:
                sync_x(nc, S, sp, b)
            sp.wait_ge(S.xc_free, 1)

        @block.tensor
        def _(pe):
            keys, values, sel = part(W, TB, "keys", C), part(W, TB, "values", HC), part(W, TB, "sel", C)
            x = S.xc[:, :, 1:1 + T]
            pe.wait_ge(S.weights_ready[k], 16)
            with pe.Fori(0, B) as b:
                pe.wait_ge(S.xc_ready, 16)
                pe.sem_inc(S.xc_ready, -16)
                pe.wait_ge(S.o_free[0], 1)
                pe.sem_inc(S.o_free[0], -1)
                for tt in range(TT):
                    for c in range(C):
                        last = nc.tensor.matmul(S.O[:, 0, tt * E:(tt + 1) * E], x[:, c, tt * P:(tt + 1) * P], sel[:, c, :],
                                                start=(c == 0), stop=(c == C - 1))
                last.then_inc(S.q_full, 1)
                for tt in range(TT):
                    pe.wait_ge(S.r_free[tt], 1)
                    pe.sem_inc(S.r_free[tt], -1)
                    for at in (0, BANK):
                        for c in range(C):
                            last = nc.tensor.matmul(S.R[:, tt, at:at + BANK], x[:, c, tt * P:(tt + 1) * P], keys[:, c, at:at + BANK],
                                                    start=(c == 0), stop=(c == C - 1))
                    last.then_inc(S.h_full, 1)
                for tt in range(TT):
                    pe.wait_ge(S.h_ready, 1)
                    pe.sem_inc(S.h_ready, -1)
                    for j in range(2):
                        pe.wait_ge(S.t_free[j], 1)
                        pe.sem_inc(S.t_free[j], -1)
                        for i in range(4):
                            last = nc.tensor.transpose(S.T[:, j, i * P:(i + 1) * P], hid[:, tt, (4 * j + i) * P:(4 * j + i + 1) * P], S.ident)
                        last.then_inc(S.at_full, 1)
                pe.wait_ge(S.t_free[0], 1)
                pe.sem_inc(S.t_free[0], -1)
                pe.wait_ge(S.t_free[1], 1)
                pe.sem_inc(S.t_free[1], -1)
                pe.sem_inc(S.t_free[0], 1)
                pe.sem_inc(S.t_free[1], 1)
                pe.wait_ge(S.o_free[0], 1)
                pe.sem_inc(S.o_free[0], -1)
                for tt in range(TT):
                    for c in range(HC):
                        last = nc.tensor.matmul(S.O[:, 0, tt * D:(tt + 1) * D], hid_t[:, c, tt * P:(tt + 1) * P], values[:, c, :],
                                                start=(c == 0), stop=(c == HC - 1))
                last.then_inc(S.y_full, 1)
                pe.wait_ge(S.o_free[1], 1)
                pe.sem_inc(S.o_free[1], -1)
                tail_pe(nc, S, pe, 1)

        @block.scalar
        def _(act):
            with act.Fori(0, B) as b:
                act.wait_ge(S.max_ready, 1)
                act.sem_inc(S.max_ready, -1)
                nc.scalar.activation(prob[:], prob[:], ACT.Exp, scale=-1.0).then_inc(S.p_ready, 1)
                for tt in range(TT):
                    for j in range(2):
                        act.wait_ge(S.at_full, 1)
                        act.sem_inc(S.at_full, -1)
                        nc.scalar.activation(hid_t[:, 4 * j:4 * j + 4, tt * P:(tt + 1) * P],
                                             S.T[:, j, :].rearrange("p (c t) -> p c t", c=4), ACT.Copy).then_inc(S.t_free[j], 1)
                tail_act(nc, S, act, 1, b)

        @block.vector
        def _(dve):
            dve.wait_ge(S.weights_ready[k], 16)
            with dve.Fori(0, B) as b:
                dve.wait_ge(S.q_full, 1)
                dve.sem_inc(S.q_full, -1)
                nc.vector.tensor_copy(prob[:].rearrange("p t e -> p (t e)"), S.O[:, 0, 0:TT * E]).then_inc(S.o_free[0], 1)
                dve.drain().then_inc(S.max_ready, 1)
                dve.wait_ge(S.p_ready, 1)
                dve.sem_inc(S.p_ready, -1)
                nc.vector.tensor_scalar(prob[:], prob[:], 1.0, None, ALU.add)
                dve.drain()
                nc.vector.reciprocal(prob[:], prob[:])
                dve.drain()
                dve_top(nc, S, dve, gate, prob, top, index, index_f, pick, CHOSEN, E)
                nc.vector.tensor_reduce(total[:], gate[:], AX.X, ALU.add)
                dve.drain()
                nc.vector.tensor_scalar(total[:], total[:], 1e-9, None, ALU.max)
                dve.drain()
                nc.vector.reciprocal(total[:], total[:])
                dve.drain()
                for tt in range(TT):
                    nc.vector.tensor_scalar(gate[:, tt, :], gate[:, tt, :], total[:, tt:tt + 1], part(W, TB, "route_scale"),
                                            ALU.mult, ALU.mult)
                dve.drain()
                for tt in range(TT):
                    dve.wait_ge(S.h_full, 1)
                    dve.sem_inc(S.h_full, -1)
                    if tt == TT - 1:
                        dve.sem_inc(S.xc_free, 1)
                    nc.vector.scalar_tensor_tensor(hid[:, tt, :].rearrange("p (e h) -> p e h", e=E),
                                                   S.R[:, tt, :].rearrange("p (e h) -> p e h", e=E), 0.0,
                                                   gate[:, tt, :].unsqueeze(2).to_broadcast([P, E, EH]), ALU.max, ALU.mult)\
                        .then_inc(S.r_free[tt], 1)
                    dve.drain().then_inc(S.h_ready, 1)
                dve_output(nc, S, dve, 0)

        @block.gpsimd
        def _(pool):
            with pool.Fori(0, B) as b:
                pool_residual(nc, S, pool, b)
                tail_pool(nc, S, pool, b)


def int8_product(nc, S, k):
    W, TB = S.arena[k % 2], PACK[k]
    with ExitStack() as ctx:
        def sb(name, shape, dt=F32):
            return ctx.enter_context(nc.sbuf_tensor(f"{name}_{k}", shape, dt))

        rhs_i = sb("rhs_i", [P, C, D])
        rhs_q = sb("rhs_q", [P, C, D], BF16)
        col_scale = sb("col_scale", [P, 2])
        col_inv = sb("col_inv", [P, 2])
        col_wide = sb("col_wide", [P, 2, P])
        rhs_scale = sb("rhs_scale", [P, D])
        row_scale = sb("row_scale", [P, TT])
        row_inv = sb("row_inv", [P, TT])
        lhs_i = sb("lhs_i", [P, TT, D])
        lhs_q = sb("lhs_q", [P, C, T], BF16)
        block = ctx.enter_context(nc.Block())

        @block.sync
        def _(sp):
            prefetch(nc, S, sp, k + 1)

        @block.tensor
        def _(pe):
            pe.wait_ge(S.setup_dve, 1)
            pe.sem_inc(S.setup_dve, -1)
            pe.wait_ge(S.o_free[0], 1)
            pe.sem_inc(S.o_free[0], -1)
            for kc in range(C):
                for nb in range(C):
                    last = nc.tensor.transpose(S.O[:, 0, kc * D + nb * P:kc * D + (nb + 1) * P], rhs_i[:, nb, kc * P:(kc + 1) * P], S.ident)
            last.then_inc(S.at_full, 1)
            pe.wait_ge(S.o_free[1], 1)
            pe.sem_inc(S.o_free[1], -1)
            for nb in range(C):
                last = nc.tensor.transpose(S.O[:, 1, nb * P:(nb + 1) * P], col_wide[:, nb, :], S.ident)
            last.then_inc(S.at_full, 1)
            with pe.Fori(0, B) as b:
                pe.wait_ge(S.q_full, 1)
                pe.sem_inc(S.q_full, -1)
                pe.wait_ge(S.o_free[0], 1)
                pe.sem_inc(S.o_free[0], -1)
                for c in range(C):
                    for tt in range(TT):
                        last = nc.tensor.transpose(S.O[:, 0, (c * TT + tt) * P:(c * TT + tt + 1) * P], lhs_i[:, tt, c * P:(c + 1) * P], S.ident)
                last.then_inc(S.at_full, 1)
                pe.wait_ge(S.o_free[0], 1)
                pe.sem_inc(S.o_free[0], -1)
                for tt in range(TT):
                    for c in range(C):
                        last = nc.tensor.matmul(S.O[:, 0, tt * D:(tt + 1) * D], lhs_q[:, c, tt * P:(tt + 1) * P], rhs_q[:, c, :],
                                                start=(c == 0), stop=(c == C - 1))
                last.then_inc(S.y_full, 1)
                pe.wait_ge(S.o_free[1], 1)
                pe.sem_inc(S.o_free[1], -1)
                tail_pe(nc, S, pe, 1)

        @block.scalar
        def _(act):
            act.wait_ge(S.at_full, 1)
            act.sem_inc(S.at_full, -1)
            nc.scalar.activation(rhs_q[:].rearrange("p c n -> p (c n)"), S.O[:, 0, :], ACT.Copy).then_inc(S.o_free[0], 1)
            act.wait_ge(S.at_full, 1)
            act.sem_inc(S.at_full, -1)
            nc.scalar.activation(rhs_scale[:], S.O[:, 1, 0:D], ACT.Copy).then_inc(S.o_free[1], 1)
            act.drain().then_inc(S.setup_act, 1)
            with act.Fori(0, B) as b:
                act.wait_ge(S.at_full, 1)
                act.sem_inc(S.at_full, -1)
                nc.scalar.activation(lhs_q[:].rearrange("p c t -> p (c t)"), S.O[:, 0, :], ACT.Copy).then_inc(S.o_free[0], 1)
                tail_act(nc, S, act, 1, b)

        @block.vector
        def _(dve):
            def quantise(out, x, scale, inv):
                nc.vector.tensor_reduce(scale[:], x, AX.X, ALU.max, apply_absolute_value=True)
                dve.drain()
                nc.vector.tensor_scalar(scale[:], scale[:], 1e-12, 1.0 / INT8_MAX, ALU.max, ALU.mult)
                dve.drain()
                nc.vector.reciprocal(inv[:], scale[:])
                dve.drain()
                for t in range(2):
                    nc.vector.tensor_scalar(out[:, t, :], x[:, t, :], inv[:, t:t + 1], ROUND, ALU.mult, ALU.add)
                dve.drain()
                nc.vector.tensor_scalar(out[:], out[:], ROUND, INT8_MAX, ALU.subtract, ALU.min)
                dve.drain()
                return nc.vector.tensor_scalar(out[:], out[:], -INT8_MAX, None, ALU.max)

            dve.wait_ge(S.weights_ready[k], 16)
            quantise(rhs_i, part(W, TB, "rhs_t", C), col_scale, col_inv)
            for nb in range(C):
                nc.vector.tensor_copy(col_wide[:, nb, :], col_scale[:, nb:nb + 1].to_broadcast([P, P]))
            dve.drain().then_inc(S.setup_dve, 1)
            dve.wait_ge(S.setup_act, 1)
            dve.sem_inc(S.setup_act, -1)
            with dve.Fori(0, B) as b:
                dve.wait_ge(S.xres_ready, 1)
                dve.sem_inc(S.xres_ready, -1)
                quantise(lhs_i, S.xres[:], row_scale, row_inv).then_inc(S.q_full, 1)
                dve.wait_ge(S.y_full, 1)
                dve.sem_inc(S.y_full, -1)
                for tt in range(TT):
                    last = nc.vector.scalar_tensor_tensor(S.ysb[:, tt, :], S.O[:, 0, tt * D:(tt + 1) * D], row_scale[:, tt:tt + 1],
                                                          rhs_scale[:], ALU.mult, ALU.mult)
                last.then_inc(S.o_free[0], 1)
                dve.drain()
                nc.vector.tensor_tensor(S.ysb[:], S.ysb[:], S.xres[:], ALU.add)
                dve.drain().then_inc(S.xres_free, 1)
                tail_dve(nc, S, dve)

        @block.gpsimd
        def _(pool):
            with pool.Fori(0, B) as b:
                pool_residual(nc, S, pool, b)
                tail_pool(nc, S, pool, b)


def selective_scan(nc, S, k):
    W, TB = S.arena[k % 2], PACK[k]
    CT, NS = 4, 16
    NCH = N // BANK
    decay = S.arena[(k + 1) % 2][:, 4096:4096 + 2 * N].rearrange("p (s n) -> p s n", s=2)
    state = S.arena[k % 2][:, 4096:4096 + 2 * N].rearrange("p (s n) -> p s n", s=2)
    with ExitStack() as ctx:
        def sb(name, shape, dt=F32):
            return ctx.enter_context(nc.sbuf_tensor(f"{name}_{k}", shape, dt))

        w = sb("w", [P, SCAN_COLS])
        xp = sb("xp", [P, N])
        delta = sb("delta", [P, N])
        u = sb("u", [P, N])
        gated = sb("gated", [P, CT, N])
        neg_a = sb("neg_a", [P, NS])
        bc = sb("bc", [P, NS])
        diag = sb("diag", [P, NS, P])
        gc = sb("gc", [P, CT, T])
        block = ctx.enter_context(nc.Block())
        banks = [(S.T, 0, S.t_free[0]), (S.T, 1, S.t_free[1]), (S.O, 0, S.o_free[0]), (S.O, 1, S.o_free[1])]

        @block.sync
        def _(sp):
            prefetch(nc, S, sp, k + 1)
            with sp.Fori(0, CT) as ct:
                sp.wait_ge(S.scan_w_free, 1)
                sp.sem_inc(S.scan_w_free, -1)
                sp.dma_start(w[:], S.scan_dram[bass.ds(ct * P, P), :]).then_inc(S.scan_w, 16)
                sp.wait_ge(S.scan_w, 16)
                sp.sem_inc(S.scan_w, -16)
                sp.sem_inc(S.scan_w_pe, 1)
                sp.sem_inc(S.scan_w_act, 1)
                sp.sem_inc(S.scan_w_pool, 1)
            sp.wait_ge(S.scan_w_free, 1)
            sp.sem_inc(S.scan_w_free, -1)
            sp.sem_inc(S.scan_w_free, 1)
            with sp.Fori(0, B) as b:
                sp.wait_ge(S.xc_free, 1)
                sp.sem_inc(S.xc_free, -1)
                sp.dma_start(gc[:], gated[:, :, bass.ds(b * T, T)]).then_inc(S.xc_ready, 16)
            sp.wait_ge(S.xc_free, 1)

        @block.tensor
        def _(pe):
            with pe.Fori(0, CT) as ct:
                pe.wait_ge(S.scan_w_pe, 1)
                pe.sem_inc(S.scan_w_pe, -1)
                j = 0
                for name in ("wd", "wx", "wg"):
                    wp = part(w, SCAN, name, C)
                    for ch in range(NCH):
                        psum, slot, free = banks[j % 4]
                        pe.wait_ge(free, 1)
                        pe.sem_inc(free, -1)
                        for c in range(C):
                            last = nc.tensor.matmul(psum[:, slot, :], wp[:, c, :], S.x_t[:, c, ch * BANK:(ch + 1) * BANK],
                                                    start=(c == 0), stop=(c == C - 1))
                        last.then_inc(S.q_full, 1)
                        j += 1
                pe.wait_ge(S.diag_ready, 1)
                pe.sem_inc(S.diag_ready, -1)
                pe.wait_ge(S.r_free[0], 1)
                pe.sem_inc(S.r_free[0], -1)
                for n in range(NS):
                    pe.wait_ge(S.state_ready, 1)
                    pe.sem_inc(S.state_ready, -1)
                    for ch in range(NCH):
                        last = nc.tensor.matmul(S.R[:, ch // 2, (ch % 2) * BANK:(ch % 2 + 1) * BANK], diag[:, n, :],
                                                state[:, n % 2, ch * BANK:(ch + 1) * BANK], start=(n == 0), stop=(n == NS - 1))
                    last.then_inc(S.state_used, 1)
            pe.wait_ge(S.weights_ready[k], 16)
            wout = part(W, TB, "wout", CT)
            with pe.Fori(0, B) as b:
                pe.wait_ge(S.xc_ready, 16)
                pe.sem_inc(S.xc_ready, -16)
                pe.wait_ge(S.o_free[0], 1)
                pe.sem_inc(S.o_free[0], -1)
                for tt in range(TT):
                    for c in range(CT):
                        last = nc.tensor.matmul(S.O[:, 0, tt * D:(tt + 1) * D], gc[:, c, tt * P:(tt + 1) * P], wout[:, c, :],
                                                start=(c == 0), stop=(c == CT - 1))
                last.then_inc(S.y_full, 1)
                pe.wait_ge(S.o_free[1], 1)
                pe.sem_inc(S.o_free[1], -1)
                tail_pe(nc, S, pe, 1)

        @block.scalar
        def _(act):
            with act.Fori(0, CT) as ct:
                act.wait_ge(S.scan_w_act, 1)
                act.sem_inc(S.scan_w_act, -1)
                nc.scalar.activation(neg_a[:], part(w, SCAN, "a_log"), ACT.Exp)
                act.drain()
                nc.scalar.activation(neg_a[:], neg_a[:], ACT.Copy, scale=-1.0)
                j = 0
                for name, func in (("bd", ACT.Relu), ("bx", ACT.Identity), ("bg", ACT.Sigmoid)):
                    for ch in range(NCH):
                        psum, slot, free = banks[j % 4]
                        cols = slice(ch * BANK, (ch + 1) * BANK)
                        if name == "bg":
                            dst = gated[:, bass.ds(ct, 1), cols].rearrange("p a n -> p (a n)")
                        else:
                            dst = (delta if name == "bd" else xp)[:, cols]
                        act.wait_ge(S.q_full, 1)
                        act.sem_inc(S.q_full, -1)
                        nc.scalar.activation(dst, psum[:, slot, :], func, bias=part(w, SCAN, name)).then_inc(free, 1)
                        j += 1
                    if name == "bx":
                        act.drain().then_inc(S.xp_ready, 1)
                act.drain().then_inc(S.gate_exp, 1)
                for n in range(NS):
                    act.wait_ge(S.decay_free, 1)
                    act.sem_inc(S.decay_free, -1)
                    nc.scalar.activation(decay[:, n % 2, :].rearrange("p (b t) -> p b t", b=B)[:, :, 1:T],
                                         delta[:].rearrange("p (b t) -> p b t", b=B)[:, :, 1:T], ACT.Exp,
                                         scale=neg_a[:, n:n + 1]).then_inc(S.decay_ready, 1)
            act.wait_ge(S.decay_free, 2)
            act.sem_inc(S.decay_free, -2)
            with act.Fori(0, B) as b:
                tail_act(nc, S, act, 1, b)

        @block.vector
        def _(dve):
            for s in range(2):
                nc.vector.memset(decay[:, s, :].rearrange("p (b t) -> p b t", b=B)[:, :, 0:1], 0.0).then_inc(S.decay_free, 1)
            with dve.Fori(0, CT) as ct:
                dve.wait_ge(S.xp_ready, 1)
                dve.sem_inc(S.xp_ready, -1)
                nc.vector.tensor_tensor(u[:], xp[:], delta[:], ALU.mult)
                dve.drain()
                for n in range(NS):
                    dve.wait_ge(S.decay_ready, 1)
                    dve.sem_inc(S.decay_ready, -1)
                    dve.wait_ge(S.state_used, 1)
                    dve.sem_inc(S.state_used, -1)
                    nc.vector.tensor_tensor_scan(state[:, n % 2, :], decay[:, n % 2, :], u[:], 0.0, ALU.mult, ALU.add)\
                        .then_inc(S.decay_free, 1)
                    dve.drain().then_inc(S.state_ready, 1)
                dve.wait_ge(S.state_used, 2)
                dve.sem_inc(S.state_used, -2)
                dve.sem_inc(S.state_used, 2)
                dve.wait_ge(S.gate_exp, 1)
                dve.sem_inc(S.gate_exp, -1)
                nc.vector.scalar_tensor_tensor(xp[:], xp[:], part(w, SCAN, "d"), S.R[:].rearrange("p s n -> p (s n)"),
                                               ALU.mult, ALU.add).then_inc(S.r_free[0], 1)
                dve.drain()
                tile = gated[:, bass.ds(ct, 1), :].rearrange("p a n -> p (a n)")
                nc.vector.tensor_tensor(tile, tile, xp[:], ALU.mult).then_inc(S.scan_w_free, 1)
            dve.wait_ge(S.state_used, 2)
            dve.sem_inc(S.state_used, -2)
            with dve.Fori(0, B) as b:
                dve.wait_ge(S.y_full, 1)
                dve.sem_inc(S.y_full, -1)
                dve.sem_inc(S.xc_free, 1)
                dve.wait_ge(S.xres_ready, 1)
                dve.sem_inc(S.xres_ready, -1)
                nc.vector.tensor_tensor(S.ysb[:], S.O[:, 0, :].rearrange("p (t d) -> p t d", t=TT), S.xres[:], ALU.add)\
                    .then_inc(S.o_free[0], 1)
                dve.drain().then_inc(S.xres_free, 1)
                tail_dve(nc, S, dve)

        @block.gpsimd
        def _(pool):
            pool.sem_inc(S.state_used, 2)
            pool.sem_inc(S.scan_w_free, 1)
            with pool.Fori(0, CT) as ct:
                pool.wait_ge(S.scan_w_pool, 1)
                pool.sem_inc(S.scan_w_pool, -1)
                nc.gpsimd.tensor_tensor(bc[:], part(w, SCAN, "b"), part(w, SCAN, "c0"), ALU.mult)
                pool.drain()
                for n in range(NS):
                    last = nc.gpsimd.tensor_scalar(diag[:, n, :], S.ident, bc[:, n:n + 1], None, ALU.mult)
                last.then_inc(S.diag_ready, 1)
            pool.wait_ge(S.weights_ready[k], 16)
            with pool.Fori(0, B) as b:
                pool_residual(nc, S, pool, b, part(W, TB, "bo"))
                tail_pool(nc, S, pool, b)


def moe_capacity(nc, S, k, out):
    W, TB = S.arena[k % 2], PACK[k]
    FC = F3 // P
    ROWS = [(0, P), (1, P), (2, CAP - 2 * P)]
    with ExitStack() as ctx:
        def sb(name, shape, dt=F32):
            return ctx.enter_context(nc.sbuf_tensor(f"{name}_{k}", shape, dt))

        logit = sb("logit", [P, TT, E3])
        nmax = sb("nmax", [P, TT])
        total = sb("total", [P, TT])
        prob = sb("prob", [P, TT, E3])
        top = sb("top", [P, TT, 8])
        index = sb("index", [P, TT, 8], U32)
        index_f = sb("index_f", [P, TT, 8])
        one_hot = sb("one_hot", [P, TT, E3])
        before = sb("before", [P, TT + 1, E3])
        ranks = sb("ranks", [P, TT, E3])
        pos = sb("pos", [P, TT])
        kept = sb("kept", [P, TT])
        slot_f = sb("slot_f", [P, TT])
        spare = sb("spare", [P, TT])
        to_f = sb("to_f", [P, TT])
        to = sb("to", [P, TT], U32)
        back = sb("back", [P, B, TT], U32)
        gates = sb("gates", [P, B, TT])
        back_b = sb("back_b", [P, TT], U32)
        gate_b = sb("gate_b", [P, TT])
        zeros = sb("zeros", [P, 5 * D])
        w1 = sb("w1", [P, 2, C, F3])
        w2 = sb("w2", [P, 2, FC, D])
        xe = sb("xe", [P, 2, 3, D])
        xe_t = sb("xe_t", [P, C, CAP])
        hid = sb("hid", [P, FC, CAP])
        ye = sb("ye", [P, 2, 3, D])
        ge = sb("ge", [P, TT, D])
        block = ctx.enter_context(nc.Block())

        @block.sync
        def _(sp):
            def weights(e, s):
                sp.dma_start(w1[:, s, :, :], S.w1_dram[bass.ds(e * P, P), :].rearrange("p (c f) -> p c f", c=C)).then_inc(S.ew_ready[s], 16)
                sp.dma_start(w2[:, s, :, :], S.w2_dram[bass.ds(e * P, P), :].rearrange("p (c f) -> p c f", c=FC)).then_inc(S.ew_ready[s], 16)

            def rows(e, s):
                sp.wait_ge(S.xe_free[s], 1)
                sp.sem_inc(S.xe_free[s], -1)
                sp.dma_start(xe[:, s, 0:2, :], S.xe_dram[bass.ds(e * CAP, 2 * P), :].rearrange("(t p) d -> p t d", p=P)).then_inc(S.xe_ready[s], 16)
                sp.dma_start(xe[0:CAP - 2 * P, s, 2, :], S.xe_dram[bass.ds(e * CAP + 2 * P, CAP - 2 * P), :]).then_inc(S.xe_ready[s], 16)

            sp.wait_ge(S.zeros_ready, 1)
            sp.sem_inc(S.zeros_ready, -1)
            for i in range(E3 * CAP // (5 * P)):
                sp.dma_start(S.xe_dram[i * 5 * P:(i + 1) * 5 * P, :].rearrange("(p r) d -> p (r d)", p=P), zeros[:]).then_inc(S.slots_clear, 16)
            sp.dma_start(S.ye_dram[ZERO_ROW:ZERO_ROW + 1, :], zeros[0:1, 0:D]).then_inc(S.slots_clear, 16)
            with sp.Fori(0, B) as b:
                sync_x(nc, S, sp, b)
            sp.wait_ge(S.xc_free, 1)
            for s in range(2):
                weights(s, s)
            sp.wait_ge(S.dispatched, 1)
            sp.sem_inc(S.dispatched, -1)
            with sp.Fori(0, E3 // 2 - 1) as pair:
                e = pair * 2
                for s in range(2):
                    rows(e + s, s)
                for s in range(2):
                    sp.wait_ge(S.ew_free[s], 1)
                    sp.sem_inc(S.ew_free[s], -1)
                    weights(e + (2 + s), s)
            for s in range(2):
                rows(E3 - 2 + s, s)
            with sp.Fori(0, B) as b:
                sp.wait_ge(S.yn_ready_pe, 1)
                sp.sem_inc(S.yn_ready_pe, -1)
                sp.dma_start(out[bass.ds(b * T, T), :].rearrange("(t p) d -> p t d", p=P), S.yn[:]).then_inc(S.out_stored, 16)
                sp.wait_ge(S.out_stored, 16)
                sp.sem_inc(S.out_stored, -16)
                sp.sem_inc(S.yn_free, 1)

        @block.tensor
        def _(pe):
            gate = part(W, TB, "gate", C)
            tri, ones = part(S.const, CONST, "tri"), part(S.const, CONST, "ones")
            pe.wait_ge(S.weights_ready[k], 16)
            with pe.Fori(0, B) as b:
                pe.wait_ge(S.xc_ready, 16)
                pe.sem_inc(S.xc_ready, -16)
                pe.wait_ge(S.o_free[0], 1)
                pe.sem_inc(S.o_free[0], -1)
                for tt in range(TT):
                    for c in range(C):
                        last = nc.tensor.matmul(S.O[:, 0, tt * E3:(tt + 1) * E3], S.xc[:, c, 1 + tt * P:1 + (tt + 1) * P], gate[:, c, :],
                                                start=(c == 0), stop=(c == C - 1))
                last.then_inc(S.q_full, 1)
                pe.wait_ge(S.h_ready, 1)
                pe.sem_inc(S.h_ready, -1)
                pe.wait_ge(S.o_free[1], 1)
                pe.sem_inc(S.o_free[1], -1)
                for tt in range(TT):
                    nc.tensor.matmul(S.O[:, 1, tt * E3:(tt + 1) * E3], tri, one_hot[:, tt, :], start=True, stop=False)
                    last = nc.tensor.matmul(S.O[:, 1, tt * E3:(tt + 1) * E3], ones, before[:, tt, :], start=False, stop=True)
                last.then_inc(S.v_full, 1)

            with pe.Fori(0, E3 // 2) as pair:
                for s in range(2):
                    pe.wait_ge(S.xe_ready[s], 32)
                    pe.sem_inc(S.xe_ready[s], -32)
                    for c in range(C):
                        pe.wait_ge(S.t_free[c], 1)
                        pe.sem_inc(S.t_free[c], -1)
                        for t, n in ROWS:
                            last = nc.tensor.transpose(S.T[:, c, t * P:t * P + n], xe[0:n, s, t, c * P:(c + 1) * P], S.ident[0:n, 0:n])
                        last.then_inc(S.at_full, 1)
                    pe.wait_ge(S.t_free[0], 1)
                    pe.sem_inc(S.t_free[0], -1)
                    pe.wait_ge(S.t_free[1], 1)
                    pe.sem_inc(S.t_free[1], -1)
                    pe.sem_inc(S.t_free[0], 1)
                    pe.sem_inc(S.t_free[1], 1)
                    pe.wait_ge(S.ew_ready[s], 32)
                    pe.sem_inc(S.ew_ready[s], -32)
                    for j in range(FC // 2):
                        pe.wait_ge(S.r_free[j % 2], 1)
                        pe.sem_inc(S.r_free[j % 2], -1)
                        for i in range(2):
                            for c in range(C):
                                last = nc.tensor.matmul(S.R[:, j % 2, i * BANK:i * BANK + CAP], w1[:, s, c, (2 * j + i) * P:(2 * j + i + 1) * P],
                                                        xe_t[:, c, :], start=(c == 0), stop=(c == C - 1))
                        last.then_inc(S.h_full if j % 2 == 0 else S.h_full_up, 1)
                    pe.wait_ge(S.r_free[0], 1)
                    pe.sem_inc(S.r_free[0], -1)
                    pe.wait_ge(S.r_free[1], 1)
                    pe.sem_inc(S.r_free[1], -1)
                    pe.sem_inc(S.r_free[0], 1)
                    pe.sem_inc(S.r_free[1], 1)
                    pe.wait_ge(S.o_free[0], 1)
                    pe.sem_inc(S.o_free[0], -1)
                    pe.wait_ge(S.o_free[1], 1)
                    pe.sem_inc(S.o_free[1], -1)
                    for t, n in ROWS:
                        for f in range(FC):
                            last = nc.tensor.matmul(S.O[0:n, t // 2, (t % 2) * D:(t % 2 + 1) * D], hid[:, f, t * P:t * P + n], w2[:, s, f, :],
                                                    start=(f == 0), stop=(f == FC - 1))
                        if t == 1:
                            last.then_inc(S.y_full, 1)
                    last.then_inc(S.v_full, 1)

        @block.scalar
        def _(act):
            with act.Fori(0, B) as b:
                act.wait_ge(S.max_ready, 1)
                act.sem_inc(S.max_ready, -1)
                for tt in range(TT):
                    nc.scalar.activation(prob[:, tt, :], logit[:, tt, :], ACT.Exp, bias=nmax[:, tt:tt + 1],
                                         accum_out=total[:, tt:tt + 1])
                act.drain().then_inc(S.p_ready, 1)
            with act.Fori(0, E3 // 2) as pair:
                e = pair * 2
                for s in range(2):
                    for c in range(C):
                        act.wait_ge(S.at_full, 1)
                        act.sem_inc(S.at_full, -1)
                        nc.scalar.activation(xe_t[:, c, :], S.T[:, c, 0:CAP], ACT.Copy).then_inc(S.t_free[c], 1)
                    act.sem_inc(S.xe_free[s], 1)
                    for j in range(0, FC // 2, 2):
                        act.wait_ge(S.h_full, 1)
                        act.sem_inc(S.h_full, -1)
                        nc.scalar.activation(hid[:, 2 * j:2 * j + 2, :], S.R[:, 0, :].rearrange("p (i n) -> p i n", i=2)[:, :, 0:CAP],
                                             ACT.Relu).then_inc(S.r_free[0], 1)
                    act.wait_ge(S.v_full, 1)
                    act.sem_inc(S.v_full, -1)
                    act.wait_ge(S.ye_stored[s], 32)
                    act.sem_inc(S.ye_stored[s], -32)
                    act.sem_inc(S.ye_free, 1)
                    n = ROWS[2][1]
                    nc.scalar.activation(ye[0:n, s, 2, :], S.O[0:n, 1, 0:D], ACT.Copy).then_inc(S.o_free[1], 1)
                    act.drain()
                    act.dma_start(S.ye_dram[bass.ds((e + s) * CAP + 2 * P, n), :], ye[0:n, s, 2, :]).then_inc(S.ye_stored[s], 16)
                    act.wait_ge(S.ye_ready, 1)
                    act.sem_inc(S.ye_ready, -1)
                    act.dma_start(S.ye_dram[bass.ds((e + s) * CAP, 2 * P), :].rearrange("(t p) d -> p t d", p=P), ye[:, s, 0:2, :])\
                        .then_inc(S.ye_stored[s], 16)
            for s in range(2):
                act.wait_ge(S.ye_stored[s], 32)
                act.sem_inc(S.ye_stored[s], -32)
            act.sem_inc(S.combined, 1)

        @block.vector
        def _(dve):
            nc.vector.memset(before[:], 0.0)
            nc.vector.tensor_scalar(spare[:, 0:1], part(S.const, CONST, "row"), float(ZERO_ROW), None, ALU.add)
            nc.vector.tensor_scalar(spare[:, 1:2], part(S.const, CONST, "row"), float(ZERO_ROW + P), None, ALU.add)
            dve.drain()
            with dve.Fori(0, B) as b:
                dve.wait_ge(S.q_full, 1)
                dve.sem_inc(S.q_full, -1)
                dve.sem_inc(S.xc_free, 1)
                nc.vector.tensor_copy(logit[:].rearrange("p t e -> p (t e)"), S.O[:, 0, 0:TT * E3]).then_inc(S.o_free[0], 1)
                dve.drain()
                nc.vector.tensor_reduce(nmax[:], logit[:], AX.X, ALU.max, negate=True).then_inc(S.max_ready, 1)
                dve.wait_ge(S.p_ready, 1)
                dve.sem_inc(S.p_ready, -1)
                nc.vector.reciprocal(total[:], total[:])
                dve.drain()
                for tt in range(TT):
                    nc.vector.tensor_scalar(prob[:, tt, :], prob[:, tt, :], total[:, tt:tt + 1], None, ALU.mult)
                dve.drain()
                for tt in range(TT):
                    nc.vector.max(top[:, tt, :], prob[:, tt, :])
                dve.drain()
                for tt in range(TT):
                    nc.vector.max_index(index[:, tt, :], top[:, tt, :], prob[:, tt, :])
                dve.drain()
                nc.vector.tensor_copy(index_f[:], index[:])
                nc.vector.tensor_copy(before[:, 0, :], before[:, TT, :])
                dve.drain()
                for tt in range(TT):
                    nc.vector.tensor_scalar(one_hot[:, tt, :], part(S.const, CONST, "iota")[:, 0:E3], index_f[:, tt, 0:1], None, ALU.is_equal)
                    dve.drain()
                    last = nc.vector.tensor_tensor(before[:, tt + 1, :], before[:, tt, :], one_hot[:, tt, :], ALU.add)
                    dve.drain()
                dve.drain().then_inc(S.h_ready, 1)
                dve.wait_ge(S.v_full, 1)
                dve.sem_inc(S.v_full, -1)
                nc.vector.tensor_tensor(ranks[:].rearrange("p t e -> p (t e)"), S.O[:, 1, 0:TT * E3],
                                        one_hot[:].rearrange("p t e -> p (t e)"), ALU.mult).then_inc(S.o_free[1], 1)
                dve.drain()
                nc.vector.tensor_reduce(pos[:], ranks[:], AX.X, ALU.add)
                dve.drain()
                nc.vector.tensor_scalar(pos[:], pos[:], 1.0, None, ALU.subtract)
                dve.drain()
                nc.vector.tensor_scalar(kept[:], pos[:], float(CAP), None, ALU.is_lt)
                nc.vector.scalar_tensor_tensor(slot_f[:], index_f[:, :, 0], float(CAP), pos[:], ALU.mult, ALU.add)
                dve.drain()
                nc.vector.tensor_tensor(gates[:, bass.ds(b, 1), :].rearrange("p a t -> p (a t)"), top[:, :, 0], kept[:], ALU.mult)
                nc.vector.tensor_tensor(to_f[:], slot_f[:], spare[:], ALU.subtract)
                nc.vector.tensor_scalar(pos[:], slot_f[:], float(ZERO_ROW), None, ALU.subtract)
                dve.drain()
                nc.vector.tensor_tensor(to_f[:], to_f[:], kept[:], ALU.mult)
                nc.vector.tensor_tensor(pos[:], pos[:], kept[:], ALU.mult)
                dve.drain()
                nc.vector.tensor_tensor(to_f[:], to_f[:], spare[:], ALU.add)
                nc.vector.tensor_scalar(pos[:], pos[:], float(ZERO_ROW), None, ALU.add)
                dve.drain()
                dve.wait_ge(S.to_free, 1)
                dve.sem_inc(S.to_free, -1)
                nc.vector.tensor_copy(back[:, bass.ds(b, 1), :].rearrange("p a t -> p (a t)"), pos[:])
                nc.vector.tensor_copy(to[:], to_f[:])
                nc.vector.tensor_scalar(spare[:], spare[:], float(T), None, ALU.add)
                dve.drain().then_inc(S.to_ready, 1)
            with dve.Fori(0, E3 // 2) as pair:
                for s in range(2):
                    for j in range(1, FC // 2, 2):
                        dve.wait_ge(S.h_full_up, 1)
                        dve.sem_inc(S.h_full_up, -1)
                        nc.vector.tensor_scalar(hid[:, 2 * j:2 * j + 2, :], S.R[:, 1, :].rearrange("p (i n) -> p i n", i=2)[:, :, 0:CAP],
                                                0.0, None, ALU.max).then_inc(S.r_free[1], 1)
                    dve.wait_ge(S.y_full, 1)
                    dve.sem_inc(S.y_full, -1)
                    dve.wait_ge(S.ye_free, 1)
                    dve.sem_inc(S.ye_free, -1)
                    dve.sem_inc(S.ew_free[s], 1)
                    nc.vector.tensor_copy(ye[:, s, 0:2, :], S.O[:, 0, :].rearrange("p (t d) -> p t d", t=TT)).then_inc(S.o_free[0], 1)
                    dve.drain().then_inc(S.ye_ready, 1)
            with dve.Fori(0, B) as b:
                dve.wait_ge(S.gathered, (b + 1) * (16 * TT))
                dve.wait_ge(S.xres_ready, 1)
                dve.sem_inc(S.xres_ready, -1)
                for tt in range(TT):
                    nc.vector.scalar_tensor_tensor(S.ysb[:, tt, :], ge[:, tt, :], gate_b[:, tt:tt + 1], S.xres[:, tt, :], ALU.mult, ALU.add)
                dve.drain().then_inc(S.xres_free, 1)
                tail_dve(nc, S, dve)

        @block.gpsimd
        def _(pool):
            nc.gpsimd.memset(zeros[:], 0.0).then_inc(S.zeros_ready, 1)
            pool.sem_inc(S.to_free, 1)
            for s in range(2):
                pool.sem_inc(S.ye_stored[s], 32)
                pool.sem_inc(S.xe_free[s], 1)
            pool.wait_ge(S.slots_clear, 16 * (E3 * CAP // (5 * P) + 1))
            pool.sem_inc(S.slots_clear, -(16 * (E3 * CAP // (5 * P) + 1)))
            with pool.Fori(0, B) as b:
                nc.gpsimd.tensor_copy(S.xres[:], S.x_nat[:, bass.ds(b * TT, TT), :])
                pool.wait_ge(S.to_ready, 1)
                pool.sem_inc(S.to_ready, -1)
                pool.drain()
                for tt in range(TT):
                    nc.gpsimd.indirect_dma_start(S.xe_dram[:, :], bass.IndirectOffsetOnAxis(ap=to[:, tt:tt + 1], axis=0),
                                                 S.xres[:, tt, :], None).then_inc(S.scattered, 16)
                pool.wait_ge(S.scattered, (b + 1) * (16 * TT))
                pool.sem_inc(S.to_free, 1)
            pool.sem_inc(S.dispatched, 1)
            pool.wait_ge(S.combined, 1)
            pool.sem_inc(S.combined, -1)
            with pool.Fori(0, B) as b:
                pool.wait_ge(S.xres_free, 1)
                pool.sem_inc(S.xres_free, -1)
                nc.gpsimd.tensor_copy(back_b[:], back[:, bass.ds(b, 1), :].rearrange("p a t -> p (a t)"))
                nc.gpsimd.tensor_copy(gate_b[:], gates[:, bass.ds(b, 1), :].rearrange("p a t -> p (a t)"))
                pool.drain()
                for tt in range(TT):
                    nc.gpsimd.indirect_dma_start(ge[:, tt, :], None, S.ye_dram[:, :],
                                                 bass.IndirectOffsetOnAxis(ap=back_b[:, tt:tt + 1], axis=0)).then_inc(S.gathered, 16)
                nc.gpsimd.tensor_copy(S.xres[:], S.x_nat[:, bass.ds(b * TT, TT), :]).then_inc(S.xres_ready, 1)
                pool_rstd(nc, S, pool)
                pool.wait_ge(S.yn_ready_pool, 1)
                pool.sem_inc(S.yn_ready_pool, -1)
                pool.sem_inc(S.yn_free, 1)


class Shared:
    pass


def decoder(nc, dram, layers=range(12)):
    with ExitStack() as ctx:
        S = Shared()

        def sb(name, shape, dt=F32):
            return ctx.enter_context(nc.sbuf_tensor(name, shape, dt))

        def sem(name):
            return ctx.enter_context(nc.semaphore(name))

        def sems(name, n=2):
            return [sem(f"{name}{i}") for i in range(n)]

        S.s_full = sem("s_full")
        S.max_ready = sem("max_ready")
        S.p_ready = sem("p_ready")
        S.t_full = sem("t_full")
        S.pt_ready = sem("pt_ready")
        S.o_full = sem("o_full")
        S.q_full = sem("q_full")
        S.k_full = sem("k_full")
        S.v_full = sem("v_full")
        S.h_full = sem("h_full")
        S.h_full_up = sem("h_full_up")
        S.y_full = sem("y_full")
        S.at_full = sem("at_full")
        S.yt_full = sem("yt_full")
        S.ln_stat = sem("ln_stat")
        S.ln_rstd = sem("ln_rstd")
        S.yn_ready_pe = sem("yn_ready_pe")
        S.yn_ready_pool = sem("yn_ready_pool")
        S.yn_free = sem("yn_free")
        S.xres_ready = sem("xres_ready")
        S.xres_free = sem("xres_free")
        S.xc_ready = sem("xc_ready")
        S.xc_free = sem("xc_free")
        S.setup_act = sem("setup_act")
        S.setup_dve = sem("setup_dve")
        S.lines_full = sem("lines_full")
        S.nat_full = sem("nat_full")
        S.line_ready = sem("line_ready")
        S.lt_full = sem("lt_full")
        S.inc_full = sem("inc_full")
        S.kpad_ready = sem("kpad_ready")
        S.lines_sb = sem("lines_sb")
        S.nat_geo = sem("nat_geo")
        S.inc_free = sem("inc_free")
        S.inc_ready = sem("inc_ready")
        S.mem_ready = sem("mem_ready")
        S.gate_exp = sem("gate_exp")
        S.norm_sum = sem("norm_sum")
        S.norm_root = sem("norm_root")
        S.ctx_ready = sem("ctx_ready")
        S.ctx_stat = sem("ctx_stat")
        S.ctx_rstd = sem("ctx_rstd")
        S.ctx_norm_ready = sem("ctx_norm_ready")
        S.ctx_nt_ready = sem("ctx_nt_ready")
        S.lat_ready = sem("lat_ready")
        S.lat_t_ready = sem("lat_t_ready")
        S.k_sb = sem("k_sb")
        S.hid_free = sem("hid_free")
        S.h_ready = sem("h_ready")
        S.sg_ready = sem("sg_ready")
        S.sh_ready = sem("sh_ready")
        S.scan_w = sem("scan_w")
        S.scan_w_pe = sem("scan_w_pe")
        S.scan_w_act = sem("scan_w_act")
        S.scan_w_pool = sem("scan_w_pool")
        S.scan_w_free = sem("scan_w_free")
        S.diag_ready = sem("diag_ready")
        S.state_ready = sem("state_ready")
        S.state_used = sem("state_used")
        S.xp_ready = sem("xp_ready")
        S.decay_ready = sem("decay_ready")
        S.decay_free = sem("decay_free")
        S.zeros_ready = sem("zeros_ready")
        S.slots_clear = sem("slots_clear")
        S.to_ready = sem("to_ready")
        S.to_free = sem("to_free")
        S.scattered = sem("scattered")
        S.dispatched = sem("dispatched")
        S.combined = sem("combined")
        S.gathered = sem("gathered")
        S.ye_free = sem("ye_free")
        S.ye_ready = sem("ye_ready")
        S.out_stored = sem("out_stored")
        S.r_free = sems("r_free")
        S.t_free = sems("t_free")
        S.o_free = sems("o_free")
        S.ew_ready = sems("ew_ready")
        S.ew_free = sems("ew_free")
        S.xe_ready = sems("xe_ready")
        S.xe_free = sems("xe_free")
        S.ye_stored = sems("ye_stored")
        S.weights_ready = sems("weights_ready", len(PACK))
        loaded = ctx.enter_context(nc.semaphore("loaded"))
        set_up = ctx.enter_context(nc.semaphore("set_up"))

        S.x_nat = sb("x_nat", [P, B * TT, D])
        S.x_t = sb("x_t", [P, C, N])
        S.ctx_t = sb("ctx_t", [P, C, B * CTX])
        S.const = sb("const", [P, sum(n for _, n in CONST.values())])
        S.masks = sb("masks", [P, 2, P], BF16)
        ident_b = sb("ident_b", [P, P], BF16)
        S.arena = [sb(f"arena{i}", [P, W_COLS]) for i in range(2)]
        S.xc = sb("xc", [P, C, 1 + T])
        S.xres = sb("xres", [P, TT, D])
        S.ysb = sb("ysb", [P, TT, D])
        S.yn = sb("yn", [P, TT, D])
        S.bst = sb("bst", [P, TT, 6])
        S.mv = sb("mv", [P, TT, 2])
        S.rstd = sb("rstd", [P, TT])
        S.ident = part(S.const, CONST, "ident")
        S.ident_b = ident_b[:]
        S.R = ctx.enter_context(nc.psum_tensor("R", [P, 2, 2 * BANK], F32))
        S.T = ctx.enter_context(nc.psum_tensor("T", [P, 2, BANK], F32))
        S.O = ctx.enter_context(nc.psum_tensor("O", [P, 2, BANK], F32))
        S.packs = [dram[f"pack{i}"] for i in range(len(PACK))]
        S.ctx_dram, S.scan_dram, S.w1_dram, S.w2_dram = dram["ctx"], dram["scan"], dram["w1"], dram["w2"]
        S.xe_dram = nc.dram_tensor("slots_in", (E3 * CAP + N, D), F32, kind="Internal").ap()
        S.ye_dram = nc.dram_tensor("slots_out", (E3 * CAP + 1, D), F32, kind="Internal").ap()

        with nc.Block() as block:
            @block.sync
            def _(sp):
                sp.dma_start(S.const[:], dram["const"]).then_inc(loaded, 16)
                sp.dma_start(S.x_t[:], dram["x_t"].rearrange("(c p) n -> p c n", p=P)).then_inc(loaded, 16)
                sp.dma_start(S.x_nat[:], dram["x"].rearrange("(t p) d -> p t d", p=P)).then_inc(loaded, 16)
                sp.dma_start(S.ctx_t[:], dram["ctx_t"].rearrange("(c p) n -> p c n", p=P)).then_inc(loaded, 16)
                prefetch(nc, S, sp, layers[0])
                for i in range(2):
                    for s in (S.r_free, S.t_free, S.o_free):
                        sp.sem_inc(s[i], 1)
                sp.sem_inc(S.xc_free, 1)
                sp.sem_inc(S.xres_free, 1)
                sp.sem_inc(S.yn_free, 2)
                sp.wait_ge(loaded, 64)

            @block.vector
            def _(dve):
                nc.vector.memset(S.xc[:], 0.0).then_inc(set_up, 1)
                dve.wait_ge(loaded, 64)
                nc.vector.tensor_copy(S.masks[:, 0, :], part(S.const, CONST, "causal"))
                nc.vector.tensor_copy(S.masks[:, 1, :], part(S.const, CONST, "block"))
                nc.vector.tensor_copy(S.ident_b, S.ident)
                dve.drain().then_inc(set_up, 1)

        build = [
            lambda k: attention16(nc, S, k, DH16 ** -0.5, mask="causal", geometry=True),
            lambda k: perceiver(nc, S, k),
            lambda k: moe_silu(nc, S, k),
            lambda k: attention16(nc, S, k, DH16 ** -0.5, mask="block", out=False),
            lambda k: perceiver(nc, S, k),
            lambda k: moe_relu(nc, S, k),
            lambda k: attention16(nc, S, k, D ** -0.5, mask="causal"),
            lambda k: attention16(nc, S, k, DH16 ** -0.5, cross=True),
            lambda k: int8_product(nc, S, k),
            lambda k: selective_scan(nc, S, k),
            lambda k: attention16(nc, S, k, DH16 ** -0.5, cross=True),
            lambda k: moe_capacity(nc, S, k, dram["out"]),
        ]
        for k in layers:
            build[k](k)
        if layers[-1] != 11:
            with nc.Block() as block:
                @block.sync
                def _(sp):
                    sp.dma_start(dram["out"].rearrange("(t p) d -> p t d", p=P), S.x_nat[:]).then_inc(loaded, 16)
                    sp.wait_ge(loaded, 80)



def pack_inputs(i):
    f = np.float32

    def mat(w):
        w = np.asarray(w)
        return w.reshape(-1, P, w.shape[1]).transpose(1, 0, 2).reshape(P, -1)

    def heads(w):
        w = np.asarray(w)
        out = np.zeros((w.shape[0], H, 32), f)
        out[:, :, :DH16] = w.reshape(-1, H, DH16)
        return out.reshape(w.shape[0], H * 32)

    def head_col(v):
        return heads(np.asarray(v).reshape(1, -1)).reshape(4, P).T

    def rep(v):
        v = np.asarray(v).reshape(1, -1)
        return np.broadcast_to(v, (P, v.shape[1]))

    def lines(w, order):
        return np.asarray(w).reshape(D, H, 4)[:, :, order].reshape(D, 96)

    def mha(wq, bq, wk, bk, wv, bv, wo=None, bo=None):
        none = np.zeros((D, D), f)
        return [mat(heads(wq)), mat(heads(wk)), mat(wv), mat(none if wo is None else wo), head_col(bq), head_col(bk), rep(bv),
                rep(np.zeros(D, f) if bo is None else bo)]

    def xatt(p, w1, b1, w2, b2):
        return [mat(i[p + "Wq"]), mat(i[p + "Wkv"]), mat(i[p + "Wo"]), rep(i[w1]), rep(i[b1]), rep(i[w2]), rep(i[b2])]

    def experts(w):
        return np.concatenate([mat(e) for e in np.asarray(w)], 1)

    a = "L0_attn_"
    qkv, qkv_b, geo = np.asarray(i[a + "qkv_w"]), np.asarray(i[a + "qkv_b"]), np.asarray(i[a + "kv_geo_w"])
    cat = lambda *x: np.concatenate(x, 1)
    w1w, w2w, w1r, w2r = (i[a + n] for n in ("w1_write", "w2_write", "w1_read", "w2_read"))
    packs = [
        [mat(heads(qkv[:, :D])), head_col(qkv_b[:D]), mat(cat(qkv[:, D:], geo)), rep(qkv_b[D:]),
         mat(cat(lines(w1w, _WI), lines(w1w, _WJ))), mat(cat(lines(w2w, _WJ), lines(w2w, _WI))),
         mat(cat(lines(w1r, _PI), lines(w1r, _PJ), lines(w2r, _PJ), lines(w2r, _PI))), mat(i[a + "out_w"]), rep(i[a + "out_b"]),
         rep(i[a + "mem_scale"]), rep(i[a + "decay_logits"]), rep(i[a + "kv_gate"])],
        xatt("L0_xattn_", "L0_xattn_ln1_w", "L0_xattn_ln1_b", "L0_xattn_ln2_w", "L0_xattn_ln2_b"),
        [experts(i["L0_ffn_w1"]), experts(i["L0_ffn_w2"]), mat(i["L0_ffn_shared_gate_up"]), mat(i["L0_ffn_shared_down"]),
         mat(cat(np.asarray(i["L0_ffn_router_w"]), np.asarray(i["L0_ffn_shared_gate_w"])))],
        mha(*(i["L1_attn_" + n] for n in ("Wq", "bq", "Wk", "bk", "Wv", "bv"))),
        xatt("L1_xattn_", "L1_xattn_ln1_g", "L1_xattn_ln1_b", "L1_xattn_ln2_g", "L1_xattn_ln2_b"),
        [mat(np.asarray(i["L1_ffn_keys"]).transpose(1, 0, 2).reshape(D, -1)), mat(np.asarray(i["L1_ffn_values"]).reshape(-1, D)),
         mat(np.asarray(i["L1_ffn_expert_sel"]).T), rep(i["L1_ffn_route_scale"])],
        mha(*(np.asarray(i["L2_attn_" + n]).T for n in ("Wq_w", "Wq_b", "Wk_w", "Wk_b", "Wv_w", "Wv_b", "Wo_w", "Wo_b"))),
        mha(*(i["L2_xattn_" + n] for n in ("Wq", "bq", "Wk", "bk", "Wv", "bv", "Wp", "bp"))),
        [mat(np.asarray(i["L2_ffn_rhs"]).T)],
        [mat(np.asarray(i["L3_attn_W_out"]).T), rep(i["L3_attn_b_out"])],
        mha(*(np.asarray(i["L3_xattn_" + n]).T for n in ("Wq", "bq", "Wk", "bk", "Wv", "bv", "Wo", "bo"))),
        [mat(i["L3_ffn_gate_w"])],
    ]
    s = "L3_attn_"
    win, wg = np.asarray(i[s + "W_in"]), np.asarray(i[s + "W_gate"])
    b_in, bg = np.asarray(i[s + "b_in"]), np.asarray(i[s + "b_gate"])
    DI = wg.shape[0]
    col = lambda v: np.asarray(v).reshape(-1, 1)
    scan = []
    for t in range(DI // P):
        r = slice(t * P, (t + 1) * P)
        r2 = slice(DI + t * P, DI + (t + 1) * P)
        scan.append(cat(mat(win[r].T), mat(win[r2].T), mat(wg[r].T), col(b_in[r]), col(b_in[r2]), col(bg[r]),
                        np.asarray(i[s + "A_log"])[r], np.asarray(i[s + "B_mat"])[r], rep(np.asarray(i[s + "C_mat"])[0]),
                        col(np.asarray(i[s + "D_vec"])[r])))
    x, c = np.asarray(i["x"]).reshape(N, D), np.asarray(i["ctx_1024"]).reshape(B * CTX, D)
    p, j = np.arange(P)[:, None], np.arange(P)[None, :]
    steps = P + p - np.arange(2 * P)[None, :]
    const = cat(np.eye(P), np.where(j <= p, 0, MASKED), np.where(p <= j, 0, MASKED), np.where(p // 64 == j // 64, 0, MASKED),
                (p <= j) * 1.0, np.ones((P, P)), np.maximum(steps, 0), (steps > 0) * 1.0, rep(np.arange(16)),
                np.full((P, 16), -0.5), np.full((P, 64), 0.5), p * 1.0)
    arrays = {f"pack{n}": cat(*parts) for n, parts in enumerate(packs)}
    arrays |= {"x": x, "x_t": x.T, "ctx": c, "ctx_t": c.T, "scan": np.concatenate(scan, 0), "const": const,
               "w1": np.concatenate([mat(e) for e in np.asarray(i["L3_ffn_w1"])], 0),
               "w2": np.concatenate([mat(e) for e in np.asarray(i["L3_ffn_w2"])], 0)}
    return {n: np.ascontiguousarray(v, dtype=f) for n, v in arrays.items()}


def kernel(**inputs):
    import concourse.bacc as bacc
    from concourse.bass_utils import run_bass_kernel_spmd

    nc = bacc.Bacc("TRN2", target_bir_lowering=False, num_devices=1)
    arrays = pack_inputs(inputs)
    dram = {n: nc.dram_tensor(f"{n}_dram", a.shape, F32, kind="ExternalInput").ap() for n, a in arrays.items()}
    dram["out"] = nc.dram_tensor("out_dram", (N, D), F32, kind="ExternalOutput").ap()
    decoder(nc, dram)
    r = run_bass_kernel_spmd(nc, [{f"{n}_dram": a for n, a in arrays.items()}], core_ids=[0])
    return r.results[0]["out_dram"].reshape(B, T, D)
```

```python
from contextlib import ExitStack

import numpy as np

import concourse.bass as bass
from concourse import mybir

F32 = mybir.dt.float32
BF16 = mybir.dt.bfloat16
I32 = mybir.dt.int32
U32 = mybir.dt.uint32
ALU = mybir.AluOpType
ACT = mybir.ActivationFunctionType
AX = mybir.AxisListType

P = 128
B = 8
T = 256
D = 256
C = D // P
TT = T // P
N = B * T
H = 16
HU = 4
HT = P // 16
LW = P // H
CTX = 77
EPS = 1e-5
MASKED = -1e30
BANK = 512
W_COLS = 9984
DH16 = D // H
VA16 = DH16 + 1
XD = 64
XI = H * XD
XK = CTX + T
VA64 = XD + 1
INT8_MAX = 127.0
ROUND = 1.5 * 2.0 ** 23
CAP = 320
E3 = 8
F3 = 1024
ZERO_ROW = E3 * CAP

_PI = [0, 0, 0, 1, 1, 2]
_PJ = [1, 2, 3, 2, 3, 3]
_WI = [2, 3, 1, 0, 2, 0]
_WJ = [3, 1, 2, 3, 0, 1]


def columns(parts):
    at, out = 0, {}
    for name, n in parts:
        out[name] = (at, n)
        at += n
    return out


CONST = columns([("ident", 128), ("causal", 128), ("causal_t", 128), ("block", 128), ("tri", 128), ("ones", 128),
                 ("steps", 256), ("past", 256), ("iota", 16), ("neg_half", 16), ("half", 64), ("row", 1),
                 ("head", HT), ("line_head", H)])
_XATT = [("wq", C * XI), ("wkv", C * 2 * XI), ("wo", (XI // P) * D),
         ("ctx_w", D), ("ctx_b", D), ("lat_w", D), ("lat_b", D)]
_MHA = [("wq", C * D), ("wk", C * D), ("wv", C * D), ("wo", C * D), ("bq", C), ("bk", C), ("bv", D), ("bo", D)]
PACK = [
    columns([("wq", C * D), ("bq", C), ("nat", C * 1024), ("nat_b", 512), ("write1", C * 192), ("write2", C * 192),
             ("read", C * 384), ("wo", C * D), ("bo", D), ("mem_scale", H), ("decay", H), ("kv_gate", 1)]),
    columns(_XATT),
    columns([("w1", 8 * C * 256), ("w2", 8 * C * 256), ("gate_up", C * 512), ("down", C * 256), ("router", C * 9)]),
    columns(_MHA),
    columns(_XATT),
    columns([("keys", C * 1024), ("values", 8 * 256), ("sel", C * 16), ("route_scale", 1)]),
    columns(_MHA),
    columns(_MHA),
    columns([("rhs_t", C * 256)]),
    columns([("wout", 4 * D), ("bo", D)]),
    columns(_MHA),
    columns([("gate", C * E3)]),
]
SCAN = columns([("wx", C * P), ("wd", C * P), ("wg", C * P), ("bx", 1), ("bd", 1), ("bg", 1), ("a_log", 16),
                ("b", 16), ("c0", 16), ("d", 1)])
SCAN_COLS = sum(n for _, n in SCAN.values())


def part(image, table, name, chunks=None):
    at, n = table[name]
    v = image[:, at:at + n]
    return v.rearrange("p (c n) -> p c n", c=chunks) if chunks else v



def tail_dve(nc, S, dve, meanwhile=None):
    for tt in range(TT):
        nc.vector.bn_stats(S.bst[:, tt, :], S.ysb[:, tt, :])
    dve.drain()
    for tt in range(TT):
        last = nc.vector.bn_aggr(S.mv[:, tt, :], S.bst[:, tt, :])
    last.then_inc(S.ln_stat, 1)
    if meanwhile:
        meanwhile()
    dve.wait_ge(S.ln_rstd, 1)
    dve.sem_inc(S.ln_rstd, -1)
    dve.wait_ge(S.yn_free, 2)
    dve.sem_inc(S.yn_free, -2)
    for tt in range(TT):
        last = nc.vector.tensor_scalar(S.yn[:, tt, :], S.ysb[:, tt, :], S.mv[:, tt, 0:1], S.rstd[:, tt:tt + 1],
                                       ALU.subtract, ALU.mult)
    last.then_inc(S.yn_ready_pe, 1)
    dve.drain().then_inc(S.yn_ready_pool, 1)


def pool_rstd(nc, S, pool):
    pool.wait_ge(S.ln_stat, 1)
    pool.sem_inc(S.ln_stat, -1)
    nc.gpsimd.tensor_scalar(S.rstd[:], S.mv[:, :, 1], EPS, None, ALU.add)
    pool.drain()
    nc.gpsimd.tensor_tensor(S.rstd[:], S.rstd[:], part(S.const, CONST, "neg_half")[:, 0:TT], ALU.pow)\
        .then_inc(S.ln_rstd, 1)


def tail_pool(nc, S, pool, b):
    pool_rstd(nc, S, pool)
    pool.wait_ge(S.yn_ready_pool, 1)
    pool.sem_inc(S.yn_ready_pool, -1)
    nc.gpsimd.tensor_copy(S.x_nat[:, bass.ds(b * TT, TT), :], S.yn[:]).then_inc(S.yn_free, 1)


def tail_pe(nc, S, pe, slot):
    pe.wait_ge(S.yn_ready_pe, 1)
    pe.sem_inc(S.yn_ready_pe, -1)
    for c in range(C):
        for tt in range(TT):
            last = nc.tensor.transpose(S.O[:, slot, (c * TT + tt) * P:(c * TT + tt + 1) * P],
                                       S.yn[:, tt, c * P:(c + 1) * P], S.ident)
    last.then_inc(S.yt_full, 1)


def tail_act(nc, S, act, slot, b):
    act.wait_ge(S.yt_full, 1)
    act.sem_inc(S.yt_full, -1)
    act.sem_inc(S.yn_free, 1)
    nc.scalar.activation(S.x_t[:, :, bass.ds(b * T, T)],
                         S.O[:, slot, :].rearrange("p (c t) -> p c t", c=C), ACT.Copy).then_inc(S.o_free[slot], 1)


def pool_residual(nc, S, pool, b, bias=None):
    pool.wait_ge(S.xres_free, 1)
    pool.sem_inc(S.xres_free, -1)
    x = S.x_nat[:, bass.ds(b * TT, TT), :]
    if bias is None:
        nc.gpsimd.tensor_copy(S.xres[:], x).then_inc(S.xres_ready, 1)
    else:
        for tt in range(TT):
            last = nc.gpsimd.tensor_tensor(S.xres[:, tt, :], S.x_nat[:, bass.ds(b * TT + tt, 1), :].rearrange("p a d -> p (a d)"), bias, ALU.add)
        last.then_inc(S.xres_ready, 1)


def dve_output(nc, S, dve, slot, meanwhile=None):
    dve.wait_ge(S.y_full, 1)
    dve.sem_inc(S.y_full, -1)
    dve.wait_ge(S.xres_ready, 1)
    dve.sem_inc(S.xres_ready, -1)
    nc.vector.tensor_tensor(S.ysb[:], S.O[:, slot, :].rearrange("p (t d) -> p t d", t=TT), S.xres[:], ALU.add)\
        .then_inc(S.o_free[slot], 1)
    dve.drain().then_inc(S.xres_free, 1)
    tail_dve(nc, S, dve, meanwhile)


def sync_x(nc, S, sp, b):
    sp.wait_ge(S.xc_free, 1)
    sp.sem_inc(S.xc_free, -1)
    sp.dma_start(S.xc[:, :, 1:1 + T], S.x_t[:, :, bass.ds(b * T, T)]).then_inc(S.xc_ready, 16)


def prefetch(nc, S, sp, k):
    if k < len(PACK):
        n = sum(w for _, w in PACK[k].values())
        sp.dma_start(S.arena[k % 2][:, 0:n], S.packs[k]).then_inc(S.weights_ready[k], 16)



def pe_units(nc, S, pe, n_units, scores, transposes, product, o_slot, beside):
    for u in range(n_units + 1):
        if 1 <= u < n_units - 1:
            scores(u + 1).then_inc(S.s_full, 1)
        if u >= 1:
            pe.wait_ge(S.pt_ready, 2)
            pe.sem_inc(S.pt_ready, -2)
            pe.wait_ge(S.o_free[o_slot(u - 1)], 1)
            pe.sem_inc(S.o_free[o_slot(u - 1)], -1)
            product(u - 1).then_inc(S.o_full, 1)
        if u < n_units:
            pe.wait_ge(S.p_ready, 1)
            pe.sem_inc(S.p_ready, -1)
            transposes(u, 0).then_inc(S.t_full, 1)
            transposes(u, 1).then_inc(S.t_full_act, 1)
        if u in beside:
            beside[u]()


def dve_maxima(S, dve, row_max, u):
    dve.wait_ge(S.s_full, 1)
    dve.sem_inc(S.s_full, -1)
    row_max(u).then_inc(S.max_ready, 1)


def dve_units(nc, S, dve, n_units, row_max, evacuate, normalise, beside):
    def norm(u):
        dve.wait_ge(S.o_full, 1)
        dve.sem_inc(S.o_full, -1)
        normalise(u)

    for u in range(n_units):
        if u + 1 < n_units:
            dve_maxima(S, dve, row_max, u + 1)
        if u >= 1:
            norm(u - 1)
        dve.wait_ge(S.t_full, 1)
        dve.sem_inc(S.t_full, -1)
        evacuate(u).then_inc(S.pt_ready, 1)
        if u in beside:
            beside[u]()
    norm(n_units - 1)


def act_exps(S, act, exps, u):
    act.wait_ge(S.max_ready, 1)
    act.sem_inc(S.max_ready, -1)
    exps(u).then_inc(S.p_ready, 1)


def act_units(nc, S, act, n_units, exps, evacuate, beside):
    for u in range(n_units):
        if u >= 1:
            act_exps(S, act, exps, u)
        act.wait_ge(S.t_full_act, 1)
        act.sem_inc(S.t_full_act, -1)
        evacuate(u).then_inc(S.pt_ready, 1)
        if u in beside:
            beside[u]()



def attention16(nc, S, k, scale, mask=None, cross=False, out=True, geometry=False):
    W, TB = S.arena[k % 2], PACK[k]
    units = [(qt, g) for qt in range(TT) for g in range(H // HU)]
    NU = len(units)
    key_tiles = 1 if cross else TT
    kn = CTX if cross else P

    def key_range(qt):
        if cross:
            return [0]
        if mask == "block":
            return [qt]
        return list(range(qt + 1)) if mask == "causal" else list(range(TT))

    def o_slot(u):
        return (1 + u) % 2

    with ExitStack() as ctx:
        def sb(name, shape, dt=F32):
            return ctx.enter_context(nc.sbuf_tensor(f"{name}_{k}", shape, dt))

        q_t = sb("q_t", [P, C, T])
        k_own = sb("k_own", [P, C, HT, key_tiles * kn])
        v = sb("v", [P, key_tiles, H, VA16])
        prob = sb("prob", [P, 2, HU * T])
        prob_t = sb("prob_t", [P, 2, 2, TT, HU // 2, P])
        neg_max = sb("neg_max", [P, 2, 4])
        rec = sb("rec", [P, 2, 4])
        attn = sb("attn", [P, TT, D])
        attn_t = sb("attn_t", [P, TT, C, P])
        cc = sb("cc", [P, C, CTX]) if cross else None
        bk_own = None if geometry else sb("bk_own", [P, HT])
        if geometry:
            lines = sb("lines", [P, TT, 2, 2, 192])
            prods = sb("prods", [P, TT, 2, 2, 96])
            line = sb("line", [P, TT, 2, H, 6])
            norm2 = sb("norm2", [P, TT, 2, H])
            line_pad = sb("line_pad", [P, TT, 2, H, LW])
            kv = sb("kv", [P, TT, 2, H, DH16])
            geo = sb("geo", [P, TT, 2, H, DH16])
            inc2 = prob
            lines_own = k_own[:].rearrange("p c h n -> p (c h) n")
            lines_read = sb("lines_read", [P, T])
            decay_w = sb("decay_w", [P, H, T])
            mem = sb("mem", [P, TT, H])
            log_decay = sb("log_decay", [P, H])
        src = cc if cross else S.xc[:, :, 1:1 + T]
        block = ctx.enter_context(nc.Block())

        @block.sync
        def _(sp):
            prefetch(nc, S, sp, k + 1)
            with sp.Fori(0, B) as b:
                sync_x(nc, S, sp, b)
                if cross:
                    sp.dma_start(cc[:], S.ctx_t[:, :, bass.ds(b * CTX, CTX)]).then_inc(S.xc_ready, 16)
            sp.wait_ge(S.xc_free, 1)

        @block.tensor
        def _(pe):
            wq = part(W, TB, "wq", C)
            wo = part(W, TB, "wo", C) if out else None
            causal = S.masks[:, 0, :]
            blocked = S.masks[:, 1, :]
            pe.wait_ge(S.weights_ready[k], 16)

            def transposed(dst, w, x):
                for t in range(C):
                    for c in range(C):
                        last = nc.tensor.matmul(dst[:, t * T:t * T + x.shape[2]], w[:, c, t * P:(t + 1) * P], x[:, c, :],
                                                start=(c == 0), stop=(c == C - 1))
                return last

            def heads_of(u):
                n = len(key_range(units[u][0])) * kn
                m = min(HU, BANK // n)
                return [(slice(t * n, (t + m) * n), t, m) for t in range(0, HU, m)]

            def scores(u):
                qt, g = units[u]
                keys = key_range(qt)
                n = len(keys) * kn
                for at, t, m in heads_of(u):
                    h = g * HU + t
                    last = nc.tensor.matmul(S.R[:, u % 2, at], q_t[:, h // HT, qt * P:(qt + 1) * P],
                                            k_own[:, h // HT, h % HT:h % HT + m, keys[0] * kn:keys[0] * kn + n],
                                            start=True, stop=(mask is None), skip_group_check=True)
                if mask is not None:
                    for at, t, m in heads_of(u):
                        last = nc.tensor.matmul(S.R[:, u % 2, at].rearrange("p (t n) -> p t n", t=m)[:, :, n - P:n], S.ident_b,
                                                (causal if mask == "causal" else blocked).unsqueeze(1).to_broadcast([P, m, P]),
                                                start=False, stop=True, skip_group_check=True)
                return last

            def transposes(u, half):
                qt, g = units[u]
                if u == 0 and half == 0:
                    pe.wait_ge(S.t_free[0], 1)
                    pe.sem_inc(S.t_free[0], -1)
                    pe.wait_ge(S.t_free[1], 1)
                    pe.sem_inc(S.t_free[1], -1)
                if u >= NU - 2 and half == 0:
                    pe.sem_inc(S.r_free[u % 2], 1)
                n = len(key_range(qt)) * kn
                for i in range(len(key_range(qt))):
                    for t in range(2 * half, 2 * half + 2):
                        last = nc.tensor.transpose(S.T[0:kn, half, (2 * i + t % 2) * P:(2 * i + t % 2 + 1) * P],
                                                   prob[:, u % 2, t * n + i * kn:t * n + (i + 1) * kn], S.ident)
                return last

            def product(u):
                qt, g = units[u]
                keys = key_range(qt)
                if u == NU - 1:
                    pe.sem_inc(S.t_free[0], 1)
                    pe.sem_inc(S.t_free[1], 1)
                for t in range(4):
                    for i, key in enumerate(keys):
                        last = nc.tensor.matmul(S.O[:, o_slot(u), t * VA16:(t + 1) * VA16],
                                                prob_t[0:kn, u % 2, t // 2, i, t % 2, :], v[0:kn, key, g * HU + t, :],
                                                start=(i == 0), stop=(i == len(keys) - 1))
                return last

            def queries():
                pe.wait_ge(S.xc_ready, 32 if cross else 16)
                pe.sem_inc(S.xc_ready, -(32 if cross else 16))
                pe.wait_ge(S.r_free[0], 1)
                pe.sem_inc(S.r_free[0], -1)
                transposed(S.R[:, 0, :], wq, S.xc[:, :, 1:1 + T]).then_inc(S.q_full, 1)

            def keys(t):
                if t == 0:
                    pe.wait_ge(S.r_free[1], 1)
                    pe.sem_inc(S.r_free[1], -1)
                wk = part(W, TB, "wk", C)
                for c in range(C):
                    last = nc.tensor.matmul(S.R[:, 1, t * BANK:t * BANK + key_tiles * kn], wk[:, c, t * P:(t + 1) * P], src[:, c, :],
                                            start=(c == 0), stop=(c == C - 1))
                last.then_inc(S.k_full if t == 0 else S.k_full_act, 1)

            def values():
                pe.wait_ge(S.t_free[0], 1)
                pe.sem_inc(S.t_free[0], -1)
                wv = part(W, TB, "wv", C)
                for i in range(key_tiles):
                    for c in range(C):
                        last = nc.tensor.matmul(S.T[0:kn, 0, i * D:(i + 1) * D], src[:, c, i * kn:(i + 1) * kn],
                                                wv[:, c, :], start=(c == 0), stop=(c == C - 1))
                last.then_inc(S.v_full, 1)

            def coordinates(tt):
                rd, wr1, wr2 = (part(W, TB, name, C) for name in ("read", "write1", "write2"))
                slot = (1 + tt) % 2
                pe.wait_ge(S.r_free[slot], 1)
                pe.sem_inc(S.r_free[slot], -1)
                now = S.xc[:, :, 1 + tt * P:1 + (tt + 1) * P]
                before = S.xc[:, :, tt * P:(tt + 1) * P]
                for x, w, at, n in ((before, wr1, 0, 192), (now, wr2, 192, 192), (now, rd, BANK, 384)):
                    for c in range(C):
                        last = nc.tensor.matmul(S.R[:, slot, at:at + n], x[:, c, :], w[:, c, :],
                                                start=(c == 0), stop=(c == C - 1))
                last.then_inc(S.lines_full, 1)

            def naturals():
                nat = part(W, TB, "nat", C)
                for tt in range(TT):
                    slot = (1 + tt) % 2
                    pe.wait_ge(S.r_free[slot], 1)
                    pe.sem_inc(S.r_free[slot], -1)
                    for at in (0, BANK):
                        for c in range(C):
                            last = nc.tensor.matmul(S.R[:, slot, at:at + BANK], S.xc[:, c, 1 + tt * P:1 + (tt + 1) * P],
                                                    nat[:, c, at:at + BANK], start=(c == 0), stop=(c == C - 1))
                    last.then_inc(S.nat_full, 1)

            def lines_transposed():
                pe.wait_ge(S.line_ready, 1)
                pe.sem_inc(S.line_ready, -1)
                for rw, full in ((0, S.lt_full), (1, S.lr_full)):
                    pe.wait_ge(S.t_free[rw], 1)
                    pe.sem_inc(S.t_free[rw], -1)
                    for tt in range(TT):
                        last = nc.tensor.transpose(S.T[:, rw, tt * P:(tt + 1) * P],
                                                   line_pad[:, tt, rw, :, :].rearrange("p h i -> p (h i)"), S.ident)
                    last.then_inc(full, 1)

            def incidences():
                pe.wait_ge(S.t_free[0], 1)
                pe.sem_inc(S.t_free[0], -1)
                pe.wait_ge(S.t_free[1], 1)
                pe.sem_inc(S.t_free[1], -1)
                pe.sem_inc(S.t_free[0], 1)
                pe.sem_inc(S.t_free[1], 1)
                for u, (qt, g) in enumerate(units):
                    n = (qt + 1) * P
                    pe.wait_ge(S.r_free[(1 + u) % 2], 1)
                    pe.sem_inc(S.r_free[(1 + u) % 2], -1)
                    for at, t, m in heads_of(u):
                        last = nc.tensor.matmul(S.R[:, (1 + u) % 2, at], lines_read[:, qt * P:(qt + 1) * P],
                                                lines_own[:, g * HU + t:g * HU + t + m, 0:n], start=True, stop=True)
                    last.then_inc(S.inc_full, 1)

            def gated_keys_transposed():
                pe.wait_ge(S.k_nat_ready, 1)
                pe.sem_inc(S.k_nat_ready, -1)
                for c in range(C):
                    pe.wait_ge(S.t_free[c], 1)
                    pe.sem_inc(S.t_free[c], -1)
                    for tt in range(TT):
                        last = nc.tensor.transpose(S.T[:, c, tt * P:(tt + 1) * P],
                                                   kv[:, tt, 0, c * HT:(c + 1) * HT, :].rearrange("p h i -> p (h i)"), S.ident)
                    last.then_inc(S.k_full, 1)
                pe.wait_ge(S.t_free[0], 1)
                pe.sem_inc(S.t_free[0], -1)
                pe.wait_ge(S.t_free[1], 1)
                pe.sem_inc(S.t_free[1], -1)
                pe.sem_inc(S.t_free[0], 1)
                pe.sem_inc(S.t_free[1], 1)

            def first_scores():
                pe.wait_ge(S.r_free[0], 1)
                pe.sem_inc(S.r_free[0], -1)
                pe.wait_ge(S.r_free[1], 1)
                pe.sem_inc(S.r_free[1], -1)
                if not geometry:
                    pe.wait_ge(S.k_sb, 1)
                    pe.sem_inc(S.k_sb, -1)
                scores(0).then_inc(S.s_full, 1)
                scores(1).then_inc(S.s_full, 1)

            def output(amid=None):
                pe.wait_ge(S.o_free[1], 1)
                pe.sem_inc(S.o_free[1], -1)
                if not out:
                    if amid:
                        amid()
                    return
                pe.wait_ge(S.o_free[0], 1)
                pe.sem_inc(S.o_free[0], -1)
                for qt in range(TT):
                    for c in range(C):
                        last = nc.tensor.transpose(S.O[:, 1, (qt * C + c) * P:(qt * C + c + 1) * P],
                                                   attn[:, qt, c * P:(c + 1) * P], S.ident)
                last.then_inc(S.at_full, 1)
                if amid:
                    amid()
                pe.wait_ge(S.o_free[1], 1)
                pe.sem_inc(S.o_free[1], -1)
                for qt in range(TT):
                    for c in range(C):
                        last = nc.tensor.matmul(S.O[:, 0, qt * D:(qt + 1) * D], attn_t[:, qt, c, :], wo[:, c, :],
                                                start=(c == 0), stop=(c == C - 1))
                last.then_inc(S.y_full, 1)

            if geometry:
                beside = {NU - 2: queries, NU - 1: lambda: coordinates(0), NU: lambda: (coordinates(1), naturals())}
                queries()
                coordinates(0)
                coordinates(1)
                naturals()
                lines_transposed()
                incidences()
                gated_keys_transposed()
            else:
                beside = {NU - 2: queries, NU - 1: lambda: keys(0), NU: values}
                queries()
                keys(0)
                values()
                keys(1)
            first_scores()
            with pe.Fori(0, B - 1):
                pe_units(nc, S, pe, NU, scores, transposes, product, o_slot, beside)
                output(None if geometry else lambda: keys(1))
                if geometry:
                    lines_transposed()
                    tail_pe(nc, S, pe, 1)
                    incidences()
                    gated_keys_transposed()
                    first_scores()
                else:
                    first_scores()
                    tail_pe(nc, S, pe, 1)
            pe_units(nc, S, pe, NU, scores, transposes, product, o_slot, {})
            output()
            tail_pe(nc, S, pe, 1)

        @block.scalar
        def _(act):
            act.wait_ge(S.weights_ready[k], 16)

            def exps(u):
                n = len(key_range(units[u][0])) * kn
                for t in range(HU):
                    last = nc.scalar.activation(prob[:, u % 2, t * n:(t + 1) * n], S.R[:, u % 2, t * n:(t + 1) * n], ACT.Exp,
                                                bias=neg_max[:, u % 2, t:t + 1])
                return last

            def evacuate(u):
                n = len(key_range(units[u][0]))
                return nc.scalar.activation(prob_t[0:kn, u % 2, 1, 0:n, :, :].rearrange("p i t q -> p (i t q)"),
                                            S.T[0:kn, 1, 0:2 * n * P], ACT.Copy)

            if geometry:
                nc.scalar.activation(log_decay[:], part(W, TB, "decay"), ACT.Exp, scale=-1.0).then_inc(S.setup_act, 1)
                act.wait_ge(S.setup_dve, 1)
                act.sem_inc(S.setup_dve, -1)
                nc.scalar.activation(log_decay[:], log_decay[:], ACT.Ln)
                act.drain()
                for h in range(H):
                    last = nc.scalar.activation(decay_w[:, h, :], part(S.const, CONST, "steps"), ACT.Exp,
                                                scale=log_decay[:, h:h + 1])
                last.then_inc(S.setup_act, 1)

            def coordinates_naturals():
                for tt in range(TT):
                    slot = (1 + tt) % 2
                    act.wait_ge(S.lines_full, 1)
                    act.sem_inc(S.lines_full, -1)
                    nc.scalar.activation(lines[:, tt, :, :, :].rearrange("p w a n -> p w (a n)"),
                                         S.R[:, slot, :].rearrange("p (w n) -> p w n", w=2)[:, :, 0:384], ACT.Copy)\
                        .then_inc(S.r_free[slot], 1)
                    act.drain().then_inc(S.lines_sb, 1)
                for tt in range(TT):
                    slot = (1 + tt) % 2
                    act.wait_ge(S.nat_geo, 1)
                    act.sem_inc(S.nat_geo, -1)
                    nc.scalar.activation(geo[:, tt, :, :, :].rearrange("p a h d -> p (a h d)"),
                                         S.R[:, slot, BANK:2 * BANK], ACT.Copy).then_inc(S.r_free[slot], 1)

            def lines_transposed():
                act.wait_ge(S.lr_full, 1)
                act.sem_inc(S.lr_full, -1)
                nc.scalar.activation(lines_read[:], S.T[:, 1, 0:T], ACT.Copy).then_inc(S.t_free[1], 1)

            def incidences():
                for u, (qt, g) in enumerate(units):
                    n = (qt + 1) * P
                    act.wait_ge(S.inc_full, 1)
                    act.sem_inc(S.inc_full, -1)
                    act.wait_ge(S.inc_free, 1)
                    act.sem_inc(S.inc_free, -1)
                    nc.scalar.activation(inc2[:, u % 2, 0:HU * n], S.R[:, (1 + u) % 2, 0:HU * n], ACT.Square)\
                        .then_inc(S.r_free[(1 + u) % 2], 1)
                    act.drain().then_inc(S.inc_ready, 1)
                act.wait_ge(S.mem_ready, 1)
                act.sem_inc(S.mem_ready, -1)
                nc.scalar.activation(mem[:], mem[:], ACT.Exp, scale=-1.0).then_inc(S.gate_exp, 1)

            def keys():
                act.wait_ge(S.k_full_act, 1)
                act.sem_inc(S.k_full_act, -1)
                act.sem_inc(S.xc_free, 1)
                for h in range(HT):
                    nc.scalar.activation(k_own[:, 1, h, :], S.R[:, 1, BANK:BANK + key_tiles * kn], ACT.Identity,
                                         bias=bk_own[:, h:h + 1], scale=part(S.const, CONST, "head")[:, h:h + 1])
                act.drain().then_inc(S.k_sb, 1)

            def attention_transposed():
                if out:
                    act.wait_ge(S.at_full, 1)
                    act.sem_inc(S.at_full, -1)
                    nc.scalar.activation(attn_t[:].rearrange("p q c t -> p (q c t)"), S.O[:, 1, :], ACT.Copy)\
                        .then_inc(S.o_free[1], 1)

            if geometry:
                coordinates_naturals()
                lines_transposed()
                incidences()
            else:
                act.wait_ge(S.setup_dve, 1)
                act.sem_inc(S.setup_dve, -1)
                keys()
            act_exps(S, act, exps, 0)
            with act.Fori(0, B - 1) as b:
                act_units(nc, S, act, NU, exps, evacuate, {})
                if geometry:
                    coordinates_naturals()
                    attention_transposed()
                    lines_transposed()
                    tail_act(nc, S, act, 1, b)
                    incidences()
                    act_exps(S, act, exps, 0)
                else:
                    attention_transposed()
                    keys()
                    act_exps(S, act, exps, 0)
                    tail_act(nc, S, act, 1, b)
            act_units(nc, S, act, NU, exps, evacuate, {})
            attention_transposed()
            tail_act(nc, S, act, 1, B - 1)
            if geometry:
                act.wait_ge(S.inc_free, 2)
                act.sem_inc(S.inc_free, -2)

        @block.vector
        def _(dve):
            dve.wait_ge(S.weights_ready[k], 16)
            bq = part(W, TB, "bq")
            nc.vector.memset(v[:, :, :, DH16:VA16], 1.0)

            def row_max(u):
                n = len(key_range(units[u][0])) * kn
                return nc.vector.tensor_reduce(neg_max[:, u % 2, :],
                                               S.R[:, u % 2, 0:HU * n].rearrange("p (t n) -> p t n", t=HU),
                                               AX.X, ALU.max, negate=True)

            def evacuate(u):
                n = len(key_range(units[u][0]))
                return nc.vector.tensor_copy(prob_t[0:kn, u % 2, 0, 0:n, :, :].rearrange("p i t q -> p (i t q)"), S.T[0:kn, 0, 0:2 * n * P])

            def normalise(u):
                qt, g = units[u]
                o = S.O[:, o_slot(u), 0:4 * VA16].rearrange("p (t d) -> p t d", t=4)
                nc.vector.reciprocal(rec[:, u % 2, :], o[:, :, DH16])
                dve.drain()
                nc.vector.tensor_tensor(attn[:, qt, g * HU * DH16:(g + 1) * HU * DH16].rearrange("p (t d) -> p t d", t=HU),
                                        o[:, :, 0:DH16], rec[:, u % 2, :].unsqueeze(2).to_broadcast([P, 4, DH16]), ALU.mult)\
                    .then_inc(S.o_free[o_slot(u)], 1)

            if geometry:
                nc.vector.memset(line_pad[:], 0.0)
                
                dve.wait_ge(S.setup_act, 1)
                dve.sem_inc(S.setup_act, -1)
                nc.vector.tensor_scalar(log_decay[:], log_decay[:], 1.0, None, ALU.add)
                dve.drain()
                nc.vector.reciprocal(log_decay[:], log_decay[:])
                dve.drain()
                nc.vector.tensor_scalar(log_decay[:], log_decay[:], 2.0 ** -63, None, ALU.max).then_inc(S.setup_dve, 1)
                dve.wait_ge(S.setup_act, 1)
                dve.sem_inc(S.setup_act, -1)
                nc.vector.tensor_tensor(decay_w[:], decay_w[:],
                                        part(S.const, CONST, "past").unsqueeze(1).to_broadcast([P, H, T]), ALU.mult)
            dve.drain()

            def queries():
                dve.wait_ge(S.q_full, 1)
                dve.sem_inc(S.q_full, -1)
                for t in range(C):
                    last = nc.vector.tensor_scalar(q_t[:, t, :], S.R[:, 0, t * T:(t + 1) * T], bq[:, t:t + 1], scale,
                                                   ALU.add, ALU.mult)
                last.then_inc(S.r_free[0], 1)

            own = part(S.const, CONST, "head").unsqueeze(2).to_broadcast([P, HT, key_tiles * kn])

            def keys():
                dve.wait_ge(S.k_full, 1)
                dve.sem_inc(S.k_full, -1)
                nc.vector.scalar_tensor_tensor(
                    k_own[:, 0, :, :], S.R[:, 1, 0:key_tiles * kn].unsqueeze(1).to_broadcast([P, HT, key_tiles * kn]),
                    part(W, TB, "bk")[:, 0:1], own, ALU.add, ALU.mult).then_inc(S.r_free[1], 1)

            def gated_keys():
                for c in range(C):
                    dve.wait_ge(S.k_full, 1)
                    dve.sem_inc(S.k_full, -1)
                    nc.vector.tensor_tensor(k_own[:, c, :, :], S.T[:, c, 0:T].unsqueeze(1).to_broadcast([P, HT, T]), own, ALU.mult)\
                        .then_inc(S.t_free[c], 1)

            def values():
                dve.wait_ge(S.v_full, 1)
                dve.sem_inc(S.v_full, -1)
                bv = part(W, TB, "bv").rearrange("p (h d) -> p h d", h=H)
                for i in range(key_tiles):
                    last = nc.vector.tensor_tensor(v[0:kn, i, :, 0:DH16],
                                                   S.T[0:kn, 0, i * D:(i + 1) * D].rearrange("p (h d) -> p h d", h=H),
                                                   bv[0:kn], ALU.add)
                last.then_inc(S.t_free[0], 1)

            def naturals():
                for tt in range(TT):
                    slot = (1 + tt) % 2
                    dve.wait_ge(S.nat_full, 1)
                    dve.sem_inc(S.nat_full, -1)
                    nc.vector.tensor_tensor(kv[:, tt, :, :, :].rearrange("p a h d -> p (a h d)"), S.R[:, slot, 0:BANK],
                                            part(W, TB, "nat_b"), ALU.add).then_inc(S.nat_geo, 1)
                dve.sem_inc(S.xc_free, 1)
                dve.wait_ge(S.lines_sb, 2)
                dve.sem_inc(S.lines_sb, -2)
                for tt in range(TT):
                    nc.vector.tensor_tensor(prods[:, tt, :, :, :].rearrange("p w a n -> p w (a n)"),
                                            lines[:, tt, :, 0, :], lines[:, tt, :, 1, :], ALU.mult)
                dve.drain()
                flat = line[:].rearrange("p t w h i -> p (t w) (h i)")
                both = prods[:].rearrange("p t w a n -> p (t w) a n")
                nc.vector.tensor_tensor(flat, both[:, :, 0, :], both[:, :, 1, :], ALU.subtract)
                dve.drain()
                nc.vector.tensor_tensor(both[:, :, 0, :], flat, flat, ALU.mult)
                dve.drain()
                nc.vector.tensor_reduce(norm2[:].rearrange("p t w h -> p (t w) h"),
                                        both[:, :, 0, :].rearrange("p a (h i) -> p a h i", i=6), AX.X, ALU.add)\
                    .then_inc(S.norm_sum, 1)

            def unit_lines():
                dve.wait_ge(S.norm_root, 1)
                dve.sem_inc(S.norm_root, -1)
                nc.vector.tensor_scalar(norm2[:], norm2[:], 1e-12, None, ALU.max)
                dve.drain()
                nc.vector.reciprocal(norm2[:], norm2[:])
                dve.drain()
                for tt in range(TT):
                    for rw in range(2):
                        last = nc.vector.tensor_tensor(line_pad[:, tt, rw, :, 0:6], line[:, tt, rw, :, :],
                                                       norm2[:, tt, rw, :].unsqueeze(2).to_broadcast([P, H, 6]), ALU.mult)
                last.then_inc(S.line_ready, 1)

            def gates():
                dve.wait_ge(S.lt_full, 1)
                dve.sem_inc(S.lt_full, -1)
                nc.vector.tensor_tensor(lines_own, S.T[:, 0, 0:T].unsqueeze(1).to_broadcast([P, H, T]),
                                        part(S.const, CONST, "line_head").unsqueeze(2).to_broadcast([P, H, T]), ALU.mult)\
                    .then_inc(S.t_free[0], 1)
                for u, (qt, g) in enumerate(units):
                    n = (qt + 1) * P
                    dve.wait_ge(S.inc_ready, 1)
                    dve.sem_inc(S.inc_ready, -1)
                    for t in range(HU):
                        h = g * HU + t
                        last = nc.vector.tensor_tensor_reduce(
                            inc2[:, u % 2, t * n:(t + 1) * n], inc2[:, u % 2, t * n:(t + 1) * n], decay_w[:, h, T - n:T], 1.0, 0.0,
                            ALU.mult, ALU.add, mem[:, qt, h:h + 1])
                    last.then_inc(S.inc_free, 1)
                dve.drain()
                nc.vector.tensor_tensor(mem[:], mem[:],
                                        part(W, TB, "mem_scale").unsqueeze(1).to_broadcast([P, TT, H]), ALU.mult)\
                    .then_inc(S.mem_ready, 1)
                dve.wait_ge(S.gate_exp, 1)
                dve.sem_inc(S.gate_exp, -1)
                nc.vector.tensor_scalar(mem[:], mem[:], 1.0, None, ALU.add)
                dve.drain()
                nc.vector.reciprocal(mem[:], mem[:])
                dve.drain()
                nc.vector.tensor_scalar(mem[:], mem[:], part(W, TB, "kv_gate"), None, ALU.mult)
                dve.drain()
                for a in range(2):
                    for tt in range(TT):
                        gate = mem[:, tt, :].unsqueeze(2).to_broadcast([P, H, DH16])
                        nc.vector.tensor_tensor(geo[:, tt, a, :, :], geo[:, tt, a, :, :], gate, ALU.mult)
                dve.drain()
                for tt in range(TT):
                    nc.vector.tensor_tensor(v[:, tt, :, 0:DH16], kv[:, tt, 1, :, :], geo[:, tt, 1, :, :], ALU.add)
                for tt in range(TT):
                    last = nc.vector.tensor_tensor(kv[:, tt, 0, :, :], kv[:, tt, 0, :, :], geo[:, tt, 0, :, :], ALU.add)
                last.then_inc(S.k_nat_ready, 1)

            def output(meanwhile=None):
                if out:
                    dve_output(nc, S, dve, 0, meanwhile)
                else:
                    dve.drain()
                    dve.wait_ge(S.xres_ready, 1)
                    dve.sem_inc(S.xres_ready, -1)
                    nc.vector.tensor_tensor(S.ysb[:], attn[:], S.xres[:], ALU.add)
                    dve.drain().then_inc(S.xres_free, 1)
                    tail_dve(nc, S, dve, meanwhile)

            def first_maxima():
                dve_maxima(S, dve, row_max, 0)

            queries()
            if geometry:
                naturals()
                unit_lines()
                gates()
                gated_keys()
            else:
                nc.vector.tensor_scalar(bk_own[:], part(S.const, CONST, "head"), part(W, TB, "bk")[:, 1:2], None, ALU.mult)\
                    .then_inc(S.setup_dve, 1)
                keys()
                values()
            first_maxima()
            with dve.Fori(0, B - 1):
                dve_units(nc, S, dve, NU, row_max, evacuate, normalise, {NU - 2: queries})
                if geometry:
                    naturals()
                    output(unit_lines)
                    gates()
                    gated_keys()
                    first_maxima()
                else:
                    values()
                    keys()
                    output(first_maxima)
            dve_units(nc, S, dve, NU, row_max, evacuate, normalise, {})
            output()

        @block.gpsimd
        def _(pool):
            pool.wait_ge(S.weights_ready[k], 16)

            def roots():
                if geometry:
                    pool.wait_ge(S.norm_sum, 1)
                    pool.sem_inc(S.norm_sum, -1)
                    flat = norm2[:].rearrange("p t w h -> p (t w h)")
                    nc.gpsimd.tensor_tensor(flat, flat, part(S.const, CONST, "half"), ALU.pow).then_inc(S.norm_root, 1)

            bias = part(W, TB, "bo") if out else None
            if geometry:
                pool.sem_inc(S.inc_free, 2)
            roots()
            pool_residual(nc, S, pool, 0, bias)
            with pool.Fori(0, B - 1) as b:
                roots()
                tail_pool(nc, S, pool, b)
                pool_residual(nc, S, pool, b + 1, bias)
            tail_pool(nc, S, pool, B - 1)



def perceiver(nc, S, k):
    W, TB = S.arena[k % 2], PACK[k]
    HP = H // 2
    units = [(qt, hp) for qt in range(TT) for hp in range(HP)]
    NU = len(units)
    LATENTS = 4
    KC = [(0, P, CTX), (1, P, CTX + P), (2, CTX, 0)]
    LC = [(t, min(P, B * CTX - t * P)) for t in range(-(-B * CTX // P))]

    def o_slot(u):
        return u % 2

    with ExitStack() as ctx:
        def sb(name, shape, dt=F32):
            return ctx.enter_context(nc.sbuf_tensor(f"{name}_{k}", shape, dt))

        ctx_n = sb("ctx_n", [P, len(LC), D])
        ctx_nt = sb("ctx_nt", [P, C, B * CTX])
        cst = sb("cst", [P, len(LC), 6])
        cmv = sb("cmv", [P, len(LC), 2])
        crs = sb("crs", [P, len(LC)])
        lat = sb("lat", [P, TT, D])
        keys_in = sb("keys_in", [P, C, XK])
        q_t = sb("q_t", [P, HP, T])
        k_t = sb("k_t", [P, HP, XK])
        v = sb("v", [P, 3, H, VA64])
        prob = sb("prob", [P, 2, 2, XK])
        prob_t = sb("prob_t", [P, 2, 2, 3, P])
        neg_max = sb("neg_max", [P, 2, 2])
        rec = sb("rec", [P, 2, 2])
        attn = sb("attn", [P, TT, XI])
        attn_t = sb("attn_t", [P, XI // P, T])
        block = ctx.enter_context(nc.Block())

        @block.sync
        def _(sp):
            prefetch(nc, S, sp, k + 1)
            for t, n in LC:
                sp.dma_start(ctx_n[0:n, t, :], S.ctx_dram[t * P:t * P + n, :]).then_inc(S.ctx_ready, 16)
            with sp.Fori(0, B) as b:
                sp.wait_ge(S.ctx_nt_ready, 1)
                sp.sem_inc(S.ctx_nt_ready, -1)
                sp.dma_start(keys_in[:, :, 0:CTX], ctx_nt[:, :, bass.ds(b * CTX, CTX)]).then_inc(S.xc_ready, 16)
            sp.wait_ge(S.ctx_nt_ready, 1)
            sp.sem_inc(S.ctx_nt_ready, -1)

        @block.tensor
        def _(pe):
            wq, wkv, wo = part(W, TB, "wq", C), part(W, TB, "wkv", C), part(W, TB, "wo", XI // P)
            pe.wait_ge(S.weights_ready[k], 16)
            pe.wait_ge(S.ctx_norm_ready, 1)
            pe.sem_inc(S.ctx_norm_ready, -1)
            for t, n in LC:
                pe.wait_ge(S.o_free[t % 2], 1)
                pe.sem_inc(S.o_free[t % 2], -1)
                for c in range(C):
                    last = nc.tensor.transpose(S.O[:, t % 2, c * P:c * P + n], ctx_n[0:n, t, c * P:(c + 1) * P], S.ident[0:n, 0:n])
                last.then_inc(S.yt_full, 1)

            def scores(u):
                qt, hp = units[u]
                for i in range(2):
                    last = nc.tensor.matmul(S.R[:, u % 2, i * BANK:i * BANK + XK],
                                            q_t[XD * i:XD * (i + 1), hp, qt * P:(qt + 1) * P],
                                            k_t[XD * i:XD * (i + 1), hp, :], start=True, stop=True)
                return last

            def transposes(u, i):
                if u == 0 and i == 0:
                    pe.wait_ge(S.t_free[0], 1)
                    pe.sem_inc(S.t_free[0], -1)
                    pe.wait_ge(S.t_free[1], 1)
                    pe.sem_inc(S.t_free[1], -1)
                if u >= NU - 2 and i == 0:
                    pe.sem_inc(S.r_free[u % 2], 1)
                for c, n, first in KC:
                    last = nc.tensor.transpose(S.T[0:n, i, c * P:(c + 1) * P], prob[:, u % 2, i, first:first + n], S.ident)
                return last

            def product(u):
                qt, hp = units[u]
                if u == NU - 1:
                    pe.sem_inc(S.t_free[0], 1)
                    pe.sem_inc(S.t_free[1], 1)
                for i in range(2):
                    for c, n, first in KC:
                        last = nc.tensor.matmul(S.O[:, o_slot(u), i * VA64:(i + 1) * VA64], prob_t[0:n, u % 2, i, c, :],
                                                v[0:n, c, 2 * hp + i, :], start=(c == 0), stop=(c == len(KC) - 1))
                return last

            def latents():
                pe.wait_ge(S.lat_ready, 1)
                pe.sem_inc(S.lat_ready, -1)
                for tt in range(TT):
                    pe.wait_ge(S.o_free[tt], 1)
                    pe.sem_inc(S.o_free[tt], -1)
                    for c in range(C):
                        last = nc.tensor.transpose(S.O[:, tt, c * P:(c + 1) * P], lat[:, tt, c * P:(c + 1) * P], S.ident)
                    last.then_inc(S.lt_full, 1)

            def queries(j):
                if j == 0:
                    pe.wait_ge(S.lat_t_ready, 1)
                    pe.sem_inc(S.lat_t_ready, -1)
                pe.wait_ge(S.r_free[j], 1)
                pe.sem_inc(S.r_free[j], -1)
                for i in range(4):
                    for c in range(C):
                        last = nc.tensor.matmul(S.R[:, j, i * T:(i + 1) * T], wq[:, c, (4 * j + i) * P:(4 * j + i + 1) * P],
                                                keys_in[:, c, CTX:XK], start=(c == 0), stop=(c == C - 1))
                last.then_inc(S.q_full, 1)

            def keys(first):
                if first == 0:
                    pe.wait_ge(S.xc_ready, 16)
                    pe.sem_inc(S.xc_ready, -16)
                for j in range(first, first + 2):
                    pe.wait_ge(S.r_free[j % 2], 1)
                    pe.sem_inc(S.r_free[j % 2], -1)
                    for i in range(2):
                        for c in range(C):
                            last = nc.tensor.matmul(S.R[:, j % 2, i * BANK:i * BANK + XK], wkv[:, c, (2 * j + i) * P:(2 * j + i + 1) * P],
                                                    keys_in[:, c, :], start=(c == 0), stop=(c == C - 1))
                    last.then_inc(S.k_full, 1)

            def values():
                for kc, n, first in KC:
                    pe.wait_ge(S.r_free[kc % 2], 1)
                    pe.sem_inc(S.r_free[kc % 2], -1)
                    for hv in range(2):
                        for c in range(C):
                            last = nc.tensor.matmul(S.R[0:n, kc % 2, hv * BANK:(hv + 1) * BANK], keys_in[:, c, first:first + n],
                                                    wkv[:, c, XI + hv * BANK:XI + (hv + 1) * BANK], start=(c == 0), stop=(c == C - 1))
                    last.then_inc(S.v_full, 1)

            def attention_transposed():
                pe.wait_ge(S.o_free[0], 1)
                pe.sem_inc(S.o_free[0], -1)
                pe.wait_ge(S.o_free[1], 1)
                pe.sem_inc(S.o_free[1], -1)
                for j in range(4):
                    pe.wait_ge(S.t_free[j % 2], 1)
                    pe.sem_inc(S.t_free[j % 2], -1)
                    for c in range(2):
                        for qt in range(TT):
                            last = nc.tensor.transpose(S.T[:, j % 2, (c * TT + qt) * P:(c * TT + qt + 1) * P],
                                                       attn[:, qt, (2 * j + c) * P:(2 * j + c + 1) * P], S.ident)
                    last.then_inc(S.at_full, 1)

            def output():
                pe.wait_ge(S.t_free[0], 1)
                pe.sem_inc(S.t_free[0], -1)
                pe.wait_ge(S.t_free[1], 1)
                pe.sem_inc(S.t_free[1], -1)
                pe.sem_inc(S.t_free[0], 1)
                pe.sem_inc(S.t_free[1], 1)
                for qt in range(TT):
                    for c in range(XI // P):
                        last = nc.tensor.matmul(S.O[:, 0, qt * D:(qt + 1) * D], attn_t[:, c, qt * P:(qt + 1) * P], wo[:, c, :],
                                                start=(c == 0), stop=(c == XI // P - 1))
                last.then_inc(S.y_full, 1)

            def first_scores():
                pe.wait_ge(S.r_free[0], 1)
                pe.sem_inc(S.r_free[0], -1)
                pe.wait_ge(S.r_free[1], 1)
                pe.sem_inc(S.r_free[1], -1)
                pe.wait_ge(S.k_sb, 1)
                pe.sem_inc(S.k_sb, -1)
                scores(0).then_inc(S.s_full, 1)
                scores(1).then_inc(S.s_full, 1)

            beside = {LATENTS + 2: latents, NU - 2: lambda: queries(0), NU - 1: lambda: queries(1), NU: lambda: keys(0)}
            latents()
            queries(0)
            queries(1)
            keys(0)
            keys(2)
            values()
            first_scores()
            with pe.Fori(0, B - 1):
                pe_units(nc, S, pe, NU, scores, transposes, product, o_slot, beside)
                attention_transposed()
                keys(2)
                output()
                values()
                first_scores()
                tail_pe(nc, S, pe, 1)
            pe_units(nc, S, pe, NU, scores, transposes, product, o_slot, {})
            attention_transposed()
            output()
            tail_pe(nc, S, pe, 1)

        @block.scalar
        def _(act):
            act.wait_ge(S.weights_ready[k], 16)
            for t, n in LC:
                act.wait_ge(S.yt_full, 1)
                act.sem_inc(S.yt_full, -1)
                last = nc.scalar.activation(ctx_nt[:, :, t * P:t * P + n],
                                            S.O[:, t % 2, 0:2 * P].rearrange("p (c t) -> p c t", c=C)[:, :, 0:n], ACT.Copy)
                last.then_inc(S.o_free[t % 2], 1)
            act.drain().then_inc(S.ctx_nt_ready, 1)

            def exps(u):
                for i in range(2):
                    last = nc.scalar.activation(prob[:, u % 2, i, :], S.R[:, u % 2, i * BANK:i * BANK + XK], ACT.Exp,
                                                bias=neg_max[:, u % 2, i:i + 1])
                return last

            def evacuate(u):
                nc.scalar.activation(prob_t[:, u % 2, 1, 0:2, :].rearrange("p c q -> p (c q)"), S.T[:, 1, 0:2 * P], ACT.Copy)
                return nc.scalar.activation(prob_t[0:CTX, u % 2, 1, 2, :], S.T[0:CTX, 1, 2 * P:3 * P], ACT.Copy)

            def latents():
                for tt in range(TT):
                    act.wait_ge(S.lt_full, 1)
                    act.sem_inc(S.lt_full, -1)
                    nc.scalar.activation(keys_in[:, :, CTX + tt * P:CTX + (tt + 1) * P],
                                         S.O[:, tt, 0:2 * P].rearrange("p (c t) -> p c t", c=C), ACT.Copy)\
                        .then_inc(S.o_free[tt], 1)
                act.drain().then_inc(S.lat_t_ready, 1)

            def keys(first):
                for j in range(first, first + 2):
                    act.wait_ge(S.k_full, 1)
                    act.sem_inc(S.k_full, -1)
                    nc.scalar.activation(k_t[:, 2 * j:2 * j + 2, :],
                                         S.R[:, j % 2, :].rearrange("p (i n) -> p i n", i=2)[:, :, 0:XK], ACT.Copy)\
                        .then_inc(S.r_free[j % 2], 1)
                if first:
                    act.drain().then_inc(S.k_sb, 1)

            def attention_transposed():
                for j in range(4):
                    act.wait_ge(S.at_full, 1)
                    act.sem_inc(S.at_full, -1)
                    nc.scalar.activation(attn_t[:, 2 * j:2 * j + 2, :], S.T[:, j % 2, :].rearrange("p (c t) -> p c t", c=2),
                                         ACT.Copy).then_inc(S.t_free[j % 2], 1)

            latents()
            keys(0)
            keys(2)
            act_exps(S, act, exps, 0)
            with act.Fori(0, B - 1) as b:
                act_units(nc, S, act, NU, exps, evacuate, {LATENTS + 2: latents})
                keys(0)
                attention_transposed()
                keys(2)
                act_exps(S, act, exps, 0)
                tail_act(nc, S, act, 1, b)
            act_units(nc, S, act, NU, exps, evacuate, {})
            attention_transposed()
            tail_act(nc, S, act, 1, B - 1)

        @block.vector
        def _(dve):
            dve.wait_ge(S.weights_ready[k], 16)
            nc.vector.memset(v[:, :, :, XD:VA64], 1.0)
            dve.wait_ge(S.ctx_ready, 16 * len(LC))
            dve.sem_inc(S.ctx_ready, -(16 * len(LC)))
            for t, n in LC:
                nc.vector.bn_stats(cst[0:n, t, :], ctx_n[0:n, t, :])
            nc.vector.memset(cmv[:], 1.0)
            dve.drain()
            for t, n in LC:
                last = nc.vector.bn_aggr(cmv[0:n, t, :], cst[0:n, t, :])
            last.then_inc(S.ctx_stat, 1)
            dve.wait_ge(S.ctx_rstd, 1)
            dve.sem_inc(S.ctx_rstd, -1)
            for t, n in LC:
                nc.vector.tensor_scalar(ctx_n[0:n, t, :], ctx_n[0:n, t, :], cmv[0:n, t, 0:1], crs[0:n, t:t + 1],
                                        ALU.subtract, ALU.mult)
            for op, name in ((ALU.mult, "ctx_w"), (ALU.add, "ctx_b")):
                dve.drain()
                for t, n in LC:
                    last = nc.vector.tensor_tensor(ctx_n[0:n, t, :], ctx_n[0:n, t, :], part(W, TB, name)[0:n, :], op)
            last.then_inc(S.ctx_norm_ready, 1)

            def row_max(u):
                return nc.vector.tensor_reduce(neg_max[:, u % 2, :],
                                               S.R[:, u % 2, :].rearrange("p (i n) -> p i n", i=2)[:, :, 0:XK],
                                               AX.X, ALU.max, negate=True)

            def evacuate(u):
                nc.vector.tensor_copy(prob_t[:, u % 2, 0, 0:2, :].rearrange("p c q -> p (c q)"), S.T[:, 0, 0:2 * P])
                return nc.vector.tensor_copy(prob_t[0:CTX, u % 2, 0, 2, :], S.T[0:CTX, 0, 2 * P:3 * P])

            def normalise(u):
                qt, hp = units[u]
                o = S.O[:, o_slot(u), 0:2 * VA64].rearrange("p (i d) -> p i d", i=2)
                nc.vector.reciprocal(rec[:, u % 2, :], o[:, :, XD])
                dve.drain()
                nc.vector.tensor_tensor(attn[:, qt, hp * P:(hp + 1) * P].rearrange("p (i d) -> p i d", i=2),
                                        o[:, :, 0:XD], rec[:, u % 2, :].unsqueeze(2).to_broadcast([P, 2, XD]), ALU.mult)\
                    .then_inc(S.o_free[o_slot(u)], 1)

            def x_of(b):
                return S.x_nat[:, bass.ds(b * TT, TT), :]

            def latent_statistics(b):
                for tt in range(TT):
                    nc.vector.bn_stats(S.bst[:, tt, :], S.x_nat[:, bass.ds(b * TT + tt, 1), :].rearrange("p a d -> p (a d)"))
                dve.drain()
                for tt in range(TT):
                    last = nc.vector.bn_aggr(S.mv[:, tt, :], S.bst[:, tt, :])
                last.then_inc(S.ln_stat, 1)

            def latents(b):
                dve.wait_ge(S.ln_rstd, 1)
                dve.sem_inc(S.ln_rstd, -1)
                for tt in range(TT):
                    last = nc.vector.tensor_scalar(lat[:, tt, :], S.x_nat[:, bass.ds(b * TT + tt, 1), :].rearrange("p a d -> p (a d)"),
                                                   S.mv[:, tt, 0:1], S.rstd[:, tt:tt + 1], ALU.subtract, ALU.mult)
                for op, name in ((ALU.mult, "lat_w"), (ALU.add, "lat_b")):
                    dve.drain()
                    last = nc.vector.tensor_tensor(lat[:], lat[:], part(W, TB, name).unsqueeze(1).to_broadcast([P, TT, D]), op)
                last.then_inc(S.lat_ready, 1)

            def queries(j):
                dve.wait_ge(S.q_full, 1)
                dve.sem_inc(S.q_full, -1)
                nc.vector.tensor_scalar(q_t[:, 4 * j:4 * j + 4, :].rearrange("p i t -> p (i t)"), S.R[:, j, :],
                                        XD ** -0.5, None, ALU.mult).then_inc(S.r_free[j], 1)

            def values():
                for kc, n, first in KC:
                    dve.wait_ge(S.v_full, 1)
                    dve.sem_inc(S.v_full, -1)
                    nc.vector.tensor_copy(v[0:n, kc, :, 0:XD], S.R[0:n, kc % 2, :].rearrange("p (h d) -> p h d", h=H))\
                        .then_inc(S.r_free[kc % 2], 1)
                dve.sem_inc(S.ctx_nt_ready, 1)

            def output(b, meanwhile=None):
                dve.wait_ge(S.y_full, 1)
                dve.sem_inc(S.y_full, -1)
                nc.vector.tensor_tensor(S.ysb[:], S.O[:, 0, :].rearrange("p (t d) -> p t d", t=TT), x_of(b), ALU.add)\
                    .then_inc(S.o_free[0], 1)
                dve.drain()
                tail_dve(nc, S, dve, meanwhile)

            latent_statistics(0)
            latents(0)
            queries(0)
            queries(1)
            values()
            dve_maxima(S, dve, row_max, 0)
            with dve.Fori(0, B - 1) as b:
                dve_units(nc, S, dve, NU, row_max, evacuate, normalise,
                          {LATENTS: lambda: latent_statistics(b + 1), LATENTS + 1: lambda: latents(b + 1),
                           NU - 2: lambda: queries(0), NU - 1: lambda: queries(1)})
                output(b, values)
                dve_maxima(S, dve, row_max, 0)
            dve_units(nc, S, dve, NU, row_max, evacuate, normalise, {})
            output(B - 1)

        @block.gpsimd
        def _(pool):
            pool.wait_ge(S.weights_ready[k], 16)
            pool.wait_ge(S.ctx_stat, 1)
            pool.sem_inc(S.ctx_stat, -1)
            nc.gpsimd.tensor_scalar(crs[:], cmv[:, :, 1], EPS, None, ALU.add)
            pool.drain()
            nc.gpsimd.tensor_tensor(crs[:], crs[:], part(S.const, CONST, "neg_half")[:, 0:len(LC)], ALU.pow).then_inc(S.ctx_rstd, 1)
            pool_rstd(nc, S, pool)
            with pool.Fori(0, B - 1) as b:
                pool_rstd(nc, S, pool)
                tail_pool(nc, S, pool, b)
            tail_pool(nc, S, pool, B - 1)



def dve_top(nc, S, dve, gate, prob, top, index, index_f, pick, n, experts):
    for tt in range(TT):
        nc.vector.max(top[:, tt, :], prob[:, tt, :])
    dve.drain()
    for tt in range(TT):
        nc.vector.max_index(index[:, tt, :], top[:, tt, :], prob[:, tt, :])
    dve.drain()
    nc.vector.tensor_copy(index_f[:], index[:])
    dve.drain()
    iota = part(S.const, CONST, "iota")[:, 0:experts]
    for tt in range(TT):
        for j in range(n):
            nc.vector.scalar_tensor_tensor(pick[:, tt, j, :], iota, index_f[:, tt, j:j + 1], prob[:, tt, :], ALU.is_equal, ALU.mult)
    dve.drain()
    nc.vector.tensor_reduce(gate[:], pick[:].rearrange("p t j e -> p t e j"), AX.X, ALU.add)
    dve.drain()


def moe_silu(nc, S, k):
    W, TB = S.arena[k % 2], PACK[k]
    E, FC = 8, 2
    with ExitStack() as ctx:
        def sb(name, shape, dt=F32):
            return ctx.enter_context(nc.sbuf_tensor(f"{name}_{k}", shape, dt))

        prob = sb("prob", [P, TT, E])
        logit = sb("logit", [P, TT, E + 1])
        nmax = sb("nmax", [P, TT])
        total = sb("total", [P, TT])
        shared_gate = sb("shared_gate", [P, TT])
        top = sb("top", [P, TT, 8])
        index = sb("index", [P, TT, 8], U32)
        index_f = sb("index_f", [P, TT, 8])
        pick = sb("pick", [P, TT, 2, E])
        gate = sb("gate", [P, TT, E])
        hid = sb("hid", [P, 2, FC * T])
        sg = sb("sg", [P, FC * T])
        block = ctx.enter_context(nc.Block())

        @block.sync
        def _(sp):
            prefetch(nc, S, sp, k + 1)
            with sp.Fori(0, B) as b:
                sync_x(nc, S, sp, b)
            sp.wait_ge(S.xc_free, 1)

        @block.tensor
        def _(pe):
            w1 = part(W, TB, "w1", E * C)
            w2 = part(W, TB, "w2", E * FC)
            gu, down, router = part(W, TB, "gate_up", C), part(W, TB, "down", FC), part(W, TB, "router", C)
            x = S.xc[:, :, 1:1 + T]
            pe.wait_ge(S.weights_ready[k], 16)

            def hidden(w, slot, full):
                for f in range(FC):
                    for c in range(C):
                        last = nc.tensor.matmul(S.R[:, slot, f * T:(f + 1) * T], w(c)[:, f * P:(f + 1) * P], x[:, c, :],
                                                start=(c == 0), stop=(c == C - 1))
                last.then_inc(full, 1)

            def outputs(src, w, slot):
                for tt in range(TT):
                    for f in range(FC):
                        last = nc.tensor.matmul(S.O[:, slot, tt * D:(tt + 1) * D], src[:, f * T + tt * P:f * T + (tt + 1) * P],
                                                w(f), start=(f == 0), stop=(f == FC - 1))
                last.then_inc(S.o_full, 1)

            with pe.Fori(0, B) as b:
                pe.wait_ge(S.xc_ready, 16)
                pe.sem_inc(S.xc_ready, -16)
                pe.wait_ge(S.o_free[0], 1)
                pe.sem_inc(S.o_free[0], -1)
                for tt in range(TT):
                    for c in range(C):
                        last = nc.tensor.matmul(S.O[:, 0, tt * 16:tt * 16 + E + 1], x[:, c, tt * P:(tt + 1) * P], router[:, c, :],
                                                start=(c == 0), stop=(c == C - 1))
                last.then_inc(S.q_full, 1)
                for e in range(E + 3):
                    if e < E + 2:
                        pe.wait_ge(S.r_free[e % 2], 1)
                        pe.sem_inc(S.r_free[e % 2], -1)
                        if e < E:
                            hidden(lambda c: w1[:, e * C + c, :], e % 2, S.h_full)
                        else:
                            hidden(lambda c: gu[:, c, (e - E) * D:(e - E + 1) * D], e % 2, S.h_full if e == E else S.h_full_up)
                    if 1 <= e <= E:
                        pe.wait_ge(S.h_ready, 1)
                        pe.sem_inc(S.h_ready, -1)
                        pe.wait_ge(S.o_free[e % 2], 1)
                        pe.sem_inc(S.o_free[e % 2], -1)
                        outputs(hid[:, (e - 1) % 2, :], lambda f: w2[:, (e - 1) * FC + f, :], e % 2)
                pe.wait_ge(S.sh_ready, 1)
                pe.sem_inc(S.sh_ready, -1)
                pe.wait_ge(S.o_free[1], 1)
                pe.sem_inc(S.o_free[1], -1)
                outputs(sg, lambda f: down[:, f, :], 1)
                pe.wait_ge(S.o_free[0], 1)
                pe.sem_inc(S.o_free[0], -1)
                pe.sem_inc(S.o_free[0], 1)
                pe.wait_ge(S.o_free[1], 1)
                pe.sem_inc(S.o_free[1], -1)
                tail_pe(nc, S, pe, 1)

        @block.scalar
        def _(act):
            act.wait_ge(S.weights_ready[k], 16)
            with act.Fori(0, B) as b:
                act.wait_ge(S.max_ready, 1)
                act.sem_inc(S.max_ready, -1)
                for tt in range(TT):
                    nc.scalar.activation(prob[:, tt, :], logit[:, tt, 0:E], ACT.Exp, bias=nmax[:, tt:tt + 1],
                                         accum_out=total[:, tt:tt + 1])
                nc.scalar.activation(shared_gate[:], logit[:, :, E], ACT.Exp, scale=-1.0)
                act.drain().then_inc(S.p_ready, 1)
                for e in range(E + 1):
                    act.wait_ge(S.h_full, 1)
                    act.sem_inc(S.h_full, -1)
                    if e < E:
                        if e >= 2:
                            act.wait_ge(S.hid_free, 1)
                            act.sem_inc(S.hid_free, -1)
                        nc.scalar.activation(hid[:, e % 2, :], S.R[:, e % 2, 0:FC * T], ACT.Silu).then_inc(S.r_free[e % 2], 1)
                        act.drain().then_inc(S.h_ready, 1)
                    else:
                        nc.scalar.activation(sg[:], S.R[:, e % 2, 0:FC * T], ACT.Silu).then_inc(S.r_free[e % 2], 1)
                        act.drain().then_inc(S.sg_ready, 1)
                act.wait_ge(S.hid_free, 2)
                act.sem_inc(S.hid_free, -2)
                tail_act(nc, S, act, 1, b)

        @block.vector
        def _(dve):
            with dve.Fori(0, B) as b:
                dve.wait_ge(S.q_full, 1)
                dve.sem_inc(S.q_full, -1)
                nc.vector.tensor_copy(logit[:], S.O[:, 0, 0:TT * 16].rearrange("p (t e) -> p t e", t=TT)[:, :, 0:E + 1])\
                    .then_inc(S.o_free[0], 1)
                dve.drain()
                nc.vector.tensor_reduce(nmax[:], logit[:, :, 0:E], AX.X, ALU.max, negate=True).then_inc(S.max_ready, 1)
                dve.wait_ge(S.p_ready, 1)
                dve.sem_inc(S.p_ready, -1)
                nc.vector.tensor_scalar(shared_gate[:], shared_gate[:], 1.0, None, ALU.add)
                nc.vector.reciprocal(total[:], total[:])
                dve.drain()
                nc.vector.reciprocal(shared_gate[:], shared_gate[:])
                for tt in range(TT):
                    nc.vector.tensor_scalar(prob[:, tt, :], prob[:, tt, :], total[:, tt:tt + 1], None, ALU.mult)
                dve.drain()
                dve_top(nc, S, dve, gate, prob, top, index, index_f, pick, 2, E)
                dve.wait_ge(S.xres_ready, 1)
                dve.sem_inc(S.xres_ready, -1)

                def add(slot, scale):
                    for tt in range(TT):
                        last = nc.vector.scalar_tensor_tensor(S.xres[:, tt, :], S.O[:, slot, tt * D:(tt + 1) * D], scale(tt),
                                                              S.xres[:, tt, :], ALU.mult, ALU.add)
                    last.then_inc(S.o_free[slot], 1)
                    dve.drain()

                for e in range(E):
                    dve.wait_ge(S.o_full, 1)
                    dve.sem_inc(S.o_full, -1)
                    dve.sem_inc(S.hid_free, 1)
                    add((e + 1) % 2, lambda tt: gate[:, tt, e:e + 1])
                dve.wait_ge(S.sg_ready, 1)
                dve.sem_inc(S.sg_ready, -1)
                dve.wait_ge(S.h_full_up, 1)
                dve.sem_inc(S.h_full_up, -1)
                nc.vector.tensor_tensor(sg[:], sg[:], S.R[:, (E + 1) % 2, 0:FC * T], ALU.mult).then_inc(S.r_free[(E + 1) % 2], 1)
                dve.drain().then_inc(S.sh_ready, 1)
                dve.wait_ge(S.o_full, 1)
                dve.sem_inc(S.o_full, -1)
                dve.sem_inc(S.xc_free, 1)
                add(1, lambda tt: shared_gate[:, tt:tt + 1])
                nc.vector.tensor_copy(S.ysb[:], S.xres[:])
                dve.drain().then_inc(S.xres_free, 1)
                tail_dve(nc, S, dve)

        @block.gpsimd
        def _(pool):
            with pool.Fori(0, B) as b:
                pool_residual(nc, S, pool, b)
                tail_pool(nc, S, pool, b)


def moe_relu(nc, S, k):
    W, TB = S.arena[k % 2], PACK[k]
    E, EH, CHOSEN = 16, 64, 4
    HC = E * EH // P
    with ExitStack() as ctx:
        def sb(name, shape, dt=F32):
            return ctx.enter_context(nc.sbuf_tensor(f"{name}_{k}", shape, dt))

        prob = sb("prob", [P, TT, E])
        top = sb("top", [P, TT, 8])
        index = sb("index", [P, TT, 8], U32)
        index_f = sb("index_f", [P, TT, 8])
        pick = sb("pick", [P, TT, CHOSEN, E])
        gate = sb("gate", [P, TT, E])
        total = sb("total", [P, TT])
        hid = sb("hid", [P, TT, E * EH])
        hid_t = sb("hid_t", [P, HC, T])
        block = ctx.enter_context(nc.Block())

        @block.sync
        def _(sp):
            prefetch(nc, S, sp, k + 1)
            with sp.Fori(0, B) as b:
                sync_x(nc, S, sp, b)
            sp.wait_ge(S.xc_free, 1)

        @block.tensor
        def _(pe):
            keys, values, sel = part(W, TB, "keys", C), part(W, TB, "values", HC), part(W, TB, "sel", C)
            x = S.xc[:, :, 1:1 + T]
            pe.wait_ge(S.weights_ready[k], 16)
            with pe.Fori(0, B) as b:
                pe.wait_ge(S.xc_ready, 16)
                pe.sem_inc(S.xc_ready, -16)
                pe.wait_ge(S.o_free[0], 1)
                pe.sem_inc(S.o_free[0], -1)
                for tt in range(TT):
                    for c in range(C):
                        last = nc.tensor.matmul(S.O[:, 0, tt * E:(tt + 1) * E], x[:, c, tt * P:(tt + 1) * P], sel[:, c, :],
                                                start=(c == 0), stop=(c == C - 1))
                last.then_inc(S.q_full, 1)
                for tt in range(TT):
                    pe.wait_ge(S.r_free[tt], 1)
                    pe.sem_inc(S.r_free[tt], -1)
                    for at in (0, BANK):
                        for c in range(C):
                            last = nc.tensor.matmul(S.R[:, tt, at:at + BANK], x[:, c, tt * P:(tt + 1) * P], keys[:, c, at:at + BANK],
                                                    start=(c == 0), stop=(c == C - 1))
                    last.then_inc(S.h_full, 1)
                for tt in range(TT):
                    pe.wait_ge(S.h_ready, 1)
                    pe.sem_inc(S.h_ready, -1)
                    for j in range(2):
                        pe.wait_ge(S.t_free[j], 1)
                        pe.sem_inc(S.t_free[j], -1)
                        for i in range(4):
                            last = nc.tensor.transpose(S.T[:, j, i * P:(i + 1) * P], hid[:, tt, (4 * j + i) * P:(4 * j + i + 1) * P], S.ident)
                        last.then_inc(S.at_full, 1)
                pe.wait_ge(S.t_free[0], 1)
                pe.sem_inc(S.t_free[0], -1)
                pe.wait_ge(S.t_free[1], 1)
                pe.sem_inc(S.t_free[1], -1)
                pe.sem_inc(S.t_free[0], 1)
                pe.sem_inc(S.t_free[1], 1)
                pe.wait_ge(S.o_free[0], 1)
                pe.sem_inc(S.o_free[0], -1)
                for tt in range(TT):
                    for c in range(HC):
                        last = nc.tensor.matmul(S.O[:, 0, tt * D:(tt + 1) * D], hid_t[:, c, tt * P:(tt + 1) * P], values[:, c, :],
                                                start=(c == 0), stop=(c == HC - 1))
                last.then_inc(S.y_full, 1)
                pe.wait_ge(S.o_free[1], 1)
                pe.sem_inc(S.o_free[1], -1)
                tail_pe(nc, S, pe, 1)

        @block.scalar
        def _(act):
            with act.Fori(0, B) as b:
                act.wait_ge(S.max_ready, 1)
                act.sem_inc(S.max_ready, -1)
                nc.scalar.activation(prob[:], prob[:], ACT.Exp, scale=-1.0).then_inc(S.p_ready, 1)
                for tt in range(TT):
                    for j in range(2):
                        act.wait_ge(S.at_full, 1)
                        act.sem_inc(S.at_full, -1)
                        nc.scalar.activation(hid_t[:, 4 * j:4 * j + 4, tt * P:(tt + 1) * P],
                                             S.T[:, j, :].rearrange("p (c t) -> p c t", c=4), ACT.Copy).then_inc(S.t_free[j], 1)
                tail_act(nc, S, act, 1, b)

        @block.vector
        def _(dve):
            dve.wait_ge(S.weights_ready[k], 16)
            with dve.Fori(0, B) as b:
                dve.wait_ge(S.q_full, 1)
                dve.sem_inc(S.q_full, -1)
                nc.vector.tensor_copy(prob[:].rearrange("p t e -> p (t e)"), S.O[:, 0, 0:TT * E]).then_inc(S.o_free[0], 1)
                dve.drain().then_inc(S.max_ready, 1)
                dve.wait_ge(S.p_ready, 1)
                dve.sem_inc(S.p_ready, -1)
                nc.vector.tensor_scalar(prob[:], prob[:], 1.0, None, ALU.add)
                dve.drain()
                nc.vector.reciprocal(prob[:], prob[:])
                dve.drain()
                dve_top(nc, S, dve, gate, prob, top, index, index_f, pick, CHOSEN, E)
                nc.vector.tensor_reduce(total[:], gate[:], AX.X, ALU.add)
                dve.drain()
                nc.vector.tensor_scalar(total[:], total[:], 1e-9, None, ALU.max)
                dve.drain()
                nc.vector.reciprocal(total[:], total[:])
                dve.drain()
                for tt in range(TT):
                    nc.vector.tensor_scalar(gate[:, tt, :], gate[:, tt, :], total[:, tt:tt + 1], part(W, TB, "route_scale"),
                                            ALU.mult, ALU.mult)
                dve.drain()
                for tt in range(TT):
                    dve.wait_ge(S.h_full, 1)
                    dve.sem_inc(S.h_full, -1)
                    if tt == TT - 1:
                        dve.sem_inc(S.xc_free, 1)
                    nc.vector.scalar_tensor_tensor(hid[:, tt, :].rearrange("p (e h) -> p e h", e=E),
                                                   S.R[:, tt, :].rearrange("p (e h) -> p e h", e=E), 0.0,
                                                   gate[:, tt, :].unsqueeze(2).to_broadcast([P, E, EH]), ALU.max, ALU.mult)\
                        .then_inc(S.r_free[tt], 1)
                    dve.drain().then_inc(S.h_ready, 1)
                dve_output(nc, S, dve, 0)

        @block.gpsimd
        def _(pool):
            with pool.Fori(0, B) as b:
                pool_residual(nc, S, pool, b)
                tail_pool(nc, S, pool, b)


def int8_product(nc, S, k):
    W, TB = S.arena[k % 2], PACK[k]
    with ExitStack() as ctx:
        def sb(name, shape, dt=F32):
            return ctx.enter_context(nc.sbuf_tensor(f"{name}_{k}", shape, dt))

        rhs_i = sb("rhs_i", [P, C, D])
        rhs_q = sb("rhs_q", [P, C, D], BF16)
        col_scale = sb("col_scale", [P, 2])
        col_inv = sb("col_inv", [P, 2])
        col_wide = sb("col_wide", [P, 2, P])
        rhs_scale = sb("rhs_scale", [P, D])
        row_scale = sb("row_scale", [P, TT])
        row_inv = sb("row_inv", [P, TT])
        lhs_i = sb("lhs_i", [P, TT, D])
        lhs_q = sb("lhs_q", [P, C, T], BF16)
        block = ctx.enter_context(nc.Block())

        @block.sync
        def _(sp):
            prefetch(nc, S, sp, k + 1)

        @block.tensor
        def _(pe):
            pe.wait_ge(S.setup_dve, 1)
            pe.sem_inc(S.setup_dve, -1)
            pe.wait_ge(S.o_free[0], 1)
            pe.sem_inc(S.o_free[0], -1)
            for kc in range(C):
                for nb in range(C):
                    last = nc.tensor.transpose(S.O[:, 0, kc * D + nb * P:kc * D + (nb + 1) * P], rhs_i[:, nb, kc * P:(kc + 1) * P], S.ident)
            last.then_inc(S.at_full, 1)
            pe.wait_ge(S.o_free[1], 1)
            pe.sem_inc(S.o_free[1], -1)
            for nb in range(C):
                last = nc.tensor.transpose(S.O[:, 1, nb * P:(nb + 1) * P], col_wide[:, nb, :], S.ident)
            last.then_inc(S.at_full, 1)
            with pe.Fori(0, B) as b:
                pe.wait_ge(S.q_full, 1)
                pe.sem_inc(S.q_full, -1)
                pe.wait_ge(S.o_free[0], 1)
                pe.sem_inc(S.o_free[0], -1)
                for c in range(C):
                    for tt in range(TT):
                        last = nc.tensor.transpose(S.O[:, 0, (c * TT + tt) * P:(c * TT + tt + 1) * P], lhs_i[:, tt, c * P:(c + 1) * P], S.ident)
                last.then_inc(S.at_full, 1)
                pe.wait_ge(S.o_free[0], 1)
                pe.sem_inc(S.o_free[0], -1)
                for tt in range(TT):
                    for c in range(C):
                        last = nc.tensor.matmul(S.O[:, 0, tt * D:(tt + 1) * D], lhs_q[:, c, tt * P:(tt + 1) * P], rhs_q[:, c, :],
                                                start=(c == 0), stop=(c == C - 1))
                last.then_inc(S.y_full, 1)
                pe.wait_ge(S.o_free[1], 1)
                pe.sem_inc(S.o_free[1], -1)
                tail_pe(nc, S, pe, 1)

        @block.scalar
        def _(act):
            act.wait_ge(S.at_full, 1)
            act.sem_inc(S.at_full, -1)
            nc.scalar.activation(rhs_q[:].rearrange("p c n -> p (c n)"), S.O[:, 0, :], ACT.Copy).then_inc(S.o_free[0], 1)
            act.wait_ge(S.at_full, 1)
            act.sem_inc(S.at_full, -1)
            nc.scalar.activation(rhs_scale[:], S.O[:, 1, 0:D], ACT.Copy).then_inc(S.o_free[1], 1)
            act.drain().then_inc(S.setup_act, 1)
            with act.Fori(0, B) as b:
                act.wait_ge(S.at_full, 1)
                act.sem_inc(S.at_full, -1)
                nc.scalar.activation(lhs_q[:].rearrange("p c t -> p (c t)"), S.O[:, 0, :], ACT.Copy).then_inc(S.o_free[0], 1)
                tail_act(nc, S, act, 1, b)

        @block.vector
        def _(dve):
            def quantise(out, x, scale, inv):
                nc.vector.tensor_reduce(scale[:], x, AX.X, ALU.max, apply_absolute_value=True)
                dve.drain()
                nc.vector.tensor_scalar(scale[:], scale[:], 1e-12, 1.0 / INT8_MAX, ALU.max, ALU.mult)
                dve.drain()
                nc.vector.reciprocal(inv[:], scale[:])
                dve.drain()
                for t in range(2):
                    nc.vector.tensor_scalar(out[:, t, :], x[:, t, :], inv[:, t:t + 1], ROUND, ALU.mult, ALU.add)
                dve.drain()
                nc.vector.tensor_scalar(out[:], out[:], ROUND, INT8_MAX, ALU.subtract, ALU.min)
                dve.drain()
                return nc.vector.tensor_scalar(out[:], out[:], -INT8_MAX, None, ALU.max)

            dve.wait_ge(S.weights_ready[k], 16)
            quantise(rhs_i, part(W, TB, "rhs_t", C), col_scale, col_inv)
            for nb in range(C):
                nc.vector.tensor_copy(col_wide[:, nb, :], col_scale[:, nb:nb + 1].to_broadcast([P, P]))
            dve.drain().then_inc(S.setup_dve, 1)
            dve.wait_ge(S.setup_act, 1)
            dve.sem_inc(S.setup_act, -1)
            with dve.Fori(0, B) as b:
                dve.wait_ge(S.xres_ready, 1)
                dve.sem_inc(S.xres_ready, -1)
                quantise(lhs_i, S.xres[:], row_scale, row_inv).then_inc(S.q_full, 1)
                dve.wait_ge(S.y_full, 1)
                dve.sem_inc(S.y_full, -1)
                for tt in range(TT):
                    last = nc.vector.scalar_tensor_tensor(S.ysb[:, tt, :], S.O[:, 0, tt * D:(tt + 1) * D], row_scale[:, tt:tt + 1],
                                                          rhs_scale[:], ALU.mult, ALU.mult)
                last.then_inc(S.o_free[0], 1)
                dve.drain()
                nc.vector.tensor_tensor(S.ysb[:], S.ysb[:], S.xres[:], ALU.add)
                dve.drain().then_inc(S.xres_free, 1)
                tail_dve(nc, S, dve)

        @block.gpsimd
        def _(pool):
            with pool.Fori(0, B) as b:
                pool_residual(nc, S, pool, b)
                tail_pool(nc, S, pool, b)


def selective_scan(nc, S, k):
    W, TB = S.arena[k % 2], PACK[k]
    CT, NS = 4, 16
    NCH = N // BANK
    decay = S.arena[(k + 1) % 2][:, 4096:4096 + 2 * N].rearrange("p (s n) -> p s n", s=2)
    state = S.arena[k % 2][:, 4096:4096 + 2 * N].rearrange("p (s n) -> p s n", s=2)
    with ExitStack() as ctx:
        def sb(name, shape, dt=F32):
            return ctx.enter_context(nc.sbuf_tensor(f"{name}_{k}", shape, dt))

        w = sb("w", [P, SCAN_COLS])
        xp = sb("xp", [P, N])
        delta = sb("delta", [P, N])
        u = sb("u", [P, N])
        gated = sb("gated", [P, CT, N])
        neg_a = sb("neg_a", [P, NS])
        bc = sb("bc", [P, NS])
        diag = sb("diag", [P, NS, P])
        gc = sb("gc", [P, CT, T])
        block = ctx.enter_context(nc.Block())
        banks = [(S.T, 0, S.t_free[0]), (S.T, 1, S.t_free[1]), (S.O, 0, S.o_free[0]), (S.O, 1, S.o_free[1])]

        @block.sync
        def _(sp):
            prefetch(nc, S, sp, k + 1)
            with sp.Fori(0, CT) as ct:
                sp.wait_ge(S.scan_w_free, 1)
                sp.sem_inc(S.scan_w_free, -1)
                sp.dma_start(w[:], S.scan_dram[bass.ds(ct * P, P), :]).then_inc(S.scan_w, 16)
                sp.wait_ge(S.scan_w, 16)
                sp.sem_inc(S.scan_w, -16)
                sp.sem_inc(S.scan_w_pe, 1)
                sp.sem_inc(S.scan_w_act, 1)
                sp.sem_inc(S.scan_w_pool, 1)
            sp.wait_ge(S.scan_w_free, 1)
            sp.sem_inc(S.scan_w_free, -1)
            sp.sem_inc(S.scan_w_free, 1)
            with sp.Fori(0, B) as b:
                sp.wait_ge(S.xc_free, 1)
                sp.sem_inc(S.xc_free, -1)
                sp.dma_start(gc[:], gated[:, :, bass.ds(b * T, T)]).then_inc(S.xc_ready, 16)
            sp.wait_ge(S.xc_free, 1)

        @block.tensor
        def _(pe):
            with pe.Fori(0, CT) as ct:
                pe.wait_ge(S.scan_w_pe, 1)
                pe.sem_inc(S.scan_w_pe, -1)
                j = 0
                for name in ("wd", "wx", "wg"):
                    wp = part(w, SCAN, name, C)
                    for ch in range(NCH):
                        psum, slot, free = banks[j % 4]
                        pe.wait_ge(free, 1)
                        pe.sem_inc(free, -1)
                        for c in range(C):
                            last = nc.tensor.matmul(psum[:, slot, :], wp[:, c, :], S.x_t[:, c, ch * BANK:(ch + 1) * BANK],
                                                    start=(c == 0), stop=(c == C - 1))
                        last.then_inc(S.q_full, 1)
                        j += 1
                pe.wait_ge(S.diag_ready, 1)
                pe.sem_inc(S.diag_ready, -1)
                pe.wait_ge(S.r_free[0], 1)
                pe.sem_inc(S.r_free[0], -1)
                for n in range(NS):
                    pe.wait_ge(S.state_ready, 1)
                    pe.sem_inc(S.state_ready, -1)
                    for ch in range(NCH):
                        last = nc.tensor.matmul(S.R[:, ch // 2, (ch % 2) * BANK:(ch % 2 + 1) * BANK], diag[:, n, :],
                                                state[:, n % 2, ch * BANK:(ch + 1) * BANK], start=(n == 0), stop=(n == NS - 1))
                    last.then_inc(S.state_used, 1)
            pe.wait_ge(S.weights_ready[k], 16)
            wout = part(W, TB, "wout", CT)
            with pe.Fori(0, B) as b:
                pe.wait_ge(S.xc_ready, 16)
                pe.sem_inc(S.xc_ready, -16)
                pe.wait_ge(S.o_free[0], 1)
                pe.sem_inc(S.o_free[0], -1)
                for tt in range(TT):
                    for c in range(CT):
                        last = nc.tensor.matmul(S.O[:, 0, tt * D:(tt + 1) * D], gc[:, c, tt * P:(tt + 1) * P], wout[:, c, :],
                                                start=(c == 0), stop=(c == CT - 1))
                last.then_inc(S.y_full, 1)
                pe.wait_ge(S.o_free[1], 1)
                pe.sem_inc(S.o_free[1], -1)
                tail_pe(nc, S, pe, 1)

        @block.scalar
        def _(act):
            with act.Fori(0, CT) as ct:
                act.wait_ge(S.scan_w_act, 1)
                act.sem_inc(S.scan_w_act, -1)
                nc.scalar.activation(neg_a[:], part(w, SCAN, "a_log"), ACT.Exp)
                act.drain()
                nc.scalar.activation(neg_a[:], neg_a[:], ACT.Copy, scale=-1.0)
                j = 0
                for name, func in (("bd", ACT.Relu), ("bx", ACT.Identity), ("bg", ACT.Sigmoid)):
                    for ch in range(NCH):
                        psum, slot, free = banks[j % 4]
                        cols = slice(ch * BANK, (ch + 1) * BANK)
                        if name == "bg":
                            dst = gated[:, bass.ds(ct, 1), cols].rearrange("p a n -> p (a n)")
                        else:
                            dst = (delta if name == "bd" else xp)[:, cols]
                        act.wait_ge(S.q_full, 1)
                        act.sem_inc(S.q_full, -1)
                        nc.scalar.activation(dst, psum[:, slot, :], func, bias=part(w, SCAN, name)).then_inc(free, 1)
                        j += 1
                    if name == "bx":
                        act.drain().then_inc(S.xp_ready, 1)
                act.drain().then_inc(S.gate_exp, 1)
                for n in range(NS):
                    act.wait_ge(S.decay_free, 1)
                    act.sem_inc(S.decay_free, -1)
                    nc.scalar.activation(decay[:, n % 2, :].rearrange("p (b t) -> p b t", b=B)[:, :, 1:T],
                                         delta[:].rearrange("p (b t) -> p b t", b=B)[:, :, 1:T], ACT.Exp,
                                         scale=neg_a[:, n:n + 1]).then_inc(S.decay_ready, 1)
            act.wait_ge(S.decay_free, 2)
            act.sem_inc(S.decay_free, -2)
            with act.Fori(0, B) as b:
                tail_act(nc, S, act, 1, b)

        @block.vector
        def _(dve):
            for s in range(2):
                nc.vector.memset(decay[:, s, :].rearrange("p (b t) -> p b t", b=B)[:, :, 0:1], 0.0).then_inc(S.decay_free, 1)
            with dve.Fori(0, CT) as ct:
                dve.wait_ge(S.xp_ready, 1)
                dve.sem_inc(S.xp_ready, -1)
                nc.vector.tensor_tensor(u[:], xp[:], delta[:], ALU.mult)
                dve.drain()
                for n in range(NS):
                    dve.wait_ge(S.decay_ready, 1)
                    dve.sem_inc(S.decay_ready, -1)
                    dve.wait_ge(S.state_used, 1)
                    dve.sem_inc(S.state_used, -1)
                    nc.vector.tensor_tensor_scan(state[:, n % 2, :], decay[:, n % 2, :], u[:], 0.0, ALU.mult, ALU.add)\
                        .then_inc(S.decay_free, 1)
                    dve.drain().then_inc(S.state_ready, 1)
                dve.wait_ge(S.state_used, 2)
                dve.sem_inc(S.state_used, -2)
                dve.sem_inc(S.state_used, 2)
                dve.wait_ge(S.gate_exp, 1)
                dve.sem_inc(S.gate_exp, -1)
                nc.vector.scalar_tensor_tensor(xp[:], xp[:], part(w, SCAN, "d"), S.R[:].rearrange("p s n -> p (s n)"),
                                               ALU.mult, ALU.add).then_inc(S.r_free[0], 1)
                dve.drain()
                tile = gated[:, bass.ds(ct, 1), :].rearrange("p a n -> p (a n)")
                nc.vector.tensor_tensor(tile, tile, xp[:], ALU.mult).then_inc(S.scan_w_free, 1)
            dve.wait_ge(S.state_used, 2)
            dve.sem_inc(S.state_used, -2)
            with dve.Fori(0, B) as b:
                dve.wait_ge(S.y_full, 1)
                dve.sem_inc(S.y_full, -1)
                dve.sem_inc(S.xc_free, 1)
                dve.wait_ge(S.xres_ready, 1)
                dve.sem_inc(S.xres_ready, -1)
                nc.vector.tensor_tensor(S.ysb[:], S.O[:, 0, :].rearrange("p (t d) -> p t d", t=TT), S.xres[:], ALU.add)\
                    .then_inc(S.o_free[0], 1)
                dve.drain().then_inc(S.xres_free, 1)
                tail_dve(nc, S, dve)

        @block.gpsimd
        def _(pool):
            pool.sem_inc(S.state_used, 2)
            pool.sem_inc(S.scan_w_free, 1)
            with pool.Fori(0, CT) as ct:
                pool.wait_ge(S.scan_w_pool, 1)
                pool.sem_inc(S.scan_w_pool, -1)
                nc.gpsimd.tensor_tensor(bc[:], part(w, SCAN, "b"), part(w, SCAN, "c0"), ALU.mult)
                pool.drain()
                for n in range(NS):
                    last = nc.gpsimd.tensor_scalar(diag[:, n, :], S.ident, bc[:, n:n + 1], None, ALU.mult)
                last.then_inc(S.diag_ready, 1)
            pool.wait_ge(S.weights_ready[k], 16)
            with pool.Fori(0, B) as b:
                pool_residual(nc, S, pool, b, part(W, TB, "bo"))
                tail_pool(nc, S, pool, b)


def moe_capacity(nc, S, k, out):
    W, TB = S.arena[k % 2], PACK[k]
    FC = F3 // P
    ROWS = [(0, P), (1, P), (2, CAP - 2 * P)]
    with ExitStack() as ctx:
        def sb(name, shape, dt=F32):
            return ctx.enter_context(nc.sbuf_tensor(f"{name}_{k}", shape, dt))

        logit = sb("logit", [P, TT, E3])
        nmax = sb("nmax", [P, TT])
        total = sb("total", [P, TT])
        prob = sb("prob", [P, TT, E3])
        top = sb("top", [P, TT, 8])
        index = sb("index", [P, TT, 8], U32)
        index_f = sb("index_f", [P, TT, 8])
        one_hot = sb("one_hot", [P, TT, E3])
        before = sb("before", [P, TT + 1, E3])
        ranks = sb("ranks", [P, TT, E3])
        pos = sb("pos", [P, TT])
        kept = sb("kept", [P, TT])
        slot_f = sb("slot_f", [P, TT])
        spare = sb("spare", [P, TT])
        to_f = sb("to_f", [P, TT])
        to = sb("to", [P, TT], U32)
        back = sb("back", [P, B, TT], U32)
        gates = sb("gates", [P, B, TT])
        back_b = sb("back_b", [P, TT], U32)
        gate_b = sb("gate_b", [P, TT])
        zeros = sb("zeros", [P, 5 * D])
        w1 = sb("w1", [P, 2, C, F3])
        w2 = sb("w2", [P, 2, FC, D])
        xe = sb("xe", [P, 2, 3, D])
        xe_t = sb("xe_t", [P, C, CAP])
        hid = sb("hid", [P, FC, CAP])
        ye = sb("ye", [P, 2, 3, D])
        ge = sb("ge", [P, TT, D])
        block = ctx.enter_context(nc.Block())

        @block.sync
        def _(sp):
            def weights(e, s):
                sp.dma_start(w1[:, s, :, :], S.w1_dram[bass.ds(e * P, P), :].rearrange("p (c f) -> p c f", c=C)).then_inc(S.ew_ready[s], 16)
                sp.dma_start(w2[:, s, :, :], S.w2_dram[bass.ds(e * P, P), :].rearrange("p (c f) -> p c f", c=FC)).then_inc(S.ew_ready[s], 16)

            def rows(e, s):
                sp.wait_ge(S.xe_free[s], 1)
                sp.sem_inc(S.xe_free[s], -1)
                sp.dma_start(xe[:, s, 0:2, :], S.xe_dram[bass.ds(e * CAP, 2 * P), :].rearrange("(t p) d -> p t d", p=P)).then_inc(S.xe_ready[s], 16)
                sp.dma_start(xe[0:CAP - 2 * P, s, 2, :], S.xe_dram[bass.ds(e * CAP + 2 * P, CAP - 2 * P), :]).then_inc(S.xe_ready[s], 16)

            sp.wait_ge(S.zeros_ready, 1)
            sp.sem_inc(S.zeros_ready, -1)
            for i in range(E3 * CAP // (5 * P)):
                sp.dma_start(S.xe_dram[i * 5 * P:(i + 1) * 5 * P, :].rearrange("(p r) d -> p (r d)", p=P), zeros[:]).then_inc(S.slots_clear, 16)
            sp.dma_start(S.ye_dram[ZERO_ROW:ZERO_ROW + 1, :], zeros[0:1, 0:D]).then_inc(S.slots_clear, 16)
            with sp.Fori(0, B) as b:
                sync_x(nc, S, sp, b)
            sp.wait_ge(S.xc_free, 1)
            for s in range(2):
                weights(s, s)
            sp.wait_ge(S.dispatched, 1)
            sp.sem_inc(S.dispatched, -1)
            with sp.Fori(0, E3 // 2 - 1) as pair:
                e = pair * 2
                for s in range(2):
                    rows(e + s, s)
                for s in range(2):
                    sp.wait_ge(S.ew_free[s], 1)
                    sp.sem_inc(S.ew_free[s], -1)
                    weights(e + (2 + s), s)
            for s in range(2):
                rows(E3 - 2 + s, s)
            with sp.Fori(0, B) as b:
                sp.wait_ge(S.yn_ready_pe, 1)
                sp.sem_inc(S.yn_ready_pe, -1)
                sp.dma_start(out[bass.ds(b * T, T), :].rearrange("(t p) d -> p t d", p=P), S.yn[:]).then_inc(S.out_stored, 16)
                sp.wait_ge(S.out_stored, 16)
                sp.sem_inc(S.out_stored, -16)
                sp.sem_inc(S.yn_free, 1)

        @block.tensor
        def _(pe):
            gate = part(W, TB, "gate", C)
            tri, ones = part(S.const, CONST, "tri"), part(S.const, CONST, "ones")
            pe.wait_ge(S.weights_ready[k], 16)
            with pe.Fori(0, B) as b:
                pe.wait_ge(S.xc_ready, 16)
                pe.sem_inc(S.xc_ready, -16)
                pe.wait_ge(S.o_free[0], 1)
                pe.sem_inc(S.o_free[0], -1)
                for tt in range(TT):
                    for c in range(C):
                        last = nc.tensor.matmul(S.O[:, 0, tt * E3:(tt + 1) * E3], S.xc[:, c, 1 + tt * P:1 + (tt + 1) * P], gate[:, c, :],
                                                start=(c == 0), stop=(c == C - 1))
                last.then_inc(S.q_full, 1)
                pe.wait_ge(S.h_ready, 1)
                pe.sem_inc(S.h_ready, -1)
                pe.wait_ge(S.o_free[1], 1)
                pe.sem_inc(S.o_free[1], -1)
                for tt in range(TT):
                    nc.tensor.matmul(S.O[:, 1, tt * E3:(tt + 1) * E3], tri, one_hot[:, tt, :], start=True, stop=False)
                    last = nc.tensor.matmul(S.O[:, 1, tt * E3:(tt + 1) * E3], ones, before[:, tt, :], start=False, stop=True)
                last.then_inc(S.v_full, 1)

            with pe.Fori(0, E3 // 2) as pair:
                for s in range(2):
                    pe.wait_ge(S.xe_ready[s], 32)
                    pe.sem_inc(S.xe_ready[s], -32)
                    for c in range(C):
                        pe.wait_ge(S.t_free[c], 1)
                        pe.sem_inc(S.t_free[c], -1)
                        for t, n in ROWS:
                            last = nc.tensor.transpose(S.T[:, c, t * P:t * P + n], xe[0:n, s, t, c * P:(c + 1) * P], S.ident[0:n, 0:n])
                        last.then_inc(S.at_full, 1)
                    pe.wait_ge(S.t_free[0], 1)
                    pe.sem_inc(S.t_free[0], -1)
                    pe.wait_ge(S.t_free[1], 1)
                    pe.sem_inc(S.t_free[1], -1)
                    pe.sem_inc(S.t_free[0], 1)
                    pe.sem_inc(S.t_free[1], 1)
                    pe.wait_ge(S.ew_ready[s], 32)
                    pe.sem_inc(S.ew_ready[s], -32)
                    for j in range(FC // 2):
                        pe.wait_ge(S.r_free[j % 2], 1)
                        pe.sem_inc(S.r_free[j % 2], -1)
                        for i in range(2):
                            for c in range(C):
                                last = nc.tensor.matmul(S.R[:, j % 2, i * BANK:i * BANK + CAP], w1[:, s, c, (2 * j + i) * P:(2 * j + i + 1) * P],
                                                        xe_t[:, c, :], start=(c == 0), stop=(c == C - 1))
                        last.then_inc(S.h_full if j % 2 == 0 else S.h_full_up, 1)
                    pe.wait_ge(S.r_free[0], 1)
                    pe.sem_inc(S.r_free[0], -1)
                    pe.wait_ge(S.r_free[1], 1)
                    pe.sem_inc(S.r_free[1], -1)
                    pe.sem_inc(S.r_free[0], 1)
                    pe.sem_inc(S.r_free[1], 1)
                    pe.wait_ge(S.o_free[0], 1)
                    pe.sem_inc(S.o_free[0], -1)
                    pe.wait_ge(S.o_free[1], 1)
                    pe.sem_inc(S.o_free[1], -1)
                    for t, n in ROWS:
                        for f in range(FC):
                            last = nc.tensor.matmul(S.O[0:n, t // 2, (t % 2) * D:(t % 2 + 1) * D], hid[:, f, t * P:t * P + n], w2[:, s, f, :],
                                                    start=(f == 0), stop=(f == FC - 1))
                        if t == 1:
                            last.then_inc(S.y_full, 1)
                    last.then_inc(S.v_full, 1)

        @block.scalar
        def _(act):
            with act.Fori(0, B) as b:
                act.wait_ge(S.max_ready, 1)
                act.sem_inc(S.max_ready, -1)
                for tt in range(TT):
                    nc.scalar.activation(prob[:, tt, :], logit[:, tt, :], ACT.Exp, bias=nmax[:, tt:tt + 1],
                                         accum_out=total[:, tt:tt + 1])
                act.drain().then_inc(S.p_ready, 1)
            with act.Fori(0, E3 // 2) as pair:
                e = pair * 2
                for s in range(2):
                    for c in range(C):
                        act.wait_ge(S.at_full, 1)
                        act.sem_inc(S.at_full, -1)
                        nc.scalar.activation(xe_t[:, c, :], S.T[:, c, 0:CAP], ACT.Copy).then_inc(S.t_free[c], 1)
                    act.sem_inc(S.xe_free[s], 1)
                    for j in range(0, FC // 2, 2):
                        act.wait_ge(S.h_full, 1)
                        act.sem_inc(S.h_full, -1)
                        nc.scalar.activation(hid[:, 2 * j:2 * j + 2, :], S.R[:, 0, :].rearrange("p (i n) -> p i n", i=2)[:, :, 0:CAP],
                                             ACT.Relu).then_inc(S.r_free[0], 1)
                    act.wait_ge(S.v_full, 1)
                    act.sem_inc(S.v_full, -1)
                    act.wait_ge(S.ye_stored[s], 32)
                    act.sem_inc(S.ye_stored[s], -32)
                    act.sem_inc(S.ye_free, 1)
                    n = ROWS[2][1]
                    nc.scalar.activation(ye[0:n, s, 2, :], S.O[0:n, 1, 0:D], ACT.Copy).then_inc(S.o_free[1], 1)
                    act.drain()
                    act.dma_start(S.ye_dram[bass.ds((e + s) * CAP + 2 * P, n), :], ye[0:n, s, 2, :]).then_inc(S.ye_stored[s], 16)
                    act.wait_ge(S.ye_ready, 1)
                    act.sem_inc(S.ye_ready, -1)
                    act.dma_start(S.ye_dram[bass.ds((e + s) * CAP, 2 * P), :].rearrange("(t p) d -> p t d", p=P), ye[:, s, 0:2, :])\
                        .then_inc(S.ye_stored[s], 16)
            for s in range(2):
                act.wait_ge(S.ye_stored[s], 32)
                act.sem_inc(S.ye_stored[s], -32)
            act.sem_inc(S.combined, 1)

        @block.vector
        def _(dve):
            nc.vector.memset(before[:], 0.0)
            nc.vector.tensor_scalar(spare[:, 0:1], part(S.const, CONST, "row"), float(ZERO_ROW), None, ALU.add)
            nc.vector.tensor_scalar(spare[:, 1:2], part(S.const, CONST, "row"), float(ZERO_ROW + P), None, ALU.add)
            dve.drain()
            with dve.Fori(0, B) as b:
                dve.wait_ge(S.q_full, 1)
                dve.sem_inc(S.q_full, -1)
                dve.sem_inc(S.xc_free, 1)
                nc.vector.tensor_copy(logit[:].rearrange("p t e -> p (t e)"), S.O[:, 0, 0:TT * E3]).then_inc(S.o_free[0], 1)
                dve.drain()
                nc.vector.tensor_reduce(nmax[:], logit[:], AX.X, ALU.max, negate=True).then_inc(S.max_ready, 1)
                dve.wait_ge(S.p_ready, 1)
                dve.sem_inc(S.p_ready, -1)
                nc.vector.reciprocal(total[:], total[:])
                dve.drain()
                for tt in range(TT):
                    nc.vector.tensor_scalar(prob[:, tt, :], prob[:, tt, :], total[:, tt:tt + 1], None, ALU.mult)
                dve.drain()
                for tt in range(TT):
                    nc.vector.max(top[:, tt, :], prob[:, tt, :])
                dve.drain()
                for tt in range(TT):
                    nc.vector.max_index(index[:, tt, :], top[:, tt, :], prob[:, tt, :])
                dve.drain()
                nc.vector.tensor_copy(index_f[:], index[:])
                nc.vector.tensor_copy(before[:, 0, :], before[:, TT, :])
                dve.drain()
                for tt in range(TT):
                    nc.vector.tensor_scalar(one_hot[:, tt, :], part(S.const, CONST, "iota")[:, 0:E3], index_f[:, tt, 0:1], None, ALU.is_equal)
                    dve.drain()
                    last = nc.vector.tensor_tensor(before[:, tt + 1, :], before[:, tt, :], one_hot[:, tt, :], ALU.add)
                    dve.drain()
                dve.drain().then_inc(S.h_ready, 1)
                dve.wait_ge(S.v_full, 1)
                dve.sem_inc(S.v_full, -1)
                nc.vector.tensor_tensor(ranks[:].rearrange("p t e -> p (t e)"), S.O[:, 1, 0:TT * E3],
                                        one_hot[:].rearrange("p t e -> p (t e)"), ALU.mult).then_inc(S.o_free[1], 1)
                dve.drain()
                nc.vector.tensor_reduce(pos[:], ranks[:], AX.X, ALU.add)
                dve.drain()
                nc.vector.tensor_scalar(pos[:], pos[:], 1.0, None, ALU.subtract)
                dve.drain()
                nc.vector.tensor_scalar(kept[:], pos[:], float(CAP), None, ALU.is_lt)
                nc.vector.scalar_tensor_tensor(slot_f[:], index_f[:, :, 0], float(CAP), pos[:], ALU.mult, ALU.add)
                dve.drain()
                nc.vector.tensor_tensor(gates[:, bass.ds(b, 1), :].rearrange("p a t -> p (a t)"), top[:, :, 0], kept[:], ALU.mult)
                nc.vector.tensor_tensor(to_f[:], slot_f[:], spare[:], ALU.subtract)
                nc.vector.tensor_scalar(pos[:], slot_f[:], float(ZERO_ROW), None, ALU.subtract)
                dve.drain()
                nc.vector.tensor_tensor(to_f[:], to_f[:], kept[:], ALU.mult)
                nc.vector.tensor_tensor(pos[:], pos[:], kept[:], ALU.mult)
                dve.drain()
                nc.vector.tensor_tensor(to_f[:], to_f[:], spare[:], ALU.add)
                nc.vector.tensor_scalar(pos[:], pos[:], float(ZERO_ROW), None, ALU.add)
                dve.drain()
                dve.wait_ge(S.to_free, 1)
                dve.sem_inc(S.to_free, -1)
                nc.vector.tensor_copy(back[:, bass.ds(b, 1), :].rearrange("p a t -> p (a t)"), pos[:])
                nc.vector.tensor_copy(to[:], to_f[:])
                nc.vector.tensor_scalar(spare[:], spare[:], float(T), None, ALU.add)
                dve.drain().then_inc(S.to_ready, 1)
            with dve.Fori(0, E3 // 2) as pair:
                for s in range(2):
                    for j in range(1, FC // 2, 2):
                        dve.wait_ge(S.h_full_up, 1)
                        dve.sem_inc(S.h_full_up, -1)
                        nc.vector.tensor_scalar(hid[:, 2 * j:2 * j + 2, :], S.R[:, 1, :].rearrange("p (i n) -> p i n", i=2)[:, :, 0:CAP],
                                                0.0, None, ALU.max).then_inc(S.r_free[1], 1)
                    dve.wait_ge(S.y_full, 1)
                    dve.sem_inc(S.y_full, -1)
                    dve.wait_ge(S.ye_free, 1)
                    dve.sem_inc(S.ye_free, -1)
                    dve.sem_inc(S.ew_free[s], 1)
                    nc.vector.tensor_copy(ye[:, s, 0:2, :], S.O[:, 0, :].rearrange("p (t d) -> p t d", t=TT)).then_inc(S.o_free[0], 1)
                    dve.drain().then_inc(S.ye_ready, 1)
            with dve.Fori(0, B) as b:
                dve.wait_ge(S.gathered, (b + 1) * (16 * TT))
                dve.wait_ge(S.xres_ready, 1)
                dve.sem_inc(S.xres_ready, -1)
                for tt in range(TT):
                    nc.vector.scalar_tensor_tensor(S.ysb[:, tt, :], ge[:, tt, :], gate_b[:, tt:tt + 1], S.xres[:, tt, :], ALU.mult, ALU.add)
                dve.drain().then_inc(S.xres_free, 1)
                tail_dve(nc, S, dve)

        @block.gpsimd
        def _(pool):
            nc.gpsimd.memset(zeros[:], 0.0).then_inc(S.zeros_ready, 1)
            pool.sem_inc(S.to_free, 1)
            for s in range(2):
                pool.sem_inc(S.ye_stored[s], 32)
                pool.sem_inc(S.xe_free[s], 1)
            pool.wait_ge(S.slots_clear, 16 * (E3 * CAP // (5 * P) + 1))
            pool.sem_inc(S.slots_clear, -(16 * (E3 * CAP // (5 * P) + 1)))
            with pool.Fori(0, B) as b:
                nc.gpsimd.tensor_copy(S.xres[:], S.x_nat[:, bass.ds(b * TT, TT), :])
                pool.wait_ge(S.to_ready, 1)
                pool.sem_inc(S.to_ready, -1)
                pool.drain()
                for tt in range(TT):
                    nc.gpsimd.indirect_dma_start(S.xe_dram[:, :], bass.IndirectOffsetOnAxis(ap=to[:, tt:tt + 1], axis=0),
                                                 S.xres[:, tt, :], None).then_inc(S.scattered, 16)
                pool.wait_ge(S.scattered, (b + 1) * (16 * TT))
                pool.sem_inc(S.to_free, 1)
            pool.sem_inc(S.dispatched, 1)
            pool.wait_ge(S.combined, 1)
            pool.sem_inc(S.combined, -1)
            with pool.Fori(0, B) as b:
                pool.wait_ge(S.xres_free, 1)
                pool.sem_inc(S.xres_free, -1)
                nc.gpsimd.tensor_copy(back_b[:], back[:, bass.ds(b, 1), :].rearrange("p a t -> p (a t)"))
                nc.gpsimd.tensor_copy(gate_b[:], gates[:, bass.ds(b, 1), :].rearrange("p a t -> p (a t)"))
                pool.drain()
                for tt in range(TT):
                    nc.gpsimd.indirect_dma_start(ge[:, tt, :], None, S.ye_dram[:, :],
                                                 bass.IndirectOffsetOnAxis(ap=back_b[:, tt:tt + 1], axis=0)).then_inc(S.gathered, 16)
                nc.gpsimd.tensor_copy(S.xres[:], S.x_nat[:, bass.ds(b * TT, TT), :]).then_inc(S.xres_ready, 1)
                pool_rstd(nc, S, pool)
                pool.wait_ge(S.yn_ready_pool, 1)
                pool.sem_inc(S.yn_ready_pool, -1)
                pool.sem_inc(S.yn_free, 1)


class Shared:
    pass


def decoder(nc, dram, layers=range(12)):
    with ExitStack() as ctx:
        S = Shared()

        def sb(name, shape, dt=F32):
            return ctx.enter_context(nc.sbuf_tensor(name, shape, dt))

        def sem(name):
            return ctx.enter_context(nc.semaphore(name))

        def sems(name, n=2):
            return [sem(f"{name}{i}") for i in range(n)]

        S.s_full = sem("s_full")
        S.max_ready = sem("max_ready")
        S.p_ready = sem("p_ready")
        S.t_full = sem("t_full")
        S.t_full_act = sem("t_full_act")
        S.pt_ready = sem("pt_ready")
        S.o_full = sem("o_full")
        S.q_full = sem("q_full")
        S.k_full = sem("k_full")
        S.k_full_act = sem("k_full_act")
        S.v_full = sem("v_full")
        S.h_full = sem("h_full")
        S.h_full_up = sem("h_full_up")
        S.y_full = sem("y_full")
        S.at_full = sem("at_full")
        S.yt_full = sem("yt_full")
        S.ln_stat = sem("ln_stat")
        S.ln_rstd = sem("ln_rstd")
        S.yn_ready_pe = sem("yn_ready_pe")
        S.yn_ready_pool = sem("yn_ready_pool")
        S.yn_free = sem("yn_free")
        S.xres_ready = sem("xres_ready")
        S.xres_free = sem("xres_free")
        S.xc_ready = sem("xc_ready")
        S.xc_free = sem("xc_free")
        S.setup_act = sem("setup_act")
        S.setup_dve = sem("setup_dve")
        S.lines_full = sem("lines_full")
        S.nat_full = sem("nat_full")
        S.line_ready = sem("line_ready")
        S.lt_full = sem("lt_full")
        S.inc_full = sem("inc_full")
        S.k_nat_ready = sem("k_nat_ready")
        S.lr_full = sem("lr_full")
        S.lines_sb = sem("lines_sb")
        S.nat_geo = sem("nat_geo")
        S.inc_free = sem("inc_free")
        S.inc_ready = sem("inc_ready")
        S.mem_ready = sem("mem_ready")
        S.gate_exp = sem("gate_exp")
        S.norm_sum = sem("norm_sum")
        S.norm_root = sem("norm_root")
        S.ctx_ready = sem("ctx_ready")
        S.ctx_stat = sem("ctx_stat")
        S.ctx_rstd = sem("ctx_rstd")
        S.ctx_norm_ready = sem("ctx_norm_ready")
        S.ctx_nt_ready = sem("ctx_nt_ready")
        S.lat_ready = sem("lat_ready")
        S.lat_t_ready = sem("lat_t_ready")
        S.k_sb = sem("k_sb")
        S.hid_free = sem("hid_free")
        S.h_ready = sem("h_ready")
        S.sg_ready = sem("sg_ready")
        S.sh_ready = sem("sh_ready")
        S.scan_w = sem("scan_w")
        S.scan_w_pe = sem("scan_w_pe")
        S.scan_w_act = sem("scan_w_act")
        S.scan_w_pool = sem("scan_w_pool")
        S.scan_w_free = sem("scan_w_free")
        S.diag_ready = sem("diag_ready")
        S.state_ready = sem("state_ready")
        S.state_used = sem("state_used")
        S.xp_ready = sem("xp_ready")
        S.decay_ready = sem("decay_ready")
        S.decay_free = sem("decay_free")
        S.zeros_ready = sem("zeros_ready")
        S.slots_clear = sem("slots_clear")
        S.to_ready = sem("to_ready")
        S.to_free = sem("to_free")
        S.scattered = sem("scattered")
        S.dispatched = sem("dispatched")
        S.combined = sem("combined")
        S.gathered = sem("gathered")
        S.ye_free = sem("ye_free")
        S.ye_ready = sem("ye_ready")
        S.out_stored = sem("out_stored")
        S.r_free = sems("r_free")
        S.t_free = sems("t_free")
        S.o_free = sems("o_free")
        S.ew_ready = sems("ew_ready")
        S.ew_free = sems("ew_free")
        S.xe_ready = sems("xe_ready")
        S.xe_free = sems("xe_free")
        S.ye_stored = sems("ye_stored")
        S.weights_ready = sems("weights_ready", len(PACK))
        loaded = ctx.enter_context(nc.semaphore("loaded"))
        set_up = ctx.enter_context(nc.semaphore("set_up"))

        S.x_nat = sb("x_nat", [P, B * TT, D])
        S.x_t = sb("x_t", [P, C, N])
        S.ctx_t = sb("ctx_t", [P, C, B * CTX])
        S.const = sb("const", [P, sum(n for _, n in CONST.values())])
        S.masks = sb("masks", [P, 2, P], BF16)
        ident_b = sb("ident_b", [P, P], BF16)
        S.arena = [sb(f"arena{i}", [P, W_COLS]) for i in range(2)]
        S.xc = sb("xc", [P, C, 1 + T])
        S.xres = sb("xres", [P, TT, D])
        S.ysb = sb("ysb", [P, TT, D])
        S.yn = sb("yn", [P, TT, D])
        S.bst = sb("bst", [P, TT, 6])
        S.mv = sb("mv", [P, TT, 2])
        S.rstd = sb("rstd", [P, TT])
        S.ident = part(S.const, CONST, "ident")
        S.ident_b = ident_b[:]
        S.R = ctx.enter_context(nc.psum_tensor("R", [P, 2, 2 * BANK], F32))
        S.T = ctx.enter_context(nc.psum_tensor("T", [P, 2, BANK], F32))
        S.O = ctx.enter_context(nc.psum_tensor("O", [P, 2, BANK], F32))
        S.packs = [dram[f"pack{i}"] for i in range(len(PACK))]
        S.ctx_dram, S.scan_dram, S.w1_dram, S.w2_dram = dram["ctx"], dram["scan"], dram["w1"], dram["w2"]
        S.xe_dram = nc.dram_tensor("slots_in", (E3 * CAP + N, D), F32, kind="Internal").ap()
        S.ye_dram = nc.dram_tensor("slots_out", (E3 * CAP + 1, D), F32, kind="Internal").ap()

        with nc.Block() as block:
            @block.sync
            def _(sp):
                sp.dma_start(S.const[:], dram["const"]).then_inc(loaded, 16)
                sp.dma_start(S.x_t[:], dram["x_t"].rearrange("(c p) n -> p c n", p=P)).then_inc(loaded, 16)
                sp.dma_start(S.x_nat[:], dram["x"].rearrange("(t p) d -> p t d", p=P)).then_inc(loaded, 16)
                sp.dma_start(S.ctx_t[:], dram["ctx_t"].rearrange("(c p) n -> p c n", p=P)).then_inc(loaded, 16)
                prefetch(nc, S, sp, layers[0])
                for i in range(2):
                    for s in (S.r_free, S.t_free, S.o_free):
                        sp.sem_inc(s[i], 1)
                sp.sem_inc(S.xc_free, 1)
                sp.sem_inc(S.xres_free, 1)
                sp.sem_inc(S.yn_free, 2)
                sp.wait_ge(loaded, 64)

            @block.vector
            def _(dve):
                nc.vector.memset(S.xc[:], 0.0).then_inc(set_up, 1)
                dve.wait_ge(loaded, 64)
                nc.vector.tensor_copy(S.masks[:, 0, :], part(S.const, CONST, "causal"))
                nc.vector.tensor_copy(S.masks[:, 1, :], part(S.const, CONST, "block"))
                nc.vector.tensor_copy(S.ident_b, S.ident)
                dve.drain().then_inc(set_up, 1)

        build = [
            lambda k: attention16(nc, S, k, DH16 ** -0.5, mask="causal", geometry=True),
            lambda k: perceiver(nc, S, k),
            lambda k: moe_silu(nc, S, k),
            lambda k: attention16(nc, S, k, DH16 ** -0.5, mask="block", out=False),
            lambda k: perceiver(nc, S, k),
            lambda k: moe_relu(nc, S, k),
            lambda k: attention16(nc, S, k, D ** -0.5, mask="causal"),
            lambda k: attention16(nc, S, k, DH16 ** -0.5, cross=True),
            lambda k: int8_product(nc, S, k),
            lambda k: selective_scan(nc, S, k),
            lambda k: attention16(nc, S, k, DH16 ** -0.5, cross=True),
            lambda k: moe_capacity(nc, S, k, dram["out"]),
        ]
        for k in layers:
            build[k](k)
        if layers[-1] != 11:
            with nc.Block() as block:
                @block.sync
                def _(sp):
                    sp.dma_start(dram["out"].rearrange("(t p) d -> p t d", p=P), S.x_nat[:]).then_inc(loaded, 16)
                    sp.wait_ge(loaded, 80)



def pack_inputs(i):
    f = np.float32

    def mat(w):
        w = np.asarray(w)
        return w.reshape(-1, P, w.shape[1]).transpose(1, 0, 2).reshape(P, -1)

    def cols(v):
        return np.asarray(v).reshape(C, P).T

    def rep(v):
        v = np.asarray(v).reshape(1, -1)
        return np.broadcast_to(v, (P, v.shape[1]))

    def lines(w, order):
        return np.asarray(w).reshape(D, H, 4)[:, :, order].reshape(D, 96)

    def mha(wq, bq, wk, bk, wv, bv, wo=None, bo=None):
        none = np.zeros((D, D), f)
        return [mat(wq), mat(wk), mat(wv), mat(none if wo is None else wo), cols(bq), cols(bk), rep(bv),
                rep(np.zeros(D, f) if bo is None else bo)]

    def xatt(p, w1, b1, w2, b2):
        return [mat(i[p + "Wq"]), mat(i[p + "Wkv"]), mat(i[p + "Wo"]), rep(i[w1]), rep(i[b1]), rep(i[w2]), rep(i[b2])]

    def experts(w):
        return np.concatenate([mat(e) for e in np.asarray(w)], 1)

    a = "L0_attn_"
    qkv, qkv_b, geo = np.asarray(i[a + "qkv_w"]), np.asarray(i[a + "qkv_b"]), np.asarray(i[a + "kv_geo_w"])
    cat = lambda *x: np.concatenate(x, 1)
    w1w, w2w, w1r, w2r = (i[a + n] for n in ("w1_write", "w2_write", "w1_read", "w2_read"))
    packs = [
        [mat(qkv[:, :D]), cols(qkv_b[:D]), mat(cat(qkv[:, D:], geo)), rep(qkv_b[D:]),
         mat(cat(lines(w1w, _WI), lines(w1w, _WJ))), mat(cat(lines(w2w, _WJ), lines(w2w, _WI))),
         mat(cat(lines(w1r, _PI), lines(w1r, _PJ), lines(w2r, _PJ), lines(w2r, _PI))), mat(i[a + "out_w"]), rep(i[a + "out_b"]),
         rep(i[a + "mem_scale"]), rep(i[a + "decay_logits"]), rep(i[a + "kv_gate"])],
        xatt("L0_xattn_", "L0_xattn_ln1_w", "L0_xattn_ln1_b", "L0_xattn_ln2_w", "L0_xattn_ln2_b"),
        [experts(i["L0_ffn_w1"]), experts(i["L0_ffn_w2"]), mat(i["L0_ffn_shared_gate_up"]), mat(i["L0_ffn_shared_down"]),
         mat(cat(np.asarray(i["L0_ffn_router_w"]), np.asarray(i["L0_ffn_shared_gate_w"])))],
        mha(*(i["L1_attn_" + n] for n in ("Wq", "bq", "Wk", "bk", "Wv", "bv"))),
        xatt("L1_xattn_", "L1_xattn_ln1_g", "L1_xattn_ln1_b", "L1_xattn_ln2_g", "L1_xattn_ln2_b"),
        [mat(np.asarray(i["L1_ffn_keys"]).transpose(1, 0, 2).reshape(D, -1)), mat(np.asarray(i["L1_ffn_values"]).reshape(-1, D)),
         mat(np.asarray(i["L1_ffn_expert_sel"]).T), rep(i["L1_ffn_route_scale"])],
        mha(*(np.asarray(i["L2_attn_" + n]).T for n in ("Wq_w", "Wq_b", "Wk_w", "Wk_b", "Wv_w", "Wv_b", "Wo_w", "Wo_b"))),
        mha(*(i["L2_xattn_" + n] for n in ("Wq", "bq", "Wk", "bk", "Wv", "bv", "Wp", "bp"))),
        [mat(np.asarray(i["L2_ffn_rhs"]).T)],
        [mat(np.asarray(i["L3_attn_W_out"]).T), rep(i["L3_attn_b_out"])],
        mha(*(np.asarray(i["L3_xattn_" + n]).T for n in ("Wq", "bq", "Wk", "bk", "Wv", "bv", "Wo", "bo"))),
        [mat(i["L3_ffn_gate_w"])],
    ]
    s = "L3_attn_"
    win, wg = np.asarray(i[s + "W_in"]), np.asarray(i[s + "W_gate"])
    b_in, bg = np.asarray(i[s + "b_in"]), np.asarray(i[s + "b_gate"])
    DI = wg.shape[0]
    col = lambda v: np.asarray(v).reshape(-1, 1)
    scan = []
    for t in range(DI // P):
        r = slice(t * P, (t + 1) * P)
        r2 = slice(DI + t * P, DI + (t + 1) * P)
        scan.append(cat(mat(win[r].T), mat(win[r2].T), mat(wg[r].T), col(b_in[r]), col(b_in[r2]), col(bg[r]),
                        np.asarray(i[s + "A_log"])[r], np.asarray(i[s + "B_mat"])[r], rep(np.asarray(i[s + "C_mat"])[0]),
                        col(np.asarray(i[s + "D_vec"])[r])))
    x, c = np.asarray(i["x"]).reshape(N, D), np.asarray(i["ctx_1024"]).reshape(B * CTX, D)
    p, j = np.arange(P)[:, None], np.arange(P)[None, :]
    steps = P + p - np.arange(2 * P)[None, :]
    const = cat(np.eye(P), np.where(j <= p, 0, MASKED), np.where(p <= j, 0, MASKED), np.where(p // 64 == j // 64, 0, MASKED),
                (p <= j) * 1.0, np.ones((P, P)), np.maximum(steps, 0), (steps > 0) * 1.0, rep(np.arange(16)),
                np.full((P, 16), -0.5), np.full((P, 64), 0.5), p * 1.0,
                (p // DH16 == np.arange(HT)) * 1.0, (p // LW == np.arange(H)) * 1.0)
    arrays = {f"pack{n}": cat(*parts) for n, parts in enumerate(packs)}
    arrays |= {"x": x, "x_t": x.T, "ctx": c, "ctx_t": c.T, "scan": np.concatenate(scan, 0), "const": const,
               "w1": np.concatenate([mat(e) for e in np.asarray(i["L3_ffn_w1"])], 0),
               "w2": np.concatenate([mat(e) for e in np.asarray(i["L3_ffn_w2"])], 0)}
    return {n: np.ascontiguousarray(v, dtype=f) for n, v in arrays.items()}


def kernel(**inputs):
    import concourse.bacc as bacc
    from concourse.bass_utils import run_bass_kernel_spmd

    nc = bacc.Bacc("TRN2", target_bir_lowering=False, num_devices=1)
    arrays = pack_inputs(inputs)
    dram = {n: nc.dram_tensor(f"{n}_dram", a.shape, F32, kind="ExternalInput").ap() for n, a in arrays.items()}
    dram["out"] = nc.dram_tensor("out_dram", (N, D), F32, kind="ExternalOutput").ap()
    decoder(nc, dram)
    r = run_bass_kernel_spmd(nc, [{f"{n}_dram": a for n, a in arrays.items()}], core_ids=[0])
    return r.results[0]["out_dram"].reshape(B, T, D)
```

```python
from contextlib import ExitStack

import numpy as np

import concourse.bass as bass
from concourse import mybir

F32 = mybir.dt.float32
BF16 = mybir.dt.bfloat16
I32 = mybir.dt.int32
U32 = mybir.dt.uint32
ALU = mybir.AluOpType
ACT = mybir.ActivationFunctionType
AX = mybir.AxisListType

P = 128
B = 8
T = 256
D = 256
C = D // P
TT = T // P
N = B * T
H = 16
HU = 4
HT = P // 16
LW = P // H
CTX = 77
EPS = 1e-5
MASKED = -1e30
BANK = 512
W_COLS = 9984
DH16 = D // H
VA16 = DH16 + 1
XD = 64
XI = H * XD
XK = CTX + T
VA64 = XD + 1
INT8_MAX = 127.0
ROUND = 1.5 * 2.0 ** 23
CAP = 320
E3 = 8
F3 = 1024
ZERO_ROW = E3 * CAP

_PI = [0, 0, 0, 1, 1, 2]
_PJ = [1, 2, 3, 2, 3, 3]
_WI = [2, 3, 1, 0, 2, 0]
_WJ = [3, 1, 2, 3, 0, 1]


def columns(parts):
    at, out = 0, {}
    for name, n in parts:
        out[name] = (at, n)
        at += n
    return out


CONST = columns([("ident", 128), ("causal", 128), ("causal_t", 128), ("block", 128), ("tri", 128), ("ones", 128),
                 ("steps", 256), ("past", 256), ("iota", 16), ("neg_half", 16), ("half", 64), ("row", 1),
                 ("head", HT), ("line_head", H)])
_XATT = [("wq", C * XI), ("wkv", C * 2 * XI), ("wo", (XI // P) * D),
         ("ctx_w", D), ("ctx_b", D), ("lat_w", D), ("lat_b", D)]
_MHA = [("wq", C * D), ("wk", C * D), ("wv", C * D), ("wo", C * D), ("bq", C), ("bk", C), ("bv", D), ("bo", D)]
PACK = [
    columns([("wq", C * D), ("bq", C), ("nat", C * 1024), ("nat_b", 512), ("write1", C * 192), ("write2", C * 192),
             ("read", C * 384), ("wo", C * D), ("bo", D), ("mem_scale", H), ("decay", H), ("kv_gate", 1)]),
    columns(_XATT),
    columns([("w1", 8 * C * 256), ("w2", 8 * C * 256), ("gate_up", C * 512), ("down", C * 256), ("router", C * 9)]),
    columns(_MHA),
    columns(_XATT),
    columns([("keys", C * 1024), ("values", 8 * 256), ("sel", C * 16), ("route_scale", 1)]),
    columns(_MHA),
    columns(_MHA),
    columns([("rhs_t", C * 256)]),
    columns([("wout", 4 * D), ("bo", D)]),
    columns(_MHA),
    columns([("gate", C * E3)]),
]
SCAN = columns([("wx", C * P), ("wd", C * P), ("wg", C * P), ("bx", 1), ("bd", 1), ("bg", 1), ("a_log", 16),
                ("b", 16), ("c0", 16), ("d", 1)])
SCAN_COLS = sum(n for _, n in SCAN.values())


def part(image, table, name, chunks=None):
    at, n = table[name]
    v = image[:, at:at + n]
    return v.rearrange("p (c n) -> p c n", c=chunks) if chunks else v



def tail_dve(nc, S, dve, meanwhile=None):
    for tt in range(TT):
        nc.vector.bn_stats(S.bst[:, tt, :], S.ysb[:, tt, :])
    dve.drain()
    for tt in range(TT):
        last = nc.vector.bn_aggr(S.mv[:, tt, :], S.bst[:, tt, :])
    last.then_inc(S.ln_stat, 1)
    if meanwhile:
        meanwhile()
    dve.wait_ge(S.ln_rstd, 1)
    dve.sem_inc(S.ln_rstd, -1)
    dve.wait_ge(S.yn_free, 2)
    dve.sem_inc(S.yn_free, -2)
    for tt in range(TT):
        last = nc.vector.tensor_scalar(S.yn[:, tt, :], S.ysb[:, tt, :], S.mv[:, tt, 0:1], S.rstd[:, tt:tt + 1],
                                       ALU.subtract, ALU.mult)
    last.then_inc(S.yn_ready_pe, 1)
    dve.drain().then_inc(S.yn_ready_pool, 1)


def pool_rstd(nc, S, pool):
    pool.wait_ge(S.ln_stat, 1)
    pool.sem_inc(S.ln_stat, -1)
    nc.gpsimd.tensor_scalar(S.rstd[:], S.mv[:, :, 1], EPS, None, ALU.add)
    pool.drain()
    nc.gpsimd.tensor_tensor(S.rstd[:], S.rstd[:], part(S.const, CONST, "neg_half")[:, 0:TT], ALU.pow)\
        .then_inc(S.ln_rstd, 1)


def tail_pool(nc, S, pool, b):
    pool_rstd(nc, S, pool)
    pool.wait_ge(S.yn_ready_pool, 1)
    pool.sem_inc(S.yn_ready_pool, -1)
    nc.gpsimd.tensor_copy(S.x_nat[:, bass.ds(b * TT, TT), :], S.yn[:]).then_inc(S.yn_free, 1)


def tail_pe(nc, S, pe, slot):
    pe.wait_ge(S.yn_ready_pe, 1)
    pe.sem_inc(S.yn_ready_pe, -1)
    for c in range(C):
        for tt in range(TT):
            last = nc.tensor.transpose(S.O[:, slot, (c * TT + tt) * P:(c * TT + tt + 1) * P],
                                       S.yn[:, tt, c * P:(c + 1) * P], S.ident)
    last.then_inc(S.yt_full, 1)


def tail_act(nc, S, act, slot, b):
    act.wait_ge(S.yt_full, 1)
    act.sem_inc(S.yt_full, -1)
    act.sem_inc(S.yn_free, 1)
    nc.scalar.activation(S.x_t[:, :, bass.ds(b * T, T)],
                         S.O[:, slot, :].rearrange("p (c t) -> p c t", c=C), ACT.Copy).then_inc(S.o_free[slot], 1)


def pool_residual(nc, S, pool, b, bias=None):
    pool.wait_ge(S.xres_free, 1)
    pool.sem_inc(S.xres_free, -1)
    x = S.x_nat[:, bass.ds(b * TT, TT), :]
    if bias is None:
        nc.gpsimd.tensor_copy(S.xres[:], x).then_inc(S.xres_ready, 1)
    else:
        for tt in range(TT):
            last = nc.gpsimd.tensor_tensor(S.xres[:, tt, :], S.x_nat[:, bass.ds(b * TT + tt, 1), :].rearrange("p a d -> p (a d)"), bias, ALU.add)
        last.then_inc(S.xres_ready, 1)


def dve_output(nc, S, dve, slot, meanwhile=None):
    dve.wait_ge(S.y_full, 1)
    dve.sem_inc(S.y_full, -1)
    dve.wait_ge(S.xres_ready, 1)
    dve.sem_inc(S.xres_ready, -1)
    nc.vector.tensor_tensor(S.ysb[:], S.O[:, slot, :].rearrange("p (t d) -> p t d", t=TT), S.xres[:], ALU.add)\
        .then_inc(S.o_free[slot], 1)
    dve.drain().then_inc(S.xres_free, 1)
    tail_dve(nc, S, dve, meanwhile)


def sync_x(nc, S, sp, b):
    sp.wait_ge(S.xc_free, 1)
    sp.sem_inc(S.xc_free, -1)
    sp.dma_start(S.xc[:, :, 1:1 + T], S.x_t[:, :, bass.ds(b * T, T)]).then_inc(S.xc_ready, 16)


def prefetch(nc, S, sp, k):
    if k < len(PACK):
        n = sum(w for _, w in PACK[k].values())
        sp.dma_start(S.arena[k % 2][:, 0:n], S.packs[k]).then_inc(S.weights_ready[k], 16)



def pe_units(nc, S, pe, n_units, scores, transposes, product, o_slot, beside, before=()):
    for u in range(n_units + 1):
        if 1 <= u < n_units - 1:
            if u + 1 in before:
                before[u + 1]()
            scores(u + 1).then_inc(S.s_full, 1)
        if u >= 1:
            pe.wait_ge(S.pt_ready, 2)
            pe.sem_inc(S.pt_ready, -2)
            pe.wait_ge(S.o_free[o_slot(u - 1)], 1)
            pe.sem_inc(S.o_free[o_slot(u - 1)], -1)
            product(u - 1).then_inc(S.o_full, 1)
        if u < n_units:
            pe.wait_ge(S.p_ready, 1)
            pe.sem_inc(S.p_ready, -1)
            transposes(u, 0).then_inc(S.t_full, 1)
            transposes(u, 1).then_inc(S.t_full_act, 1)
        if u in beside:
            beside[u]()


def dve_maxima(S, dve, row_max, u):
    dve.wait_ge(S.s_full, 1)
    dve.sem_inc(S.s_full, -1)
    row_max(u).then_inc(S.max_ready, 1)


def dve_units(nc, S, dve, n_units, row_max, evacuate, normalise, beside):
    def norm(u):
        dve.wait_ge(S.o_full, 1)
        dve.sem_inc(S.o_full, -1)
        normalise(u)

    for u in range(n_units):
        if u + 1 < n_units:
            dve_maxima(S, dve, row_max, u + 1)
        if u >= 1:
            norm(u - 1)
        dve.wait_ge(S.t_full, 1)
        dve.sem_inc(S.t_full, -1)
        evacuate(u).then_inc(S.pt_ready, 1)
        if u in beside:
            beside[u]()
    norm(n_units - 1)


def act_exps(S, act, exps, u):
    act.wait_ge(S.max_ready, 1)
    act.sem_inc(S.max_ready, -1)
    exps(u).then_inc(S.p_ready, 1)


def act_units(nc, S, act, n_units, exps, evacuate, beside):
    for u in range(n_units):
        if u >= 1:
            act_exps(S, act, exps, u)
        if u in beside:
            beside[u]()
        act.wait_ge(S.t_full_act, 1)
        act.sem_inc(S.t_full_act, -1)
        evacuate(u).then_inc(S.pt_ready, 1)



def attention16(nc, S, k, scale, mask=None, cross=False, out=True, geometry=False):
    W, TB = S.arena[k % 2], PACK[k]
    units = [(qt, g) for qt in range(TT) for g in range(H // HU)]
    NU = len(units)
    key_tiles = 1 if cross else TT
    kn = CTX if cross else P

    def key_range(qt):
        if cross:
            return [0]
        if mask == "block":
            return [qt]
        return list(range(qt + 1)) if mask == "causal" else list(range(TT))

    def o_slot(u):
        return (1 + u) % 2

    with ExitStack() as ctx:
        def sb(name, shape, dt=F32):
            return ctx.enter_context(nc.sbuf_tensor(f"{name}_{k}", shape, dt))

        q_t = sb("q_t", [P, C, T])
        k_own = sb("k_own", [P, C, HT, key_tiles * kn])
        v = sb("v", [P, key_tiles, H, VA16])
        prob = sb("prob", [P, 2, HU * T])
        prob_t = sb("prob_t", [P, 2, 2, TT, HU // 2, P])
        neg_max = sb("neg_max", [P, 2, 4])
        rec = sb("rec", [P, 2, 4])
        attn = sb("attn", [P, TT, D])
        attn_t = sb("attn_t", [P, TT, C, P])
        cc = sb("cc", [P, C, CTX]) if cross else None
        bk_own = None if geometry else sb("bk_own", [P, HT])
        if geometry:
            lines = sb("lines", [P, TT, 2, 2, 192])
            prods = sb("prods", [P, TT, 2, 2, 96])
            line = sb("line", [P, TT, 2, H, 6])
            norm2 = sb("norm2", [P, TT, 2, H])
            line_pad = sb("line_pad", [P, TT, 2, H, LW])
            kv = sb("kv", [P, TT, 2, H, DH16])
            geo = sb("geo", [P, TT, 2, H, DH16])
            inc2 = prob
            lines_own = k_own[:].rearrange("p c h n -> p (c h) n")
            lines_read = sb("lines_read", [P, T])
            decay_w = sb("decay_w", [P, H, T])
            mem = sb("mem", [P, TT, H])
            log_decay = sb("log_decay", [P, H])
        src = cc if cross else S.xc[:, :, 1:1 + T]
        block = ctx.enter_context(nc.Block())

        @block.sync
        def _(sp):
            def inputs(b):
                sync_x(nc, S, sp, b)
                if cross:
                    sp.dma_start(cc[:], S.ctx_t[:, :, bass.ds(b * CTX, CTX)]).then_inc(S.xc_ready, 16)

            inputs(0)
            prefetch(nc, S, sp, k + 1)
            with sp.Fori(1, B) as b:
                inputs(b)
            sp.wait_ge(S.xc_free, 1)

        @block.tensor
        def _(pe):
            wq = part(W, TB, "wq", C)
            wo = part(W, TB, "wo", C) if out else None
            causal = S.masks[:, 0, :]
            blocked = S.masks[:, 1, :]
            pe.wait_ge(S.weights_ready[k], 16)

            def transposed(dst, w, x):
                for t in range(C):
                    for c in range(C):
                        last = nc.tensor.matmul(dst[:, t * T:t * T + x.shape[2]], w[:, c, t * P:(t + 1) * P], x[:, c, :],
                                                start=(c == 0), stop=(c == C - 1))
                return last

            def heads_of(u):
                n = len(key_range(units[u][0])) * kn
                m = min(HU, BANK // n)
                return [(slice(t * n, (t + m) * n), t, m) for t in range(0, HU, m)]

            def scores(u):
                qt, g = units[u]
                keys = key_range(qt)
                n = len(keys) * kn
                for at, t, m in heads_of(u):
                    h = g * HU + t
                    last = nc.tensor.matmul(S.R[:, u % 2, at], q_t[:, h // HT, qt * P:(qt + 1) * P],
                                            k_own[:, h // HT, h % HT:h % HT + m, keys[0] * kn:keys[0] * kn + n],
                                            start=True, stop=(mask is None), skip_group_check=True)
                if mask is not None:
                    for at, t, m in heads_of(u):
                        last = nc.tensor.matmul(S.R[:, u % 2, at].rearrange("p (t n) -> p t n", t=m)[:, :, n - P:n], S.ident_b,
                                                (causal if mask == "causal" else blocked).unsqueeze(1).to_broadcast([P, m, P]),
                                                start=False, stop=True, skip_group_check=True)
                return last

            def transposes(u, half):
                qt, g = units[u]
                if u == 0 and half == 0:
                    pe.wait_ge(S.t_free[0], 1)
                    pe.sem_inc(S.t_free[0], -1)
                    pe.wait_ge(S.t_free[1], 1)
                    pe.sem_inc(S.t_free[1], -1)
                if u >= NU - 2 and half == 0:
                    pe.sem_inc(S.r_free[u % 2], 1)
                n = len(key_range(qt)) * kn
                for i in range(len(key_range(qt))):
                    for t in range(2 * half, 2 * half + 2):
                        last = nc.tensor.transpose(S.T[0:kn, half, (2 * i + t % 2) * P:(2 * i + t % 2 + 1) * P],
                                                   prob[:, u % 2, t * n + i * kn:t * n + (i + 1) * kn], S.ident)
                return last

            def product(u):
                qt, g = units[u]
                keys = key_range(qt)
                if u == NU - 1:
                    pe.sem_inc(S.t_free[0], 1)
                    pe.sem_inc(S.t_free[1], 1)
                for t in range(4):
                    for i, key in enumerate(keys):
                        last = nc.tensor.matmul(S.O[:, o_slot(u), t * VA16:(t + 1) * VA16],
                                                prob_t[0:kn, u % 2, t // 2, i, t % 2, :], v[0:kn, key, g * HU + t, :],
                                                start=(i == 0), stop=(i == len(keys) - 1))
                return last

            def queries():
                if not geometry:
                    pe.wait_ge(S.xc_ready, 32 if cross else 16)
                    pe.sem_inc(S.xc_ready, -(32 if cross else 16))
                pe.wait_ge(S.r_free[0], 1)
                pe.sem_inc(S.r_free[0], -1)
                transposed(S.R[:, 0, :], wq, S.xc[:, :, 1:1 + T]).then_inc(S.q_full, 1)

            def keys(t):
                if t == 0:
                    pe.wait_ge(S.r_free[1], 1)
                    pe.sem_inc(S.r_free[1], -1)
                wk = part(W, TB, "wk", C)
                for c in range(C):
                    last = nc.tensor.matmul(S.R[:, 1, t * BANK:t * BANK + key_tiles * kn], wk[:, c, t * P:(t + 1) * P], src[:, c, :],
                                            start=(c == 0), stop=(c == C - 1))
                last.then_inc(S.k_full if t == 0 else S.k_full_act, 1)

            def values():
                pe.wait_ge(S.t_free[0], 1)
                pe.sem_inc(S.t_free[0], -1)
                wv = part(W, TB, "wv", C)
                for i in range(key_tiles):
                    for c in range(C):
                        last = nc.tensor.matmul(S.T[0:kn, 0, i * D:(i + 1) * D], src[:, c, i * kn:(i + 1) * kn],
                                                wv[:, c, :], start=(c == 0), stop=(c == C - 1))
                last.then_inc(S.v_full, 1)

            def naturals(i):
                tt, slot = i % 4 // 2, i % 2
                if i == 0:
                    pe.wait_ge(S.xc_ready, 16)
                    pe.sem_inc(S.xc_ready, -16)
                now = S.xc[:, :, 1 + tt * P:1 + (tt + 1) * P]
                before = S.xc[:, :, tt * P:(tt + 1) * P]
                nat, rd, wr1, wr2 = (part(W, TB, name, C) for name in ("nat", "read", "write1", "write2"))
                if i >= 4:
                    works = ((now, nat[:, :, slot * BANK:(slot + 1) * BANK], 0, BANK),)
                elif slot == 0:
                    works = ((before, wr1, 0, 192), (now, wr2, 192, 192))
                else:
                    works = ((now, rd, 0, 384),)
                pe.wait_ge(S.r_free[slot], 1)
                pe.sem_inc(S.r_free[slot], -1)
                for x, w, at, n in works:
                    for c in range(C):
                        last = nc.tensor.matmul(S.R[:, slot, BANK + at:BANK + at + n], x[:, c, :], w[:, c, :],
                                                start=(c == 0), stop=(c == C - 1))
                last.then_inc(S.nat_full if i in (4, 6) else S.nat_full_act, 1)

            def naturals_amid(first, n):
                if first == 0:
                    pe.sem_inc(S.r_free[0], 1)
                    pe.sem_inc(S.r_free[1], 1)
                for i in range(first, first + n):
                    naturals(i)

            def slot_back(slot):
                pe.wait_ge(S.r_free[slot], 1)
                pe.sem_inc(S.r_free[slot], -1)

            def lines_transposed():
                pe.wait_ge(S.line_ready, 1)
                pe.sem_inc(S.line_ready, -1)
                for rw, full in ((0, S.lt_full), (1, S.lr_full)):
                    pe.wait_ge(S.t_free[rw], 1)
                    pe.sem_inc(S.t_free[rw], -1)
                    for tt in range(TT):
                        for i in range(rw + 1):
                            last = nc.tensor.transpose(S.T[:, rw, i * T + tt * P:i * T + (tt + 1) * P],
                                                       line_pad[:, tt, rw - i, :, :].rearrange("p h i -> p (h i)"), S.ident)
                    last.then_inc(full, 1)

            def incidences(first):
                if first == 0:
                    pe.wait_ge(S.t_free[0], 1)
                    pe.sem_inc(S.t_free[0], -1)
                    pe.wait_ge(S.t_free[1], 1)
                    pe.sem_inc(S.t_free[1], -1)
                    pe.sem_inc(S.t_free[0], 1)
                    pe.sem_inc(S.t_free[1], 1)
                for u, (qt, g) in list(enumerate(units))[first:first + NU // 2]:
                    n = (qt + 1) * P
                    pe.wait_ge(S.r_free[(1 + u) % 2], 1)
                    pe.sem_inc(S.r_free[(1 + u) % 2], -1)
                    for at, t, m in heads_of(u):
                        last = nc.tensor.matmul(S.R[:, (1 + u) % 2, at], lines_read[:, qt * P:(qt + 1) * P],
                                                lines_own[:, g * HU + t:g * HU + t + m, 0:n], start=True, stop=True)
                    last.then_inc(S.inc_full, 1)

            def gated_keys_transposed():
                pe.wait_ge(S.k_nat_ready, 1)
                pe.sem_inc(S.k_nat_ready, -1)
                for c in range(C):
                    pe.wait_ge(S.t_free[c], 1)
                    pe.sem_inc(S.t_free[c], -1)
                    for tt in range(TT):
                        last = nc.tensor.transpose(S.T[:, c, tt * P:(tt + 1) * P],
                                                   kv[:, tt, 0, c * HT:(c + 1) * HT, :].rearrange("p h i -> p (h i)"), S.ident)
                    last.then_inc(S.k_full if c == 0 else S.k_full_act, 1)
                pe.wait_ge(S.t_free[0], 1)
                pe.sem_inc(S.t_free[0], -1)
                pe.wait_ge(S.t_free[1], 1)
                pe.sem_inc(S.t_free[1], -1)
                pe.sem_inc(S.t_free[0], 1)
                pe.sem_inc(S.t_free[1], 1)

            def first_scores():
                pe.wait_ge(S.r_free[0], 1)
                pe.sem_inc(S.r_free[0], -1)
                pe.wait_ge(S.r_free[1], 1)
                pe.sem_inc(S.r_free[1], -1)
                if not geometry:
                    pe.wait_ge(S.k_sb, 1)
                    pe.sem_inc(S.k_sb, -1)
                scores(0).then_inc(S.s_full, 1)
                scores(1).then_inc(S.s_full, 1)

            def output(amid=None):
                pe.wait_ge(S.o_free[1], 1)
                pe.sem_inc(S.o_free[1], -1)
                if not out:
                    if amid:
                        amid()
                    return
                pe.wait_ge(S.o_free[0], 1)
                pe.sem_inc(S.o_free[0], -1)
                for qt in range(TT):
                    for c in range(C):
                        last = nc.tensor.transpose(S.O[:, 1, (qt * C + c) * P:(qt * C + c + 1) * P],
                                                   attn[:, qt, c * P:(c + 1) * P], S.ident)
                last.then_inc(S.at_full, 1)
                if amid:
                    amid()
                pe.wait_ge(S.o_free[1], 1)
                pe.sem_inc(S.o_free[1], -1)
                for qt in range(TT):
                    for c in range(C):
                        last = nc.tensor.matmul(S.O[:, 0, qt * D:(qt + 1) * D], attn_t[:, qt, c, :], wo[:, c, :],
                                                start=(c == 0), stop=(c == C - 1))
                last.then_inc(S.y_full, 1)

            if geometry:
                beside = {0: lambda: naturals_amid(0, 3), 1: lambda: naturals_amid(3, 3), 2: lambda: naturals_amid(6, 2), NU - 2: queries}
                before = {4: lambda: slot_back(0), 5: lambda: slot_back(1)}
                for i in range(8):
                    naturals(i)
                queries()
                lines_transposed()
                incidences(0)
                incidences(NU // 2)
                gated_keys_transposed()
            else:
                before = {}
                beside = {NU - 2: queries, NU - 1: lambda: keys(0), NU: values}
                queries()
                keys(0)
                values()
                keys(1)
            first_scores()
            with pe.Fori(0, B - 1):
                pe_units(nc, S, pe, NU, scores, transposes, product, o_slot, beside, before)
                if geometry:
                    lines_transposed()
                output(None if geometry else lambda: keys(1))
                if geometry:
                    incidences(0)
                    tail_pe(nc, S, pe, 1)
                    incidences(NU // 2)
                    gated_keys_transposed()
                    first_scores()
                else:
                    first_scores()
                    tail_pe(nc, S, pe, 1)
            pe_units(nc, S, pe, NU, scores, transposes, product, o_slot, {}, {})
            output()
            tail_pe(nc, S, pe, 1)

        @block.scalar
        def _(act):
            act.wait_ge(S.weights_ready[k], 16)

            def exps(u):
                n = len(key_range(units[u][0])) * kn
                for t in range(HU):
                    last = nc.scalar.activation(prob[:, u % 2, t * n:(t + 1) * n], S.R[:, u % 2, t * n:(t + 1) * n], ACT.Exp,
                                                bias=neg_max[:, u % 2, t:t + 1])
                return last

            def evacuate(u):
                n = len(key_range(units[u][0]))
                return nc.scalar.activation(prob_t[0:kn, u % 2, 1, 0:n, :, :].rearrange("p i t q -> p (i t q)"),
                                            S.T[0:kn, 1, 0:2 * n * P], ACT.Copy)

            if geometry:
                nc.scalar.activation(log_decay[:], part(W, TB, "decay"), ACT.Exp, scale=-1.0).then_inc(S.setup_act, 1)
                act.wait_ge(S.setup_dve, 1)
                act.sem_inc(S.setup_dve, -1)
                nc.scalar.activation(log_decay[:], log_decay[:], ACT.Ln)
                act.drain()
                for h in range(H):
                    last = nc.scalar.activation(decay_w[:, h, :], part(S.const, CONST, "steps"), ACT.Exp,
                                                scale=log_decay[:, h:h + 1])
                last.then_inc(S.setup_act, 1)

            def naturals(i):
                tt, slot = i % 4 // 2, i % 2
                if i in (4, 6):
                    return
                act.wait_ge(S.nat_full_act, 1)
                act.sem_inc(S.nat_full_act, -1)
                if i < 4:
                    nc.scalar.activation(lines[:, tt, slot, :, :].rearrange("p a n -> p (a n)"), S.R[:, slot, BANK:BANK + 384], ACT.Copy)\
                        .then_inc(S.r_free[slot], 1)
                    act.drain().then_inc(S.lines_sb, 1)
                else:
                    nc.scalar.activation(geo[:, tt, :, :, :].rearrange("p a h d -> p (a h d)"),
                                         S.R[:, slot, BANK:2 * BANK], ACT.Copy).then_inc(S.r_free[slot], 1)

            def naturals_amid(first, n):
                for i in range(first, first + n):
                    naturals(i)

            def lines_transposed():
                act.wait_ge(S.lr_full, 1)
                act.sem_inc(S.lr_full, -1)
                nc.scalar.activation(lines_read[:], S.T[:, 1, 0:T], ACT.Copy)
                for h in range(HT, H):
                    last = nc.scalar.activation(lines_own[:, h, :], S.T[:, 1, T:2 * T], ACT.Copy,
                                                scale=part(S.const, CONST, "line_head")[:, h:h + 1])
                last.then_inc(S.t_free[1], 1)

            def incidences(first):
                for u, (qt, g) in list(enumerate(units))[first:first + NU // 2]:
                    n = (qt + 1) * P
                    act.wait_ge(S.inc_full, 1)
                    act.sem_inc(S.inc_full, -1)
                    act.wait_ge(S.inc_free, 1)
                    act.sem_inc(S.inc_free, -1)
                    nc.scalar.activation(inc2[:, u % 2, 0:HU * n], S.R[:, (1 + u) % 2, 0:HU * n], ACT.Square)\
                        .then_inc(S.r_free[(1 + u) % 2], 1)
                    act.drain().then_inc(S.inc_ready, 1)

            def gates():
                act.wait_ge(S.mem_ready, 1)
                act.sem_inc(S.mem_ready, -1)
                nc.scalar.activation(mem[:], mem[:], ACT.Exp, scale=-1.0).then_inc(S.gate_exp, 1)
                act.wait_ge(S.k_full_act, 1)
                act.sem_inc(S.k_full_act, -1)
                for h in range(HT):
                    last = nc.scalar.activation(k_own[:, 1, h, :], S.T[:, 1, 0:T], ACT.Copy,
                                                scale=part(S.const, CONST, "head")[:, h:h + 1])
                last.then_inc(S.t_free[1], 1)

            def keys():
                act.wait_ge(S.k_full_act, 1)
                act.sem_inc(S.k_full_act, -1)
                act.sem_inc(S.xc_free, 1)
                for h in range(HT):
                    nc.scalar.activation(k_own[:, 1, h, :], S.R[:, 1, BANK:BANK + key_tiles * kn], ACT.Identity,
                                         bias=bk_own[:, h:h + 1], scale=part(S.const, CONST, "head")[:, h:h + 1])
                act.drain().then_inc(S.k_sb, 1)

            def attention_transposed():
                if out:
                    act.wait_ge(S.at_full, 1)
                    act.sem_inc(S.at_full, -1)
                    nc.scalar.activation(attn_t[:].rearrange("p q c t -> p (q c t)"), S.O[:, 1, :], ACT.Copy)\
                        .then_inc(S.o_free[1], 1)

            if geometry:
                naturals_amid(0, 8)
                lines_transposed()
                incidences(0)
                incidences(NU // 2)
                gates()
            else:
                act.wait_ge(S.setup_dve, 1)
                act.sem_inc(S.setup_dve, -1)
                keys()
            act_exps(S, act, exps, 0)
            beside = {}
            if geometry:
                beside = {1: lambda: naturals_amid(0, 3), 2: lambda: naturals_amid(3, 3), 3: lambda: naturals_amid(6, 2)}
            with act.Fori(0, B - 1) as b:
                act_units(nc, S, act, NU, exps, evacuate, beside)
                if geometry:
                    lines_transposed()
                    attention_transposed()
                    incidences(0)
                    tail_act(nc, S, act, 1, b)
                    incidences(NU // 2)
                    gates()
                    act_exps(S, act, exps, 0)
                else:
                    attention_transposed()
                    keys()
                    act_exps(S, act, exps, 0)
                    tail_act(nc, S, act, 1, b)
            act_units(nc, S, act, NU, exps, evacuate, {})
            attention_transposed()
            tail_act(nc, S, act, 1, B - 1)
            if geometry:
                act.wait_ge(S.inc_free, 2)
                act.sem_inc(S.inc_free, -2)

        @block.vector
        def _(dve):
            dve.wait_ge(S.weights_ready[k], 16)
            bq = part(W, TB, "bq")
            nc.vector.memset(v[:, :, :, DH16:VA16], 1.0)

            def row_max(u):
                n = len(key_range(units[u][0])) * kn
                return nc.vector.tensor_reduce(neg_max[:, u % 2, :],
                                               S.R[:, u % 2, 0:HU * n].rearrange("p (t n) -> p t n", t=HU),
                                               AX.X, ALU.max, negate=True)

            def evacuate(u):
                n = len(key_range(units[u][0]))
                return nc.vector.tensor_copy(prob_t[0:kn, u % 2, 0, 0:n, :, :].rearrange("p i t q -> p (i t q)"), S.T[0:kn, 0, 0:2 * n * P])

            def normalise(u):
                qt, g = units[u]
                o = S.O[:, o_slot(u), 0:4 * VA16].rearrange("p (t d) -> p t d", t=4)
                nc.vector.reciprocal(rec[:, u % 2, :], o[:, :, DH16])
                dve.drain()
                nc.vector.tensor_tensor(attn[:, qt, g * HU * DH16:(g + 1) * HU * DH16].rearrange("p (t d) -> p t d", t=HU),
                                        o[:, :, 0:DH16], rec[:, u % 2, :].unsqueeze(2).to_broadcast([P, 4, DH16]), ALU.mult)\
                    .then_inc(S.o_free[o_slot(u)], 1)

            if geometry:
                nc.vector.memset(line_pad[:], 0.0)
                
                dve.wait_ge(S.setup_act, 1)
                dve.sem_inc(S.setup_act, -1)
                nc.vector.tensor_scalar(log_decay[:], log_decay[:], 1.0, None, ALU.add)
                dve.drain()
                nc.vector.reciprocal(log_decay[:], log_decay[:])
                dve.drain()
                nc.vector.tensor_scalar(log_decay[:], log_decay[:], 2.0 ** -63, None, ALU.max).then_inc(S.setup_dve, 1)
                dve.wait_ge(S.setup_act, 1)
                dve.sem_inc(S.setup_act, -1)
                nc.vector.tensor_tensor(decay_w[:], decay_w[:],
                                        part(S.const, CONST, "past").unsqueeze(1).to_broadcast([P, H, T]), ALU.mult)
            dve.drain()

            def queries():
                dve.wait_ge(S.q_full, 1)
                dve.sem_inc(S.q_full, -1)
                for t in range(C):
                    last = nc.vector.tensor_scalar(q_t[:, t, :], S.R[:, 0, t * T:(t + 1) * T], bq[:, t:t + 1], scale,
                                                   ALU.add, ALU.mult)
                last.then_inc(S.r_free[0], 1)
                if geometry:
                    dve.sem_inc(S.xc_free, 1)

            own = part(S.const, CONST, "head").unsqueeze(2).to_broadcast([P, HT, key_tiles * kn])

            def keys():
                dve.wait_ge(S.k_full, 1)
                dve.sem_inc(S.k_full, -1)
                nc.vector.scalar_tensor_tensor(
                    k_own[:, 0, :, :], S.R[:, 1, 0:key_tiles * kn].unsqueeze(1).to_broadcast([P, HT, key_tiles * kn]),
                    part(W, TB, "bk")[:, 0:1], own, ALU.add, ALU.mult).then_inc(S.r_free[1], 1)

            def gated_keys():
                dve.wait_ge(S.k_full, 1)
                dve.sem_inc(S.k_full, -1)
                nc.vector.tensor_tensor(k_own[:, 0, :, :], S.T[:, 0, 0:T].unsqueeze(1).to_broadcast([P, HT, T]), own, ALU.mult)\
                    .then_inc(S.t_free[0], 1)

            def values():
                dve.wait_ge(S.v_full, 1)
                dve.sem_inc(S.v_full, -1)
                bv = part(W, TB, "bv").rearrange("p (h d) -> p h d", h=H)
                for i in range(key_tiles):
                    last = nc.vector.tensor_tensor(v[0:kn, i, :, 0:DH16],
                                                   S.T[0:kn, 0, i * D:(i + 1) * D].rearrange("p (h d) -> p h d", h=H),
                                                   bv[0:kn], ALU.add)
                last.then_inc(S.t_free[0], 1)

            def naturals(tt):
                dve.wait_ge(S.nat_full, 1)
                dve.sem_inc(S.nat_full, -1)
                nc.vector.tensor_tensor(kv[:, tt, :, :, :].rearrange("p a h d -> p (a h d)"), S.R[:, 0, BANK:2 * BANK],
                                        part(W, TB, "nat_b"), ALU.add).then_inc(S.r_free[0], 1)

            def line_norms():
                dve.wait_ge(S.lines_sb, 4)
                dve.sem_inc(S.lines_sb, -4)
                for tt in range(TT):
                    nc.vector.tensor_tensor(prods[:, tt, :, :, :].rearrange("p w a n -> p w (a n)"),
                                            lines[:, tt, :, 0, :], lines[:, tt, :, 1, :], ALU.mult)
                dve.drain()
                flat = line[:].rearrange("p t w h i -> p (t w) (h i)")
                both = prods[:].rearrange("p t w a n -> p (t w) a n")
                nc.vector.tensor_tensor(flat, both[:, :, 0, :], both[:, :, 1, :], ALU.subtract)
                dve.drain()
                nc.vector.tensor_tensor(both[:, :, 0, :], flat, flat, ALU.mult)
                dve.drain()
                nc.vector.tensor_reduce(norm2[:].rearrange("p t w h -> p (t w) h"),
                                        both[:, :, 0, :].rearrange("p a (h i) -> p a h i", i=6), AX.X, ALU.add)\
                    .then_inc(S.norm_sum, 1)

            def unit_lines():
                dve.wait_ge(S.norm_root, 1)
                dve.sem_inc(S.norm_root, -1)
                nc.vector.tensor_scalar(norm2[:], norm2[:], 1e-12, None, ALU.max)
                dve.drain()
                nc.vector.reciprocal(norm2[:], norm2[:])
                dve.drain()
                for tt in range(TT):
                    for rw in range(2):
                        last = nc.vector.tensor_tensor(line_pad[:, tt, rw, :, 0:6], line[:, tt, rw, :, :],
                                                       norm2[:, tt, rw, :].unsqueeze(2).to_broadcast([P, H, 6]), ALU.mult)
                last.then_inc(S.line_ready, 1)

            def lines_to_heads():
                dve.wait_ge(S.lt_full, 1)
                dve.sem_inc(S.lt_full, -1)
                nc.vector.tensor_tensor(lines_own[:, 0:HT, :], S.T[:, 0, 0:T].unsqueeze(1).to_broadcast([P, HT, T]),
                                        part(S.const, CONST, "line_head")[:, 0:HT].unsqueeze(2).to_broadcast([P, HT, T]), ALU.mult)\
                    .then_inc(S.t_free[0], 1)

            def gates():
                for u, (qt, g) in enumerate(units):
                    n = (qt + 1) * P
                    dve.wait_ge(S.inc_ready, 1)
                    dve.sem_inc(S.inc_ready, -1)
                    for t in range(HU):
                        h = g * HU + t
                        last = nc.vector.tensor_tensor_reduce(
                            inc2[:, u % 2, t * n:(t + 1) * n], inc2[:, u % 2, t * n:(t + 1) * n], decay_w[:, h, T - n:T], 1.0, 0.0,
                            ALU.mult, ALU.add, mem[:, qt, h:h + 1])
                    last.then_inc(S.inc_free, 1)
                dve.drain()
                nc.vector.tensor_tensor(mem[:], mem[:],
                                        part(W, TB, "mem_scale").unsqueeze(1).to_broadcast([P, TT, H]), ALU.mult)\
                    .then_inc(S.mem_ready, 1)
                dve.wait_ge(S.gate_exp, 1)
                dve.sem_inc(S.gate_exp, -1)
                nc.vector.tensor_scalar(mem[:], mem[:], 1.0, None, ALU.add)
                dve.drain()
                nc.vector.reciprocal(mem[:], mem[:])
                dve.drain()
                nc.vector.tensor_scalar(mem[:], mem[:], part(W, TB, "kv_gate"), None, ALU.mult)
                dve.drain()
                for a in range(2):
                    for tt in range(TT):
                        gate = mem[:, tt, :].unsqueeze(2).to_broadcast([P, H, DH16])
                        nc.vector.tensor_tensor(geo[:, tt, a, :, :], geo[:, tt, a, :, :], gate, ALU.mult)
                dve.drain()
                for tt in range(TT):
                    nc.vector.tensor_tensor(v[:, tt, :, 0:DH16], kv[:, tt, 1, :, :], geo[:, tt, 1, :, :], ALU.add)
                for tt in range(TT):
                    last = nc.vector.tensor_tensor(kv[:, tt, 0, :, :], kv[:, tt, 0, :, :], geo[:, tt, 0, :, :], ALU.add)
                last.then_inc(S.k_nat_ready, 1)

            def output(meanwhile=None):
                if out:
                    dve_output(nc, S, dve, 0, meanwhile)
                else:
                    dve.drain()
                    dve.wait_ge(S.xres_ready, 1)
                    dve.sem_inc(S.xres_ready, -1)
                    nc.vector.tensor_tensor(S.ysb[:], attn[:], S.xres[:], ALU.add)
                    dve.drain().then_inc(S.xres_free, 1)
                    tail_dve(nc, S, dve, meanwhile)

            def first_maxima():
                dve_maxima(S, dve, row_max, 0)

            if geometry:
                for tt in range(TT):
                    naturals(tt)
                queries()
                line_norms()
                unit_lines()
                lines_to_heads()
                gates()
                gated_keys()
                beside = {1: lambda: naturals(0), 2: lambda: naturals(1), 3: line_norms, NU - 2: queries, NU - 1: unit_lines}
            else:
                beside = {NU - 2: queries}
                queries()
                nc.vector.tensor_scalar(bk_own[:], part(S.const, CONST, "head"), part(W, TB, "bk")[:, 1:2], None, ALU.mult)\
                    .then_inc(S.setup_dve, 1)
                keys()
                values()
            first_maxima()
            with dve.Fori(0, B - 1):
                dve_units(nc, S, dve, NU, row_max, evacuate, normalise, beside)
                if geometry:
                    lines_to_heads()
                    output()
                    gates()
                    gated_keys()
                    first_maxima()
                else:
                    values()
                    keys()
                    output(first_maxima)
            dve_units(nc, S, dve, NU, row_max, evacuate, normalise, {})
            output()

        @block.gpsimd
        def _(pool):
            pool.wait_ge(S.weights_ready[k], 16)

            def roots():
                if geometry:
                    pool.wait_ge(S.norm_sum, 1)
                    pool.sem_inc(S.norm_sum, -1)
                    flat = norm2[:].rearrange("p t w h -> p (t w h)")
                    nc.gpsimd.tensor_tensor(flat, flat, part(S.const, CONST, "half"), ALU.pow).then_inc(S.norm_root, 1)

            bias = part(W, TB, "bo") if out else None
            if geometry:
                pool.sem_inc(S.inc_free, 2)
                pool.wait_ge(S.x_ready, 32)
            roots()
            pool_residual(nc, S, pool, 0, bias)
            with pool.Fori(0, B - 1) as b:
                roots()
                tail_pool(nc, S, pool, b)
                pool_residual(nc, S, pool, b + 1, bias)
            tail_pool(nc, S, pool, B - 1)



def perceiver(nc, S, k):
    W, TB = S.arena[k % 2], PACK[k]
    HP = H // 2
    units = [(qt, hp) for qt in range(TT) for hp in range(HP)]
    NU = len(units)
    LATENTS = 4
    KC = [(0, P, CTX), (1, P, CTX + P), (2, CTX, 0)]
    LC = [(t, min(P, B * CTX - t * P)) for t in range(-(-B * CTX // P))]

    def o_slot(u):
        return u % 2

    with ExitStack() as ctx:
        def sb(name, shape, dt=F32):
            return ctx.enter_context(nc.sbuf_tensor(f"{name}_{k}", shape, dt))

        ctx_n = sb("ctx_n", [P, len(LC), D])
        ctx_nt = sb("ctx_nt", [P, C, B * CTX])
        cst = sb("cst", [P, len(LC), 6])
        cmv = sb("cmv", [P, len(LC), 2])
        crs = sb("crs", [P, len(LC)])
        lat = sb("lat", [P, TT, D])
        keys_in = sb("keys_in", [P, C, XK])
        q_t = sb("q_t", [P, HP, T])
        k_t = sb("k_t", [P, HP, XK])
        v = sb("v", [P, 3, H, VA64])
        prob = sb("prob", [P, 2, 2, XK])
        prob_t = sb("prob_t", [P, 2, 2, 3, P])
        neg_max = sb("neg_max", [P, 2, 2])
        rec = sb("rec", [P, 2, 2])
        attn = sb("attn", [P, TT, XI])
        attn_t = sb("attn_t", [P, XI // P, T])
        block = ctx.enter_context(nc.Block())

        @block.sync
        def _(sp):
            for t, n in LC:
                sp.dma_start(ctx_n[0:n, t, :], S.ctx_dram[t * P:t * P + n, :]).then_inc(S.ctx_ready, 16)

            def context(b):
                sp.wait_ge(S.ctx_nt_ready, 1)
                sp.sem_inc(S.ctx_nt_ready, -1)
                sp.dma_start(keys_in[:, :, 0:CTX], ctx_nt[:, :, bass.ds(b * CTX, CTX)]).then_inc(S.xc_ready, 16)

            context(0)
            prefetch(nc, S, sp, k + 1)
            with sp.Fori(1, B) as b:
                context(b)
            sp.wait_ge(S.ctx_nt_ready, 1)
            sp.sem_inc(S.ctx_nt_ready, -1)

        @block.tensor
        def _(pe):
            wq, wkv, wo = part(W, TB, "wq", C), part(W, TB, "wkv", C), part(W, TB, "wo", XI // P)
            pe.wait_ge(S.weights_ready[k], 16)

            def context():
                pe.wait_ge(S.ctx_norm_ready, 1)
                pe.sem_inc(S.ctx_norm_ready, -1)
                for t, n in LC:
                    pe.wait_ge(S.o_free[t % 2], 1)
                    pe.sem_inc(S.o_free[t % 2], -1)
                    for c in range(C):
                        last = nc.tensor.transpose(S.O[:, t % 2, c * P:c * P + n], ctx_n[0:n, t, c * P:(c + 1) * P], S.ident[0:n, 0:n])
                    last.then_inc(S.yt_full, 1)

            def scores(u):
                qt, hp = units[u]
                for i in range(2):
                    last = nc.tensor.matmul(S.R[:, u % 2, i * BANK:i * BANK + XK],
                                            q_t[XD * i:XD * (i + 1), hp, qt * P:(qt + 1) * P],
                                            k_t[XD * i:XD * (i + 1), hp, :], start=True, stop=True)
                return last

            def transposes(u, i):
                if u == 0 and i == 0:
                    pe.wait_ge(S.t_free[0], 1)
                    pe.sem_inc(S.t_free[0], -1)
                    pe.wait_ge(S.t_free[1], 1)
                    pe.sem_inc(S.t_free[1], -1)
                if u >= NU - 2 and i == 0:
                    pe.sem_inc(S.r_free[u % 2], 1)
                for c, n, first in KC:
                    last = nc.tensor.transpose(S.T[0:n, i, c * P:(c + 1) * P], prob[:, u % 2, i, first:first + n], S.ident)
                return last

            def product(u):
                qt, hp = units[u]
                if u == NU - 1:
                    pe.sem_inc(S.t_free[0], 1)
                    pe.sem_inc(S.t_free[1], 1)
                for i in range(2):
                    for c, n, first in KC:
                        last = nc.tensor.matmul(S.O[:, o_slot(u), i * VA64:(i + 1) * VA64], prob_t[0:n, u % 2, i, c, :],
                                                v[0:n, c, 2 * hp + i, :], start=(c == 0), stop=(c == len(KC) - 1))
                return last

            def latents():
                pe.wait_ge(S.lat_ready, 1)
                pe.sem_inc(S.lat_ready, -1)
                for tt in range(TT):
                    pe.wait_ge(S.o_free[tt], 1)
                    pe.sem_inc(S.o_free[tt], -1)
                    for c in range(C):
                        last = nc.tensor.transpose(S.O[:, tt, c * P:(c + 1) * P], lat[:, tt, c * P:(c + 1) * P], S.ident)
                    last.then_inc(S.lt_full, 1)

            def queries(j):
                if j == 0:
                    pe.wait_ge(S.lat_t_ready, 1)
                    pe.sem_inc(S.lat_t_ready, -1)
                pe.wait_ge(S.r_free[j], 1)
                pe.sem_inc(S.r_free[j], -1)
                for i in range(4):
                    for c in range(C):
                        last = nc.tensor.matmul(S.R[:, j, i * T:(i + 1) * T], wq[:, c, (4 * j + i) * P:(4 * j + i + 1) * P],
                                                keys_in[:, c, CTX:XK], start=(c == 0), stop=(c == C - 1))
                last.then_inc(S.q_full, 1)

            def context_columns():
                pe.wait_ge(S.xc_ready, 16)
                pe.sem_inc(S.xc_ready, -16)

            def keys(first):
                for j in range(first, first + 2):
                    pe.wait_ge(S.r_free[j % 2], 1)
                    pe.sem_inc(S.r_free[j % 2], -1)
                    for i in range(2):
                        for c in range(C):
                            last = nc.tensor.matmul(S.R[:, j % 2, i * BANK:i * BANK + XK], wkv[:, c, (2 * j + i) * P:(2 * j + i + 1) * P],
                                                    keys_in[:, c, :], start=(c == 0), stop=(c == C - 1))
                    last.then_inc(S.k_full, 1)

            def values():
                for kc, n, first in KC:
                    pe.wait_ge(S.r_free[kc % 2], 1)
                    pe.sem_inc(S.r_free[kc % 2], -1)
                    for hv in range(2):
                        for c in range(C):
                            last = nc.tensor.matmul(S.R[0:n, kc % 2, hv * BANK:(hv + 1) * BANK], keys_in[:, c, first:first + n],
                                                    wkv[:, c, XI + hv * BANK:XI + (hv + 1) * BANK], start=(c == 0), stop=(c == C - 1))
                    last.then_inc(S.v_full, 1)

            def attention_transposed():
                pe.wait_ge(S.o_free[0], 1)
                pe.sem_inc(S.o_free[0], -1)
                pe.wait_ge(S.o_free[1], 1)
                pe.sem_inc(S.o_free[1], -1)
                for j in range(4):
                    pe.wait_ge(S.t_free[j % 2], 1)
                    pe.sem_inc(S.t_free[j % 2], -1)
                    for c in range(2):
                        for qt in range(TT):
                            last = nc.tensor.transpose(S.T[:, j % 2, (c * TT + qt) * P:(c * TT + qt + 1) * P],
                                                       attn[:, qt, (2 * j + c) * P:(2 * j + c + 1) * P], S.ident)
                    last.then_inc(S.at_full, 1)

            def output():
                pe.wait_ge(S.t_free[0], 1)
                pe.sem_inc(S.t_free[0], -1)
                pe.wait_ge(S.t_free[1], 1)
                pe.sem_inc(S.t_free[1], -1)
                pe.sem_inc(S.t_free[0], 1)
                pe.sem_inc(S.t_free[1], 1)
                for qt in range(TT):
                    for c in range(XI // P):
                        last = nc.tensor.matmul(S.O[:, 0, qt * D:(qt + 1) * D], attn_t[:, c, qt * P:(qt + 1) * P], wo[:, c, :],
                                                start=(c == 0), stop=(c == XI // P - 1))
                last.then_inc(S.y_full, 1)

            def first_scores():
                pe.wait_ge(S.r_free[0], 1)
                pe.sem_inc(S.r_free[0], -1)
                pe.wait_ge(S.r_free[1], 1)
                pe.sem_inc(S.r_free[1], -1)
                pe.wait_ge(S.k_sb, 1)
                pe.sem_inc(S.k_sb, -1)
                scores(0).then_inc(S.s_full, 1)
                scores(1).then_inc(S.s_full, 1)

            beside = {LATENTS + 2: latents, NU - 2: lambda: queries(0), NU - 1: lambda: queries(1), NU: lambda: (context_columns(), keys(0))}
            context()
            latents()
            queries(0)
            queries(1)
            context_columns()
            keys(0)
            keys(2)
            values()
            first_scores()
            with pe.Fori(0, B - 1):
                pe_units(nc, S, pe, NU, scores, transposes, product, o_slot, beside)
                attention_transposed()
                keys(2)
                output()
                values()
                first_scores()
                tail_pe(nc, S, pe, 1)
            pe_units(nc, S, pe, NU, scores, transposes, product, o_slot, {})
            attention_transposed()
            output()
            tail_pe(nc, S, pe, 1)

        @block.scalar
        def _(act):
            act.wait_ge(S.weights_ready[k], 16)

            def exps(u):
                for i in range(2):
                    last = nc.scalar.activation(prob[:, u % 2, i, :], S.R[:, u % 2, i * BANK:i * BANK + XK], ACT.Exp,
                                                bias=neg_max[:, u % 2, i:i + 1])
                return last

            def evacuate(u):
                nc.scalar.activation(prob_t[:, u % 2, 1, 0:2, :].rearrange("p c q -> p (c q)"), S.T[:, 1, 0:2 * P], ACT.Copy)
                return nc.scalar.activation(prob_t[0:CTX, u % 2, 1, 2, :], S.T[0:CTX, 1, 2 * P:3 * P], ACT.Copy)

            def latents():
                for tt in range(TT):
                    act.wait_ge(S.lt_full, 1)
                    act.sem_inc(S.lt_full, -1)
                    nc.scalar.activation(keys_in[:, :, CTX + tt * P:CTX + (tt + 1) * P],
                                         S.O[:, tt, 0:2 * P].rearrange("p (c t) -> p c t", c=C), ACT.Copy)\
                        .then_inc(S.o_free[tt], 1)
                act.drain().then_inc(S.lat_t_ready, 1)

            def keys(first):
                for j in range(first, first + 2):
                    act.wait_ge(S.k_full, 1)
                    act.sem_inc(S.k_full, -1)
                    nc.scalar.activation(k_t[:, 2 * j:2 * j + 2, :],
                                         S.R[:, j % 2, :].rearrange("p (i n) -> p i n", i=2)[:, :, 0:XK], ACT.Copy)\
                        .then_inc(S.r_free[j % 2], 1)
                if first:
                    act.drain().then_inc(S.k_sb, 1)

            def attention_transposed():
                for j in range(4):
                    act.wait_ge(S.at_full, 1)
                    act.sem_inc(S.at_full, -1)
                    nc.scalar.activation(attn_t[:, 2 * j:2 * j + 2, :], S.T[:, j % 2, :].rearrange("p (c t) -> p c t", c=2),
                                         ACT.Copy).then_inc(S.t_free[j % 2], 1)

            for t, n in LC:
                act.wait_ge(S.yt_full, 1)
                act.sem_inc(S.yt_full, -1)
                last = nc.scalar.activation(ctx_nt[:, :, t * P:t * P + n],
                                            S.O[:, t % 2, 0:2 * P].rearrange("p (c t) -> p c t", c=C)[:, :, 0:n], ACT.Copy)
                last.then_inc(S.o_free[t % 2], 1)
            act.drain().then_inc(S.ctx_nt_ready, 1)
            latents()
            keys(0)
            keys(2)
            act_exps(S, act, exps, 0)
            with act.Fori(0, B - 1) as b:
                act_units(nc, S, act, NU, exps, evacuate, {LATENTS + 3: latents})
                keys(0)
                attention_transposed()
                keys(2)
                act_exps(S, act, exps, 0)
                tail_act(nc, S, act, 1, b)
            act_units(nc, S, act, NU, exps, evacuate, {})
            attention_transposed()
            tail_act(nc, S, act, 1, B - 1)

        @block.vector
        def _(dve):
            dve.wait_ge(S.weights_ready[k], 16)
            nc.vector.memset(v[:, :, :, XD:VA64], 1.0)
            def row_max(u):
                return nc.vector.tensor_reduce(neg_max[:, u % 2, :],
                                               S.R[:, u % 2, :].rearrange("p (i n) -> p i n", i=2)[:, :, 0:XK],
                                               AX.X, ALU.max, negate=True)

            def evacuate(u):
                nc.vector.tensor_copy(prob_t[:, u % 2, 0, 0:2, :].rearrange("p c q -> p (c q)"), S.T[:, 0, 0:2 * P])
                return nc.vector.tensor_copy(prob_t[0:CTX, u % 2, 0, 2, :], S.T[0:CTX, 0, 2 * P:3 * P])

            def normalise(u):
                qt, hp = units[u]
                o = S.O[:, o_slot(u), 0:2 * VA64].rearrange("p (i d) -> p i d", i=2)
                nc.vector.reciprocal(rec[:, u % 2, :], o[:, :, XD])
                dve.drain()
                nc.vector.tensor_tensor(attn[:, qt, hp * P:(hp + 1) * P].rearrange("p (i d) -> p i d", i=2),
                                        o[:, :, 0:XD], rec[:, u % 2, :].unsqueeze(2).to_broadcast([P, 2, XD]), ALU.mult)\
                    .then_inc(S.o_free[o_slot(u)], 1)

            def x_of(b):
                return S.x_nat[:, bass.ds(b * TT, TT), :]

            def latent_statistics(b):
                for tt in range(TT):
                    nc.vector.bn_stats(S.bst[:, tt, :], S.x_nat[:, bass.ds(b * TT + tt, 1), :].rearrange("p a d -> p (a d)"))
                dve.drain()
                for tt in range(TT):
                    last = nc.vector.bn_aggr(S.mv[:, tt, :], S.bst[:, tt, :])
                last.then_inc(S.ln_stat, 1)

            def latents(b):
                dve.wait_ge(S.ln_rstd, 1)
                dve.sem_inc(S.ln_rstd, -1)
                for tt in range(TT):
                    last = nc.vector.tensor_scalar(lat[:, tt, :], S.x_nat[:, bass.ds(b * TT + tt, 1), :].rearrange("p a d -> p (a d)"),
                                                   S.mv[:, tt, 0:1], S.rstd[:, tt:tt + 1], ALU.subtract, ALU.mult)
                for op, name in ((ALU.mult, "lat_w"), (ALU.add, "lat_b")):
                    dve.drain()
                    last = nc.vector.tensor_tensor(lat[:], lat[:], part(W, TB, name).unsqueeze(1).to_broadcast([P, TT, D]), op)
                last.then_inc(S.lat_ready, 1)

            def queries(j):
                dve.wait_ge(S.q_full, 1)
                dve.sem_inc(S.q_full, -1)
                nc.vector.tensor_scalar(q_t[:, 4 * j:4 * j + 4, :].rearrange("p i t -> p (i t)"), S.R[:, j, :],
                                        XD ** -0.5, None, ALU.mult).then_inc(S.r_free[j], 1)

            def values():
                for kc, n, first in KC:
                    dve.wait_ge(S.v_full, 1)
                    dve.sem_inc(S.v_full, -1)
                    nc.vector.tensor_copy(v[0:n, kc, :, 0:XD], S.R[0:n, kc % 2, :].rearrange("p (h d) -> p h d", h=H))\
                        .then_inc(S.r_free[kc % 2], 1)
                dve.sem_inc(S.ctx_nt_ready, 1)

            def output(b, meanwhile=None):
                dve.wait_ge(S.y_full, 1)
                dve.sem_inc(S.y_full, -1)
                nc.vector.tensor_tensor(S.ysb[:], S.O[:, 0, :].rearrange("p (t d) -> p t d", t=TT), x_of(b), ALU.add)\
                    .then_inc(S.o_free[0], 1)
                dve.drain()
                tail_dve(nc, S, dve, meanwhile)

            dve.wait_ge(S.ctx_ready, 16 * len(LC))
            dve.sem_inc(S.ctx_ready, -(16 * len(LC)))
            for t, n in LC:
                nc.vector.bn_stats(cst[0:n, t, :], ctx_n[0:n, t, :])
            nc.vector.memset(cmv[:], 1.0)
            dve.drain()
            for t, n in LC:
                last = nc.vector.bn_aggr(cmv[0:n, t, :], cst[0:n, t, :])
            last.then_inc(S.ctx_stat, 1)
            dve.wait_ge(S.ctx_rstd, 1)
            dve.sem_inc(S.ctx_rstd, -1)
            for t, n in LC:
                nc.vector.tensor_scalar(ctx_n[0:n, t, :], ctx_n[0:n, t, :], cmv[0:n, t, 0:1], crs[0:n, t:t + 1],
                                        ALU.subtract, ALU.mult)
            for op, name in ((ALU.mult, "ctx_w"), (ALU.add, "ctx_b")):
                dve.drain()
                for t, n in LC:
                    last = nc.vector.tensor_tensor(ctx_n[0:n, t, :], ctx_n[0:n, t, :], part(W, TB, name)[0:n, :], op)
            last.then_inc(S.ctx_norm_ready, 1)
            latent_statistics(0)
            latents(0)
            queries(0)
            queries(1)
            values()
            dve_maxima(S, dve, row_max, 0)
            with dve.Fori(0, B - 1) as b:
                dve_units(nc, S, dve, NU, row_max, evacuate, normalise,
                          {LATENTS: lambda: latent_statistics(b + 1), LATENTS + 1: lambda: latents(b + 1),
                           NU - 2: lambda: queries(0), NU - 1: lambda: queries(1)})
                output(b, values)
                dve_maxima(S, dve, row_max, 0)
            dve_units(nc, S, dve, NU, row_max, evacuate, normalise, {})
            output(B - 1)

        @block.gpsimd
        def _(pool):
            pool.wait_ge(S.weights_ready[k], 16)
            pool.wait_ge(S.ctx_stat, 1)
            pool.sem_inc(S.ctx_stat, -1)
            nc.gpsimd.tensor_scalar(crs[:], cmv[:, :, 1], EPS, None, ALU.add)
            pool.drain()
            nc.gpsimd.tensor_tensor(crs[:], crs[:], part(S.const, CONST, "neg_half")[:, 0:len(LC)], ALU.pow).then_inc(S.ctx_rstd, 1)
            pool_rstd(nc, S, pool)
            with pool.Fori(0, B - 1) as b:
                pool_rstd(nc, S, pool)
                tail_pool(nc, S, pool, b)
            tail_pool(nc, S, pool, B - 1)



def pe_logits(nc, S, pe, w, n):
    pe.wait_ge(S.o_free[0], 1)
    pe.sem_inc(S.o_free[0], -1)
    for tt in range(B * TT):
        for c in range(C):
            last = nc.tensor.matmul(S.O[:, 0, tt * 16:tt * 16 + n], S.x_t[:, c, tt * P:(tt + 1) * P], w[:, c, :],
                                    start=(c == 0), stop=(c == C - 1))
    last.then_inc(S.q_full, 1)


def dve_top(nc, S, dve, gate, prob, top, index, index_f, pick, n, experts):
    NT = B * TT
    for tt in range(NT):
        nc.vector.max(top[:, tt, :], prob[:, tt, :])
    dve.drain()
    for tt in range(NT):
        nc.vector.max_index(index[:, tt, :], top[:, tt, :], prob[:, tt, :])
    dve.drain()
    nc.vector.tensor_copy(index_f[:], index[:])
    dve.drain()
    each = [P, NT, experts]
    for j in range(n):
        nc.vector.tensor_tensor(pick[:, :, j, :], part(S.const, CONST, "iota")[:, 0:experts].unsqueeze(1).to_broadcast(each),
                                index_f[:, :, j:j + 1].to_broadcast(each), ALU.is_equal)
    dve.drain()
    for j in range(n):
        nc.vector.tensor_tensor(pick[:, :, j, :], pick[:, :, j, :], prob[:], ALU.mult)
    dve.drain()
    nc.vector.tensor_reduce(gate[:], pick[:].rearrange("p t j e -> p t e j"), AX.X, ALU.add)
    dve.drain()


def x_tile(S, b, tt):
    return S.x_nat[:, bass.ds(b * TT + tt, 1), :].rearrange("p a d -> p (a d)")


def moe_silu(nc, S, k):
    W, TB = S.arena[k % 2], PACK[k]
    E, FC, NT = 8, 2, B * TT
    with ExitStack() as ctx:
        def sb(name, shape, dt=F32):
            return ctx.enter_context(nc.sbuf_tensor(f"{name}_{k}", shape, dt))

        prob = sb("prob", [P, NT, E])
        total = sb("total", [P, NT])
        shared_gate = sb("shared_gate", [P, NT])
        top = sb("top", [P, NT, 8])
        index = sb("index", [P, NT, 8], U32)
        index_f = sb("index_f", [P, NT, 8])
        pick = sb("pick", [P, NT, 2, E])
        gate = sb("gate", [P, NT, E])
        gate_b = sb("gate_b", [P, TT, E])
        shared_b = sb("shared_b", [P, TT])
        hid = sb("hid", [P, 2, FC * T])
        sg = sb("sg", [P, FC * T])
        block = ctx.enter_context(nc.Block())

        @block.sync
        def _(sp):
            prefetch(nc, S, sp, k + 1)

        @block.tensor
        def _(pe):
            w1 = part(W, TB, "w1", E * C)
            w2 = part(W, TB, "w2", E * FC)
            gu, down = part(W, TB, "gate_up", C), part(W, TB, "down", FC)
            pe.wait_ge(S.weights_ready[k], 16)

            def hidden(e, b):
                pe.wait_ge(S.r_free[e % 2], 1)
                pe.sem_inc(S.r_free[e % 2], -1)
                for f in range(FC):
                    for c in range(C):
                        w = w1[:, e * C + c, :] if e < E else gu[:, c, (e - E) * D:(e - E + 1) * D]
                        last = nc.tensor.matmul(S.R[:, e % 2, f * T:(f + 1) * T], w[:, f * P:(f + 1) * P],
                                                S.x_t[:, c, bass.ds(b * T, T)], start=(c == 0), stop=(c == C - 1))
                last.then_inc(S.h_full if e <= E else S.h_full_up, 1)

            def outputs(src, w, slot):
                pe.wait_ge(S.o_free[slot], 1)
                pe.sem_inc(S.o_free[slot], -1)
                for tt in range(TT):
                    for f in range(FC):
                        last = nc.tensor.matmul(S.O[:, slot, tt * D:(tt + 1) * D], src[:, f * T + tt * P:f * T + (tt + 1) * P],
                                                w[:, f, :], start=(f == 0), stop=(f == FC - 1))
                last.then_inc(S.o_full, 1)

            def expert(e):
                pe.wait_ge(S.h_ready, 1)
                pe.sem_inc(S.h_ready, -1)
                outputs(hid[:, e % 2, :], w2[:, e * FC:(e + 1) * FC, :], (e + 1) % 2)

            def others(b):
                for e in range(2, E + 2):
                    hidden(e, b)
                    if e <= E:
                        expert(e - 1)

            def shared():
                pe.wait_ge(S.sh_ready, 1)
                pe.sem_inc(S.sh_ready, -1)
                outputs(sg, down, 1)

            def tail():
                pe.wait_ge(S.o_free[0], 1)
                pe.sem_inc(S.o_free[0], -1)
                tail_pe(nc, S, pe, 0)

            pe_logits(nc, S, pe, part(W, TB, "router", C), E + 1)
            hidden(0, 0)
            hidden(1, 0)
            expert(0)
            with pe.Fori(0, B - 1) as b:
                others(b)
                hidden(0, b + 1)
                shared()
                hidden(1, b + 1)
                expert(0)
                tail()
            others(B - 1)
            shared()
            tail()

        @block.scalar
        def _(act):
            act.wait_ge(S.weights_ready[k], 16)
            act.sem_inc(S.hid_free, 2)
            act.wait_ge(S.max_ready, 1)
            act.sem_inc(S.max_ready, -1)
            nc.scalar.activation(prob[:], prob[:], ACT.Exp)
            nc.scalar.activation(shared_gate[:], shared_gate[:], ACT.Exp, scale=-1.0)
            act.drain().then_inc(S.p_ready, 1)

            def silu(e):
                act.wait_ge(S.h_full, 1)
                act.sem_inc(S.h_full, -1)
                if e < E:
                    act.wait_ge(S.hid_free, 1)
                    act.sem_inc(S.hid_free, -1)
                    nc.scalar.activation(hid[:, e % 2, :], S.R[:, e % 2, 0:FC * T], ACT.Silu).then_inc(S.r_free[e % 2], 1)
                    act.drain().then_inc(S.h_ready, 1)
                else:
                    nc.scalar.activation(sg[:], S.R[:, e % 2, 0:FC * T], ACT.Silu).then_inc(S.r_free[e % 2], 1)
                    act.drain().then_inc(S.sg_ready, 1)

            silu(0)
            silu(1)
            with act.Fori(0, B - 1) as b:
                for e in range(2, E + 1):
                    silu(e)
                silu(0)
                silu(1)
                tail_act(nc, S, act, 0, b)
            for e in range(2, E + 1):
                silu(e)
            tail_act(nc, S, act, 0, B - 1)
            act.wait_ge(S.hid_free, 2)
            act.sem_inc(S.hid_free, -2)

        @block.vector
        def _(dve):
            each = [P, NT, E]
            dve.wait_ge(S.q_full, 1)
            dve.sem_inc(S.q_full, -1)
            logits = S.O[:, 0, 0:NT * 16].rearrange("p (t e) -> p t e", t=NT)
            nc.vector.tensor_reduce(total[:], logits[:, :, 0:E], AX.X, ALU.max)
            nc.vector.tensor_copy(shared_gate[:], logits[:, :, E])
            dve.drain()
            nc.vector.tensor_tensor(prob[:], logits[:, :, 0:E], total[:].unsqueeze(2).to_broadcast(each), ALU.subtract).then_inc(S.o_free[0], 1)
            dve.drain().then_inc(S.max_ready, 1)
            dve.wait_ge(S.p_ready, 1)
            dve.sem_inc(S.p_ready, -1)
            nc.vector.tensor_reduce(total[:], prob[:], AX.X, ALU.add)
            nc.vector.tensor_scalar(shared_gate[:], shared_gate[:], 1.0, None, ALU.add)
            dve.drain()
            nc.vector.reciprocal(total[:], total[:])
            nc.vector.reciprocal(shared_gate[:], shared_gate[:])
            dve.drain()
            nc.vector.tensor_tensor(prob[:], prob[:], total[:].unsqueeze(2).to_broadcast(each), ALU.mult)
            dve.drain()
            dve_top(nc, S, dve, gate, prob, top, index, index_f, pick, 2, E)

            def batch(b):
                nc.vector.tensor_copy(gate_b[:], gate[:, bass.ds(b * TT, TT), :])
                nc.vector.tensor_copy(shared_b[:], shared_gate[:, bass.ds(b * TT, TT)])
                dve.drain()
                for e in range(E):
                    dve.wait_ge(S.o_full, 1)
                    dve.sem_inc(S.o_full, -1)
                    dve.sem_inc(S.hid_free, 1)
                    for tt in range(TT):
                        last = nc.vector.scalar_tensor_tensor(S.ysb[:, tt, :], S.O[:, (e + 1) % 2, tt * D:(tt + 1) * D], gate_b[:, tt, e:e + 1],
                                                              x_tile(S, b, tt) if e == 0 else S.ysb[:, tt, :], ALU.mult, ALU.add)
                    last.then_inc(S.o_free[(e + 1) % 2], 1)
                    dve.drain()
                dve.wait_ge(S.sg_ready, 1)
                dve.sem_inc(S.sg_ready, -1)
                dve.wait_ge(S.h_full_up, 1)
                dve.sem_inc(S.h_full_up, -1)
                nc.vector.tensor_tensor(sg[:], sg[:], S.R[:, (E + 1) % 2, 0:FC * T], ALU.mult).then_inc(S.r_free[(E + 1) % 2], 1)
                dve.drain().then_inc(S.sh_ready, 1)
                dve.wait_ge(S.o_full, 1)
                dve.sem_inc(S.o_full, -1)
                for tt in range(TT):
                    last = nc.vector.scalar_tensor_tensor(S.ysb[:, tt, :], S.O[:, 1, tt * D:(tt + 1) * D], shared_b[:, tt:tt + 1],
                                                          S.ysb[:, tt, :], ALU.mult, ALU.add)
                last.then_inc(S.o_free[1], 1)
                dve.drain()
                tail_dve(nc, S, dve)

            with dve.Fori(0, B) as b:
                batch(b)

        @block.gpsimd
        def _(pool):
            with pool.Fori(0, B) as b:
                tail_pool(nc, S, pool, b)


def moe_relu(nc, S, k):
    W, TB = S.arena[k % 2], PACK[k]
    E, EH, CHOSEN, NT = 16, 64, 4, B * TT
    HC = E * EH // P
    with ExitStack() as ctx:
        def sb(name, shape, dt=F32):
            return ctx.enter_context(nc.sbuf_tensor(f"{name}_{k}", shape, dt))

        prob = sb("prob", [P, NT, E])
        top = sb("top", [P, NT, 8])
        index = sb("index", [P, NT, 8], U32)
        index_f = sb("index_f", [P, NT, 8])
        pick = sb("pick", [P, NT, CHOSEN, E])
        gate = sb("gate", [P, NT, E])
        total = sb("total", [P, NT])
        hid = sb("hid", [P, TT, E * EH])
        hid_t = sb("hid_t", [P, HC, T])
        block = ctx.enter_context(nc.Block())

        @block.sync
        def _(sp):
            sync_x(nc, S, sp, 0)
            prefetch(nc, S, sp, k + 1)
            with sp.Fori(1, B) as b:
                sync_x(nc, S, sp, b)
            sp.wait_ge(S.xc_free, 1)

        @block.tensor
        def _(pe):
            keys, values = part(W, TB, "keys", C), part(W, TB, "values", HC)
            x = S.xc[:, :, 1:1 + T]
            pe.wait_ge(S.weights_ready[k], 16)

            def hidden():
                pe.wait_ge(S.xc_ready, 16)
                pe.sem_inc(S.xc_ready, -16)
                for tt in range(TT):
                    pe.wait_ge(S.r_free[tt], 1)
                    pe.sem_inc(S.r_free[tt], -1)
                    for at in (0, BANK):
                        for c in range(C):
                            last = nc.tensor.matmul(S.R[:, tt, at:at + BANK], x[:, c, tt * P:(tt + 1) * P], keys[:, c, at:at + BANK],
                                                    start=(c == 0), stop=(c == C - 1))
                    last.then_inc(S.h_full, 1)

            def outputs():
                for tt in range(TT):
                    pe.wait_ge(S.h_ready, 1)
                    pe.sem_inc(S.h_ready, -1)
                    for j in range(2):
                        pe.wait_ge(S.t_free[j], 1)
                        pe.sem_inc(S.t_free[j], -1)
                        for i in range(4):
                            last = nc.tensor.transpose(S.T[:, j, i * P:(i + 1) * P], hid[:, tt, (4 * j + i) * P:(4 * j + i + 1) * P], S.ident)
                        last.then_inc(S.at_full, 1)
                pe.wait_ge(S.t_free[0], 1)
                pe.sem_inc(S.t_free[0], -1)
                pe.wait_ge(S.t_free[1], 1)
                pe.sem_inc(S.t_free[1], -1)
                pe.sem_inc(S.t_free[0], 1)
                pe.sem_inc(S.t_free[1], 1)
                pe.wait_ge(S.o_free[0], 1)
                pe.sem_inc(S.o_free[0], -1)
                for tt in range(TT):
                    for c in range(HC):
                        last = nc.tensor.matmul(S.O[:, 0, tt * D:(tt + 1) * D], hid_t[:, c, tt * P:(tt + 1) * P], values[:, c, :],
                                                start=(c == 0), stop=(c == HC - 1))
                last.then_inc(S.y_full, 1)

            def tail():
                pe.wait_ge(S.o_free[1], 1)
                pe.sem_inc(S.o_free[1], -1)
                tail_pe(nc, S, pe, 1)

            pe_logits(nc, S, pe, part(W, TB, "sel", C), E)
            hidden()
            outputs()
            with pe.Fori(0, B - 1):
                hidden()
                tail()
                outputs()
            tail()

        @block.scalar
        def _(act):
            act.wait_ge(S.max_ready, 1)
            act.sem_inc(S.max_ready, -1)
            nc.scalar.activation(prob[:], prob[:], ACT.Exp, scale=-1.0).then_inc(S.p_ready, 1)

            def hidden_transposed():
                for tt in range(TT):
                    for j in range(2):
                        act.wait_ge(S.at_full, 1)
                        act.sem_inc(S.at_full, -1)
                        nc.scalar.activation(hid_t[:, 4 * j:4 * j + 4, tt * P:(tt + 1) * P],
                                             S.T[:, j, :].rearrange("p (c t) -> p c t", c=4), ACT.Copy).then_inc(S.t_free[j], 1)

            with act.Fori(0, B) as b:
                hidden_transposed()
                tail_act(nc, S, act, 1, b)

        @block.vector
        def _(dve):
            dve.wait_ge(S.weights_ready[k], 16)
            each = [P, NT, E]
            dve.wait_ge(S.q_full, 1)
            dve.sem_inc(S.q_full, -1)
            nc.vector.tensor_copy(prob[:].rearrange("p t e -> p (t e)"), S.O[:, 0, 0:NT * 16]).then_inc(S.o_free[0], 1)
            dve.drain().then_inc(S.max_ready, 1)
            dve.wait_ge(S.p_ready, 1)
            dve.sem_inc(S.p_ready, -1)
            nc.vector.tensor_scalar(prob[:], prob[:], 1.0, None, ALU.add)
            dve.drain()
            nc.vector.reciprocal(prob[:], prob[:])
            dve.drain()
            dve_top(nc, S, dve, gate, prob, top, index, index_f, pick, CHOSEN, E)
            nc.vector.tensor_reduce(total[:], gate[:], AX.X, ALU.add)
            dve.drain()
            nc.vector.tensor_scalar(total[:], total[:], 1e-9, None, ALU.max)
            dve.drain()
            nc.vector.reciprocal(total[:], total[:])
            dve.drain()
            nc.vector.tensor_tensor(gate[:], gate[:], total[:].unsqueeze(2).to_broadcast(each), ALU.mult)
            dve.drain()
            nc.vector.tensor_scalar(gate[:], gate[:], part(W, TB, "route_scale"), None, ALU.mult)
            dve.drain()
            with dve.Fori(0, B) as b:
                for tt in range(TT):
                    dve.wait_ge(S.h_full, 1)
                    dve.sem_inc(S.h_full, -1)
                    if tt == TT - 1:
                        dve.sem_inc(S.xc_free, 1)
                    nc.vector.scalar_tensor_tensor(hid[:, tt, :].rearrange("p (e h) -> p e h", e=E),
                                                   S.R[:, tt, :].rearrange("p (e h) -> p e h", e=E), 0.0,
                                                   gate[:, bass.ds(b * TT + tt, 1), :].rearrange("p a e -> p (a e)").unsqueeze(2).to_broadcast([P, E, EH]),
                                                   ALU.max, ALU.mult).then_inc(S.r_free[tt], 1)
                    dve.drain().then_inc(S.h_ready, 1)
                dve.wait_ge(S.y_full, 1)
                dve.sem_inc(S.y_full, -1)
                nc.vector.tensor_tensor(S.ysb[:], S.O[:, 0, :].rearrange("p (t d) -> p t d", t=TT), S.x_nat[:, bass.ds(b * TT, TT), :], ALU.add)\
                    .then_inc(S.o_free[0], 1)
                dve.drain()
                tail_dve(nc, S, dve)

        @block.gpsimd
        def _(pool):
            with pool.Fori(0, B) as b:
                tail_pool(nc, S, pool, b)


def int8_product(nc, S, k):
    W, TB = S.arena[k % 2], PACK[k]
    with ExitStack() as ctx:
        def sb(name, shape, dt=F32):
            return ctx.enter_context(nc.sbuf_tensor(f"{name}_{k}", shape, dt))

        rhs_i = sb("rhs_i", [P, C, D])
        rhs_q = sb("rhs_q", [P, C, D], BF16)
        col_scale = sb("col_scale", [P, 2])
        col_inv = sb("col_inv", [P, 2])
        col_wide = sb("col_wide", [P, 2, P])
        rhs_scale = sb("rhs_scale", [P, D])
        row_scale = sb("row_scale", [P, TT])
        row_inv = sb("row_inv", [P, TT])
        lhs_i = sb("lhs_i", [P, TT, D])
        lhs_q = sb("lhs_q", [P, C, T], BF16)
        block = ctx.enter_context(nc.Block())

        @block.sync
        def _(sp):
            prefetch(nc, S, sp, k + 1)

        @block.tensor
        def _(pe):
            pe.wait_ge(S.setup_dve, 1)
            pe.sem_inc(S.setup_dve, -1)
            pe.wait_ge(S.o_free[0], 1)
            pe.sem_inc(S.o_free[0], -1)
            for kc in range(C):
                for nb in range(C):
                    last = nc.tensor.transpose(S.O[:, 0, kc * D + nb * P:kc * D + (nb + 1) * P], rhs_i[:, nb, kc * P:(kc + 1) * P], S.ident)
            last.then_inc(S.at_full, 1)
            pe.wait_ge(S.o_free[1], 1)
            pe.sem_inc(S.o_free[1], -1)
            for nb in range(C):
                last = nc.tensor.transpose(S.O[:, 1, nb * P:(nb + 1) * P], col_wide[:, nb, :], S.ident)
            last.then_inc(S.at_full, 1)

            def product():
                pe.wait_ge(S.q_full, 1)
                pe.sem_inc(S.q_full, -1)
                pe.wait_ge(S.o_free[0], 1)
                pe.sem_inc(S.o_free[0], -1)
                for c in range(C):
                    for tt in range(TT):
                        last = nc.tensor.transpose(S.O[:, 0, (c * TT + tt) * P:(c * TT + tt + 1) * P], lhs_i[:, tt, c * P:(c + 1) * P], S.ident)
                last.then_inc(S.at_full, 1)
                pe.wait_ge(S.o_free[0], 1)
                pe.sem_inc(S.o_free[0], -1)
                for tt in range(TT):
                    for c in range(C):
                        last = nc.tensor.matmul(S.O[:, 0, tt * D:(tt + 1) * D], lhs_q[:, c, tt * P:(tt + 1) * P], rhs_q[:, c, :],
                                                start=(c == 0), stop=(c == C - 1))
                last.then_inc(S.y_full, 1)

            def tail():
                pe.wait_ge(S.o_free[1], 1)
                pe.sem_inc(S.o_free[1], -1)
                tail_pe(nc, S, pe, 1)

            product()
            with pe.Fori(0, B - 1):
                product()
                tail()
            tail()

        @block.scalar
        def _(act):
            act.wait_ge(S.at_full, 1)
            act.sem_inc(S.at_full, -1)
            nc.scalar.activation(rhs_q[:].rearrange("p c n -> p (c n)"), S.O[:, 0, :], ACT.Copy).then_inc(S.o_free[0], 1)
            act.wait_ge(S.at_full, 1)
            act.sem_inc(S.at_full, -1)
            nc.scalar.activation(rhs_scale[:], S.O[:, 1, 0:D], ACT.Copy).then_inc(S.o_free[1], 1)
            act.drain().then_inc(S.setup_act, 1)

            def rows():
                act.wait_ge(S.at_full, 1)
                act.sem_inc(S.at_full, -1)
                nc.scalar.activation(lhs_q[:].rearrange("p c t -> p (c t)"), S.O[:, 0, :], ACT.Copy).then_inc(S.o_free[0], 1)

            rows()
            with act.Fori(0, B - 1) as b:
                rows()
                tail_act(nc, S, act, 1, b)
            tail_act(nc, S, act, 1, B - 1)

        @block.vector
        def _(dve):
            def quantise(out, x, scale, inv):
                nc.vector.tensor_reduce(scale[:], x, AX.X, ALU.max, apply_absolute_value=True)
                dve.drain()
                nc.vector.tensor_scalar(scale[:], scale[:], 1e-12, 1.0 / INT8_MAX, ALU.max, ALU.mult)
                dve.drain()
                nc.vector.reciprocal(inv[:], scale[:])
                dve.drain()
                for t in range(2):
                    nc.vector.tensor_scalar(out[:, t, :], x[:, t, :], inv[:, t:t + 1], ROUND, ALU.mult, ALU.add)
                dve.drain()
                nc.vector.tensor_scalar(out[:], out[:], ROUND, INT8_MAX, ALU.subtract, ALU.min)
                dve.drain()
                return nc.vector.tensor_scalar(out[:], out[:], -INT8_MAX, None, ALU.max)

            def rows(b):
                quantise(lhs_i, S.x_nat[:, bass.ds(b * TT, TT), :], row_scale, row_inv).then_inc(S.q_full, 1)

            def output(b, meanwhile=None):
                dve.wait_ge(S.y_full, 1)
                dve.sem_inc(S.y_full, -1)
                for tt in range(TT):
                    last = nc.vector.scalar_tensor_tensor(S.ysb[:, tt, :], S.O[:, 0, tt * D:(tt + 1) * D], row_scale[:, tt:tt + 1],
                                                          rhs_scale[:], ALU.mult, ALU.mult)
                last.then_inc(S.o_free[0], 1)
                dve.drain()
                nc.vector.tensor_tensor(S.ysb[:], S.ysb[:], S.x_nat[:, bass.ds(b * TT, TT), :], ALU.add)
                dve.drain()
                tail_dve(nc, S, dve, meanwhile)

            dve.wait_ge(S.weights_ready[k], 16)
            quantise(rhs_i, part(W, TB, "rhs_t", C), col_scale, col_inv)
            for nb in range(C):
                nc.vector.tensor_copy(col_wide[:, nb, :], col_scale[:, nb:nb + 1].to_broadcast([P, P]))
            dve.drain().then_inc(S.setup_dve, 1)
            dve.wait_ge(S.setup_act, 1)
            dve.sem_inc(S.setup_act, -1)
            rows(0)
            with dve.Fori(0, B - 1) as b:
                output(b, lambda: rows(b + 1))
            output(B - 1)

        @block.gpsimd
        def _(pool):
            with pool.Fori(0, B) as b:
                tail_pool(nc, S, pool, b)


def selective_scan(nc, S, k):
    W, TB = S.arena[k % 2], PACK[k]
    CT, NS = 4, 16
    NCH = N // BANK
    decay = S.arena[(k + 1) % 2][:, 4096:4096 + 2 * N].rearrange("p (s n) -> p s n", s=2)
    state = S.arena[k % 2][:, 4096:4096 + 2 * N].rearrange("p (s n) -> p s n", s=2)
    with ExitStack() as ctx:
        def sb(name, shape, dt=F32):
            return ctx.enter_context(nc.sbuf_tensor(f"{name}_{k}", shape, dt))

        w = sb("w", [P, SCAN_COLS])
        xp = sb("xp", [P, N])
        delta = sb("delta", [P, N])
        u = sb("u", [P, N])
        gated = sb("gated", [P, CT, N])
        neg_a = sb("neg_a", [P, NS])
        bc = sb("bc", [P, NS])
        diag = sb("diag", [P, NS, P])
        gc = sb("gc", [P, CT, T])
        block = ctx.enter_context(nc.Block())
        banks = [(S.T, 0, S.t_free[0]), (S.T, 1, S.t_free[1]), (S.O, 0, S.o_free[0]), (S.O, 1, S.o_free[1])]

        @block.sync
        def _(sp):
            def weights(ct):
                sp.wait_ge(S.scan_w_free, 1)
                sp.sem_inc(S.scan_w_free, -1)
                sp.dma_start(w[:], S.scan_dram[bass.ds(ct * P, P), :]).then_inc(S.scan_w, 16)
                sp.wait_ge(S.scan_w, 16)
                sp.sem_inc(S.scan_w, -16)
                sp.sem_inc(S.scan_w_pe, 1)
                sp.sem_inc(S.scan_w_act, 1)
                sp.sem_inc(S.scan_w_pool, 1)

            weights(0)
            prefetch(nc, S, sp, k + 1)
            with sp.Fori(1, CT) as ct:
                weights(ct)
            sp.wait_ge(S.scan_w_free, 1)
            sp.sem_inc(S.scan_w_free, -1)
            sp.sem_inc(S.scan_w_free, 1)
            with sp.Fori(0, B) as b:
                sp.wait_ge(S.xc_free, 1)
                sp.sem_inc(S.xc_free, -1)
                sp.dma_start(gc[:], gated[:, :, bass.ds(b * T, T)]).then_inc(S.xc_ready, 16)
            sp.wait_ge(S.xc_free, 1)

        @block.tensor
        def _(pe):
            with pe.Fori(0, CT) as ct:
                pe.wait_ge(S.scan_w_pe, 1)
                pe.sem_inc(S.scan_w_pe, -1)
                j = 0
                for name in ("wd", "wx", "wg"):
                    wp = part(w, SCAN, name, C)
                    for ch in range(NCH):
                        psum, slot, free = banks[j % 4]
                        pe.wait_ge(free, 1)
                        pe.sem_inc(free, -1)
                        for c in range(C):
                            last = nc.tensor.matmul(psum[:, slot, :], wp[:, c, :], S.x_t[:, c, ch * BANK:(ch + 1) * BANK],
                                                    start=(c == 0), stop=(c == C - 1))
                        last.then_inc(S.q_full, 1)
                        j += 1
                pe.wait_ge(S.diag_ready, 1)
                pe.sem_inc(S.diag_ready, -1)
                pe.wait_ge(S.r_free[0], 1)
                pe.sem_inc(S.r_free[0], -1)
                for n in range(NS):
                    pe.wait_ge(S.state_ready, 1)
                    pe.sem_inc(S.state_ready, -1)
                    for ch in range(NCH):
                        last = nc.tensor.matmul(S.R[:, ch // 2, (ch % 2) * BANK:(ch % 2 + 1) * BANK], diag[:, n, :],
                                                state[:, n % 2, ch * BANK:(ch + 1) * BANK], start=(n == 0), stop=(n == NS - 1))
                    last.then_inc(S.state_used, 1)
            pe.wait_ge(S.weights_ready[k], 16)
            wout = part(W, TB, "wout", CT)
            with pe.Fori(0, B) as b:
                pe.wait_ge(S.xc_ready, 16)
                pe.sem_inc(S.xc_ready, -16)
                pe.wait_ge(S.o_free[0], 1)
                pe.sem_inc(S.o_free[0], -1)
                for tt in range(TT):
                    for c in range(CT):
                        last = nc.tensor.matmul(S.O[:, 0, tt * D:(tt + 1) * D], gc[:, c, tt * P:(tt + 1) * P], wout[:, c, :],
                                                start=(c == 0), stop=(c == CT - 1))
                last.then_inc(S.y_full, 1)
                pe.wait_ge(S.o_free[1], 1)
                pe.sem_inc(S.o_free[1], -1)
                tail_pe(nc, S, pe, 1)

        @block.scalar
        def _(act):
            with act.Fori(0, CT) as ct:
                act.wait_ge(S.scan_w_act, 1)
                act.sem_inc(S.scan_w_act, -1)
                nc.scalar.activation(neg_a[:], part(w, SCAN, "a_log"), ACT.Exp)
                act.drain()
                nc.scalar.activation(neg_a[:], neg_a[:], ACT.Copy, scale=-1.0)
                j = 0
                for name, func in (("bd", ACT.Relu), ("bx", ACT.Identity), ("bg", ACT.Sigmoid)):
                    for ch in range(NCH):
                        psum, slot, free = banks[j % 4]
                        cols = slice(ch * BANK, (ch + 1) * BANK)
                        if name == "bg":
                            dst = gated[:, bass.ds(ct, 1), cols].rearrange("p a n -> p (a n)")
                        else:
                            dst = (delta if name == "bd" else xp)[:, cols]
                        act.wait_ge(S.q_full, 1)
                        act.sem_inc(S.q_full, -1)
                        nc.scalar.activation(dst, psum[:, slot, :], func, bias=part(w, SCAN, name)).then_inc(free, 1)
                        j += 1
                    if name == "bx":
                        act.drain().then_inc(S.xp_ready, 1)
                act.drain().then_inc(S.gate_exp, 1)
                for n in range(NS):
                    act.wait_ge(S.decay_free, 1)
                    act.sem_inc(S.decay_free, -1)
                    nc.scalar.activation(decay[:, n % 2, :].rearrange("p (b t) -> p b t", b=B)[:, :, 1:T],
                                         delta[:].rearrange("p (b t) -> p b t", b=B)[:, :, 1:T], ACT.Exp,
                                         scale=neg_a[:, n:n + 1]).then_inc(S.decay_ready, 1)
            act.wait_ge(S.decay_free, 2)
            act.sem_inc(S.decay_free, -2)
            with act.Fori(0, B) as b:
                tail_act(nc, S, act, 1, b)

        @block.vector
        def _(dve):
            for s in range(2):
                nc.vector.memset(decay[:, s, :].rearrange("p (b t) -> p b t", b=B)[:, :, 0:1], 0.0).then_inc(S.decay_free, 1)
            with dve.Fori(0, CT) as ct:
                dve.wait_ge(S.xp_ready, 1)
                dve.sem_inc(S.xp_ready, -1)
                nc.vector.tensor_tensor(u[:], xp[:], delta[:], ALU.mult)
                dve.drain()
                for n in range(NS):
                    dve.wait_ge(S.decay_ready, 1)
                    dve.sem_inc(S.decay_ready, -1)
                    dve.wait_ge(S.state_used, 1)
                    dve.sem_inc(S.state_used, -1)
                    nc.vector.tensor_tensor_scan(state[:, n % 2, :], decay[:, n % 2, :], u[:], 0.0, ALU.mult, ALU.add)\
                        .then_inc(S.decay_free, 1)
                    dve.drain().then_inc(S.state_ready, 1)
                dve.wait_ge(S.state_used, 2)
                dve.sem_inc(S.state_used, -2)
                dve.sem_inc(S.state_used, 2)
                dve.wait_ge(S.gate_exp, 1)
                dve.sem_inc(S.gate_exp, -1)
                nc.vector.scalar_tensor_tensor(xp[:], xp[:], part(w, SCAN, "d"), S.R[:].rearrange("p s n -> p (s n)"),
                                               ALU.mult, ALU.add).then_inc(S.r_free[0], 1)
                dve.drain()
                tile = gated[:, bass.ds(ct, 1), :].rearrange("p a n -> p (a n)")
                nc.vector.tensor_tensor(tile, tile, xp[:], ALU.mult).then_inc(S.scan_w_free, 1)
            dve.wait_ge(S.state_used, 2)
            dve.sem_inc(S.state_used, -2)
            with dve.Fori(0, B) as b:
                dve.wait_ge(S.y_full, 1)
                dve.sem_inc(S.y_full, -1)
                dve.sem_inc(S.xc_free, 1)
                dve.wait_ge(S.xres_ready, 1)
                dve.sem_inc(S.xres_ready, -1)
                nc.vector.tensor_tensor(S.ysb[:], S.O[:, 0, :].rearrange("p (t d) -> p t d", t=TT), S.xres[:], ALU.add)\
                    .then_inc(S.o_free[0], 1)
                dve.drain().then_inc(S.xres_free, 1)
                tail_dve(nc, S, dve)

        @block.gpsimd
        def _(pool):
            pool.sem_inc(S.state_used, 2)
            pool.sem_inc(S.scan_w_free, 1)
            with pool.Fori(0, CT) as ct:
                pool.wait_ge(S.scan_w_pool, 1)
                pool.sem_inc(S.scan_w_pool, -1)
                nc.gpsimd.tensor_tensor(bc[:], part(w, SCAN, "b"), part(w, SCAN, "c0"), ALU.mult)
                pool.drain()
                for n in range(NS):
                    last = nc.gpsimd.tensor_scalar(diag[:, n, :], S.ident, bc[:, n:n + 1], None, ALU.mult)
                last.then_inc(S.diag_ready, 1)
            pool.wait_ge(S.weights_ready[k], 16)
            with pool.Fori(0, B) as b:
                pool_residual(nc, S, pool, b, part(W, TB, "bo"))
                tail_pool(nc, S, pool, b)


def moe_capacity(nc, S, k, out):
    W, TB = S.arena[k % 2], PACK[k]
    FC = F3 // P
    NT = B * TT
    GROUPS = 4
    GT = NT // GROUPS
    ROWS = [(0, P), (1, P), (2, CAP - 2 * P)]
    ge = S.arena[(k + 1) % 2][:, 0:NT * D].rearrange("p (t d) -> p t d", t=NT)
    y = S.arena[(k + 1) % 2][:, NT * D:2 * NT * D].rearrange("p (t d) -> p t d", t=NT)
    with ExitStack() as ctx:
        def sb(name, shape, dt=F32):
            return ctx.enter_context(nc.sbuf_tensor(f"{name}_{k}", shape, dt))

        prob = sb("prob", [P, NT, E3])
        total = sb("total", [P, NT])
        top = sb("top", [P, NT, 8])
        index = sb("index", [P, NT, 8], U32)
        index_f = sb("index_f", [P, NT, 8])
        one_hot = sb("one_hot", [P, NT, E3])
        count = sb("count", [P, E3, NT])
        until = sb("until", [P, E3, NT])
        carry = sb("carry", [P, E3, NT])
        ranks = sb("ranks", [P, NT, E3])
        pos = sb("pos", [P, NT])
        kept = sb("kept", [P, NT])
        slot_f = sb("slot_f", [P, NT])
        spare = sb("spare", [P, NT])
        to_f = sb("to_f", [P, NT])
        to = sb("to", [P, NT], U32)
        back = sb("back", [P, NT], U32)
        gates = sb("gates", [P, NT])
        bst = sb("bst", [P, NT, 6])
        mv = sb("mv", [P, NT, 2])
        rstd = sb("rstd", [P, NT])
        zeros = sb("zeros", [P, 5 * D])
        w1 = sb("w1", [P, 2, C, F3])
        w2 = sb("w2", [P, 2, FC, D])
        xe = sb("xe", [P, 2, 3, D])
        xe_t = sb("xe_t", [P, C, CAP])
        hid = sb("hid", [P, FC, CAP])
        ye = sb("ye", [P, 2, 3, D])
        block = ctx.enter_context(nc.Block())

        @block.sync
        def _(sp):
            def weights(e, s):
                sp.dma_start(w1[:, s, :, :], S.w1_dram[bass.ds(e * P, P), :].rearrange("p (c f) -> p c f", c=C)).then_inc(S.ew_ready[s], 16)
                sp.dma_start(w2[:, s, :, :], S.w2_dram[bass.ds(e * P, P), :].rearrange("p (c f) -> p c f", c=FC)).then_inc(S.ew_ready[s], 16)

            def rows(e, s):
                sp.wait_ge(S.xe_free[s], 1)
                sp.sem_inc(S.xe_free[s], -1)
                sp.dma_start(xe[:, s, 0:2, :], S.xe_dram[bass.ds(e * CAP, 2 * P), :].rearrange("(t p) d -> p t d", p=P)).then_inc(S.xe_ready[s], 16)
                sp.dma_start(xe[0:CAP - 2 * P, s, 2, :], S.xe_dram[bass.ds(e * CAP + 2 * P, CAP - 2 * P), :]).then_inc(S.xe_ready[s], 16)

            sp.wait_ge(S.zeros_ready, 1)
            sp.sem_inc(S.zeros_ready, -1)
            for i in range(E3 * CAP // (5 * P)):
                sp.dma_start(S.xe_dram[i * 5 * P:(i + 1) * 5 * P, :].rearrange("(p r) d -> p (r d)", p=P), zeros[:]).then_inc(S.slots_clear, 16)
            sp.dma_start(S.ye_dram[ZERO_ROW:ZERO_ROW + 1, :], zeros[0:1, 0:D]).then_inc(S.slots_clear, 16)
            for s in range(2):
                weights(s, s)
            sp.wait_ge(S.dispatched, 1)
            sp.sem_inc(S.dispatched, -1)
            for s in range(2):
                rows(s, s)
            with sp.Fori(0, E3 // 2 - 1) as pair:
                e = pair * 2
                for s in range(2):
                    rows(e + (2 + s), s)
                    sp.wait_ge(S.ew_free[s], 1)
                    sp.sem_inc(S.ew_free[s], -1)
                    weights(e + (2 + s), s)
            with sp.Fori(0, GROUPS) as g:
                sp.wait_ge(S.yn_ready_pe, 1)
                sp.sem_inc(S.yn_ready_pe, -1)
                sp.dma_start(out[bass.ds(g * (GT * P), GT * P), :].rearrange("(t p) d -> p t d", p=P), y[:, bass.ds(g * GT, GT), :])\
                    .then_inc(S.out_stored, 16)
            sp.wait_ge(S.out_stored, 16 * GROUPS)

        @block.tensor
        def _(pe):
            gate = part(W, TB, "gate", C)
            tri, ones = part(S.const, CONST, "tri"), part(S.const, CONST, "ones")
            pe.wait_ge(S.weights_ready[k], 16)
            pe.wait_ge(S.o_free[0], 1)
            pe.sem_inc(S.o_free[0], -1)
            for tt in range(NT):
                for c in range(C):
                    last = nc.tensor.matmul(S.O[:, 0, tt * E3:(tt + 1) * E3], S.x_t[:, c, tt * P:(tt + 1) * P], gate[:, c, :],
                                            start=(c == 0), stop=(c == C - 1))
            last.then_inc(S.q_full, 1)
            pe.wait_ge(S.h_ready, 1)
            pe.sem_inc(S.h_ready, -1)
            pe.wait_ge(S.o_free[1], 1)
            pe.sem_inc(S.o_free[1], -1)
            pe.wait_ge(S.o_free[0], 1)
            pe.sem_inc(S.o_free[0], -1)
            flat = one_hot[:].rearrange("p t e -> p (t e)")
            nc.tensor.matmul(S.O[:, 0, 0:NT * E3], ones, flat, start=True, stop=True)
            nc.tensor.matmul(S.O[:, 1, 0:NT * E3], tri, flat, start=True, stop=True).then_inc(S.v_full, 1)

            def transposes(s):
                pe.wait_ge(S.xe_ready[s], 32)
                pe.sem_inc(S.xe_ready[s], -32)
                for c in range(C):
                    pe.wait_ge(S.t_free[c], 1)
                    pe.sem_inc(S.t_free[c], -1)
                    for t, n in ROWS:
                        last = nc.tensor.transpose(S.T[:, c, t * P:t * P + n], xe[0:n, s, t, c * P:(c + 1) * P], S.ident[0:n, 0:n])
                    last.then_inc(S.at_full, 1)

            def expert(s, last_one=False):
                pe.wait_ge(S.t_free[0], 1)
                pe.sem_inc(S.t_free[0], -1)
                pe.wait_ge(S.t_free[1], 1)
                pe.sem_inc(S.t_free[1], -1)
                pe.sem_inc(S.t_free[0], 1)
                pe.sem_inc(S.t_free[1], 1)
                pe.wait_ge(S.ew_ready[s], 32)
                pe.sem_inc(S.ew_ready[s], -32)
                for j in range(FC // 2):
                    pe.wait_ge(S.r_free[j % 2], 1)
                    pe.sem_inc(S.r_free[j % 2], -1)
                    for i in range(2):
                        for c in range(C):
                            last = nc.tensor.matmul(S.R[:, j % 2, i * BANK:i * BANK + CAP], w1[:, s, c, (2 * j + i) * P:(2 * j + i + 1) * P],
                                                    xe_t[:, c, :], start=(c == 0), stop=(c == C - 1))
                    last.then_inc(S.h_full if j % 2 == 0 else S.h_full_up, 1)
                if not last_one:
                    transposes(1 - s)
                pe.wait_ge(S.r_free[0], 1)
                pe.sem_inc(S.r_free[0], -1)
                pe.wait_ge(S.r_free[1], 1)
                pe.sem_inc(S.r_free[1], -1)
                pe.sem_inc(S.r_free[0], 1)
                pe.sem_inc(S.r_free[1], 1)
                pe.wait_ge(S.o_free[0], 1)
                pe.sem_inc(S.o_free[0], -1)
                pe.wait_ge(S.o_free[1], 1)
                pe.sem_inc(S.o_free[1], -1)
                for t, n in ROWS:
                    for f in range(FC):
                        last = nc.tensor.matmul(S.O[0:n, t // 2, (t % 2) * D:(t % 2 + 1) * D], hid[:, f, t * P:t * P + n], w2[:, s, f, :],
                                                start=(f == 0), stop=(f == FC - 1))
                    if t == 1:
                        last.then_inc(S.y_full, 1)
                last.then_inc(S.v_full_act, 1)

            transposes(0)
            with pe.Fori(0, E3 // 2 - 1):
                expert(0)
                expert(1)
            expert(0)
            expert(1, last_one=True)

        @block.scalar
        def _(act):
            act.wait_ge(S.max_ready, 1)
            act.sem_inc(S.max_ready, -1)
            nc.scalar.activation(prob[:], prob[:], ACT.Exp).then_inc(S.p_ready, 1)

            def transposes(s):
                for c in range(C):
                    act.wait_ge(S.at_full, 1)
                    act.sem_inc(S.at_full, -1)
                    nc.scalar.activation(xe_t[:, c, :], S.T[:, c, 0:CAP], ACT.Copy).then_inc(S.t_free[c], 1)
                act.sem_inc(S.xe_free[s], 1)

            def expert(e, s, last_one=False):
                for j in range(0, FC // 2, 2):
                    act.wait_ge(S.h_full, 1)
                    act.sem_inc(S.h_full, -1)
                    nc.scalar.activation(hid[:, 2 * j:2 * j + 2, :], S.R[:, 0, :].rearrange("p (i n) -> p i n", i=2)[:, :, 0:CAP],
                                         ACT.Relu).then_inc(S.r_free[0], 1)
                if not last_one:
                    transposes(1 - s)
                act.wait_ge(S.v_full_act, 1)
                act.sem_inc(S.v_full_act, -1)
                act.wait_ge(S.ye_stored[s], 32)
                act.sem_inc(S.ye_stored[s], -32)
                act.sem_inc(S.ye_free, 1)
                n = ROWS[2][1]
                nc.scalar.activation(ye[0:n, s, 2, :], S.O[0:n, 1, 0:D], ACT.Copy).then_inc(S.o_free[1], 1)
                act.drain()
                act.dma_start(S.ye_dram[bass.ds(e * CAP + 2 * P, n), :], ye[0:n, s, 2, :]).then_inc(S.ye_stored[s], 16)
                act.wait_ge(S.ye_ready, 1)
                act.sem_inc(S.ye_ready, -1)
                act.dma_start(S.ye_dram[bass.ds(e * CAP, 2 * P), :].rearrange("(t p) d -> p t d", p=P), ye[:, s, 0:2, :])\
                    .then_inc(S.ye_stored[s], 16)

            transposes(0)
            with act.Fori(0, E3 // 2 - 1) as pair:
                expert(pair * 2, 0)
                expert(pair * 2 + 1, 1)
            expert(E3 - 2, 0)
            expert(E3 - 1, 1, last_one=True)
            for s in range(2):
                act.wait_ge(S.ye_stored[s], 32)
                act.sem_inc(S.ye_stored[s], -32)
            act.sem_inc(S.combined, 1)

        @block.vector
        def _(dve):
            iota = part(S.const, CONST, "iota")
            nc.vector.memset(carry[:], 1.0)
            nc.vector.tensor_scalar(spare[:], iota, float(P), float(ZERO_ROW), ALU.mult, ALU.add)
            dve.drain()
            nc.vector.memset(carry[:, :, 0:1], 0.0)
            nc.vector.tensor_scalar(spare[:], spare[:], part(S.const, CONST, "row"), None, ALU.add)
            dve.wait_ge(S.q_full, 1)
            dve.sem_inc(S.q_full, -1)
            logits = S.O[:, 0, 0:NT * E3].rearrange("p (t e) -> p t e", t=NT)
            nc.vector.tensor_reduce(total[:], logits, AX.X, ALU.max)
            dve.drain()
            nc.vector.tensor_tensor(prob[:], logits, total[:].unsqueeze(2).to_broadcast([P, NT, E3]), ALU.subtract).then_inc(S.o_free[0], 1)
            dve.drain().then_inc(S.max_ready, 1)
            dve.wait_ge(S.p_ready, 1)
            dve.sem_inc(S.p_ready, -1)
            nc.vector.tensor_reduce(total[:], prob[:], AX.X, ALU.add)
            dve.drain()
            nc.vector.reciprocal(total[:], total[:])
            dve.drain()
            nc.vector.tensor_tensor(prob[:], prob[:], total[:].unsqueeze(2).to_broadcast([P, NT, E3]), ALU.mult)
            dve.drain()
            for tt in range(NT):
                nc.vector.max(top[:, tt, :], prob[:, tt, :])
            dve.drain()
            for tt in range(NT):
                nc.vector.max_index(index[:, tt, :], top[:, tt, :], prob[:, tt, :])
            dve.drain()
            nc.vector.tensor_copy(index_f[:], index[:])
            dve.drain()
            nc.vector.tensor_tensor(one_hot[:], iota[:, 0:E3].unsqueeze(1).to_broadcast([P, NT, E3]),
                                    index_f[:, :, 0:1].to_broadcast([P, NT, E3]), ALU.is_equal).then_inc(S.h_ready, 1)
            dve.wait_ge(S.v_full, 1)
            dve.sem_inc(S.v_full, -1)
            nc.vector.tensor_copy(count[:], S.O[:, 0, 0:NT * E3].rearrange("p (t e) -> p e t", t=NT)).then_inc(S.o_free[0], 1)
            dve.drain()
            nc.vector.tensor_tensor_scan(until[:].rearrange("p e t -> p (e t)"), carry[:].rearrange("p e t -> p (e t)"),
                                         count[:].rearrange("p e t -> p (e t)"), 0.0, ALU.mult, ALU.add)
            dve.drain()
            nc.vector.tensor_tensor(until[:], until[:], count[:], ALU.subtract)
            dve.drain()
            nc.vector.tensor_tensor(ranks[:], S.O[:, 1, 0:NT * E3].rearrange("p (t e) -> p t e", t=NT),
                                    until[:].rearrange("p e t -> p t e"), ALU.add).then_inc(S.o_free[1], 1)
            dve.drain()
            nc.vector.tensor_tensor(ranks[:], ranks[:], one_hot[:], ALU.mult)
            dve.drain()
            nc.vector.tensor_reduce(pos[:], ranks[:], AX.X, ALU.add)
            dve.drain()
            nc.vector.tensor_scalar(pos[:], pos[:], 1.0, None, ALU.subtract)
            dve.drain()
            nc.vector.tensor_scalar(kept[:], pos[:], float(CAP), None, ALU.is_lt)
            nc.vector.scalar_tensor_tensor(slot_f[:], index_f[:, :, 0], float(CAP), pos[:], ALU.mult, ALU.add)
            dve.drain()
            nc.vector.tensor_tensor(gates[:], top[:, :, 0], kept[:], ALU.mult)
            nc.vector.tensor_tensor(to_f[:], slot_f[:], spare[:], ALU.subtract)
            nc.vector.tensor_scalar(pos[:], slot_f[:], float(ZERO_ROW), None, ALU.subtract)
            dve.drain()
            nc.vector.tensor_tensor(to_f[:], to_f[:], kept[:], ALU.mult)
            nc.vector.tensor_tensor(pos[:], pos[:], kept[:], ALU.mult)
            dve.drain()
            nc.vector.tensor_tensor(to_f[:], to_f[:], spare[:], ALU.add)
            nc.vector.tensor_scalar(pos[:], pos[:], float(ZERO_ROW), None, ALU.add)
            dve.drain()
            nc.vector.tensor_copy(to[:], to_f[:])
            nc.vector.tensor_copy(back[:], pos[:])
            dve.drain().then_inc(S.to_ready, 1)
            with dve.Fori(0, E3 // 2):
                for s in range(2):
                    for j in range(1, FC // 2, 2):
                        dve.wait_ge(S.h_full_up, 1)
                        dve.sem_inc(S.h_full_up, -1)
                        nc.vector.tensor_scalar(hid[:, 2 * j:2 * j + 2, :], S.R[:, 1, :].rearrange("p (i n) -> p i n", i=2)[:, :, 0:CAP],
                                                0.0, None, ALU.max).then_inc(S.r_free[1], 1)
                    dve.wait_ge(S.y_full, 1)
                    dve.sem_inc(S.y_full, -1)
                    dve.wait_ge(S.ye_free, 1)
                    dve.sem_inc(S.ye_free, -1)
                    dve.sem_inc(S.ew_free[s], 1)
                    nc.vector.tensor_copy(ye[:, s, 0:2, :], S.O[:, 0, :].rearrange("p (t d) -> p t d", t=TT)).then_inc(S.o_free[0], 1)
                    dve.drain().then_inc(S.ye_ready, 1)
            for g in range(GROUPS):
                dve.wait_ge(S.gathered[g], 16 * GT)
                for tt in range(g * GT, (g + 1) * GT):
                    nc.vector.scalar_tensor_tensor(y[:, tt, :], ge[:, tt, :], gates[:, tt:tt + 1], S.x_nat[:, tt, :], ALU.mult, ALU.add)
                dve.drain()
                for tt in range(g * GT, (g + 1) * GT):
                    nc.vector.bn_stats(bst[:, tt, :], y[:, tt, :])
            dve.drain()
            for tt in range(NT):
                last = nc.vector.bn_aggr(mv[:, tt, :], bst[:, tt, :])
            last.then_inc(S.ln_stat, 1)
            dve.wait_ge(S.ln_rstd, 1)
            dve.sem_inc(S.ln_rstd, -1)
            for tt in range(NT):
                last = nc.vector.tensor_scalar(y[:, tt, :], y[:, tt, :], mv[:, tt, 0:1], rstd[:, tt:tt + 1], ALU.subtract, ALU.mult)
                if (tt + 1) % GT == 0:
                    last.then_inc(S.yn_ready_pe, 1)

        @block.gpsimd
        def _(pool):
            nc.gpsimd.memset(zeros[:], 0.0).then_inc(S.zeros_ready, 1)
            for s in range(2):
                pool.sem_inc(S.ye_stored[s], 32)
                pool.sem_inc(S.xe_free[s], 1)
            pool.wait_ge(S.slots_clear, 16 * (E3 * CAP // (5 * P) + 1))
            pool.wait_ge(S.to_ready, 1)
            pool.sem_inc(S.to_ready, -1)
            for tt in range(NT):
                nc.gpsimd.indirect_dma_start(S.xe_dram[:, :], bass.IndirectOffsetOnAxis(ap=to[:, tt:tt + 1], axis=0),
                                             S.x_nat[:, tt, :], None).then_inc(S.scattered, 16)
            pool.wait_ge(S.scattered, 16 * NT)
            pool.sem_inc(S.dispatched, 1)
            pool.wait_ge(S.combined, 1)
            pool.sem_inc(S.combined, -1)
            for tt in range(NT):
                nc.gpsimd.indirect_dma_start(ge[:, tt, :], None, S.ye_dram[:, :],
                                             bass.IndirectOffsetOnAxis(ap=back[:, tt:tt + 1], axis=0)).then_inc(S.gathered[tt // GT], 16)
            pool.wait_ge(S.ln_stat, 1)
            pool.sem_inc(S.ln_stat, -1)
            nc.gpsimd.tensor_scalar(rstd[:], mv[:, :, 1], EPS, None, ALU.add)
            pool.drain()
            nc.gpsimd.tensor_tensor(rstd[:], rstd[:], part(S.const, CONST, "neg_half"), ALU.pow).then_inc(S.ln_rstd, 1)


class Shared:
    pass


def decoder(nc, dram, layers=range(12)):
    with ExitStack() as ctx:
        S = Shared()

        def sb(name, shape, dt=F32):
            return ctx.enter_context(nc.sbuf_tensor(name, shape, dt))

        def sem(name):
            return ctx.enter_context(nc.semaphore(name))

        def sems(name, n=2):
            return [sem(f"{name}{i}") for i in range(n)]

        S.s_full = sem("s_full")
        S.max_ready = sem("max_ready")
        S.p_ready = sem("p_ready")
        S.t_full = sem("t_full")
        S.t_full_act = sem("t_full_act")
        S.pt_ready = sem("pt_ready")
        S.o_full = sem("o_full")
        S.q_full = sem("q_full")
        S.k_full = sem("k_full")
        S.k_full_act = sem("k_full_act")
        S.v_full = sem("v_full")
        S.v_full_act = sem("v_full_act")
        S.h_full = sem("h_full")
        S.h_full_up = sem("h_full_up")
        S.y_full = sem("y_full")
        S.at_full = sem("at_full")
        S.yt_full = sem("yt_full")
        S.ln_stat = sem("ln_stat")
        S.ln_rstd = sem("ln_rstd")
        S.yn_ready_pe = sem("yn_ready_pe")
        S.yn_ready_pool = sem("yn_ready_pool")
        S.yn_free = sem("yn_free")
        S.x_ready = sem("x_ready")
        S.xres_ready = sem("xres_ready")
        S.xres_free = sem("xres_free")
        S.xc_ready = sem("xc_ready")
        S.xc_free = sem("xc_free")
        S.setup_act = sem("setup_act")
        S.setup_dve = sem("setup_dve")
        S.nat_full = sem("nat_full")
        S.nat_full_act = sem("nat_full_act")
        S.line_ready = sem("line_ready")
        S.lt_full = sem("lt_full")
        S.inc_full = sem("inc_full")
        S.k_nat_ready = sem("k_nat_ready")
        S.lr_full = sem("lr_full")
        S.lines_sb = sem("lines_sb")
        S.inc_free = sem("inc_free")
        S.inc_ready = sem("inc_ready")
        S.mem_ready = sem("mem_ready")
        S.gate_exp = sem("gate_exp")
        S.norm_sum = sem("norm_sum")
        S.norm_root = sem("norm_root")
        S.ctx_ready = sem("ctx_ready")
        S.ctx_stat = sem("ctx_stat")
        S.ctx_rstd = sem("ctx_rstd")
        S.ctx_norm_ready = sem("ctx_norm_ready")
        S.ctx_nt_ready = sem("ctx_nt_ready")
        S.lat_ready = sem("lat_ready")
        S.lat_t_ready = sem("lat_t_ready")
        S.k_sb = sem("k_sb")
        S.hid_free = sem("hid_free")
        S.h_ready = sem("h_ready")
        S.sg_ready = sem("sg_ready")
        S.sh_ready = sem("sh_ready")
        S.scan_w = sem("scan_w")
        S.scan_w_pe = sem("scan_w_pe")
        S.scan_w_act = sem("scan_w_act")
        S.scan_w_pool = sem("scan_w_pool")
        S.scan_w_free = sem("scan_w_free")
        S.diag_ready = sem("diag_ready")
        S.state_ready = sem("state_ready")
        S.state_used = sem("state_used")
        S.xp_ready = sem("xp_ready")
        S.decay_ready = sem("decay_ready")
        S.decay_free = sem("decay_free")
        S.zeros_ready = sem("zeros_ready")
        S.slots_clear = sem("slots_clear")
        S.to_ready = sem("to_ready")
        S.to_free = sem("to_free")
        S.scattered = sem("scattered")
        S.dispatched = sem("dispatched")
        S.combined = sem("combined")
        S.gathered = sems("gathered", 4)
        S.ye_free = sem("ye_free")
        S.ye_ready = sem("ye_ready")
        S.out_stored = sem("out_stored")
        S.r_free = sems("r_free")
        S.t_free = sems("t_free")
        S.o_free = sems("o_free")
        S.ew_ready = sems("ew_ready")
        S.ew_free = sems("ew_free")
        S.xe_ready = sems("xe_ready")
        S.xe_free = sems("xe_free")
        S.ye_stored = sems("ye_stored")
        S.weights_ready = sems("weights_ready", len(PACK))
        loaded = ctx.enter_context(nc.semaphore("loaded"))
        set_up = ctx.enter_context(nc.semaphore("set_up"))

        S.x_nat = sb("x_nat", [P, B * TT, D])
        S.x_t = sb("x_t", [P, C, N])
        S.ctx_t = sb("ctx_t", [P, C, B * CTX])
        S.const = sb("const", [P, sum(n for _, n in CONST.values())])
        S.masks = sb("masks", [P, 2, P], BF16)
        ident_b = sb("ident_b", [P, P], BF16)
        S.arena = [sb(f"arena{i}", [P, W_COLS]) for i in range(2)]
        S.xc = sb("xc", [P, C, 1 + T])
        S.xres = sb("xres", [P, TT, D])
        S.ysb = sb("ysb", [P, TT, D])
        S.yn = sb("yn", [P, TT, D])
        S.bst = sb("bst", [P, TT, 6])
        S.mv = sb("mv", [P, TT, 2])
        S.rstd = sb("rstd", [P, TT])
        S.ident = part(S.const, CONST, "ident")
        S.ident_b = ident_b[:]
        S.R = ctx.enter_context(nc.psum_tensor("R", [P, 2, 2 * BANK], F32))
        S.T = ctx.enter_context(nc.psum_tensor("T", [P, 2, BANK], F32))
        S.O = ctx.enter_context(nc.psum_tensor("O", [P, 2, BANK], F32))
        S.packs = [dram[f"pack{i}"] for i in range(len(PACK))]
        S.ctx_dram, S.scan_dram, S.w1_dram, S.w2_dram = dram["ctx"], dram["scan"], dram["w1"], dram["w2"]
        S.xe_dram = nc.dram_tensor("slots_in", (E3 * CAP + N, D), F32, kind="Internal").ap()
        S.ye_dram = nc.dram_tensor("slots_out", (E3 * CAP + 1, D), F32, kind="Internal").ap()

        with nc.Block() as block:
            @block.sync
            def _(sp):
                sp.dma_start(S.x_t[:], dram["x_t"].rearrange("(c p) n -> p c n", p=P)).then_inc(loaded, 16)
                sp.dma_start(S.const[:], dram["const"]).then_inc(loaded, 16)
                prefetch(nc, S, sp, layers[0])
                sp.dma_start(S.x_nat[:], dram["x"].rearrange("(t p) d -> p t d", p=P)).then_inc(S.x_ready, 16)
                sp.dma_start(S.ctx_t[:], dram["ctx_t"].rearrange("(c p) n -> p c n", p=P)).then_inc(S.x_ready, 16)
                for i in range(2):
                    for s in (S.r_free, S.t_free, S.o_free):
                        sp.sem_inc(s[i], 1)
                sp.sem_inc(S.xc_free, 1)
                sp.sem_inc(S.xres_free, 1)
                sp.sem_inc(S.yn_free, 2)
                sp.wait_ge(loaded, 32)
                if layers[0] != 0:
                    sp.wait_ge(S.x_ready, 32)

            @block.vector
            def _(dve):
                nc.vector.memset(S.xc[:], 0.0).then_inc(set_up, 1)
                dve.wait_ge(loaded, 32)
                nc.vector.tensor_copy(S.masks[:, 0, :], part(S.const, CONST, "causal"))
                nc.vector.tensor_copy(S.masks[:, 1, :], part(S.const, CONST, "block"))
                nc.vector.tensor_copy(S.ident_b, S.ident)
                dve.drain().then_inc(set_up, 1)

        build = [
            lambda k: attention16(nc, S, k, DH16 ** -0.5, mask="causal", geometry=True),
            lambda k: perceiver(nc, S, k),
            lambda k: moe_silu(nc, S, k),
            lambda k: attention16(nc, S, k, DH16 ** -0.5, mask="block", out=False),
            lambda k: perceiver(nc, S, k),
            lambda k: moe_relu(nc, S, k),
            lambda k: attention16(nc, S, k, D ** -0.5, mask="causal"),
            lambda k: attention16(nc, S, k, DH16 ** -0.5, cross=True),
            lambda k: int8_product(nc, S, k),
            lambda k: selective_scan(nc, S, k),
            lambda k: attention16(nc, S, k, DH16 ** -0.5, cross=True),
            lambda k: moe_capacity(nc, S, k, dram["out"]),
        ]
        for k in layers:
            build[k](k)
        if layers[-1] != 11:
            with nc.Block() as block:
                @block.sync
                def _(sp):
                    sp.dma_start(dram["out"].rearrange("(t p) d -> p t d", p=P), S.x_nat[:]).then_inc(loaded, 16)
                    sp.wait_ge(loaded, 48)



def pack_inputs(i):
    f = np.float32

    def mat(w):
        w = np.asarray(w)
        return w.reshape(-1, P, w.shape[1]).transpose(1, 0, 2).reshape(P, -1)

    def cols(v):
        return np.asarray(v).reshape(C, P).T

    def rep(v):
        v = np.asarray(v).reshape(1, -1)
        return np.broadcast_to(v, (P, v.shape[1]))

    def lines(w, order):
        return np.asarray(w).reshape(D, H, 4)[:, :, order].reshape(D, 96)

    def mha(wq, bq, wk, bk, wv, bv, wo=None, bo=None):
        none = np.zeros((D, D), f)
        return [mat(wq), mat(wk), mat(wv), mat(none if wo is None else wo), cols(bq), cols(bk), rep(bv),
                rep(np.zeros(D, f) if bo is None else bo)]

    def xatt(p, w1, b1, w2, b2):
        return [mat(i[p + "Wq"]), mat(i[p + "Wkv"]), mat(i[p + "Wo"]), rep(i[w1]), rep(i[b1]), rep(i[w2]), rep(i[b2])]

    def experts(w):
        return np.concatenate([mat(e) for e in np.asarray(w)], 1)

    a = "L0_attn_"
    qkv, qkv_b, geo = np.asarray(i[a + "qkv_w"]), np.asarray(i[a + "qkv_b"]), np.asarray(i[a + "kv_geo_w"])
    cat = lambda *x: np.concatenate(x, 1)
    w1w, w2w, w1r, w2r = (i[a + n] for n in ("w1_write", "w2_write", "w1_read", "w2_read"))
    packs = [
        [mat(qkv[:, :D]), cols(qkv_b[:D]), mat(cat(qkv[:, D:], geo)), rep(qkv_b[D:]),
         mat(cat(lines(w1w, _WI), lines(w1w, _WJ))), mat(cat(lines(w2w, _WJ), lines(w2w, _WI))),
         mat(cat(lines(w1r, _PI), lines(w1r, _PJ), lines(w2r, _PJ), lines(w2r, _PI))), mat(i[a + "out_w"]), rep(i[a + "out_b"]),
         rep(i[a + "mem_scale"]), rep(i[a + "decay_logits"]), rep(i[a + "kv_gate"])],
        xatt("L0_xattn_", "L0_xattn_ln1_w", "L0_xattn_ln1_b", "L0_xattn_ln2_w", "L0_xattn_ln2_b"),
        [experts(i["L0_ffn_w1"]), experts(i["L0_ffn_w2"]), mat(i["L0_ffn_shared_gate_up"]), mat(i["L0_ffn_shared_down"]),
         mat(cat(np.asarray(i["L0_ffn_router_w"]), np.asarray(i["L0_ffn_shared_gate_w"])))],
        mha(*(i["L1_attn_" + n] for n in ("Wq", "bq", "Wk", "bk", "Wv", "bv"))),
        xatt("L1_xattn_", "L1_xattn_ln1_g", "L1_xattn_ln1_b", "L1_xattn_ln2_g", "L1_xattn_ln2_b"),
        [mat(np.asarray(i["L1_ffn_keys"]).transpose(1, 0, 2).reshape(D, -1)), mat(np.asarray(i["L1_ffn_values"]).reshape(-1, D)),
         mat(np.asarray(i["L1_ffn_expert_sel"]).T), rep(i["L1_ffn_route_scale"])],
        mha(*(np.asarray(i["L2_attn_" + n]).T for n in ("Wq_w", "Wq_b", "Wk_w", "Wk_b", "Wv_w", "Wv_b", "Wo_w", "Wo_b"))),
        mha(*(i["L2_xattn_" + n] for n in ("Wq", "bq", "Wk", "bk", "Wv", "bv", "Wp", "bp"))),
        [mat(np.asarray(i["L2_ffn_rhs"]).T)],
        [mat(np.asarray(i["L3_attn_W_out"]).T), rep(i["L3_attn_b_out"])],
        mha(*(np.asarray(i["L3_xattn_" + n]).T for n in ("Wq", "bq", "Wk", "bk", "Wv", "bv", "Wo", "bo"))),
        [mat(i["L3_ffn_gate_w"])],
    ]
    s = "L3_attn_"
    win, wg = np.asarray(i[s + "W_in"]), np.asarray(i[s + "W_gate"])
    b_in, bg = np.asarray(i[s + "b_in"]), np.asarray(i[s + "b_gate"])
    DI = wg.shape[0]
    col = lambda v: np.asarray(v).reshape(-1, 1)
    scan = []
    for t in range(DI // P):
        r = slice(t * P, (t + 1) * P)
        r2 = slice(DI + t * P, DI + (t + 1) * P)
        scan.append(cat(mat(win[r].T), mat(win[r2].T), mat(wg[r].T), col(b_in[r]), col(b_in[r2]), col(bg[r]),
                        np.asarray(i[s + "A_log"])[r], np.asarray(i[s + "B_mat"])[r], rep(np.asarray(i[s + "C_mat"])[0]),
                        col(np.asarray(i[s + "D_vec"])[r])))
    x, c = np.asarray(i["x"]).reshape(N, D), np.asarray(i["ctx_1024"]).reshape(B * CTX, D)
    p, j = np.arange(P)[:, None], np.arange(P)[None, :]
    steps = P + p - np.arange(2 * P)[None, :]
    const = cat(np.eye(P), np.where(j <= p, 0, MASKED), np.where(p <= j, 0, MASKED), np.where(p // 64 == j // 64, 0, MASKED),
                (p <= j) * 1.0, np.ones((P, P)), np.maximum(steps, 0), (steps > 0) * 1.0, rep(np.arange(16)),
                np.full((P, 16), -0.5), np.full((P, 64), 0.5), p * 1.0,
                (p // DH16 == np.arange(HT)) * 1.0, (p // LW == np.arange(H)) * 1.0)
    arrays = {f"pack{n}": cat(*parts) for n, parts in enumerate(packs)}
    arrays |= {"x": x, "x_t": x.T, "ctx": c, "ctx_t": c.T, "scan": np.concatenate(scan, 0), "const": const,
               "w1": np.concatenate([mat(e) for e in np.asarray(i["L3_ffn_w1"])], 0),
               "w2": np.concatenate([mat(e) for e in np.asarray(i["L3_ffn_w2"])], 0)}
    return {n: np.ascontiguousarray(v, dtype=f) for n, v in arrays.items()}


def kernel(**inputs):
    import concourse.bacc as bacc
    from concourse.bass_utils import run_bass_kernel_spmd

    nc = bacc.Bacc("TRN2", target_bir_lowering=False, num_devices=1)
    arrays = pack_inputs(inputs)
    dram = {n: nc.dram_tensor(f"{n}_dram", a.shape, F32, kind="ExternalInput").ap() for n, a in arrays.items()}
    dram["out"] = nc.dram_tensor("out_dram", (N, D), F32, kind="ExternalOutput").ap()
    decoder(nc, dram)
    r = run_bass_kernel_spmd(nc, [{f"{n}_dram": a for n, a in arrays.items()}], core_ids=[0])
    return r.results[0]["out_dram"].reshape(B, T, D)
```
